# Optimizing a Trainium2 kernel written in Bass

```python
import numpy as np
import jax
import jax.numpy as jnp

def _softmax(x, axis=-1):
    return jax.nn.softmax(x, axis=axis)

def _gelu(x):
    return jax.nn.gelu(x, approximate=True)

def _silu(x):
    return jax.nn.silu(x)

def _sigmoid(x):
    return jax.nn.sigmoid(x)

def _layernorm(x, axis=-1, eps=1e-05):
    m = jnp.mean(x, axis=axis, keepdims=True)
    v = jnp.var(x, axis=axis, keepdims=True)
    return (x - m) / jnp.sqrt(v + eps)

def _scatter_add(tgt, idx, src, axis=0):
    return tgt.at[idx].add(src)

def _segment_sum(src, seg, n):
    return jax.ops.segment_sum(src, seg, n)
kernel_name = 'mk_hybrid_d4_jaxref_r8_b51f23'

def setup_inputs(seed: int=0):
    np.random.seed(seed)
    _w = jnp.asarray

    def _L0_attn_a_setup():
        import jax, jax.numpy as jnp
        import numpy as np
        DM, EXP, N, K, FRAC = (128, 2, 16, 4, 16)
        D = DM * EXP
        DTR = D // FRAC
        EPS = 1e-06

        def _mamba_block(x, rms_w, in_W, in_b, conv_w, conv_b, A_log, dbc_W, dbc_b, dup_W, dup_b, out_W, out_b):
            residual = x
            h = x * jax.lax.rsqrt(jnp.mean(x * x, axis=-1, keepdims=True) + EPS) * rms_w
            proj = h @ in_W + in_b
            x1, g = (proj[..., :D], proj[..., D:])
            xt = jnp.transpose(x1, (0, 2, 1))
            xc = jax.lax.conv_general_dilated(xt, conv_w[:, None, :], window_strides=(1,), padding=[(K - 1, 0)], feature_group_count=D, dimension_numbers=('NCH', 'OIH', 'NCH'))
            xc = xc + conv_b[:, None]
            x1 = jax.nn.silu(jnp.transpose(xc, (0, 2, 1)))
            A = -jnp.exp(A_log)
            dbc = x1 @ dbc_W + dbc_b
            delta, Bm, Cm = (dbc[..., :DTR], dbc[..., DTR:DTR + N], dbc[..., DTR + N:])
            delta = jax.nn.softplus(delta @ dup_W + dup_b)
            A_disc = jnp.exp(delta[..., None] * A)
            B_x = delta[..., None] * Bm[:, :, None, :] * x1[..., None]
            Ad_t = jnp.transpose(A_disc, (1, 0, 2, 3))
            Bx_t = jnp.transpose(B_x, (1, 0, 2, 3))

            def step(hc, inp):
                a, b = inp
                hc = a * hc + b
                return (hc, hc)
            h0 = jnp.zeros((x.shape[0], D, N), x1.dtype)
            _, hs = jax.lax.scan(step, h0, (Ad_t, Bx_t))
            y = jnp.einsum('tbdn,btn->btd', hs, Cm)
            y = jax.nn.silu(g) * y
            out = y @ out_W + out_b
            return out + residual
        key = jax.random.key(seed)
        ks = jax.random.split(key, 12)
        s = lambda fan: 1.0 / np.sqrt(fan)
        x = jax.random.normal(ks[0], (2, 128, DM), jnp.float32)
        rms_w = jnp.ones((DM,), jnp.float32)
        in_W = jax.random.normal(ks[1], (DM, 2 * D), jnp.float32) * s(DM)
        in_b = jax.random.normal(ks[2], (2 * D,), jnp.float32) * s(DM)
        conv_w = jax.random.normal(ks[3], (D, K), jnp.float32) * s(K)
        conv_b = jax.random.normal(ks[4], (D,), jnp.float32) * s(K)
        A_log = jnp.log(jnp.tile(jnp.arange(1, N + 1, dtype=jnp.float32), (D, 1)))
        dbc_W = jax.random.normal(ks[5], (D, DTR + 2 * N), jnp.float32) * s(D)
        dbc_b = jax.random.normal(ks[6], (DTR + 2 * N,), jnp.float32) * s(D)
        dup_W = jax.random.normal(ks[7], (DTR, D), jnp.float32) * s(DTR)
        dup_b = jax.random.normal(ks[8], (D,), jnp.float32) * s(DTR)
        out_W = jax.random.normal(ks[9], (D, DM), jnp.float32) * s(D)
        out_b = jax.random.normal(ks[10], (DM,), jnp.float32) * s(D)
        return dict(x=x, rms_w=rms_w, in_W=in_W, in_b=in_b, conv_w=conv_w, conv_b=conv_b, A_log=A_log, dbc_W=dbc_W, dbc_b=dbc_b, dup_W=dup_W, dup_b=dup_b, out_W=out_W, out_b=out_b)
    _L0_attn_a_in = _L0_attn_a_setup()

    def _L0_attn_b_setup():
        import jax, jax.numpy as jnp
        import numpy as np
        import math
        N_HEAD = 16
        HEAD_QKV = 128
        WM_DECAY_LENGTH = 256
        WM_DECAY_RATE = 1.0
        WM_ECHOIC = 16

        def decay_weight_matrix(n):
            dl = WM_DECAY_LENGTH - WM_ECHOIC + 1
            nums = jnp.linspace(0.0, 1.0, dl)
            decay_values = 1.0 - jnp.power(nums, 1.0 / (np.e * WM_DECAY_RATE))
            decay_values = jnp.concatenate([jnp.ones(WM_ECHOIC - 1), decay_values])
            decay_values = decay_values[:n]
            idx = jnp.arange(n)[:, None] - jnp.arange(n)[None, :]
            mat = decay_values[jnp.clip(idx, 0, n - 1)]
            return jnp.tril(mat).astype(jnp.float32)
        key = jax.random.key(seed)
        k1, k2, k3 = jax.random.split(key, 3)
        B, T, C = (2, 256, 128)
        x = jax.random.normal(k1, (B, T, C), dtype=jnp.float32)
        W_attn = jax.random.normal(k2, (C, 3 * HEAD_QKV), dtype=jnp.float32) * (1.0 / math.sqrt(C))
        W_proj = jax.random.normal(k3, (HEAD_QKV, C), dtype=jnp.float32) * (1.0 / math.sqrt(HEAD_QKV))
        return {'x': x, 'W_attn': W_attn, 'W_proj': W_proj}
    _L0_attn_b_in = _L0_attn_b_setup()

    def _L0_ffn_setup():
        import jax, jax.numpy as jnp
        import numpy as np
        EPS = 1e-08

        def _ternary_linear(x, w):
            alpha = jnp.mean(jnp.abs(w))
            w_t = jnp.sign(w) * (jnp.abs(w) > 0.5 * alpha).astype(w.dtype)
            w_q = w + jax.lax.stop_gradient(w_t - w)
            d = x.shape[-1]
            rms = jnp.sqrt(jnp.sum(x * x, axis=-1, keepdims=True)) / jnp.sqrt(jnp.asarray(d, x.dtype))
            x_norm = x / (rms + EPS)
            return jnp.einsum('bsd,fd->bsf', x_norm, w_q)
        key = jax.random.key(seed)
        k1, k2, k3 = jax.random.split(key, 3)
        d_model, d_ff = (128, 512)
        B, S = (4, 512)
        x = jax.random.normal(k1, (B, S, d_model), dtype=jnp.float32)
        w_up = jax.random.normal(k2, (d_ff, d_model), dtype=jnp.float32) * 0.02
        w_down = jax.random.normal(k3, (d_model, d_ff), dtype=jnp.float32) * 0.02
        return {'x': x, 'w_up': w_up, 'w_down': w_down}
    _L0_ffn_in = _L0_ffn_setup()

    def _L1_attn_a_setup():
        import jax, jax.numpy as jnp
        import numpy as np
        import math
        DIM = 128
        N_HEADS = 16
        HEAD_DIM = DIM // N_HEADS

        def rope(x):
            S = x.shape[-2]
            D = x.shape[-1]
            pos = jnp.arange(S, dtype=x.dtype)[:, None]
            dim = jnp.arange(D // 2, dtype=x.dtype)[None, :]
            theta = pos / jnp.exp(2.0 * dim / D * math.log(10000.0))
            sin = jnp.sin(theta)[None, None]
            cos = jnp.cos(theta)[None, None]
            x1 = x[..., ::2]
            x2 = x[..., 1::2]
            out1 = x1 * cos - x2 * sin
            out2 = x1 * sin + x2 * cos
            return jnp.stack([out1, out2], axis=-1).reshape(x.shape)
        key = jax.random.key(seed)
        ks = jax.random.split(key, 9)
        B, S = (2, 256)
        s = 1.0 / math.sqrt(DIM)
        inp = {'x': jax.random.normal(ks[0], (B, S, DIM), dtype=jnp.float32), 'wq': jax.random.normal(ks[1], (DIM, DIM), dtype=jnp.float32) * s, 'bq': jnp.zeros((DIM,), dtype=jnp.float32), 'wk': jax.random.normal(ks[2], (DIM, DIM), dtype=jnp.float32) * s, 'bk': jnp.zeros((DIM,), dtype=jnp.float32), 'wv': jax.random.normal(ks[3], (DIM, DIM), dtype=jnp.float32) * s, 'bv': jnp.zeros((DIM,), dtype=jnp.float32), 'wo': jax.random.normal(ks[4], (DIM, DIM), dtype=jnp.float32) * s, 'bo': jnp.zeros((DIM,), dtype=jnp.float32)}
        return inp
    _L1_attn_a_in = _L1_attn_a_setup()

    def _L1_attn_b_setup():
        import jax, jax.numpy as jnp
        import numpy as np
        D_MODEL = 128
        NUM_HEADS = 16
        D_K = D_MODEL // NUM_HEADS
        MAX_SEQ = 256

        def _rope_tables(seq_len):
            inv_freq = 1.0 / 10000.0 ** (jnp.arange(0, D_K, 2, dtype=jnp.float32) / D_K)
            pos = jnp.arange(seq_len, dtype=jnp.float32)
            freqs = jnp.einsum('i,j->ij', pos, inv_freq)
            return (jnp.cos(freqs), jnp.sin(freqs))

        def _apply_rope(x, cos_half, sin_half):
            x_even = x[..., ::2]
            x_odd = x[..., 1::2]
            r_even = x_even * cos_half - x_odd * sin_half
            r_odd = x_even * sin_half + x_odd * cos_half
            return jnp.stack([r_even, r_odd], axis=-1).reshape(x.shape)
        key = jax.random.key(seed)
        ks = jax.random.split(key, 9)
        B, S = (2, 256)
        scale = 1.0 / np.sqrt(D_MODEL)
        x = jax.random.normal(ks[0], (B, S, D_MODEL), dtype=jnp.float32)
        Wq = jax.random.normal(ks[1], (D_MODEL, D_MODEL), dtype=jnp.float32) * scale
        Wk = jax.random.normal(ks[2], (D_MODEL, D_MODEL), dtype=jnp.float32) * scale
        Wv = jax.random.normal(ks[3], (D_MODEL, D_MODEL), dtype=jnp.float32) * scale
        Wo = jax.random.normal(ks[4], (D_MODEL, D_MODEL), dtype=jnp.float32) * scale
        bq = jnp.zeros((D_MODEL,), jnp.float32)
        bk = jnp.zeros((D_MODEL,), jnp.float32)
        bv = jnp.zeros((D_MODEL,), jnp.float32)
        bo = jnp.zeros((D_MODEL,), jnp.float32)
        return {'x': x, 'Wq': Wq, 'bq': bq, 'Wk': Wk, 'bk': bk, 'Wv': Wv, 'bv': bv, 'Wo': Wo, 'bo': bo}
    _L1_attn_b_in = _L1_attn_b_setup()

    def _L1_ffn_setup():
        import jax, jax.numpy as jnp
        import numpy as np
        B, T, D, E = (4, 128, 128, 8)
        HD = 4 * D
        key = jax.random.key(seed)
        k1, k2, k3, k4 = jax.random.split(key, 4)
        std = 0.5 * D ** (-0.5)
        bound = 3.0 ** 0.5 * std
        x = jax.random.normal(k1, (B, T, D), dtype=jnp.float32)
        router_w = jax.random.normal(k2, (E, D), dtype=jnp.float32) * 0.02
        expert_fc = jax.random.uniform(k3, (E, D, HD), dtype=jnp.float32, minval=-bound, maxval=bound)
        expert_proj = jax.random.normal(k4, (E, D, HD), dtype=jnp.float32) * 0.02
        return {'x': x, 'router_w': router_w, 'expert_fc': expert_fc, 'expert_proj': expert_proj}
    _L1_ffn_in = _L1_ffn_setup()

    def _L2_attn_a_setup():
        import jax, jax.numpy as jnp
        import numpy as np
        import math
        B, N, D, H = (1, 512, 128, 16)
        HS = D // H
        NEG_INF = -10000.0
        key = jax.random.key(seed)
        k1, k2, k3, k4, k5 = jax.random.split(key, 5)
        return {'encodings': jax.random.normal(k1, (B, N, D), dtype=jnp.float32), 'attn_W': jax.random.normal(k2, (D, 3 * D), dtype=jnp.float32) * 0.02, 'attn_b': jax.random.normal(k3, (3 * D,), dtype=jnp.float32) * 0.02, 'out_W': jax.random.normal(k4, (D, D), dtype=jnp.float32) * 0.02, 'out_b': jax.random.normal(k5, (D,), dtype=jnp.float32) * 0.02}
    _L2_attn_a_in = _L2_attn_a_setup()

    def _L2_attn_b_setup():
        import jax, jax.numpy as jnp
        import numpy as np
        D_MODEL = 128
        D_STATE = 128
        D_CONV = 4
        EXPAND = 2
        NHEADS = 32
        NGROUPS = 1
        D_INNER = EXPAND * D_MODEL
        HEADDIM = D_INNER // NHEADS
        CHUNK = 32
        BATCH, SEQLEN = (2, 256)
        D_IN_PROJ = 2 * D_INNER + 2 * NGROUPS * D_STATE + NHEADS
        CONV_DIM = D_INNER + 2 * NGROUPS * D_STATE
        LN_EPS = 1e-05

        def _segsum(x):
            T = x.shape[-1]
            cs = jnp.cumsum(x, axis=-1)
            diff = cs[..., :, None] - cs[..., None, :]
            mask = jnp.tril(jnp.ones((T, T), bool))
            return jnp.where(mask, diff, -jnp.inf)

        def _ssd_chunked(X, A, B, C, chunk):
            b, l, h, p = X.shape
            c = l // chunk
            X = X.reshape(b, c, chunk, h, p)
            B = B.reshape(b, c, chunk, h, -1)
            C = C.reshape(b, c, chunk, h, -1)
            A = A.reshape(b, c, chunk, h).transpose(0, 3, 1, 2)
            A_cs = jnp.cumsum(A, axis=-1)
            L = jnp.exp(_segsum(A))
            Y_diag = jnp.einsum('bclhn,bcshn,bhcls,bcshp->bclhp', C, B, L, X)
            decay_states = jnp.exp(A_cs[..., -1:] - A_cs)
            states = jnp.einsum('bclhn,bhcl,bclhp->bchpn', B, decay_states, X)
            states = jnp.concatenate([jnp.zeros_like(states[:, :1]), states], axis=1)
            decay_chunk = jnp.exp(_segsum(jnp.pad(A_cs[..., -1], ((0, 0), (0, 0), (1, 0)))))
            new_states = jnp.einsum('bhzc,bchpn->bzhpn', decay_chunk, states)
            states = new_states[:, :-1]
            Y_off = jnp.einsum('bclhn,bchpn,bhcl->bclhp', C, states, jnp.exp(A_cs))
            return (Y_diag + Y_off).reshape(b, l, h, p)
        key = jax.random.key(seed)
        ks = jax.random.split(key, 8)
        dt = jnp.exp(jax.random.uniform(ks[4], (NHEADS,)) * (np.log(0.1) - np.log(0.001)) + np.log(0.001))
        dt = jnp.clip(dt, 0.0001, None)
        inv_dt = dt + jnp.log(-jnp.expm1(-dt))
        A = jax.random.uniform(ks[5], (NHEADS,), minval=1.0, maxval=16.0)
        return {'u': jax.random.normal(ks[0], (BATCH, SEQLEN, D_MODEL), jnp.float32), 'in_proj_w': jax.random.normal(ks[1], (D_IN_PROJ, D_MODEL), jnp.float32) * D_MODEL ** (-0.5), 'conv_w': jax.random.normal(ks[2], (CONV_DIM, D_CONV), jnp.float32) * D_CONV ** (-0.5), 'conv_b': jnp.zeros((CONV_DIM,), jnp.float32), 'dt_bias': inv_dt.astype(jnp.float32), 'A_log': jnp.log(A).astype(jnp.float32), 'ln_w': jnp.ones((D_INNER,), jnp.float32), 'out_proj_w': jax.random.normal(ks[3], (D_MODEL, D_INNER), jnp.float32) * D_INNER ** (-0.5)}
    _L2_attn_b_in = _L2_attn_b_setup()

    def _L2_ffn_setup():
        import jax, jax.numpy as jnp
        import numpy as np
        EMB = 128
        FF = 4 * EMB

        def _ternary(w):
            scale = jnp.maximum(jnp.mean(jnp.abs(w)), 1e-08)
            w_t = jnp.clip(jnp.round(w / scale), -1.0, 1.0)
            return w + jax.lax.stop_gradient(w_t - w)
        key = jax.random.key(seed)
        kx, k1, k2, kb1, kb2 = jax.random.split(key, 5)
        x = jax.random.normal(kx, (4, 256, EMB), dtype=jnp.float32)
        lim1 = 1.0 / np.sqrt(EMB)
        lim2 = 1.0 / np.sqrt(FF)
        W1 = jax.random.uniform(k1, (FF, EMB), jnp.float32, -lim1, lim1)
        b1 = jax.random.uniform(kb1, (FF,), jnp.float32, -lim1, lim1)
        W2 = jax.random.uniform(k2, (EMB, FF), jnp.float32, -lim2, lim2)
        b2 = jax.random.uniform(kb2, (EMB,), jnp.float32, -lim2, lim2)
        return {'x': x, 'W1': W1, 'b1': b1, 'W2': W2, 'b2': b2}
    _L2_ffn_in = _L2_ffn_setup()

    def _L3_attn_a_setup():
        import jax, jax.numpy as jnp
        import numpy as np
        B, T, D, N = (4, 128, 128, 16)

        def _depthwise_conv3_same(x, w, b):
            xp = jnp.pad(x, ((0, 0), (1, 1), (0, 0)))
            return xp[:, :-2] * w[:, 0] + xp[:, 1:-1] * w[:, 1] + xp[:, 2:] * w[:, 2] + b

        def _selective_scan(x, A, Wb, bb, Wc, bc, Wdt, bdt):
            dt = jax.nn.softplus(x @ Wdt + bdt)
            Bm = x @ Wb + bb
            Cm = x @ Wc + bc
            dA = jnp.exp(dt[..., None] * A)
            dBx = dt[..., None] * Bm[:, :, None, :] * x[..., None]

            def step(h, ins):
                dA_t, dBx_t, C_t = ins
                h = dA_t * h + dBx_t
                y = jnp.einsum('bdn,bn->bd', h, C_t)
                return (h, y)
            h0 = jnp.zeros((x.shape[0], x.shape[2], A.shape[1]), x.dtype)
            _, ys = jax.lax.scan(step, h0, (dA.transpose(1, 0, 2, 3), dBx.transpose(1, 0, 2, 3), Cm.transpose(1, 0, 2)))
            return ys.transpose(1, 0, 2)
        key = jax.random.key(seed)
        ks = jax.random.split(key, 16)
        s = 1.0 / np.sqrt(D)
        inp = {'u': jax.random.normal(ks[0], (B, T, D), jnp.float32), 'Win': jax.random.normal(ks[1], (D, D), jnp.float32) * s, 'b_in': jnp.zeros((D,), jnp.float32), 'Wg': jax.random.normal(ks[2], (D, D), jnp.float32) * s, 'bg': jnp.zeros((D,), jnp.float32), 'Wout': jax.random.normal(ks[3], (D, D), jnp.float32) * s, 'bout': jnp.zeros((D,), jnp.float32), 'convw': jax.random.normal(ks[4], (D, 3), jnp.float32) * 0.5, 'convb': jnp.zeros((D,), jnp.float32), 'A': -jnp.exp(jax.random.normal(ks[5], (D, N), jnp.float32) * 0.5), 'Wb': jax.random.normal(ks[6], (D, N), jnp.float32) * s, 'bb': jnp.zeros((N,), jnp.float32), 'Wc': jax.random.normal(ks[7], (D, N), jnp.float32) * s, 'bc': jnp.zeros((N,), jnp.float32), 'Wdt': jax.random.normal(ks[8], (D, D), jnp.float32) * s, 'bdt': jnp.full((D,), -2.0, jnp.float32)}
        return inp
    _L3_attn_a_in = _L3_attn_a_setup()

    def _L3_attn_b_setup():
        import jax, jax.numpy as jnp
        import numpy as np
        D_IN = 128
        D_OUT = 128
        H = 16
        G = 4
        LF = 2
        HEAD_OUT = D_OUT // H
        DQ = HEAD_OUT // LF
        B, T = (2, 256)

        def _alibi_bias(T, dtype):
            slopes = jnp.asarray(2.0 ** (-8.0 * np.arange(1, H + 1) / H), dtype=dtype)
            pos = jnp.arange(T)
            rel = (pos[None, :] - pos[:, None]).astype(dtype)
            return slopes[:, None, None] * rel[None, :, :]
        key = jax.random.key(seed)
        ks = jax.random.split(key, 7)
        s = 0.02
        return {'x': jax.random.normal(ks[0], (B, T, D_IN), dtype=jnp.float32), 'Wq': jax.random.normal(ks[1], (D_IN, D_OUT // LF), dtype=jnp.float32) * s, 'Wk': jax.random.normal(ks[2], (D_IN, D_OUT // LF // G), dtype=jnp.float32) * s, 'Wv': jax.random.normal(ks[3], (D_IN, D_OUT // G), dtype=jnp.float32) * s, 'Wp': jax.random.normal(ks[4], (D_OUT, D_OUT), dtype=jnp.float32) * s, 'bp': jnp.zeros((D_OUT,), dtype=jnp.float32)}
    _L3_attn_b_in = _L3_attn_b_setup()

    def _L3_ffn_setup():
        import jax, jax.numpy as jnp
        import numpy as np
        D_IN, D_HID = (128, 512)

        def _ternary(key, shape):
            return jax.random.randint(key, shape, -1, 2).astype(jnp.float32)

        def _tlin(x, w, s):
            return jnp.einsum('bsi,oi->bso', x, w) * s
        key = jax.random.key(seed)
        ks = jax.random.split(key, 12)
        inv = lambda fan: 1.0 / np.sqrt(fan).astype(np.float32)
        return {'x': jax.random.normal(ks[0], (4, 256, D_IN), dtype=jnp.float32), 'w1_w': _ternary(ks[1], (D_HID, D_IN)), 'w1_s': jax.random.uniform(ks[2], (D_HID,), dtype=jnp.float32) * inv(D_IN), 'w2_w': _ternary(ks[3], (D_HID, D_IN)), 'w2_s': jax.random.uniform(ks[4], (D_HID,), dtype=jnp.float32) * inv(D_IN), 'h1_w': _ternary(ks[5], (D_HID, D_HID)), 'h1_s': jax.random.uniform(ks[6], (D_HID,), dtype=jnp.float32) * inv(D_HID), 'h2_w': _ternary(ks[7], (D_HID, D_HID)), 'h2_s': jax.random.uniform(ks[8], (D_HID,), dtype=jnp.float32) * inv(D_HID), 'w3_w': _ternary(ks[9], (D_IN, D_HID)), 'w3_s': jax.random.uniform(ks[10], (D_IN,), dtype=jnp.float32) * inv(D_HID)}
    _L3_ffn_in = _L3_ffn_setup()
    _d = {'L0_attn_a_x': _L0_attn_a_in['x'], 'L0_attn_a_rms_w': _L0_attn_a_in['rms_w'], 'L0_attn_a_in_W': _L0_attn_a_in['in_W'], 'L0_attn_a_in_b': _L0_attn_a_in['in_b'], 'L0_attn_a_conv_w': _L0_attn_a_in['conv_w'], 'L0_attn_a_conv_b': _L0_attn_a_in['conv_b'], 'L0_attn_a_A_log': _L0_attn_a_in['A_log'], 'L0_attn_a_dbc_W': _L0_attn_a_in['dbc_W'], 'L0_attn_a_dbc_b': _L0_attn_a_in['dbc_b'], 'L0_attn_a_dup_W': _L0_attn_a_in['dup_W'], 'L0_attn_a_dup_b': _L0_attn_a_in['dup_b'], 'L0_attn_a_out_W': _L0_attn_a_in['out_W'], 'L0_attn_a_out_b': _L0_attn_a_in['out_b'], 'L0_attn_b_W_attn': _L0_attn_b_in['W_attn'], 'L0_attn_b_W_proj': _L0_attn_b_in['W_proj'], 'L0_ffn_w_up': _L0_ffn_in['w_up'], 'L0_ffn_w_down': _L0_ffn_in['w_down'], 'L1_attn_a_wq': _L1_attn_a_in['wq'], 'L1_attn_a_bq': _L1_attn_a_in['bq'], 'L1_attn_a_wk': _L1_attn_a_in['wk'], 'L1_attn_a_bk': _L1_attn_a_in['bk'], 'L1_attn_a_wv': _L1_attn_a_in['wv'], 'L1_attn_a_bv': _L1_attn_a_in['bv'], 'L1_attn_a_wo': _L1_attn_a_in['wo'], 'L1_attn_a_bo': _L1_attn_a_in['bo'], 'L1_attn_b_Wq': _L1_attn_b_in['Wq'], 'L1_attn_b_bq': _L1_attn_b_in['bq'], 'L1_attn_b_Wk': _L1_attn_b_in['Wk'], 'L1_attn_b_bk': _L1_attn_b_in['bk'], 'L1_attn_b_Wv': _L1_attn_b_in['Wv'], 'L1_attn_b_bv': _L1_attn_b_in['bv'], 'L1_attn_b_Wo': _L1_attn_b_in['Wo'], 'L1_attn_b_bo': _L1_attn_b_in['bo'], 'L1_ffn_router_w': _L1_ffn_in['router_w'], 'L1_ffn_expert_fc': _L1_ffn_in['expert_fc'], 'L1_ffn_expert_proj': _L1_ffn_in['expert_proj'], 'L2_attn_a_attn_W': _L2_attn_a_in['attn_W'], 'L2_attn_a_attn_b': _L2_attn_a_in['attn_b'], 'L2_attn_a_out_W': _L2_attn_a_in['out_W'], 'L2_attn_a_out_b': _L2_attn_a_in['out_b'], 'L2_attn_b_in_proj_w': _L2_attn_b_in['in_proj_w'], 'L2_attn_b_conv_w': _L2_attn_b_in['conv_w'], 'L2_attn_b_conv_b': _L2_attn_b_in['conv_b'], 'L2_attn_b_dt_bias': _L2_attn_b_in['dt_bias'], 'L2_attn_b_A_log': _L2_attn_b_in['A_log'], 'L2_attn_b_ln_w': _L2_attn_b_in['ln_w'], 'L2_attn_b_out_proj_w': _L2_attn_b_in['out_proj_w'], 'L2_ffn_W1': _L2_ffn_in['W1'], 'L2_ffn_b1': _L2_ffn_in['b1'], 'L2_ffn_W2': _L2_ffn_in['W2'], 'L2_ffn_b2': _L2_ffn_in['b2'], 'L3_attn_a_Win': _L3_attn_a_in['Win'], 'L3_attn_a_b_in': _L3_attn_a_in['b_in'], 'L3_attn_a_Wg': _L3_attn_a_in['Wg'], 'L3_attn_a_bg': _L3_attn_a_in['bg'], 'L3_attn_a_Wout': _L3_attn_a_in['Wout'], 'L3_attn_a_bout': _L3_attn_a_in['bout'], 'L3_attn_a_convw': _L3_attn_a_in['convw'], 'L3_attn_a_convb': _L3_attn_a_in['convb'], 'L3_attn_a_A': _L3_attn_a_in['A'], 'L3_attn_a_Wb': _L3_attn_a_in['Wb'], 'L3_attn_a_bb': _L3_attn_a_in['bb'], 'L3_attn_a_Wc': _L3_attn_a_in['Wc'], 'L3_attn_a_bc': _L3_attn_a_in['bc'], 'L3_attn_a_Wdt': _L3_attn_a_in['Wdt'], 'L3_attn_a_bdt': _L3_attn_a_in['bdt'], 'L3_attn_b_Wq': _L3_attn_b_in['Wq'], 'L3_attn_b_Wk': _L3_attn_b_in['Wk'], 'L3_attn_b_Wv': _L3_attn_b_in['Wv'], 'L3_attn_b_Wp': _L3_attn_b_in['Wp'], 'L3_attn_b_bp': _L3_attn_b_in['bp'], 'L3_ffn_w1_w': _L3_ffn_in['w1_w'], 'L3_ffn_w1_s': _L3_ffn_in['w1_s'], 'L3_ffn_w2_w': _L3_ffn_in['w2_w'], 'L3_ffn_w2_s': _L3_ffn_in['w2_s'], 'L3_ffn_h1_w': _L3_ffn_in['h1_w'], 'L3_ffn_h1_s': _L3_ffn_in['h1_s'], 'L3_ffn_h2_w': _L3_ffn_in['h2_w'], 'L3_ffn_h2_s': _L3_ffn_in['h2_s'], 'L3_ffn_w3_w': _L3_ffn_in['w3_w'], 'L3_ffn_w3_s': _L3_ffn_in['w3_s']}
    _x0 = _d['L0_attn_a_x']
    _d['L0_attn_a_x'] = jax.random.normal(jax.random.fold_in(jax.random.key(seed), 1), (4, 1024, 128), dtype=_x0.dtype)
    del _x0
    return _d

def reference(L0_attn_a_x, L0_attn_a_rms_w, L0_attn_a_in_W, L0_attn_a_in_b, L0_attn_a_conv_w, L0_attn_a_conv_b, L0_attn_a_A_log, L0_attn_a_dbc_W, L0_attn_a_dbc_b, L0_attn_a_dup_W, L0_attn_a_dup_b, L0_attn_a_out_W, L0_attn_a_out_b, L0_attn_b_W_attn, L0_attn_b_W_proj, L0_ffn_w_up, L0_ffn_w_down, L1_attn_a_wq, L1_attn_a_bq, L1_attn_a_wk, L1_attn_a_bk, L1_attn_a_wv, L1_attn_a_bv, L1_attn_a_wo, L1_attn_a_bo, L1_attn_b_Wq, L1_attn_b_bq, L1_attn_b_Wk, L1_attn_b_bk, L1_attn_b_Wv, L1_attn_b_bv, L1_attn_b_Wo, L1_attn_b_bo, L1_ffn_router_w, L1_ffn_expert_fc, L1_ffn_expert_proj, L2_attn_a_attn_W, L2_attn_a_attn_b, L2_attn_a_out_W, L2_attn_a_out_b, L2_attn_b_in_proj_w, L2_attn_b_conv_w, L2_attn_b_conv_b, L2_attn_b_dt_bias, L2_attn_b_A_log, L2_attn_b_ln_w, L2_attn_b_out_proj_w, L2_ffn_W1, L2_ffn_b1, L2_ffn_W2, L2_ffn_b2, L3_attn_a_Win, L3_attn_a_b_in, L3_attn_a_Wg, L3_attn_a_bg, L3_attn_a_Wout, L3_attn_a_bout, L3_attn_a_convw, L3_attn_a_convb, L3_attn_a_A, L3_attn_a_Wb, L3_attn_a_bb, L3_attn_a_Wc, L3_attn_a_bc, L3_attn_a_Wdt, L3_attn_a_bdt, L3_attn_b_Wq, L3_attn_b_Wk, L3_attn_b_Wv, L3_attn_b_Wp, L3_attn_b_bp, L3_ffn_w1_w, L3_ffn_w1_s, L3_ffn_w2_w, L3_ffn_w2_s, L3_ffn_h1_w, L3_ffn_h1_s, L3_ffn_h2_w, L3_ffn_h2_s, L3_ffn_w3_w, L3_ffn_w3_s):

    def _L0_attn_a_ref(x, rms_w, in_W, in_b, conv_w, conv_b, A_log, dbc_W, dbc_b, dup_W, dup_b, out_W, out_b):
        import jax, jax.numpy as jnp
        import numpy as np
        DM, EXP, N, K, FRAC = (128, 2, 16, 4, 16)
        D = DM * EXP
        DTR = D // FRAC
        EPS = 1e-06

        def _mamba_block(x, rms_w, in_W, in_b, conv_w, conv_b, A_log, dbc_W, dbc_b, dup_W, dup_b, out_W, out_b):
            residual = x
            h = x * jax.lax.rsqrt(jnp.mean(x * x, axis=-1, keepdims=True) + EPS) * rms_w
            proj = h @ in_W + in_b
            x1, g = (proj[..., :D], proj[..., D:])
            xt = jnp.transpose(x1, (0, 2, 1))
            xc = jax.lax.conv_general_dilated(xt, conv_w[:, None, :], window_strides=(1,), padding=[(K - 1, 0)], feature_group_count=D, dimension_numbers=('NCH', 'OIH', 'NCH'))
            xc = xc + conv_b[:, None]
            x1 = jax.nn.silu(jnp.transpose(xc, (0, 2, 1)))
            A = -jnp.exp(A_log)
            dbc = x1 @ dbc_W + dbc_b
            delta, Bm, Cm = (dbc[..., :DTR], dbc[..., DTR:DTR + N], dbc[..., DTR + N:])
            delta = jax.nn.softplus(delta @ dup_W + dup_b)
            A_disc = jnp.exp(delta[..., None] * A)
            B_x = delta[..., None] * Bm[:, :, None, :] * x1[..., None]
            Ad_t = jnp.transpose(A_disc, (1, 0, 2, 3))
            Bx_t = jnp.transpose(B_x, (1, 0, 2, 3))

            def step(hc, inp):
                a, b = inp
                hc = a * hc + b
                return (hc, hc)
            h0 = jnp.zeros((x.shape[0], D, N), x1.dtype)
            _, hs = jax.lax.scan(step, h0, (Ad_t, Bx_t))
            y = jnp.einsum('tbdn,btn->btd', hs, Cm)
            y = jax.nn.silu(g) * y
            out = y @ out_W + out_b
            return out + residual
        return _mamba_block(x, rms_w, in_W, in_b, conv_w, conv_b, A_log, dbc_W, dbc_b, dup_W, dup_b, out_W, out_b)

    def _L0_attn_b_ref(x, W_attn, W_proj):
        import jax, jax.numpy as jnp
        import numpy as np
        import math
        N_HEAD = 16
        HEAD_QKV = 128
        WM_DECAY_LENGTH = 256
        WM_DECAY_RATE = 1.0
        WM_ECHOIC = 16

        def decay_weight_matrix(n):
            dl = WM_DECAY_LENGTH - WM_ECHOIC + 1
            nums = jnp.linspace(0.0, 1.0, dl)
            decay_values = 1.0 - jnp.power(nums, 1.0 / (np.e * WM_DECAY_RATE))
            decay_values = jnp.concatenate([jnp.ones(WM_ECHOIC - 1), decay_values])
            decay_values = decay_values[:n]
            idx = jnp.arange(n)[:, None] - jnp.arange(n)[None, :]
            mat = decay_values[jnp.clip(idx, 0, n - 1)]
            return jnp.tril(mat).astype(jnp.float32)
        B, T, C = x.shape
        hd = HEAD_QKV // N_HEAD
        qkv = x @ W_attn
        q, k, v = jnp.split(qkv, 3, axis=-1)
        q = q.reshape(B, T, N_HEAD, hd).transpose(0, 2, 1, 3)
        k = k.reshape(B, T, N_HEAD, hd).transpose(0, 2, 1, 3)
        v = v.reshape(B, T, N_HEAD, hd).transpose(0, 2, 1, 3)
        att = jnp.einsum('bhqd,bhkd->bhqk', q, k) * (1.0 / math.sqrt(hd))
        causal = jnp.tril(jnp.ones((T, T), dtype=bool))
        att = jnp.where(causal, att, -jnp.inf)
        att = jax.nn.softmax(att, axis=-1)
        att = att * decay_weight_matrix(T)
        y = jnp.einsum('bhqk,bhkd->bhqd', att, v)
        y = y.transpose(0, 2, 1, 3).reshape(B, T, HEAD_QKV)
        return y @ W_proj

    def _L0_ffn_ref(x, w_up, w_down):
        import jax, jax.numpy as jnp
        import numpy as np
        EPS = 1e-08

        def _ternary_linear(x, w):
            alpha = jnp.mean(jnp.abs(w))
            w_t = jnp.sign(w) * (jnp.abs(w) > 0.5 * alpha).astype(w.dtype)
            w_q = w + jax.lax.stop_gradient(w_t - w)
            d = x.shape[-1]
            rms = jnp.sqrt(jnp.sum(x * x, axis=-1, keepdims=True)) / jnp.sqrt(jnp.asarray(d, x.dtype))
            x_norm = x / (rms + EPS)
            return jnp.einsum('bsd,fd->bsf', x_norm, w_q)
        h = jax.nn.gelu(_ternary_linear(x, w_up), approximate=False)
        return _ternary_linear(h, w_down)

    def _L1_attn_a_ref(x, wq, bq, wk, bk, wv, bv, wo, bo):
        import jax, jax.numpy as jnp
        import numpy as np
        import math
        DIM = 128
        N_HEADS = 16
        HEAD_DIM = DIM // N_HEADS

        def rope(x):
            S = x.shape[-2]
            D = x.shape[-1]
            pos = jnp.arange(S, dtype=x.dtype)[:, None]
            dim = jnp.arange(D // 2, dtype=x.dtype)[None, :]
            theta = pos / jnp.exp(2.0 * dim / D * math.log(10000.0))
            sin = jnp.sin(theta)[None, None]
            cos = jnp.cos(theta)[None, None]
            x1 = x[..., ::2]
            x2 = x[..., 1::2]
            out1 = x1 * cos - x2 * sin
            out2 = x1 * sin + x2 * cos
            return jnp.stack([out1, out2], axis=-1).reshape(x.shape)
        B, S, _ = x.shape

        def proj(w, b):
            y = jnp.einsum('bsd,ed->bse', x, w) + b
            return y.reshape(B, S, N_HEADS, HEAD_DIM).transpose(0, 2, 1, 3)
        q = rope(proj(wq, bq))
        k = rope(proj(wk, bk))
        v = proj(wv, bv)
        score = jnp.einsum('bhqd,bhkd->bhqk', q, k) / math.sqrt(HEAD_DIM)
        causal = jnp.tril(jnp.ones((S, S), dtype=bool))
        score = jnp.where(causal[None, None], score, -jnp.inf)
        attn = jax.nn.softmax(score, axis=-1)
        out = jnp.einsum('bhqk,bhkd->bhqd', attn, v)
        out = out.transpose(0, 2, 1, 3).reshape(B, S, DIM)
        return jnp.einsum('bsd,ed->bse', out, wo) + bo

    def _L1_attn_b_ref(x, Wq, bq, Wk, bk, Wv, bv, Wo, bo):
        import jax, jax.numpy as jnp
        import numpy as np
        D_MODEL = 128
        NUM_HEADS = 16
        D_K = D_MODEL // NUM_HEADS
        MAX_SEQ = 256

        def _rope_tables(seq_len):
            inv_freq = 1.0 / 10000.0 ** (jnp.arange(0, D_K, 2, dtype=jnp.float32) / D_K)
            pos = jnp.arange(seq_len, dtype=jnp.float32)
            freqs = jnp.einsum('i,j->ij', pos, inv_freq)
            return (jnp.cos(freqs), jnp.sin(freqs))

        def _apply_rope(x, cos_half, sin_half):
            x_even = x[..., ::2]
            x_odd = x[..., 1::2]
            r_even = x_even * cos_half - x_odd * sin_half
            r_odd = x_even * sin_half + x_odd * cos_half
            return jnp.stack([r_even, r_odd], axis=-1).reshape(x.shape)
        B, S, _ = x.shape
        H, dk = (NUM_HEADS, D_K)
        q = (x @ Wq + bq).reshape(B, S, H, dk)
        k = (x @ Wk + bk).reshape(B, S, H, dk)
        v = (x @ Wv + bv).reshape(B, S, H, dk)
        cos_half, sin_half = _rope_tables(S)
        cos_half = cos_half[None, :, None, :]
        sin_half = sin_half[None, :, None, :]
        q = _apply_rope(q, cos_half, sin_half)
        k = _apply_rope(k, cos_half, sin_half)
        q = q.transpose(0, 2, 1, 3)
        k = k.transpose(0, 2, 1, 3)
        v = v.transpose(0, 2, 1, 3)
        scores = jnp.einsum('bhqd,bhkd->bhqk', q, k) / jnp.sqrt(jnp.float32(dk))
        causal = jnp.where(jnp.tril(jnp.ones((S, S), jnp.float32)) == 0, -1000000000.0, 0.0)
        scores = scores + causal
        attn = jax.nn.softmax(scores, axis=-1)
        out = jnp.einsum('bhqk,bhkd->bhqd', attn, v)
        out = out.transpose(0, 2, 1, 3).reshape(B, S, H * dk)
        return out @ Wo + bo

    def _L1_ffn_ref(x, router_w, expert_fc, expert_proj):
        import jax, jax.numpy as jnp
        import numpy as np
        B, T, D, E = (4, 128, 128, 8)
        HD = 4 * D
        logits = jnp.einsum('btd,ed->bte', x, router_w)
        probs = jax.nn.softmax(logits, axis=-1)
        expert_ids = jnp.argmax(probs, axis=-1)
        mask = jax.nn.one_hot(expert_ids, E, dtype=x.dtype)
        h = jnp.einsum('btd,edh->ebth', x, expert_fc)
        h = jnp.square(jax.nn.relu(h))
        out_e = jnp.einsum('ebth,edh->ebtd', h, expert_proj)
        output = jnp.einsum('ebtd,bte->btd', out_e, mask)
        return output

    def _L2_attn_a_ref(encodings, attn_W, attn_b, out_W, out_b):
        import jax, jax.numpy as jnp
        import numpy as np
        import math
        B, N, D, H = (1, 512, 128, 16)
        HS = D // H
        NEG_INF = -10000.0
        b, n, d = encodings.shape
        qkv = encodings @ attn_W + attn_b
        qkv = qkv.reshape(b, n, H, 3 * HS).transpose(0, 2, 1, 3)
        q, k, v = jnp.split(qkv, 3, axis=-1)
        scores = jnp.einsum('bhki,bhqi->bhkq', k, q) / math.sqrt(HS)
        mask = jnp.arange(n)[:, None] <= jnp.arange(n)[None, :]
        scores = jnp.where(mask, scores, jnp.float32(NEG_INF))
        prob = jax.nn.softmax(scores, axis=2)
        combined = jnp.einsum('bhkq,bhkl->bhql', prob, v)
        out = combined.transpose(0, 2, 1, 3).reshape(b, n, d)
        return out @ out_W + out_b

    def _L2_attn_b_ref(u, in_proj_w, conv_w, conv_b, dt_bias, A_log, ln_w, out_proj_w):
        import jax, jax.numpy as jnp
        import numpy as np
        D_MODEL = 128
        D_STATE = 128
        D_CONV = 4
        EXPAND = 2
        NHEADS = 32
        NGROUPS = 1
        D_INNER = EXPAND * D_MODEL
        HEADDIM = D_INNER // NHEADS
        CHUNK = 32
        BATCH, SEQLEN = (2, 256)
        D_IN_PROJ = 2 * D_INNER + 2 * NGROUPS * D_STATE + NHEADS
        CONV_DIM = D_INNER + 2 * NGROUPS * D_STATE
        LN_EPS = 1e-05

        def _segsum(x):
            T = x.shape[-1]
            cs = jnp.cumsum(x, axis=-1)
            diff = cs[..., :, None] - cs[..., None, :]
            mask = jnp.tril(jnp.ones((T, T), bool))
            return jnp.where(mask, diff, -jnp.inf)

        def _ssd_chunked(X, A, B, C, chunk):
            b, l, h, p = X.shape
            c = l // chunk
            X = X.reshape(b, c, chunk, h, p)
            B = B.reshape(b, c, chunk, h, -1)
            C = C.reshape(b, c, chunk, h, -1)
            A = A.reshape(b, c, chunk, h).transpose(0, 3, 1, 2)
            A_cs = jnp.cumsum(A, axis=-1)
            L = jnp.exp(_segsum(A))
            Y_diag = jnp.einsum('bclhn,bcshn,bhcls,bcshp->bclhp', C, B, L, X)
            decay_states = jnp.exp(A_cs[..., -1:] - A_cs)
            states = jnp.einsum('bclhn,bhcl,bclhp->bchpn', B, decay_states, X)
            states = jnp.concatenate([jnp.zeros_like(states[:, :1]), states], axis=1)
            decay_chunk = jnp.exp(_segsum(jnp.pad(A_cs[..., -1], ((0, 0), (0, 0), (1, 0)))))
            new_states = jnp.einsum('bhzc,bchpn->bzhpn', decay_chunk, states)
            states = new_states[:, :-1]
            Y_off = jnp.einsum('bclhn,bchpn,bhcl->bclhp', C, states, jnp.exp(A_cs))
            return (Y_diag + Y_off).reshape(b, l, h, p)
        b, l, _ = u.shape
        zxbcdt = u @ in_proj_w.T
        z = zxbcdt[..., :D_INNER]
        xBC = zxbcdt[..., D_INNER:D_INNER + CONV_DIM]
        dt = jax.nn.softplus(zxbcdt[..., -NHEADS:] + dt_bias)
        A = -jnp.exp(A_log)
        xp = jnp.pad(xBC, ((0, 0), (D_CONV - 1, 0), (0, 0)))
        acc = conv_b
        for k in range(D_CONV):
            acc = acc + xp[:, k:k + l, :] * conv_w[:, k]
        xBC = jax.nn.silu(acc)
        x = xBC[..., :D_INNER].reshape(b, l, NHEADS, HEADDIM)
        Bm = xBC[..., D_INNER:D_INNER + NGROUPS * D_STATE].reshape(b, l, NGROUPS, D_STATE)
        Cm = xBC[..., D_INNER + NGROUPS * D_STATE:].reshape(b, l, NGROUPS, D_STATE)
        rep = NHEADS // NGROUPS
        Bh = jnp.repeat(Bm, rep, axis=2)
        Ch = jnp.repeat(Cm, rep, axis=2)
        y = _ssd_chunked(x * dt[..., None], A * dt, Bh, Ch, CHUNK)
        y = y.reshape(b, l, D_INNER)
        mu = y.mean(-1, keepdims=True)
        var = y.var(-1, keepdims=True)
        y = (y - mu) / jnp.sqrt(var + LN_EPS) * ln_w
        y = y * jax.nn.silu(z)
        return y @ out_proj_w.T

    def _L2_ffn_ref(x, W1, b1, W2, b2):
        import jax, jax.numpy as jnp
        import numpy as np
        EMB = 128
        FF = 4 * EMB

        def _ternary(w):
            scale = jnp.maximum(jnp.mean(jnp.abs(w)), 1e-08)
            w_t = jnp.clip(jnp.round(w / scale), -1.0, 1.0)
            return w + jax.lax.stop_gradient(w_t - w)
        h = jnp.einsum('bsd,fd->bsf', x, _ternary(W1)) + b1
        h = jax.nn.gelu(h, approximate=False)
        out = jnp.einsum('bsf,df->bsd', h, _ternary(W2)) + b2
        return out

    def _L3_attn_a_ref(u, Win, b_in, Wg, bg, Wout, bout, convw, convb, A, Wb, bb, Wc, bc, Wdt, bdt):
        import jax, jax.numpy as jnp
        import numpy as np
        B, T, D, N = (4, 128, 128, 16)

        def _depthwise_conv3_same(x, w, b):
            xp = jnp.pad(x, ((0, 0), (1, 1), (0, 0)))
            return xp[:, :-2] * w[:, 0] + xp[:, 1:-1] * w[:, 1] + xp[:, 2:] * w[:, 2] + b

        def _selective_scan(x, A, Wb, bb, Wc, bc, Wdt, bdt):
            dt = jax.nn.softplus(x @ Wdt + bdt)
            Bm = x @ Wb + bb
            Cm = x @ Wc + bc
            dA = jnp.exp(dt[..., None] * A)
            dBx = dt[..., None] * Bm[:, :, None, :] * x[..., None]

            def step(h, ins):
                dA_t, dBx_t, C_t = ins
                h = dA_t * h + dBx_t
                y = jnp.einsum('bdn,bn->bd', h, C_t)
                return (h, y)
            h0 = jnp.zeros((x.shape[0], x.shape[2], A.shape[1]), x.dtype)
            _, ys = jax.lax.scan(step, h0, (dA.transpose(1, 0, 2, 3), dBx.transpose(1, 0, 2, 3), Cm.transpose(1, 0, 2)))
            return ys.transpose(1, 0, 2)
        x = u @ Win + b_in
        x = _depthwise_conv3_same(x, convw, convb)
        x = jax.nn.silu(x)
        x_ssm = _selective_scan(x, A, Wb, bb, Wc, bc, Wdt, bdt)
        z = jax.nn.silu(u @ Wg + bg)
        return x_ssm * z @ Wout + bout

    def _L3_attn_b_ref(x, Wq, Wk, Wv, Wp, bp):
        import jax, jax.numpy as jnp
        import numpy as np
        D_IN = 128
        D_OUT = 128
        H = 16
        G = 4
        LF = 2
        HEAD_OUT = D_OUT // H
        DQ = HEAD_OUT // LF
        B, T = (2, 256)

        def _alibi_bias(T, dtype):
            slopes = jnp.asarray(2.0 ** (-8.0 * np.arange(1, H + 1) / H), dtype=dtype)
            pos = jnp.arange(T)
            rel = (pos[None, :] - pos[:, None]).astype(dtype)
            return slopes[:, None, None] * rel[None, :, :]
        b, t, _ = x.shape
        q = x @ Wq
        k = jnp.tile(x @ Wk, (1, 1, G))
        v = jnp.tile(x @ Wv, (1, 1, G))
        q = q.reshape(b, t, H, DQ).transpose(0, 2, 1, 3)
        k = k.reshape(b, t, H, DQ).transpose(0, 2, 1, 3)
        v = v.reshape(b, t, H, HEAD_OUT).transpose(0, 2, 1, 3)
        scores = jnp.einsum('bhqd,bhkd->bhqk', q, k)
        causal = jnp.triu(jnp.ones((t, t), dtype=bool), k=1)
        scores = jnp.where(causal, -jnp.inf, scores)
        scores = (scores + _alibi_bias(t, scores.dtype)) / jnp.sqrt(jnp.asarray(DQ, scores.dtype))
        w = jax.nn.softmax(scores, axis=-1)
        ctx = jnp.einsum('bhqk,bhkd->bqhd', w, v).reshape(b, t, D_OUT)
        return ctx @ Wp + bp

    def _L3_ffn_ref(x, w1_w, w1_s, w2_w, w2_s, h1_w, h1_s, h2_w, h2_s, w3_w, w3_s):
        import jax, jax.numpy as jnp
        import numpy as np
        D_IN, D_HID = (128, 512)

        def _ternary(key, shape):
            return jax.random.randint(key, shape, -1, 2).astype(jnp.float32)

        def _tlin(x, w, s):
            return jnp.einsum('bsi,oi->bso', x, w) * s
        h = jax.nn.silu(_tlin(x, w1_w, w1_s)) * _tlin(x, w2_w, w2_s)
        h = jax.nn.gelu(_tlin(h, h1_w, h1_s), approximate=False)
        h = jax.nn.gelu(_tlin(h, h2_w, h2_s), approximate=False)
        return _tlin(h, w3_w, w3_s)
    x = L0_attn_a_x
    x = x + _L0_attn_a_ref(_layernorm(x, axis=-1), L0_attn_a_rms_w, L0_attn_a_in_W, L0_attn_a_in_b, L0_attn_a_conv_w, L0_attn_a_conv_b, L0_attn_a_A_log, L0_attn_a_dbc_W, L0_attn_a_dbc_b, L0_attn_a_dup_W, L0_attn_a_dup_b, L0_attn_a_out_W, L0_attn_a_out_b)
    x = x + _L0_ffn_ref(_layernorm(x, axis=-1), L0_ffn_w_up, L0_ffn_w_down)
    x = x + _L0_attn_b_ref(_layernorm(x, axis=-1), L0_attn_b_W_attn, L0_attn_b_W_proj)
    x = x + _L0_ffn_ref(_layernorm(x, axis=-1), L0_ffn_w_up, L0_ffn_w_down)
    x = x + _L1_attn_a_ref(_layernorm(x, axis=-1), L1_attn_a_wq, L1_attn_a_bq, L1_attn_a_wk, L1_attn_a_bk, L1_attn_a_wv, L1_attn_a_bv, L1_attn_a_wo, L1_attn_a_bo)
    x = x + _L1_ffn_ref(_layernorm(x, axis=-1), L1_ffn_router_w, L1_ffn_expert_fc, L1_ffn_expert_proj)
    x = x + _L1_attn_b_ref(_layernorm(x, axis=-1), L1_attn_b_Wq, L1_attn_b_bq, L1_attn_b_Wk, L1_attn_b_bk, L1_attn_b_Wv, L1_attn_b_bv, L1_attn_b_Wo, L1_attn_b_bo)
    x = x + _L1_ffn_ref(_layernorm(x, axis=-1), L1_ffn_router_w, L1_ffn_expert_fc, L1_ffn_expert_proj)
    x = x + _L2_attn_a_ref(_layernorm(x, axis=-1), L2_attn_a_attn_W, L2_attn_a_attn_b, L2_attn_a_out_W, L2_attn_a_out_b)
    x = x + _L2_ffn_ref(_layernorm(x, axis=-1), L2_ffn_W1, L2_ffn_b1, L2_ffn_W2, L2_ffn_b2)
    x = x + _L2_attn_b_ref(_layernorm(x, axis=-1), L2_attn_b_in_proj_w, L2_attn_b_conv_w, L2_attn_b_conv_b, L2_attn_b_dt_bias, L2_attn_b_A_log, L2_attn_b_ln_w, L2_attn_b_out_proj_w)
    x = x + _L2_ffn_ref(_layernorm(x, axis=-1), L2_ffn_W1, L2_ffn_b1, L2_ffn_W2, L2_ffn_b2)
    x = x + _L3_attn_a_ref(_layernorm(x, axis=-1), L3_attn_a_Win, L3_attn_a_b_in, L3_attn_a_Wg, L3_attn_a_bg, L3_attn_a_Wout, L3_attn_a_bout, L3_attn_a_convw, L3_attn_a_convb, L3_attn_a_A, L3_attn_a_Wb, L3_attn_a_bb, L3_attn_a_Wc, L3_attn_a_bc, L3_attn_a_Wdt, L3_attn_a_bdt)
    x = x + _L3_ffn_ref(_layernorm(x, axis=-1), L3_ffn_w1_w, L3_ffn_w1_s, L3_ffn_w2_w, L3_ffn_w2_s, L3_ffn_h1_w, L3_ffn_h1_s, L3_ffn_h2_w, L3_ffn_h2_s, L3_ffn_w3_w, L3_ffn_w3_s)
    x = x + _L3_attn_b_ref(_layernorm(x, axis=-1), L3_attn_b_Wq, L3_attn_b_Wk, L3_attn_b_Wv, L3_attn_b_Wp, L3_attn_b_bp)
    x = x + _L3_ffn_ref(_layernorm(x, axis=-1), L3_ffn_w1_w, L3_ffn_w1_s, L3_ffn_w2_w, L3_ffn_w2_s, L3_ffn_h1_w, L3_ffn_h1_s, L3_ffn_h2_w, L3_ffn_h2_s, L3_ffn_w3_w, L3_ffn_w3_s)
    return x

_drawn_inputs = setup_inputs


def setup_inputs(seed=0):
    import zlib

    import numpy as np

    out = dict(_drawn_inputs(seed))
    spreads = {'L0_attn_a_rms_w': (1.0, 0.2),
     'L1_attn_a_bq': (0.0, 0.1),
     'L1_attn_a_bk': (0.0, 0.1),
     'L1_attn_a_bv': (0.0, 0.1),
     'L1_attn_a_bo': (0.0, 0.1),
     'L1_attn_b_bq': (0.0, 0.1),
     'L1_attn_b_bk': (0.0, 0.1),
     'L1_attn_b_bv': (0.0, 0.1),
     'L1_attn_b_bo': (0.0, 0.1),
     'L2_attn_b_conv_b': (0.0, 0.1),
     'L2_attn_b_ln_w': (1.0, 0.2),
     'L3_attn_a_b_in': (0.0, 0.1),
     'L3_attn_a_bg': (0.0, 0.1),
     'L3_attn_a_bout': (0.0, 0.1),
     'L3_attn_a_convb': (0.0, 0.1),
     'L3_attn_a_bb': (0.0, 0.1),
     'L3_attn_a_bc': (0.0, 0.1),
     'L3_attn_a_bdt': (-2.0, 0.2),
     'L3_attn_b_bp': (0.0, 0.1)}
    factors = {}
    for name, (base, spread) in spreads.items():
        noise = np.random.default_rng([zlib.crc32(name.encode()), seed]).standard_normal(out[name].shape)
        drawn = base * np.exp(spread * noise) if base else spread * noise
        out[name] = jnp.asarray(drawn.astype(out[name].dtype))
    for name, factor in factors.items():
        out[name] = (out[name] * factor).astype(out[name].dtype)
    return out
```

```python
from contextlib import ExitStack, contextmanager

import numpy as np
import concourse.bass as bass
from concourse import mybir

ALU = mybir.AluOpType
ACT = mybir.ActivationFunctionType
AX = mybir.AxisListType
F32 = mybir.dt.float32
BF16 = mybir.dt.bfloat16
ds = bass.ds

LAYERS = list(range(16))
P = 128
B, S, D = 4, 1024, 128
T = B * S
NT = 512
TILES = T // NT
LN_EPS = 1e-5
RMS_EPS = 1e-6
NEG = -1e30


@contextmanager
def stage(nc, tag):
    with ExitStack() as ctx:
        sems = []

        def sb(name, shape, dt=F32):
            return ctx.enter_context(nc.sbuf_tensor(f"{tag}_{name}", shape, dt))

        def ps(name, shape):
            return ctx.enter_context(nc.psum_tensor(f"{tag}_ps_{name}", shape, F32))

        def sem(name):
            s = nc.alloc_semaphore(f"{tag}_{name}")
            sems.append(s)
            return s

        yield sb, ps, sem
        nc.clear_and_free_semaphores(sems)
        nc.all_engine_barrier()


class Net:

    def __init__(self, nc, ctx, dram):
        self.nc, self.dram = nc, dram
        sb = lambda n, s, d=F32: ctx.enter_context(nc.sbuf_tensor(n, s, d))
        self.x = sb("x_res", [P, T])
        self.xn = sb("x_norm", [P, T])
        self.ident = sb("ident", [P, P])
        self.center = sb("center", [P, P])
        self.ones = sb("ones_over_1", [P, P])
        self.mean = sb("ones_over_d", [P, P])
        self.identb = sb("ident_bf16", [P, P], BF16)
        self.cols = sb("const_cols", [P, 8])
        self.ln_eps = self.cols[:, 0:1]
        self.rms_eps = self.cols[:, 1:2]
        self.one = self.cols[:, 2:3]
        self.zero = self.cols[:, 3:4]
        self.tiny = self.cols[:, 4:5]


def load_consts(net):
    nc = net.nc
    with stage(nc, "init") as (sb, ps, sem):
        loaded, made = sem("loaded"), sem("made")
        with nc.Block() as block:
            @block.sync
            def _(sp):
                sp.dma_start(net.x[:, :], net.dram["x"]).then_inc(loaded, 16)
                sp.dma_start(net.ident[:, :], net.dram["ident"]).then_inc(loaded, 16)
                sp.wait_ge(loaded, 32)

            @block.vector
            def _(dve):
                for j, v in enumerate((LN_EPS, RMS_EPS, 1.0, 0.0, 1e-19)):
                    nc.vector.memset(net.cols[:, j:j + 1], v)
                nc.vector.memset(net.ones[:, :], 1.0)
                nc.vector.memset(net.mean[:, :], 1.0 / D)
                dve.wait_ge(loaded, 32)
                nc.vector.tensor_scalar(net.center[:, :], net.ident[:, :], -1.0 / D, None, ALU.add)
                nc.vector.tensor_copy(net.identb[:, :], net.ident[:, :])


def store_out(net, out):
    nc = net.nc
    with stage(nc, "fin") as (sb, ps, sem):
        stored = sem("stored")
        with nc.Block() as block:
            @block.sync
            def _(sp):
                sp.dma_start(out, net.x[:, :]).then_inc(stored, 16)
                sp.wait_ge(stored, 16)


def layer_norm(net, tag, rms=None):
    nc = net.nc
    x, xn = net.x, net.xn
    with stage(nc, tag) as (sb, ps, sem):
        cen = ps("centered", [P, 2, NT])
        var = ps("var", [P, 2, NT])
        sq = sb("squares", [P, 2, NT])
        lnv = sb("log_var", [P, 2, NT])
        rstd = sb("rstd", [P, 2, NT])
        ms = sb("mean_square", [P, 2, NT]) if rms else None
        lms = sb("log_ms", [P, 2, NT]) if rms else None
        cen_free = sem("centered_free")
        cen_ready, sq_ready, var_ready = sem("centered"), sem("squares"), sem("var")
        ln_ready, rstd_ready = sem("log_var"), sem("rstd")
        ms_ready, lms_ready, rt_ready, f_ready = sem("ms"), sem("lms"), sem("root"), sem("factor")
        with nc.Block() as block:
            @block.tensor
            def _(pe):
                with pe.Fori(0, TILES // 2) as i:
                    for p in range(2):
                        pe.wait_ge(cen_free, 2 * i + p + 1)
                        nc.tensor.matmul(cen[:, p, :], net.center[:, :], x[:, ds((2 * i + p) * NT, NT)],
                                         start=True, stop=True).then_inc(cen_ready, 1)
                    for p in range(2):
                        pe.wait_ge(sq_ready, 2 * i + p + 1)
                        nc.tensor.matmul(var[:, p, :], net.mean[:, :], sq[:, p, :],
                                         start=True, stop=True).then_inc(var_ready, 1)

            @block.scalar
            def _(act):
                nc.scalar.preload_act_table_set("natural_log_exp_and_others")
                with act.Fori(0, TILES // 2) as i:
                    for p in range(2):
                        act.wait_ge(cen_ready, 2 * i + p + 1)
                        nc.scalar.activation(sq[:, p, :], cen[:, p, :], ACT.Square).then_inc(sq_ready, 1)
                    for p in range(2):
                        act.wait_ge(var_ready, 2 * i + p + 1)
                        nc.scalar.activation(lnv[:, p, :], var[:, p, :], ACT.Ln,
                                             bias=net.ln_eps).then_inc(ln_ready, 1)
                        act.wait_ge(ln_ready, 2 * i + p + 1)
                        nc.scalar.activation(rstd[:, p, :], lnv[:, p, :], ACT.Exp,
                                             scale=-0.5).then_inc(rstd_ready, 1)
                        if rms:
                            act.wait_ge(ms_ready, 2 * i + p + 1)
                            nc.scalar.activation(lms[:, p, :], ms[:, p, :], ACT.Ln).then_inc(lms_ready, 1)
                            act.wait_ge(lms_ready, 2 * i + p + 1)
                            nc.scalar.activation(rms[2][:, ds((2 * i + p) * NT, NT)], lms[:, p, :], ACT.Exp,
                                                 scale=0.5 if rms[0] == "div" else -0.5).then_inc(rt_ready, 1)

            @block.vector
            def _(dve):
                dve.sem_inc(cen_free, 2)
                with dve.Fori(0, TILES // 2) as i:
                    for p in range(2):
                        tok = ds((2 * i + p) * NT, NT)
                        dve.wait_ge(rstd_ready, 2 * i + p + 1)
                        last = nc.vector.tensor_tensor(xn[:, tok], cen[:, p, :], rstd[:, p, :], ALU.mult)
                        if rms:
                            last.then_inc(f_ready, 1)
                            nc.vector.tensor_tensor(ms[:, p, :], var[:, p, :], rstd[:, p, :],
                                                    ALU.mult).then_inc(f_ready, 1)
                            dve.wait_ge(f_ready, 4 * i + 2 * p + 2)
                            nc.vector.tensor_tensor(ms[:, p, :], ms[:, p, :], rstd[:, p, :],
                                                    ALU.mult).then_inc(cen_free, 1)
                            dve.wait_ge(cen_free, 2 * i + p + 3)
                            nc.vector.tensor_scalar(ms[:, p, :], ms[:, p, :],
                                                    1e-19 if rms[0] == "div" else rms[1], None,
                                                    ALU.max if rms[0] == "div" else ALU.add
                                                    ).then_inc(ms_ready, 1)
                        else:
                            last.then_inc(cen_free, 1)
                if rms and rms[0] == "div":
                    dve.wait_ge(rt_ready, TILES)
                    f = rms[2]
                    nc.vector.tensor_scalar(f[:, :], f[:, :], rms[1], None, ALU.add).then_inc(ms_ready, 1)
                    dve.wait_ge(ms_ready, TILES + 1)
                    nc.vector.reciprocal(f[:, :], f[:, :])


def ternary_ffn(net, tag, wup, wdn, rms_in, floor, b1=None, b2=None):
    nc, x, xn = net.nc, net.x, net.xn
    FC = 4
    NW = P * FC * P
    with stage(nc, tag) as (sb, ps, sem):
        if rms_in:
            fac = sb("rms_factor", [P, T])
            layer_norm(net, tag + "_ln", ("div", 1e-8, fac))
        else:
            layer_norm(net, tag + "_ln")
        w = [sb("w_up", [P, FC * P]), sb("w_down", [P, FC * P])]
        wt = [sb("q_up", [P, FC * P]), sb("q_down", [P, FC * P])]
        neg = sb("below", [P, FC * P])
        absum = sb("abs_sum", [P, 2])
        thr = sb("threshold", [P, 4])
        bias = sb("biases", [P, 8])
        g = sb("hidden", [P, 2, FC, NT])
        gsq = sb("hidden_sq", [P, FC, NT])
        ssum = sb("sum_sq", [P, NT])
        y = sb("down", [P, T])
        msq = sb("mean_sq", [P, T]) if rms_in else None
        pw = ps("weight_sum", [P, NT])
        ph = ps("up", [P, 2, 2, NT])
        py = ps("down_acc", [P, 2, NT])
        pm = ps("ms_acc", [P, NT])
        w_in, abs_ready, wsum_ready, w_ready, chain = (sem(n) for n in (
            "weights_in", "abs_ready", "wsum_ready", "w_ready", "chain"))
        x_ready, up_ready, gelu_done, g_free = (sem(n) for n in (
            "x_ready", "up_ready", "gelu_done", "g_free"))
        ss_ready, dn_ready, dn_free, tail_a = (sem(n) for n in ("ss_ready", "dn_ready", "dn_free", "tail_act"))
        with nc.Block() as block:
            @block.sync
            def _(sp):
                sp.dma_start(w[0][:, :], net.dram[wup]).then_inc(w_in, 16)
                sp.dma_start(w[1][:, :].rearrange("p (k d) -> p k d", k=FC),
                             net.dram[wdn].rearrange("(k p) d -> p k d", p=P)).then_inc(w_in, 16)
                if b1:
                    sp.dma_start(bias[:, 0:4], net.dram[b1]).then_inc(w_in, 16)
                    sp.dma_start(bias[:, 4:5], net.dram[b2]).then_inc(w_in, 16)

            def down(pe, i, p):
                pe.wait_ge(gelu_done, 4 * i + 2 * p + 4)
                pe.wait_ge(dn_free, 2 * i + p + 1)
                for k in range(FC):
                    mm = nc.tensor.matmul(py[:, p, :], wt[1][:, k * P:(k + 1) * P], g[:, p, k, :],
                                          start=(k == 0), stop=(k == FC - 1))
                mm.then_inc(dn_ready, 1)
                if rms_in:
                    pe.wait_ge(ss_ready, 2 * i + p + 1)
                    nc.tensor.matmul(pm[:, :], net.ones[:, :], ssum[:, :], start=True, stop=True).then_inc(dn_ready, 1)

            @block.tensor
            def _(pe):
                pe.wait_ge(abs_ready, 1)
                nc.tensor.matmul(pw[:, 0:2], net.ones[:, :], absum[:, :], start=True, stop=True).then_inc(wsum_ready, 1)
                pe.wait_ge(w_ready, 1)
                with pe.Fori(0, TILES // 2) as i:
                    for p in range(2):
                        if rms_in:
                            pe.wait_ge(x_ready, 2 * i + p + 1)
                        for half in range(2):
                            pe.wait_ge(gelu_done, 4 * i + 2 * p + half + 1)
                            for c in range(2):
                                k = 2 * half + c
                                mm = nc.tensor.matmul(ph[:, half, c, :], wt[0][:, k * P:(k + 1) * P],
                                                      xn[:, ds((2 * i + p) * NT, NT)], start=True, stop=True)
                            mm.then_inc(up_ready, 1)
                        if p == 1:
                            down(pe, i, 0)
                    down(pe, i, 1)

            @block.scalar
            def _(act):
                act.sem_inc(gelu_done, 2)
                with act.Fori(0, TILES // 2) as i:
                    for p in range(2):
                        act.wait_ge(g_free, 2 * i + p + 1)
                        for half in range(2):
                            act.wait_ge(up_ready, 4 * i + 2 * p + half + 1)
                            if b1:
                                for c in range(2):
                                    k = 2 * half + c
                                    a = nc.scalar.activation(g[:, p, k, :], ph[:, half, c, :],
                                                             ACT.Gelu, bias=bias[:, k:k + 1])
                            else:
                                a = nc.scalar.activation(g[:, p, 2 * half:2 * half + 2, :], ph[:, half, :, :], ACT.Gelu)
                            a.then_inc(gelu_done, 1)
                if rms_in:
                    act.wait_ge(tail_a, 1)
                    nc.scalar.activation(msq[:, :], msq[:, :], ACT.Ln).then_inc(tail_a, 1)
                    act.wait_ge(tail_a, 2)
                    nc.scalar.activation(msq[:, :], msq[:, :], ACT.Exp, scale=0.5).then_inc(tail_a, 1)

            @block.vector
            def _(dve):
                dve.wait_ge(w_in, 64 if b1 else 32)
                for m in range(2):
                    last = nc.vector.tensor_reduce(absum[:, m:m + 1], w[m][:, :], AX.X, ALU.add,
                                                   apply_absolute_value=True)
                last.then_inc(abs_ready, 1)
                dve.wait_ge(wsum_ready, 1)
                nc.vector.tensor_scalar(thr[:, 0:2], pw[:, 0:2], 1.0 / NW, floor, ALU.mult, ALU.max).then_inc(chain, 1)
                dve.wait_ge(chain, 1)
                nc.vector.tensor_scalar(thr[:, 2:4], thr[:, 0:2], -0.5, None, ALU.mult).then_inc(chain, 1)
                dve.wait_ge(chain, 2)
                nc.vector.tensor_scalar(thr[:, 0:2], thr[:, 0:2], 0.5, None, ALU.mult).then_inc(chain, 1)
                dve.wait_ge(chain, 3)
                n = 3
                for m in range(2):
                    nc.vector.tensor_scalar(neg[:, :], w[m][:, :], thr[:, 2 + m:3 + m], None, ALU.is_lt).then_inc(chain, 1)
                    n += 1
                    dve.wait_ge(chain, n)
                    nc.vector.scalar_tensor_tensor(wt[m][:, :], w[m][:, :], thr[:, m:m + 1], neg[:, :],
                                                   ALU.is_gt, ALU.subtract).then_inc(chain, 1)
                    n += 1
                    dve.wait_ge(chain, n)
                    nc.vector.tensor_tensor(wt[m][:, :], wt[m][:, :], w[m][:, :], ALU.subtract).then_inc(chain, 1)
                    n += 1
                    dve.wait_ge(chain, n)
                    nc.vector.tensor_tensor(wt[m][:, :], w[m][:, :], wt[m][:, :], ALU.add).then_inc(chain, 1)
                    n += 1
                    dve.wait_ge(chain, n)
                dve.sem_inc(w_ready, 1)
                dve.sem_inc(g_free, 2)
                dve.sem_inc(dn_free, 2)
                if rms_in:
                    with dve.Fori(0, TILES) as i:
                        tok = ds(i * NT, NT)
                        nc.vector.tensor_tensor(xn[:, tok], xn[:, tok], fac[:, tok], ALU.mult).then_inc(x_ready, 1)
                with dve.Fori(0, TILES // 2) as i:
                    for p in range(2):
                        tok = ds((2 * i + p) * NT, NT)
                        if rms_in:
                            dve.wait_ge(gelu_done, 4 * i + 2 * p + 4)
                            c0 = n + (2 * i + p) * 3
                            nc.vector.tensor_tensor(gsq[:, :, :], g[:, p, :, :], g[:, p, :, :], ALU.mult).then_inc(chain, 1)
                            dve.wait_ge(chain, c0 + 1)
                            nc.vector.tensor_tensor(gsq[:, 0:2, :], gsq[:, 0:2, :], gsq[:, 2:4, :], ALU.add).then_inc(chain, 1)
                            dve.wait_ge(chain, c0 + 2)
                            nc.vector.tensor_tensor(ssum[:, :], gsq[:, 0, :], gsq[:, 1, :], ALU.add).then_inc(chain, 1)
                            dve.wait_ge(chain, c0 + 3)
                            dve.sem_inc(ss_ready, 1)
                            dve.wait_ge(dn_ready, 2 * (2 * i + p) + 2)
                            nc.vector.tensor_copy(y[:, tok], py[:, p, :]).then_inc(x_ready, 1)
                            nc.vector.tensor_scalar(msq[:, tok], pm[:, :], 1.0 / (FC * P), 1e-19,
                                                    ALU.mult, ALU.max).then_inc(x_ready, 1)
                            dve.wait_ge(x_ready, TILES + (2 * i + p) * 2 + 2)
                        else:
                            dve.wait_ge(dn_ready, 2 * i + p + 1)
                            nc.vector.scalar_tensor_tensor(x[:, tok], py[:, p, :], bias[:, 4:5], x[:, tok],
                                                           ALU.add, ALU.add).then_inc(x_ready, 1)
                            dve.wait_ge(x_ready, 2 * i + p + 1)
                        dve.sem_inc(g_free, 1)
                        dve.sem_inc(dn_free, 1)
                if rms_in:
                    dve.sem_inc(tail_a, 1)
                    dve.wait_ge(tail_a, 3)
                    nc.vector.tensor_scalar(msq[:, :], msq[:, :], 1e-8, None, ALU.add).then_inc(tail_a, 1)
                    dve.wait_ge(tail_a, 4)
                    nc.vector.reciprocal(msq[:, :], msq[:, :]).then_inc(tail_a, 1)
                    dve.wait_ge(tail_a, 5)
                    nc.vector.tensor_tensor(y[:, :], y[:, :], msq[:, :], ALU.mult).then_inc(tail_a, 1)
                    dve.wait_ge(tail_a, 6)
                    nc.vector.tensor_tensor(x[:, :], x[:, :], y[:, :], ALU.add)


HEADS = 16
GROUPS = B * HEADS // 4
KT = S // P
DECAY_SPAN = 384


def attention(net, tag, w, dq, scale, rope=False, alibi=False, decay=False, bias=False, out_bias=False):
    nc, x, xn, dram = net.nc, net.x, net.xn, net.dram
    R = HEADS * dq
    GR = 4 * dq
    r0 = 6 * dq + (9 if alibi else 0)
    layer_norm(net, tag + "_ln")
    parts = {n: nc.dram_tensor(f"{tag}_{n}_parts", (3, B * R, S), BF16, kind="Internal").ap() for n in "qk"}
    heads_out = nc.dram_tensor(f"{tag}_heads_out", (B * P, S), F32, kind="Internal").ap()
    sums = nc.dram_tensor(f"{tag}_sums", (4 * GROUPS, S), F32, kind="Internal").ap()
    rsums = nc.dram_tensor(f"{tag}_rsums", (4 * GROUPS, S), F32, kind="Internal").ap()
    with ExitStack() as ctx:
        v = ctx.enter_context(nc.sbuf_tensor(f"{tag}_v", [P, GROUPS, KT, 4, 9], F32))
        attn_project(net, tag, w, dq, rope, bias, decay, parts, v)
        attn_core(net, tag, w, dq, r0, scale, alibi, decay, parts, v, heads_out, sums)
    attn_output(net, tag, w, out_bias, heads_out, sums, rsums)


def attn_project(net, tag, w, dq, rope, bias, decay, parts, v):
    nc, xn, dram = net.nc, net.xn, net.dram
    R = HEADS * dq
    with stage(nc, tag + "_proj") as (sb, ps, sem):
        ws = [sb(f"w{n}", [P, P]) for n in range(4 if rope else 2)]
        wv = sb("wv", [P, P])
        bcol = sb("bias_cols", [P, 4])
        bv = sb("bias_v", [P, P])
        tab = sb("cos_sin", [P, 2, S]) if rope else None
        t1, t2 = sb("t1", [P, 2, NT]), sb("t2", [P, 2, NT])
        part = sb("parts", [P, 2, 3, T], BF16)
        pq = ps("qk", [P, 4, NT])
        pv = ps("v", [P, 2, NT])
        w_in, mm_ready, mm_free, v_ready, v_free = (sem(n) for n in ("w_in", "mm", "mm_free", "v_mm", "v_free"))
        val, hi, rest, mid, low, made, stored, t_free = (sem(n) for n in (
            "value", "hi", "rest", "mid", "low", "made", "stored", "t_free"))
        n_in = [0]
        NW = len(ws)
        with nc.Block() as block:
            @block.sync
            def _(sp):
                for j, n in enumerate(("wq", "wk", "wq_sw", "wk_sw")[:NW]):
                    sp.dma_start(ws[j][:, :], dram[w[n]]).then_inc(w_in, 16)
                    n_in[0] += 16
                    if bias:
                        sp.dma_start(bcol[0:R, j:j + 1], dram[w["b" + n[1:]]]).then_inc(w_in, 16)
                        n_in[0] += 16
                sp.dma_start(wv[:, :], dram[w["wv"]]).then_inc(w_in, 16)
                n_in[0] += 16
                if bias:
                    sp.dma_start(bv[:, :], dram[w["bv"]].to_broadcast((P, P))).then_inc(w_in, 16)
                    n_in[0] += 16
                if rope:
                    sp.dma_start(tab[:, :, :], dram["rope"]).then_inc(w_in, 16)
                    n_in[0] += 16
                for b in range(B):
                    sp.wait_ge(hi, 4 * (b + 1))
                    sp.wait_ge(mid, 4 * (b + 1))
                    sp.wait_ge(low, 4 * (b + 1))
                    for j, n in enumerate("qk"):
                        sp.dma_start(parts[n].rearrange("s (b r) t -> b r s t", b=B)[b],
                                     part[0:R, j, :, b * S:(b + 1) * S]).then_inc(stored, 16)
                sp.wait_ge(stored, 32 * B)

            @block.tensor
            def _(pe):
                pe.wait_ge(w_in, n_in[0])
                with pe.Fori(0, TILES) as i:
                    for j in range(2):
                        pe.wait_ge(mm_free, 2 * i + j + 1)
                        for m in range(j, NW, 2):
                            mm = nc.tensor.matmul(pq[:, m, :], ws[m][:, :], xn[:, ds(i * NT, NT)],
                                                  start=True, stop=True)
                        mm.then_inc(mm_ready, 1)
                for m in range(T // P):
                    if m % 4 == 0 and m >= 8:
                        pe.wait_ge(v_free, m // 4 - 1)
                    mm = nc.tensor.matmul(pv[:, m // 4 % 2, m % 4 * P:(m % 4 + 1) * P],
                                          xn[:, m * P:(m + 1) * P], wv[:, :], start=True, stop=True)
                    if m % 4 == 3:
                        mm.then_inc(v_ready, 1)

            @block.vector
            def _(dve):
                nc.vector.memset(v[:, :, :, :, 8:9], 0.0 if decay else 1.0)
                dve.wait_ge(w_in, n_in[0])
                dve.sem_inc(mm_free, 2)
                with dve.Fori(0, B) as b:
                    for h in range(2):
                        for j in range(2):
                            n = 4 * b + 2 * h + j
                            dve.wait_ge(mm_ready, n + 1)
                            dve.wait_ge(t_free, n + 1)
                            if rope:
                                nc.vector.scalar_tensor_tensor(t1[0:R, j, :], pq[0:R, j, :], bcol[0:R, j:j + 1],
                                                               tab[0:R, 0, h * NT:(h + 1) * NT], ALU.add, ALU.mult)
                                nc.vector.scalar_tensor_tensor(t2[0:R, j, :], pq[0:R, 2 + j, :], bcol[0:R, 2 + j:3 + j],
                                                               tab[0:R, 1, h * NT:(h + 1) * NT], ALU.add, ALU.mult
                                                               ).then_inc(made, 1)
                                dve.wait_ge(made, n + 1)
                                nc.vector.tensor_tensor(t1[0:R, j, :], t1[0:R, j, :], t2[0:R, j, :],
                                                        ALU.add).then_inc(val, 1)
                            elif bias:
                                nc.vector.tensor_scalar(t1[0:R, j, :], pq[0:R, j, :], bcol[0:R, j:j + 1], None,
                                                        ALU.add).then_inc(val, 1)
                            else:
                                nc.vector.tensor_copy(t1[0:R, j, :], pq[0:R, j, :]).then_inc(val, 1)
                            dve.wait_ge(val, n + 1)
                            dve.sem_inc(mm_free, 1)
                for m in range(T // P // 4):
                    dve.wait_ge(v_ready, m + 1)
                    for c in range(4):
                        tile = 4 * m + c
                        dst = v[:, 4 * (tile // KT):4 * (tile // KT) + 4, tile % KT, :, 0:8]
                        src = pv[:, m % 2, c * P:(c + 1) * P].rearrange("p (g h e) -> p g h e", g=4, e=8)
                        if bias:
                            a = nc.vector.tensor_tensor(dst, src, bv[:, :].rearrange("p (g h e) -> p g h e", g=4, e=8),
                                                        ALU.add)
                        else:
                            a = nc.vector.tensor_copy(dst, src)
                    a.then_inc(v_free, 1)

            @block.scalar
            def _(act):
                with act.Fori(0, TILES) as i:
                    for j in range(2):
                        n = 2 * i + j
                        tok = ds(i * NT, NT)
                        act.wait_ge(val, n + 1)
                        nc.scalar.activation(part[0:R, j, 0, tok], t1[0:R, j, :], ACT.Copy).then_inc(hi, 1)
                        act.wait_ge(rest, n + 1)
                        nc.scalar.activation(part[0:R, j, 1, tok], t1[0:R, j, :], ACT.Copy).then_inc(mid, 1)

            @block.gpsimd
            def _(pool):
                pool.sem_inc(t_free, 2)
                with pool.Fori(0, TILES) as i:
                    for j in range(2):
                        n = 2 * i + j
                        tok = ds(i * NT, NT)
                        pool.wait_ge(hi, n + 1)
                        nc.gpsimd.tensor_tensor(t1[0:R, j, :], t1[0:R, j, :], part[0:R, j, 0, tok],
                                                ALU.subtract).then_inc(rest, 1)
                        pool.wait_ge(mid, n + 1)
                        nc.gpsimd.tensor_tensor(part[0:R, j, 2, tok], t1[0:R, j, :], part[0:R, j, 1, tok],
                                                ALU.subtract).then_inc(low, 1)
                        pool.wait_ge(low, n + 1)
                        pool.sem_inc(t_free, 1)


def attn_core(net, tag, w, dq, r0, scale, alibi, decay, parts, v, heads_out, sums):
    nc, dram = net.nc, net.dram
    GR = 4 * dq
    first = [(qt, 0, min(qt + 1, 4) * P) for qt in range(KT)]
    P1 = 4 * 12
    with stage(nc, tag + "_core") as (sb, ps, sem):
        qs = [sb(f"q_rows{u}", [64, 4, S], BF16) for u in range(2)]
        ks = [sb(f"k_rows{u}", [64, 4, S], BF16) for u in range(2)]
        vs = [sb(f"v_group{u}", [P, KT, 4, 9]) for u in range(2)]
        pt = sb("probs", [P, 2, 4, S])
        pw = sb("probs_decayed", [P, 2, 4, DECAY_SPAN]) if decay else None
        dtab = sb("decay", [P, DECAY_SPAN]) if decay else None
        ones9 = sb("ones9", [P, 9]) if decay else None
        maskq = sb("mask_q_rows", [P, P], BF16)
        maskk = sb("mask_k_rows", [P, P], BF16)
        mx = sb("chunk_max", [P, 2, 4, 12])
        nm = sb("neg_max", [P, 2, 4, 8])
        mrest = sb("max_rest", [32, 2, P])
        mpart = sb("max_parts", [32, 2, 3, P], BF16)
        oev = sb("out_sums", [P, 2, S])
        pa = [ps(f"scores_a{n}", [P, NT]) for n in range(2)]
        pb = [ps(f"scores_b{n}", [P, S]) for n in range(2)]
        acc = ps("acc", [P, S])
        c_in, stack_in = sem("consts_in"), [sem("stack_in0"), sem("stack_in1")]
        a_ready, a_free = sem("scores_a"), sem("scores_a_free")
        b_ready, b_free = sem("scores_b"), sem("exp_done")
        m_chain, nm_ready, mp_ready, m_in = (sem(n) for n in ("max_chain", "neg_max", "max_parts", "max_rows_in"))
        vs_ready, acc_free, pv_done = (sem(n) for n in ("v_group", "acc_free", "pv_done"))
        o_stored, dec_ready, z_ready = [sem("out_stored0"), sem("out_stored1")], sem("decayed"), sem("acc_zeroed")

        def load_stack(sp, n, u):
            at = 0
            for cnt, qp in ((3, 0), (2, 1), (1, 2)):
                for c in range(cnt):
                    src = parts["q"][qp, ds(n * GR, GR), :].rearrange("(j d) t -> d j t", j=4)
                    sp.dma_start(qs[u][at + c * dq:at + (c + 1) * dq, :, :], src).then_inc(stack_in[u], 16)
                    src = parts["k"][c, ds(n * GR, GR), :].rearrange("(j d) t -> d j t", j=4)
                    sp.dma_start(ks[u][at + c * dq:at + (c + 1) * dq, :, :], src).then_inc(stack_in[u], 16)
                at += cnt * dq
            if alibi:
                sp.dma_start(qs[u][6 * dq:r0, :, :], dram["alibi_q"][ds(n * 9, 9)]).then_inc(stack_in[u], 16)

        NST = 16 * (12 + (1 if alibi else 0))
        CIN = 16 * (4 + (2 if alibi else 0) + (2 if decay else 0))
        PV0 = KT + 1

        with nc.Block() as block:
            order = [(qt, j, c) for qt in range(KT) for j in range(4) for c in range(1 if qt < 4 else 2)]
            P1_AT = {key: k for k, key in enumerate(order)}

            @block.sync
            def _(sp):
                sp.dma_start(maskq[:, :], dram["mask_q"]).then_inc(c_in, 16)
                sp.dma_start(maskk[:, :], dram["mask_k"]).then_inc(c_in, 16)
                if decay:
                    sp.dma_start(dtab[:, :], dram["decay"]).then_inc(c_in, 16)
                    sp.dma_start(ones9[:, :], dram["ones9"]).then_inc(c_in, 16)
                for u in range(2):
                    sp.dma_start(ks[u][r0:r0 + 3, :, :], dram["ones_rows"]).then_inc(c_in, 16)
                    if alibi:
                        sp.dma_start(ks[u][6 * dq:r0, :, :], dram["alibi_k"]).then_inc(c_in, 16)
                for u in range(2):
                    load_stack(sp, u, u)

                def max_rows(n, u):
                    sp.wait_ge(mp_ready, n + 1)
                    for s in range(3):
                        sp.dma_start(qs[u][r0 + s:r0 + s + 1, :, :].rearrange("o j (k q) -> o (j k) q", q=P),
                                     mpart[:, u, s, :]).then_inc(m_in, 16)

                def output(n, u):
                    sp.wait_ge(acc_free, n + 2)
                    for j in range(4):
                        sp.dma_start(heads_out[ds(n * 32 + 8 * j, 8), :],
                                     oev[32 * j:32 * j + 8, u, :]).then_inc(o_stored[u], 16)
                        sp.dma_start(sums[ds(n * 4 + j, 1), :],
                                     oev[32 * j + 8:32 * j + 9, u, :]).then_inc(o_stored[u], 16)

                def one(n, u, load=True, nxt=True):
                    if nxt:
                        max_rows(n + 1, 1 - u)
                    sp.wait_ge(pv_done, KT * (n + 1) + PV0)
                    if load:
                        load_stack(sp, n + 2, u)
                    output(n, u)

                max_rows(0, 0)
                with sp.Fori(0, GROUPS // 2 - 1) as i:
                    one(2 * i, 0)
                    one(2 * i + 1, 1)
                one(GROUPS - 2, 0, load=False)
                one(GROUPS - 1, 1, load=False, nxt=False)
                for u in range(2):
                    sp.wait_ge(o_stored[u], 8 * 16 * GROUPS // 2 + 16)

            def p1_chunks(pe, n, u, pair, qt):
                if qt == 0:
                    pe.wait_ge(stack_in[u], NST * (pair + 1))
                for j in range(4):
                    for c in range(1 if qt < 4 else 2):
                        k = P1_AT[(qt, j, c)]
                        a0, a1 = c * NT, min((c + 1) * NT, (qt + 1) * P)
                        slot = (k + u) % 2
                        pe.wait_ge(a_free, n * (P1 + 1) + k + 1)
                        diag = a1 == (qt + 1) * P
                        mm = nc.tensor.matmul(pa[slot][:, 0:a1 - a0], qs[u][0:r0, j, qt * P:(qt + 1) * P],
                                              ks[u][0:r0, j, a0:a1], start=True, stop=not diag)
                        if diag:
                            mm = nc.tensor.matmul(pa[slot][:, a1 - a0 - P:a1 - a0], net.identb[:, :], maskq[:, :],
                                                  start=False, stop=True)
                        mm.then_inc(a_ready, 1)

            def p1_turn(pe, n, u):
                pe.wait_ge(nm_ready, n + 1)
                pe.wait_ge(a_free, n * (P1 + 1) + P1 + 1)
                nc.tensor.transpose(pa[(P1 + u) % 2][0:32, 0:P], nm[:, u, :, :].rearrange("p j k -> p (j k)"),
                                    net.ident[:, :]).then_inc(a_ready, 1)

            def p2_scores(pe, n, u, kt):
                if kt == 0:
                    pe.wait_ge(m_in, 48 * (n + 1))
                for j in range(4):
                    pe.wait_ge(b_free, 32 * n + 4 * kt + j + 1)
                    for c in range(2):
                        a0, a1 = max(c * NT, kt * P), (c + 1) * NT
                        if a0 >= a1:
                            continue
                        diag = a0 == kt * P
                        mm = nc.tensor.matmul(pb[j % 2][:, a0:a1], ks[u][0:r0 + 3, j, kt * P:(kt + 1) * P],
                                              qs[u][0:r0 + 3, j, a0:a1], start=True, stop=not diag)
                        if diag:
                            mm = nc.tensor.matmul(pb[j % 2][:, a0:a0 + P], net.identb[:, :], maskk[:, :],
                                                  start=False, stop=True)
                    mm.then_inc(b_ready, 1)

            def p2_values(pe, n, u, kt):
                pe.wait_ge(b_free, 32 * n + 4 * kt + 4 + 2)
                if decay:
                    pe.wait_ge(dec_ready, KT * n + kt + 1)
                if kt == 0:
                    pe.wait_ge(vs_ready, n + 1)
                    pe.wait_ge(acc_free, n + 1)
                for c in range(2):
                    a0, a1 = max(c * NT, kt * P), (c + 1) * NT
                    if a0 >= a1:
                        continue
                    last_kt = kt == 4 * c + 3
                    for j in range(4):
                        o = acc[32 * j:32 * j + 9, :]
                        mm = nc.tensor.matmul(o[:, a0:a1], ones9[:, :] if decay else vs[u][:, kt, j, :],
                                              pt[:, kt % 2, j, a0:a1], start=(kt == 0), stop=last_kt and not decay,
                                              tile_position=(0, 32 * j))
                    if decay:
                        d1 = min(a1, kt * P + DECAY_SPAN)
                        if a0 < d1:
                            for j in range(4):
                                mm = nc.tensor.matmul(acc[32 * j:32 * j + 9, a0:d1], vs[u][:, kt, j, :],
                                                      pw[:, kt % 2, j, a0 - kt * P:d1 - kt * P], start=False,
                                                      stop=last_kt, tile_position=(0, 32 * j))
                mm.then_inc(pv_done, 1)

            @block.tensor
            def _(pe):
                pe.wait_ge(c_in, CIN)
                pe.wait_ge(z_ready, 1)
                for qt in range(KT):
                    p1_chunks(pe, 0, 0, 0, qt)
                p1_turn(pe, 0, 0)

                def one(n, u, pair, nxt=True):
                    for kt in range(KT):
                        if nxt:
                            p1_chunks(pe, n + 1, 1 - u, pair + u, kt)
                        p2_scores(pe, n, u, kt)
                        if kt:
                            p2_values(pe, n, u, kt - 1)
                    if nxt:
                        p1_turn(pe, n + 1, 1 - u)
                    p2_values(pe, n, u, KT - 1)

                with pe.Fori(0, GROUPS // 2 - 1) as i:
                    one(2 * i, 0, i)
                    one(2 * i + 1, 1, i)
                one(GROUPS - 2, 0, GROUPS // 2 - 1)
                one(GROUPS - 1, 1, GROUPS // 2 - 1, nxt=False)

            @block.scalar
            def _(act):
                nc.scalar.preload_act_table_set("natural_log_exp_and_others")
                act.sem_inc(b_free, 2)

                def one(n, u):
                    for kt in range(KT):
                        for j in range(4):
                            act.wait_ge(b_ready, 32 * n + 4 * kt + j + 1)
                            if j == 0:
                                act.wait_ge(pv_done, KT * n + kt - 1 + PV0)
                            nc.scalar.activation(pt[:, kt % 2, j, kt * P:S], pb[j % 2][:, kt * P:S], ACT.Exp,
                                                 scale=scale).then_inc(b_free, 1)

                with act.Fori(0, GROUPS // 2) as i:
                    one(2 * i, 0)
                    one(2 * i + 1, 1)

            @block.gpsimd
            def _(pool):
                if decay:
                    pool.wait_ge(c_in, CIN)

                def one(n, u):
                    pool.wait_ge(pv_done, KT * n - KT + PV0)
                    nc.gpsimd.tensor_copy(vs[u][:, :, :, :], v[:, ds(n, 1), :, :, :].rearrange(
                        "p o k j e -> p (o k) j e")).then_inc(vs_ready, 1)
                    if decay:
                        for kt in range(KT):
                            wd = min(DECAY_SPAN, S - kt * P)
                            pool.wait_ge(b_free, 32 * n + 4 * kt + 6)
                            nc.gpsimd.tensor_tensor(
                                pw[:, kt % 2, :, 0:wd], pt[:, kt % 2, :, kt * P:kt * P + wd],
                                dtab[:, 0:wd].unsqueeze(1).to_broadcast((P, 4, wd)), ALU.mult
                            ).then_inc(dec_ready, 1)

                with pool.Fori(0, GROUPS // 2) as i:
                    one(2 * i, 0)
                    one(2 * i + 1, 1)

            @block.vector
            def _(dve):
                nc.vector.memset(acc[:, :], 0.0).then_inc(z_ready, 1)
                dve.sem_inc(a_free, 2)
                dve.sem_inc(pv_done, PV0)
                dve.sem_inc(acc_free, 1)
                for u in range(2):
                    dve.sem_inc(o_stored[u], 16)

                def p1_max(n, u):
                    for k, (qt, j, c) in enumerate(order):
                        a0, a1 = c * NT, min((c + 1) * NT, (qt + 1) * P)
                        dve.wait_ge(a_ready, n * (P1 + 1) + k + 1)
                        nc.vector.tensor_reduce(mx[:, u, j, qt + 4 * c:qt + 4 * c + 1], pa[(k + u) % 2][:, 0:a1 - a0],
                                                AX.X, ALU.max).then_inc(a_free, 1)

                def p1_rows(n, u):
                    dve.wait_ge(a_free, n * (P1 + 1) + P1 + 2)
                    nc.vector.tensor_scalar(nm[:, u, :, 0:4], mx[:, u, :, 0:4], -1.0, None, ALU.mult)
                    nc.vector.tensor_tensor(nm[:, u, :, 4:8], mx[:, u, :, 4:8], mx[:, u, :, 8:12],
                                            ALU.max).then_inc(m_chain, 1)
                    dve.wait_ge(m_chain, 4 * n + 1)
                    nc.vector.tensor_scalar(nm[:, u, :, 4:8], nm[:, u, :, 4:8], -1.0, None, ALU.mult).then_inc(nm_ready, 1)
                    t = pa[(P1 + u) % 2]
                    dve.wait_ge(a_ready, n * (P1 + 1) + P1 + 1)
                    nc.vector.tensor_copy(mpart[:, u, 0, :], t[0:32, 0:P]).then_inc(m_chain, 1)
                    dve.wait_ge(m_chain, 4 * n + 2)
                    nc.vector.tensor_tensor(mrest[:, u, :], t[0:32, 0:P], mpart[:, u, 0, :], ALU.subtract).then_inc(m_chain, 1)
                    dve.wait_ge(m_chain, 4 * n + 3)
                    nc.vector.tensor_copy(mpart[:, u, 1, :], mrest[:, u, :]).then_inc(m_chain, 1)
                    dve.wait_ge(m_chain, 4 * n + 4)
                    nc.vector.tensor_tensor(mpart[:, u, 2, :], mrest[:, u, :], mpart[:, u, 1, :],
                                            ALU.subtract).then_inc(mp_ready, 1)
                    dve.sem_inc(a_free, 1)

                def evac(n, u):
                    dve.wait_ge(pv_done, KT * (n + 1) + PV0)
                    nc.vector.tensor_copy(oev[:, u, :], acc[:, :]).then_inc(acc_free, 1)

                def one(n, u, pair, nxt=True):
                    if nxt:
                        p1_max(n + 1, 1 - u)
                        p1_rows(n + 1, 1 - u)
                    dve.wait_ge(o_stored[u], 8 * 16 * pair + 16)
                    evac(n, u)

                p1_max(0, 0)
                p1_rows(0, 0)
                with dve.Fori(0, GROUPS // 2 - 1) as i:
                    one(2 * i, 0, i)
                    one(2 * i + 1, 1, i)
                one(GROUPS - 2, 0, GROUPS // 2 - 1)
                one(GROUPS - 1, 1, GROUPS // 2 - 1, nxt=False)


def attn_output(net, tag, w, out_bias, heads_out, sums, rsums):
    nc, x, dram = net.nc, net.x, net.dram
    with stage(nc, tag + "_out") as (sb, ps, sem):
        wo = sb("wo", [P, P])
        bo = sb("bo", [P, 1])
        o = sb("heads", [P, T])
        r = sb("inverse", [P, T])
        s = sb("sums", [P, 4 * GROUPS * S // P])
        py = ps("proj", [P, 2, NT])
        s_in, r_made, r_out, r_in, o_ready, y_ready, y_free = (sem(n) for n in (
            "s_in", "r_made", "r_out", "r_in", "o_ready", "y_ready", "y_free"))
        with nc.Block() as block:
            @block.sync
            def _(sp):
                half = S // 2
                lay = lambda t: t.rearrange("r (a c) -> (r a) c", a=2)
                sp.dma_start(s[:, :], lay(sums)).then_inc(s_in, 16)
                sp.dma_start(wo[:, :], dram[w["wo"]]).then_inc(r_in, 16)
                if out_bias:
                    sp.dma_start(bo[:, :], dram[w["bo"]]).then_inc(r_in, 16)
                sp.dma_start(o[:, :].rearrange("p (b t) -> p b t", b=B),
                             heads_out.rearrange("(b p) t -> p b t", b=B)).then_inc(r_in, 16)
                sp.wait_ge(r_made, 1)
                sp.dma_start(lay(rsums), s[:, :]).then_inc(r_out, 16)
                sp.wait_ge(r_out, 16)
                for h in range(HEADS):
                    src = rsums.rearrange("(b h) t -> h b t", h=HEADS)[h:h + 1].to_broadcast((8, B, S))
                    sp.dma_start(r[8 * h:8 * h + 8, :].rearrange("p (b t) -> p b t", b=B), src).then_inc(r_in, 16)

            @block.vector
            def _(dve):
                dve.wait_ge(s_in, 16)
                nc.vector.reciprocal(s[:, :], s[:, :]).then_inc(r_made, 1)
                dve.wait_ge(r_in, 16 * (2 + HEADS + (1 if out_bias else 0)))
                dve.sem_inc(y_free, 2)
                with dve.Fori(0, TILES) as i:
                    tok = ds(i * NT, NT)
                    nc.vector.tensor_tensor(o[:, tok], o[:, tok], r[:, tok], ALU.mult).then_inc(o_ready, 1)
                with dve.Fori(0, TILES // 2) as i:
                    for p in range(2):
                        tok = ds((2 * i + p) * NT, NT)
                        dve.wait_ge(y_ready, 2 * i + p + 1)
                        if out_bias:
                            nc.vector.scalar_tensor_tensor(x[:, tok], py[:, p, :], bo[:, 0:1], x[:, tok],
                                                           ALU.add, ALU.add).then_inc(y_free, 1)
                        else:
                            nc.vector.tensor_tensor(x[:, tok], py[:, p, :], x[:, tok], ALU.add).then_inc(y_free, 1)

            @block.tensor
            def _(pe):
                with pe.Fori(0, TILES // 2) as i:
                    for p in range(2):
                        pe.wait_ge(o_ready, 2 * i + p + 1)
                        pe.wait_ge(y_free, 2 * i + p + 1)
                        nc.tensor.matmul(py[:, p, :], wo[:, :], o[:, ds((2 * i + p) * NT, NT)],
                                         start=True, stop=True).then_inc(y_ready, 1)


EXPERTS = 8
HC = 4


def experts_ffn(net, tag, w):
    nc, x, xn, dram = net.nc, net.x, net.xn, net.dram
    NTOK = T // P
    layer_norm(net, tag + "_ln")
    with stage(nc, tag) as (sb, ps, sem):
        fc = sb("expert_fc", [P, EXPERTS, HC * P])
        pj = sb("expert_proj", [P, EXPERTS, HC, P])
        rw = sb("router", [P, EXPERTS])
        sel = sb("expert_select", [P, EXPERTS, P], BF16)
        mask_t = sb("mask_rows", [P, T], BF16)
        loaded, routed = sem("loaded"), sem("routed")
        with stage(nc, tag + "_route") as (sb2, ps2, sem2):
            rank = sb2("rank", [P, NTOK, EXPERTS])
            top = sb2("top", [P, 2, NTOK, 1])
            eq = sb2("is_top", [P, 2, NTOK, EXPERTS])
            pl = ps2("logits", [P, NTOK, EXPERTS])
            pt = ps2("mask_rows", [EXPERTS, 2, NT])
            lg, chain, turned, copied = (sem2(n) for n in ("logits", "chain", "turned", "copied"))
            with nc.Block() as block:
                @block.sync
                def _(sp):
                    sp.dma_start(rw[:, :], dram[w["router"]]).then_inc(routed, 16)
                    sp.dma_start(sel[:, :, :], dram["expert_select"]).then_inc(loaded, 16)
                    sp.dma_start(fc[:, :, :], dram[w["fc"]]).then_inc(loaded, 16)
                    sp.dma_start(pj[:, :, :, :], dram[w["proj"]]).then_inc(loaded, 16)

                @block.tensor
                def _(pe):
                    pe.wait_ge(routed, 16)
                    for m in range(NTOK):
                        mm = nc.tensor.matmul(pl[:, m, :], xn[:, m * P:(m + 1) * P], rw[:, :], start=True, stop=True)
                    mm.then_inc(lg, 1)
                    pe.wait_ge(chain, 5)
                    for m in range(NTOK):
                        if m % 4 == 0 and m >= 8:
                            pe.wait_ge(copied, m // 4 - 1)
                        mm = nc.tensor.transpose(pt[:, m // 4 % 2, m % 4 * P:(m % 4 + 1) * P], eq[:, 1, m, :],
                                                 net.ident[:, :])
                        if m % 4 == 3:
                            mm.then_inc(turned, 1)

                @block.vector
                def _(dve):
                    nc.vector.memset(mask_t[:, :], 0.0)
                    for e in range(EXPERTS):
                        nc.vector.memset(rank[:, :, e:e + 1], float(EXPERTS - e))
                    wide = lambda t: t.to_broadcast((P, NTOK, EXPERTS))
                    dve.wait_ge(lg, 1)
                    nc.vector.tensor_reduce(top[:, 0, :, 0], pl[:, :, :], AX.X, ALU.max).then_inc(chain, 1)
                    dve.wait_ge(chain, 1)
                    nc.vector.tensor_tensor(eq[:, 0, :, :], pl[:, :, :], wide(top[:, 0, :, :]), ALU.is_equal).then_inc(chain, 1)
                    dve.wait_ge(chain, 2)
                    nc.vector.tensor_tensor(eq[:, 0, :, :], eq[:, 0, :, :], rank[:, :, :], ALU.mult).then_inc(chain, 1)
                    dve.wait_ge(chain, 3)
                    nc.vector.tensor_reduce(top[:, 1, :, 0], eq[:, 0, :, :], AX.X, ALU.max).then_inc(chain, 1)
                    dve.wait_ge(chain, 4)
                    nc.vector.tensor_tensor(eq[:, 1, :, :], eq[:, 0, :, :], wide(top[:, 1, :, :]), ALU.is_equal).then_inc(chain, 1)
                    for m in range(TILES):
                        dve.wait_ge(turned, m + 1)
                        nc.vector.tensor_copy(mask_t[0:EXPERTS, m * NT:(m + 1) * NT], pt[:, m % 2, :]).then_inc(copied, 1)

        xm = sb("masked", [P, 2, NT])
        r = sb("relu", [P, 2, 2, NT])
        h = sb("hidden", [P, 2, HC, NT])
        pb = ps("mask", [P, 2, NT])
        pu = ps("up", [P, 2, 2, NT])
        py = ps("down", [P, NT])
        bc_ready, xm_ready, up_ready, relu_done, sq_done, dn_done, y_free = (sem(n) for n in (
            "mask", "masked", "up", "relu", "square", "down", "y_free"))
        E = EXPERTS
        with nc.Block() as block:
            @block.tensor
            def _(pe):
                pe.wait_ge(loaded, 48)

                def spread(i, e):
                    n = E * i + e
                    pe.wait_ge(xm_ready, n + 1)
                    nc.tensor.matmul(pb[:, e % 2, :], sel[:, e, :], mask_t[:, ds(i * NT, NT)],
                                     start=True, stop=True).then_inc(bc_ready, 1)

                def up(i, e):
                    n = E * i + e
                    pe.wait_ge(xm_ready, n + 3)
                    for half in range(2):
                        pe.wait_ge(relu_done, 2 * n + half + 1)
                        for c in range(2):
                            k = 2 * half + c
                            mm = nc.tensor.matmul(pu[:, half, c, :], fc[:, e, k * P:(k + 1) * P], xm[:, e % 2, :],
                                                  start=True, stop=True)
                        mm.then_inc(up_ready, 1)

                def down(i, e):
                    n = E * i + e
                    pe.wait_ge(sq_done, 2 * n + 4)
                    if e == 0:
                        pe.wait_ge(y_free, i + 1)
                    for k in range(HC):
                        mm = nc.tensor.matmul(py[:, :], pj[:, e, k, :], h[:, e % 2, k, :],
                                              start=(e == 0 and k == 0), stop=(e == E - 1 and k == HC - 1))
                    mm.then_inc(dn_done, 1)

                with pe.Fori(0, TILES) as i:
                    spread(i, 0)
                    spread(i, 1)
                    for e in range(E):
                        up(i, e)
                        if e:
                            down(i, e - 1)
                        if 1 <= e < E - 1:
                            spread(i, e + 1)
                    down(i, E - 1)

            @block.scalar
            def _(act):
                act.sem_inc(relu_done, 2)
                with act.Fori(0, TILES) as i:
                    for e in range(E):
                        for half in range(2):
                            n = 2 * (E * i + e) + half
                            act.wait_ge(up_ready, n + 1)
                            act.wait_ge(sq_done, n + 1)
                            nc.scalar.activation(r[:, half, :, :], pu[:, half, :, :], ACT.Relu).then_inc(relu_done, 1)

            @block.vector
            def _(dve):
                dve.sem_inc(xm_ready, 2)
                dve.sem_inc(sq_done, 2)
                dve.sem_inc(dn_done, 2)
                dve.sem_inc(y_free, 1)

                def masked(i, e):
                    n = E * i + e
                    dve.wait_ge(bc_ready, n + 1)
                    nc.vector.tensor_tensor(xm[:, e % 2, :], pb[:, e % 2, :], xn[:, ds(i * NT, NT)],
                                            ALU.mult).then_inc(xm_ready, 1)

                with dve.Fori(0, TILES) as i:
                    masked(i, 0)
                    masked(i, 1)
                    for e in range(E):
                        n = E * i + e
                        dve.wait_ge(dn_done, n + 1)
                        for half in range(2):
                            dve.wait_ge(relu_done, 2 * n + half + 3)
                            nc.vector.tensor_tensor(h[:, e % 2, 2 * half:2 * half + 2, :], r[:, half, :, :],
                                                    r[:, half, :, :], ALU.mult).then_inc(sq_done, 1)
                        if 1 <= e < E - 1:
                            masked(i, e + 1)
                    dve.wait_ge(dn_done, E * i + E + 2)
                    tok = ds(i * NT, NT)
                    nc.vector.tensor_tensor(x[:, tok], py[:, :], x[:, tok], ALU.add).then_inc(y_free, 1)


def gated_ffn(net, tag):
    nc, x, xn, dram = net.nc, net.x, net.xn, net.dram
    layer_norm(net, tag + "_ln")
    with stage(nc, tag) as (sb, ps, sem):
        w12 = [sb("w1", [P, HC * P]), sb("w2", [P, HC * P])]
        wh = [sb("h1", [P, HC, HC * P]), sb("h2", [P, HC, HC * P])]
        w3 = sb("w3", [P, HC, P])
        sc = sb("scales", [P, 17])
        h0 = sb("gated", [P, HC, T])
        loaded = sem("loaded")
        with stage(nc, tag + "_gate") as (sb2, ps2, sem2):
            sg = sb2("silu", [P, 2, NT])
            pg = ps2("gate_up", [P, 2, 2, NT])
            ready, silu, done = sem2("ready"), sem2("silu"), sem2("done")
            with nc.Block() as block:
                @block.sync
                def _(sp):
                    for t, n in ((w12[0], "w1"), (w12[1], "w2"), (sc, "scales")):
                        sp.dma_start(t[:, :], dram["g3_" + n]).then_inc(loaded, 16)
                    sp.dma_start(wh[0][:, :, :], dram["g3_h1"]).then_inc(loaded, 16)
                    sp.dma_start(wh[1][:, :, :], dram["g3_h2"]).then_inc(loaded, 16)
                    sp.dma_start(w3[:, :, :], dram["g3_w3"]).then_inc(loaded, 16)

                @block.tensor
                def _(pe):
                    pe.wait_ge(loaded, 96)
                    with pe.Fori(0, TILES) as i:
                        for k in range(HC):
                            pe.wait_ge(done, HC * i + k + 1)
                            for m in range(2):
                                mm = nc.tensor.matmul(pg[:, k % 2, m, :], w12[m][:, k * P:(k + 1) * P],
                                                      xn[:, ds(i * NT, NT)], start=True, stop=True)
                            mm.then_inc(ready, 1)

                @block.scalar
                def _(act):
                    act.wait_ge(loaded, 96)
                    nc.scalar.preload_act_table_set("silu_and_others")
                    with act.Fori(0, TILES) as i:
                        for k in range(HC):
                            act.wait_ge(ready, HC * i + k + 1)
                            act.wait_ge(done, HC * i + k + 1)
                            nc.scalar.activation(sg[:, k % 2, :], pg[:, k % 2, 0, :], ACT.Silu,
                                                 scale=sc[:, k:k + 1]).then_inc(silu, 1)

                @block.vector
                def _(dve):
                    dve.sem_inc(done, 2)
                    with dve.Fori(0, TILES) as i:
                        for k in range(HC):
                            dve.wait_ge(silu, HC * i + k + 1)
                            nc.vector.scalar_tensor_tensor(h0[:, k, ds(i * NT, NT)], pg[:, k % 2, 1, :],
                                                           sc[:, 4 + k:5 + k], sg[:, k % 2, :], ALU.mult,
                                                           ALU.mult).then_inc(done, 1)

        g = [sb("gelu1", [P, 2, HC, NT]), sb("gelu2", [P, 2, HC, NT])]
        ph = ps("hidden", [P, 4, NT])
        py = ps("out", [P, 2, NT])
        h_ready, h_done, y_ready, y_free = (sem(n) for n in ("hidden", "gelu", "y", "y_free"))
        with nc.Block() as block:
            @block.tensor
            def _(pe):
                def layer(i, p, m):
                    for k in range(HC):
                        n = 16 * i + 8 * m + 4 * p + k
                        pe.wait_ge(h_done, n + 1)
                        if m and k == 0:
                            pe.wait_ge(h_done, 4 + 16 * i + 4 * p + 4)
                        for c in range(HC):
                            src = g[0][:, p, c, :] if m else h0[:, c, ds((2 * i + p) * NT, NT)]
                            mm = nc.tensor.matmul(ph[:, k, :], wh[m][:, c, k * P:(k + 1) * P], src,
                                                  start=(c == 0), stop=(c == HC - 1))
                        mm.then_inc(h_ready, 1)

                with pe.Fori(0, TILES // 2) as i:
                    for m in range(2):
                        for p in range(2):
                            layer(i, p, m)
                    for p in range(2):
                        pe.wait_ge(h_done, 4 + 16 * i + 8 + 4 * p + 4)
                        pe.wait_ge(y_free, 2 * i + p + 1)
                        for c in range(HC):
                            mm = nc.tensor.matmul(py[:, p, :], w3[:, c, :], g[1][:, p, c, :],
                                                  start=(c == 0), stop=(c == HC - 1))
                        mm.then_inc(y_ready, 1)

            @block.scalar
            def _(act):
                act.sem_inc(h_done, 4)
                with act.Fori(0, TILES // 2) as i:
                    for m in range(2):
                        for p in range(2):
                            for k in range(HC):
                                n = 16 * i + 8 * m + 4 * p + k
                                act.wait_ge(h_ready, n + 1)
                                if m and k == 0:
                                    act.wait_ge(y_ready, 2 * i + p + 1)
                                nc.scalar.activation(g[m][:, p, k, :], ph[:, k, :], ACT.Gelu,
                                                     scale=sc[:, 8 + 4 * m + k:9 + 4 * m + k]).then_inc(h_done, 1)

            @block.vector
            def _(dve):
                dve.sem_inc(y_free, 2)
                dve.sem_inc(y_ready, 2)
                with dve.Fori(0, TILES // 2) as i:
                    for p in range(2):
                        tok = ds((2 * i + p) * NT, NT)
                        dve.wait_ge(y_ready, 2 * i + p + 3)
                        nc.vector.scalar_tensor_tensor(x[:, tok], py[:, p, :], sc[:, 16:17], x[:, tok],
                                                       ALU.mult, ALU.add).then_inc(y_free, 1)


NS = 16


def selective_ssm(net, tag, w, H, taps, left, rms, low_rank, a_is_log, residual):
    nc, x, xn, dram = net.nc, net.x, net.xn, net.dram
    PADDED = S + taps - 1
    with stage(nc, tag) as (sb, ps, sem):
        gate = sb("gate", [P, H, T])
        xs = sb("xs", [P, H, T])
        cols = sb("cols", [P, 64])
        bin_, cvb, dtb, dbb, rmsw, bout = (cols[:, a:b] for a, b in ((0, 4), (4, 6), (6, 8), (8, 9), (9, 10), (10, 11)))
        cvw = cols[:, 16:16 + H * taps].rearrange("p (h k) -> p h k", h=H)
        acol = sb("a_cols", [P, H, NS])
        w_dbc = sb("w_dbc", [P, H, P])
        w_dt = sb("w_dt", [P, H, P])
        w_out = sb("w_out", [P, H, P])
        spread = sb("spread", [P, 32, P], BF16)
        loaded = sem("loaded")
        with ExitStack() as fctx:
            fac = fctx.enter_context(nc.sbuf_tensor(f"{tag}_rms_factor", [P, T], F32)) if rms else None
            layer_norm(net, tag + "_ln", ("rsqrt", RMS_EPS, fac) if rms else None)
            ssm_input(net, tag, w, H, taps, left, rms, fac, gate, xs, cols, bin_, cvb, rmsw, cvw, acol, w_dbc, w_dt,
                      w_out, spread, loaded, PADDED)
        delta = sb("delta", [P, H, T])
        bcp = sb("bc_parts", [P, T], BF16)
        ssm_delta(net, tag, H, low_rank, a_is_log, xs, delta, bcp, dtb, dbb, acol, w_dbc, w_dt)
        ssm_scan(net, tag, H, xs, delta, bcp, acol, spread)
        ssm_output(net, tag, H, xs, gate, w_out, bout, residual)


def ssm_input(net, tag, w, H, taps, left, rms, fac, gate, xs, cols, bin_, cvb, rmsw, cvw, acol, w_dbc, w_dt, w_out,
              spread, loaded, PADDED):
    nc, x, xn, dram = net.nc, net.x, net.xn, net.dram
    with stage(nc, tag + "_in") as (sb, ps, sem):
        win = sb("w_in", [P, 2 * H * P])
        xp = sb("padded", [P, H, B, PADDED])
        hh = sb("rms_normed", [P, 2, NT])
        cv = sb("conv", [P, 2, 2, S])
        pp = ps("proj", [P, 4, NT])
        h_ready, p_ready, p_free, padded, conv, xs_done, chain, pads = (sem(n) for n in (
            "h", "proj", "proj_free", "padded", "conv", "xs", "chain", "pads"))
        M = 2 * H
        with nc.Block() as block:
            @block.sync
            def _(sp):
                for t, n in ((win, "win"), (cols, "cols")):
                    sp.dma_start(t[:, :], dram[w + n]).then_inc(loaded, 16)
                for t, n in ((acol, "a"), (w_dbc, "dbc"), (w_dt, "dt"), (w_out, "out")):
                    sp.dma_start(t[:, :, :], dram[w + n]).then_inc(loaded, 16)
                sp.dma_start(spread[:, :, :], dram["bc_spread"]).then_inc(loaded, 16)

            @block.tensor
            def _(pe):
                pe.wait_ge(loaded, 112)
                with pe.Fori(0, TILES // 2) as i:
                    for p in range(2):
                        tok = ds((2 * i + p) * NT, NT)
                        if rms:
                            pe.wait_ge(h_ready, 2 * i + p + 1)
                        for m in range(M):
                            n = (2 * i + p) * M + m
                            pe.wait_ge(p_free, n + 1)
                            nc.tensor.matmul(pp[:, (p * M + m) % 4, :], win[:, m * P:(m + 1) * P],
                                             hh[:, p, :] if rms else xn[:, tok], start=True, stop=True
                                             ).then_inc(p_ready, 1)

            @block.scalar
            def _(act):
                act.wait_ge(loaded, 112)
                act.wait_ge(chain, 1)
                act.sem_inc(p_free, 4)
                nc.scalar.preload_act_table_set("silu_and_others")
                with act.Fori(0, B) as b:
                    for p in range(2):
                        tok = ds((2 * b + p) * NT, NT)
                        for m in range(M):
                            act.wait_ge(p_ready, (2 * b + p) * M + m + 1)
                            src = pp[:, (p * M + m) % 4, :]
                            if m < H:
                                dst = xp[:, m, ds(b, 1), left + p * NT:left + (p + 1) * NT].rearrange("p o t -> p (o t)")
                                nc.scalar.activation(dst, src, ACT.Identity, bias=bin_[:, m:m + 1]).then_inc(p_free, 1)
                            else:
                                nc.scalar.activation(gate[:, m - H, tok], src, ACT.Silu,
                                                     bias=bin_[:, m:m + 1]).then_inc(p_free, 1)
                with act.Fori(0, B) as b:
                    for h in range(H):
                        act.wait_ge(conv, H * b + h + 1)
                        nc.scalar.activation(xs[:, h, ds(b * S, S)], cv[:, 1, h, :], ACT.Silu).then_inc(xs_done, 1)

            @block.vector
            def _(dve):
                nc.vector.memset(xp[:, :, :, 0:left], 0.0).then_inc(pads, 1)
                if taps - 1 - left:
                    nc.vector.memset(xp[:, :, :, left + S:PADDED], 0.0).then_inc(pads, 1)
                dve.wait_ge(pads, 2 if taps - 1 - left else 1)
                dve.sem_inc(xs_done, H)
                dve.wait_ge(loaded, 112)
                dve.sem_inc(chain, 1)
                if rms:
                    with dve.Fori(0, TILES // 2) as i:
                        for p in range(2):
                            tok = ds((2 * i + p) * NT, NT)
                            dve.wait_ge(p_free, (2 * i + p) * M + 1)
                            nc.vector.scalar_tensor_tensor(hh[:, p, :], xn[:, tok], rmsw[:, 0:1], fac[:, tok],
                                                           ALU.mult, ALU.mult).then_inc(h_ready, 1)
                with dve.Fori(0, B) as b:
                    for h in range(H):
                        dve.wait_ge(p_free, 4 + (2 * b + 2) * M)
                        dve.wait_ge(xs_done, H * b + h + 1)
                        for k in range(taps):
                            src = xp[:, h, ds(b, 1), k:k + S].rearrange("p o t -> p (o t)")
                            last = k == taps - 1
                            dst = cv[:, 1 if last else 0, h, :]
                            if k == 0:
                                a = nc.vector.tensor_scalar(dst, src, cvw[:, h, 0:1], cvb[:, h:h + 1], ALU.mult, ALU.add)
                            else:
                                dve.wait_ge(chain, (H * b + h) * (taps - 1) + k + 1)
                                a = nc.vector.scalar_tensor_tensor(dst, src, cvw[:, h, k:k + 1], cv[:, 0, h, :],
                                                                   ALU.mult, ALU.add)
                            a.then_inc(conv if last else chain, 1)


def ssm_delta(net, tag, H, low_rank, a_is_log, xs, delta, bcp, dtb, dbb, acol, w_dbc, w_dt):
    nc = net.nc
    with stage(nc, tag + "_dt") as (sb, ps, sem):
        z = sb("dbc", [P, 2, NT])
        hi = sb("hi", [P, 2, NT], BF16)
        mid = sb("mid", [P, 2, NT], BF16)
        rest = sb("rest", [P, 2, NT])
        ab = sb("softplus", [P, 2, H, 3, NT])
        mx = sb("before_softplus", [P, 2, H, NT])
        pz = ps("dbc", [P, 2, NT])
        pd = ps("delta", [P, 2, H, NT])
        z_ready, z_done, d_ready, l_done, u_done, parts, a_chain, d_chain = (sem(n) for n in (
            "dbc", "dbc_done", "delta", "log_done", "u_done", "parts", "act_chain", "dve_chain"))
        with nc.Block() as block:
            @block.tensor
            def _(pe):
                with pe.Fori(0, TILES // 2) as i:
                    for p in range(2):
                        pe.wait_ge(z_done, 2 * i + p + 1)
                        for h in range(H):
                            mm = nc.tensor.matmul(pz[:, p, :], w_dbc[:, h, :], xs[:, h, ds((2 * i + p) * NT, NT)],
                                                  start=(h == 0), stop=(h == H - 1))
                        mm.then_inc(z_ready, 1)
                    for p in range(2):
                        if low_rank:
                            pe.wait_ge(z_done, 2 * i + p + 3)
                        pe.wait_ge(u_done, 2 * i + p + 1)
                        for h in range(H):
                            src = z[:, p, :] if low_rank else xs[:, h, ds((2 * i + p) * NT, NT)]
                            mm = nc.tensor.matmul(pd[:, p, h, :], w_dt[:, h, :], src, start=True, stop=True)
                        mm.then_inc(d_ready, 1)

            @block.scalar
            def _(act):
                nc.scalar.preload_act_table_set("natural_log_exp_and_others")
                C = [0]
                if a_is_log:
                    nc.scalar.activation(acol[:, :, :], acol[:, :, :], ACT.Exp).then_inc(a_chain, 1)
                    C[0] = 1
                with act.Fori(0, TILES // 2) as i:
                    for p in range(2):
                        act.wait_ge(d_chain, 2 * (2 * i + p) + 1)
                        for h in range(H):
                            q = (2 * i + p) * H + h
                            nc.scalar.activation(ab[:, p, h, 0, :], mx[:, p, h, :], ACT.Abs).then_inc(a_chain, 1)
                            act.wait_ge(a_chain, 2 * q + C[0] + 1)
                            nc.scalar.activation(ab[:, p, h, 1, :], ab[:, p, h, 0, :], ACT.Exp,
                                                 scale=-1.0).then_inc(a_chain, 1)
                            act.wait_ge(a_chain, 2 * q + C[0] + 2)
                            a = nc.scalar.activation(ab[:, p, h, 2, :], ab[:, p, h, 1, :], ACT.Ln, bias=net.one)
                        a.then_inc(l_done, 1)

            @block.vector
            def _(dve):
                dve.sem_inc(z_done, 2)
                dve.sem_inc(u_done, 2)
                if a_is_log:
                    dve.wait_ge(a_chain, 1)
                    nc.vector.tensor_scalar(acol[:, :, :], acol[:, :, :], -1.0, None, ALU.mult)
                K = 3 + 2
                with dve.Fori(0, TILES // 2) as i:
                    for p in range(2):
                        t = 2 * i + p
                        tok = ds(t * NT, NT)
                        dve.wait_ge(z_ready, t + 1)
                        nc.vector.tensor_scalar(z[:, p, :], pz[:, p, :], dbb[:, 0:1], None, ALU.add).then_inc(z_done, 1)
                        dve.wait_ge(z_done, t + 3)
                        nc.vector.tensor_copy(hi[0:96, p, :], z[0:96, p, :]).then_inc(parts, 1)
                        dve.wait_ge(parts, 3 * t + 1)
                        nc.vector.tensor_tensor(rest[0:96, p, :], z[0:96, p, :], hi[0:96, p, :], ALU.subtract
                                                ).then_inc(parts, 1)
                        nc.vector.tensor_copy(bcp[0:32, tok], hi[0:32, p, :])
                        dve.wait_ge(parts, 3 * t + 2)
                        nc.vector.tensor_copy(mid[0:96, p, :], rest[0:96, p, :]).then_inc(parts, 1)
                        dve.wait_ge(parts, 3 * t + 3)
                        nc.vector.tensor_copy(bcp[32:64, tok], mid[32:64, p, :])
                        nc.vector.tensor_tensor(bcp[64:96, tok], rest[64:96, p, :], mid[64:96, p, :], ALU.subtract)
                    for p in range(2):
                        t = 2 * i + p
                        tok = ds(t * NT, NT)
                        dve.wait_ge(d_ready, t + 1)
                        for h in range(H):
                            a = nc.vector.tensor_scalar(mx[:, p, h, :], pd[:, p, h, :], dtb[:, h:h + 1], None,
                                                        ALU.add)
                        a.then_inc(d_chain, 1)
                        dve.wait_ge(l_done, t + 1)
                        nc.vector.scalar_tensor_tensor(delta[:, :, tok], mx[:, p, :, :], 0.0, ab[:, p, :, 2, :],
                                                       ALU.max, ALU.add).then_inc(d_chain, 1)
                        dve.wait_ge(d_chain, 2 * t + 2)
                        nc.vector.tensor_tensor(xs[:, :, tok], xs[:, :, tok], delta[:, :, tok],
                                                ALU.mult).then_inc(u_done, 1)


def ssm_scan(net, tag, H, xs, delta, bcp, acol, spread):
    nc = net.nc
    with stage(nc, tag + "_scan") as (sb, ps, sem):
        decay = sb("decay", [P, 2, S])
        bs = sb("b_rows", [P, 2, S])
        bx = sb("bx", [P, 2, S])
        hs = sb("states", [P, 2, S])
        hc = sb("states_c", [P, 2, S])
        pb, pc = ps("b_rows", [P, S]), ps("c_rows", [P, S])
        acc = ps("y", [P, H, S])
        b_ready, bs_done, c_ready, hc_done, y_done, y_out, a_done, bx_done, scanned, paced = (
            sem(n) for n in ("b_rows", "b_copied", "c_rows", "states_c", "summed", "y_out", "decay", "bx", "scanned",
                             "paced"))
        with nc.Block() as block:
            @block.tensor
            def _(pe):
                def add_up(b, n):
                    for h in range(H):
                        q = (NS * b + n) * H + h
                        pe.wait_ge(hc_done, q + 1 + H)
                        if n == 0:
                            pe.wait_ge(y_out, b + 1)
                        for c in range(2):
                            mm = nc.tensor.matmul(acc[:, h, c * NT:(c + 1) * NT], net.ident[:, :],
                                                  hc[:, (n * H + h) % 2, c * NT:(c + 1) * NT],
                                                  start=(n == 0), stop=(n == NS - 1))
                        mm.then_inc(y_done, 1)

                with pe.Fori(0, B) as b:
                    for n in range(NS):
                        s = NS * b + n
                        pe.wait_ge(bs_done, s + 1)
                        for c in range(2):
                            mm = nc.tensor.matmul(pb[:, c * NT:(c + 1) * NT], spread[0:96, n, :],
                                                  bcp[0:96, ds(b * S + c * NT, NT)], start=True, stop=True)
                        mm.then_inc(b_ready, 1)
                        pe.wait_ge(hc_done, H * s + H)
                        for c in range(2):
                            mm = nc.tensor.matmul(pc[:, c * NT:(c + 1) * NT], spread[0:96, NS + n, :],
                                                  bcp[0:96, ds(b * S + c * NT, NT)], start=True, stop=True)
                        mm.then_inc(c_ready, 1)
                        if n:
                            add_up(b, n - 1)
                    add_up(b, NS - 1)

            @block.scalar
            def _(act):
                nc.scalar.preload_act_table_set("natural_log_exp_and_others")
                act.sem_inc(bs_done, 1)
                with act.Fori(0, B) as b:
                    for n in range(NS):
                        s = NS * b + n
                        act.wait_ge(b_ready, s + 1)
                        act.wait_ge(bx_done, H * s + H)
                        nc.scalar.activation(bs[:, n % 2, :], pb[:, :], ACT.Copy).then_inc(bs_done, 1)
                        for h in range(H):
                            q = H * s + h
                            act.wait_ge(scanned, q + 1)
                            act.sem_inc(paced, 1)
                            nc.scalar.activation(decay[:, (n * H + h) % 2, :], delta[:, h, ds(b * S, S)], ACT.Exp,
                                                 scale=acol[:, h, n:n + 1]).then_inc(a_done, 1)

            @block.gpsimd
            def _(pool):
                pool.sem_inc(bx_done, 2 * H)
                with pool.Fori(0, B) as b:
                    for n in range(NS):
                        s = NS * b + n
                        pool.wait_ge(bs_done, s + 2)
                        for h in range(H):
                            q = H * s + h
                            pool.wait_ge(scanned, q + 1)
                            pool.sem_inc(paced, 1)
                            nc.gpsimd.tensor_tensor(bx[:, (n * H + h) % 2, :], xs[:, h, ds(b * S, S)], bs[:, n % 2, :],
                                                    ALU.mult).then_inc(bx_done, 1)

            @block.vector
            def _(dve):
                dve.sem_inc(scanned, 2)
                dve.sem_inc(hc_done, H)
                dve.sem_inc(y_done, 2)
                dve.sem_inc(y_out, 1)
                with dve.Fori(0, B) as b:
                    for n in range(NS):
                        for h in range(H):
                            q = (NS * b + n) * H + h
                            r = (n * H + h) % 2
                            dve.wait_ge(a_done, q + 1)
                            dve.wait_ge(bx_done, q + 2 * H + 1)
                            nc.vector.tensor_tensor_scan(hs[:, r, :], decay[:, r, :], bx[:, r, :], 0.0, ALU.mult,
                                                         ALU.add).then_inc(scanned, 1)
                            if h == 0:
                                dve.wait_ge(c_ready, NS * b + n + 1)
                            dve.wait_ge(y_done, q + 1)
                            dve.wait_ge(scanned, q + 3)
                            nc.vector.tensor_tensor(hc[:, r, :], hs[:, r, :], pc[:, :], ALU.mult).then_inc(hc_done, 1)
                    dve.wait_ge(y_done, H * NS * (b + 1) + 2)
                    nc.vector.tensor_copy(xs[:, :, ds(b * S, S)], acc[:, :, :]).then_inc(y_out, 1)


def ssm_output(net, tag, H, y, gate, w_out, bout, residual):
    nc, x, xn = net.nc, net.x, net.xn
    with stage(nc, tag + "_out") as (sb, ps, sem):
        py = ps("proj", [P, 2, NT])
        gated, ready, free, added = sem("gated"), sem("ready"), sem("free"), sem("added")
        with nc.Block() as block:
            @block.gpsimd
            def _(pool):
                with pool.Fori(0, TILES) as i:
                    tok = ds(i * NT, NT)
                    nc.gpsimd.tensor_tensor(y[:, :, tok], y[:, :, tok], gate[:, :, tok], ALU.mult).then_inc(gated, 1)

            @block.tensor
            def _(pe):
                with pe.Fori(0, TILES // 2) as i:
                    for p in range(2):
                        pe.wait_ge(gated, 2 * i + p + 1)
                        pe.wait_ge(free, 2 * i + p + 1)
                        for h in range(H):
                            mm = nc.tensor.matmul(py[:, p, :], w_out[:, h, :], y[:, h, ds((2 * i + p) * NT, NT)],
                                                  start=(h == 0), stop=(h == H - 1))
                        mm.then_inc(ready, 1)

            @block.vector
            def _(dve):
                if residual:
                    nc.vector.tensor_tensor(x[:, :], x[:, :], xn[:, :], ALU.add).then_inc(added, 1)
                    dve.wait_ge(added, 1)
                dve.sem_inc(free, 2)
                with dve.Fori(0, TILES // 2) as i:
                    for p in range(2):
                        tok = ds((2 * i + p) * NT, NT)
                        dve.wait_ge(ready, 2 * i + p + 1)
                        nc.vector.scalar_tensor_tensor(x[:, tok], py[:, p, :], bout[:, 0:1], x[:, tok],
                                                       ALU.add, ALU.add).then_inc(free, 1)


SSD_HEADS, SSD_P = 32, 8
UNITS = T // P
CPS = S // P


def ssd(net, tag):
    nc, x, xn, dram = net.nc, net.x, net.xn, net.dram
    taps, DI = 4, 2 * P
    PADDED = S + taps - 1
    layer_norm(net, tag + "_ln")
    with stage(nc, tag) as (sb, ps, sem):
        xbc = sb("xbc", [P, 4, B, PADDED])
        zs = sb("gate", [P, UNITS, DI])
        dt = sb("dt", [P, UNITS, SSD_HEADS])
        e_cs = sb("exp_cs", [P, UNITS, SSD_HEADS])
        e_out = sb("exp_rest", [P, UNITS, SSD_HEADS])
        e_all = sb("exp_chunk", [P, UNITS, SSD_HEADS])
        csp = sb("cs_parts", [96, T], BF16)
        w_out = sb("w_out", [P, 2, P])
        ssd_input(net, tag, xbc, zs, dt, w_out, PADDED, taps, DI)
        ssd_steps(net, tag, dt, e_cs, e_out, e_all, csp)
        ssd_chunks(net, tag, xbc, dt, e_cs, e_out, e_all, csp, DI)
        ssd_output(net, tag, xbc, zs, w_out, DI)


def ssd_input(net, tag, xbc, zs, dt, w_out, PADDED, taps, DI):
    nc, xn, dram = net.nc, net.xn, net.dram
    with stage(nc, tag + "_in") as (sb, ps, sem):
        w = sb("w_xbc", [P, 4 * P])
        wz = sb("w_z_dt", [P, DI + SSD_HEADS])
        cvw = sb("conv_w", [P, 4, taps + 1])
        dtb = sb("dt_bias", [P, SSD_HEADS])
        lnw = sb("ln_w", [P, DI])
        cv = sb("conv", [P, 2, 2, S])
        pp = ps("proj", [P, 4, NT])
        pz = ps("z", [P, 2, NT])
        loaded, p_ready, p_free, z_ready, z_silu, z_free, conv, xs_done, chain, pads = (sem(n) for n in (
            "loaded", "proj", "proj_free", "z", "z_silu", "z_free", "conv", "xs", "chain", "pads"))
        with nc.Block() as block:
            @block.sync
            def _(sp):
                for t, n in ((w, "w"), (wz, "wz")):
                    sp.dma_start(t[:, :], dram["d2_" + n]).then_inc(loaded, 16)
                sp.dma_start(cvw[:, :, :], dram["d2_conv"]).then_inc(loaded, 16)
                sp.dma_start(w_out[:, :, :], dram["d2_out"]).then_inc(loaded, 16)
                sp.dma_start(dtb[:, :], dram["d2_dtb"].to_broadcast((P, SSD_HEADS))).then_inc(loaded, 16)
                sp.dma_start(lnw[:, :], dram["d2_lnw"].to_broadcast((P, DI))).then_inc(loaded, 16)

            @block.tensor
            def _(pe):
                pe.wait_ge(loaded, 96)
                with pe.Fori(0, TILES) as i:
                    for m in range(4):
                        pe.wait_ge(p_free, 4 * i + m + 1)
                        nc.tensor.matmul(pp[:, m, :], w[:, m * P:(m + 1) * P], xn[:, ds(i * NT, NT)],
                                         start=True, stop=True).then_inc(p_ready, 1)
                for u in range(UNITS):
                    if u >= 2:
                        pe.wait_ge(z_free, u - 1)
                    nc.tensor.matmul(pz[:, u % 2, 0:DI + SSD_HEADS], xn[:, u * P:(u + 1) * P], wz[:, :],
                                     start=True, stop=True).then_inc(z_ready, 1)

            @block.scalar
            def _(act):
                nc.scalar.preload_act_table_set("silu_and_others")
                act.sem_inc(p_free, 4)
                with act.Fori(0, B) as b:
                    for p in range(2):
                        for m in range(4):
                            act.wait_ge(p_ready, 8 * b + 4 * p + m + 1)
                            dst = xbc[:, m, ds(b, 1), 3 + p * NT:3 + (p + 1) * NT].rearrange("p o t -> p (o t)")
                            nc.scalar.activation(dst, pp[:, m, :], ACT.Copy).then_inc(p_free, 1)
                for u in range(UNITS):
                    act.wait_ge(z_ready, u + 1)
                    nc.scalar.activation(zs[:, u, :], pz[:, u % 2, 0:DI], ACT.Silu).then_inc(z_silu, 1)
                with act.Fori(0, B) as b:
                    for m in range(4):
                        act.wait_ge(conv, 4 * b + m + 1)
                        dst = xbc[:, m, ds(b, 1), 0:S].rearrange("p o t -> p (o t)")
                        nc.scalar.activation(dst, cv[:, 1, m % 2, :], ACT.Silu).then_inc(xs_done, 1)

            @block.vector
            def _(dve):
                nc.vector.memset(xbc[:, :, :, 0:taps - 1], 0.0).then_inc(pads, 1)
                dve.wait_ge(pads, 1)
                dve.sem_inc(xs_done, 2)
                dve.wait_ge(loaded, 96)
                for u in range(UNITS):
                    dve.wait_ge(z_silu, u + 1)
                    nc.vector.tensor_tensor(dt[:, u, :], pz[:, u % 2, DI:DI + SSD_HEADS], dtb[:, :],
                                            ALU.add).then_inc(z_free, 1)
                with dve.Fori(0, B) as b:
                    for m in range(4):
                        dve.wait_ge(p_free, 4 + 8 * b + 8)
                        dve.wait_ge(xs_done, 4 * b + m + 1)
                        for k in range(taps):
                            src = xbc[:, m, ds(b, 1), k:k + S].rearrange("p o t -> p (o t)")
                            last = k == taps - 1
                            dst = cv[:, 1 if last else 0, m % 2, :]
                            if k == 0:
                                a = nc.vector.tensor_scalar(dst, src, cvw[:, m, 0:1], cvw[:, m, taps:taps + 1],
                                                            ALU.mult, ALU.add)
                            else:
                                dve.wait_ge(chain, (4 * b + m) * (taps - 1) + k)
                                a = nc.vector.scalar_tensor_tensor(dst, src, cvw[:, m, k:k + 1], cv[:, 0, m % 2, :],
                                                                   ALU.mult, ALU.add)
                            a.then_inc(conv if last else chain, 1)

            @block.gpsimd
            def _(pool):
                pool.wait_ge(loaded, 96)
                for u in range(UNITS):
                    pool.wait_ge(z_silu, u + 1)
                    nc.gpsimd.tensor_tensor(zs[:, u, :], zs[:, u, :], lnw[:, :], ALU.mult)


def ssd_steps(net, tag, dt, e_cs, e_out, e_all, csp):
    nc, dram = net.nc, net.dram
    W = UNITS * SSD_HEADS
    flat = lambda t: t[:, :, :].rearrange("p u h -> p (u h)")
    with stage(nc, tag + "_dt") as (sb, ps, sem):
        tri = sb("triangle", [P, P])
        last = sb("last_row", [P, P])
        arow = sb("a_row", [P, 1, SSD_HEADS])
        t1, t2, t3 = sb("t1", [P, W]), sb("t2", [P, W]), sb("t3", [P, W])
        cs = sb("cs", [P, UNITS, SSD_HEADS])
        rest = sb("rest", [SSD_HEADS, 2, NT])
        pc = ps("cs", [P, W])
        pl = ps("cs_end", [P, W])
        pt = ps("turned", [SSD_HEADS, 2, NT])
        loaded, c, pe_done, turned, taken = (sem(n) for n in ("loaded", "chain", "products", "turned", "taken"))
        part = sem("parts")
        with nc.Block() as block:
            @block.sync
            def _(sp):
                sp.dma_start(tri[:, :], dram["triangle"]).then_inc(loaded, 16)
                sp.dma_start(last[:, :], dram["last_row"]).then_inc(loaded, 16)
                sp.dma_start(arow[:, 0, :], dram["d2_alog"].to_broadcast((P, SSD_HEADS))).then_inc(loaded, 16)

            @block.scalar
            def _(act):
                nc.scalar.preload_act_table_set("natural_log_exp_and_others")
                act.wait_ge(loaded, 48)
                nc.scalar.activation(t1[:, :], flat(dt), ACT.Abs).then_inc(c, 1)
                act.wait_ge(c, 1)
                nc.scalar.activation(t2[:, :], t1[:, :], ACT.Exp, scale=-1.0).then_inc(c, 1)
                act.wait_ge(c, 2)
                nc.scalar.activation(t3[:, :], t2[:, :], ACT.Ln, bias=net.one).then_inc(c, 1)
                nc.scalar.activation(arow[:, :, :], arow[:, :, :], ACT.Exp).then_inc(c, 1)
                act.wait_ge(c, 8)
                nc.scalar.activation(flat(e_cs), flat(cs), ACT.Exp).then_inc(c, 1)
                nc.scalar.activation(flat(e_all), t2[:, :], ACT.Exp).then_inc(c, 1)
                nc.scalar.activation(flat(e_out), t3[:, :], ACT.Exp).then_inc(c, 1)

            @block.vector
            def _(dve):
                dve.wait_ge(c, 4)
                nc.vector.scalar_tensor_tensor(flat(dt), flat(dt), 0.0, t3[:, :], ALU.max, ALU.add).then_inc(c, 1)
                dve.wait_ge(c, 5)
                nc.vector.scalar_tensor_tensor(t1[:, :].rearrange("p (u h) -> p u h", u=UNITS), dt[:, :, :], -1.0,
                                               arow[:, :, :].to_broadcast((P, UNITS, SSD_HEADS)), ALU.mult,
                                               ALU.mult).then_inc(c, 1)
                dve.wait_ge(pe_done, 1)
                nc.vector.tensor_copy(flat(cs), pc[:, :]).then_inc(taken, 1)
                dve.wait_ge(pe_done, 2)
                nc.vector.tensor_copy(t2[:, :], pl[:, :]).then_inc(c, 1)
                dve.wait_ge(c, 7)
                dve.wait_ge(taken, 1)
                nc.vector.tensor_tensor(t3[:, :], t2[:, :], flat(cs), ALU.subtract).then_inc(c, 1)
                for m in range(TILES):
                    tok = slice(m * NT, (m + 1) * NT)
                    dve.wait_ge(turned, m + 1)
                    nc.vector.tensor_copy(csp[0:32, tok], pt[:, m % 2, :]).then_inc(part, 1)
                    dve.wait_ge(part, 4 * m + 1)
                    nc.vector.tensor_tensor(rest[:, m % 2, :], pt[:, m % 2, :], csp[0:32, tok],
                                            ALU.subtract).then_inc(part, 1)
                    dve.wait_ge(part, 4 * m + 2)
                    nc.vector.tensor_copy(csp[32:64, tok], rest[:, m % 2, :]).then_inc(part, 1)
                    dve.wait_ge(part, 4 * m + 3)
                    nc.vector.tensor_copy(t1[0:32, 0:NT], csp[32:64, tok]).then_inc(part, 1)
                    dve.wait_ge(part, 4 * m + 4)
                    nc.vector.tensor_tensor(csp[64:96, tok], rest[:, m % 2, :], t1[0:32, 0:NT],
                                            ALU.subtract).then_inc(taken, 1)
                dve.wait_ge(c, 11)
                first = lambda t: t[:, :, :].rearrange("p (b c) h -> p b c h", b=B)[:, :, 0, :]
                nc.vector.memset(first(e_cs), 0.0)
                nc.vector.memset(first(e_all), 0.0)

            @block.tensor
            def _(pe):
                pe.wait_ge(c, 6)
                for k in range(W // NT):
                    mm = nc.tensor.matmul(pc[:, k * NT:(k + 1) * NT], tri[:, :], t1[:, k * NT:(k + 1) * NT],
                                          start=True, stop=True)
                mm.then_inc(pe_done, 1)
                pe.wait_ge(taken, 1)
                for k in range(W // NT):
                    mm = nc.tensor.matmul(pl[:, k * NT:(k + 1) * NT], last[:, :],
                                          cs[:, :, :].rearrange("p u h -> p (u h)")[:, k * NT:(k + 1) * NT],
                                          start=True, stop=True)
                mm.then_inc(pe_done, 1)
                for u in range(UNITS):
                    if u % 4 == 0 and u >= 8:
                        pe.wait_ge(taken, u // 4)
                    mm = nc.tensor.transpose(pt[:, u // 4 % 2, u % 4 * P:(u % 4 + 1) * P], cs[:, u, :], net.ident[:, :])
                    if u % 4 == 3:
                        mm.then_inc(turned, 1)


def ssd_chunks(net, tag, xbc, dt, e_cs, e_out, e_all, csp, DI):
    nc, dram = net.nc, net.dram
    HG = 8
    NG = SSD_HEADS // HG
    wide = lambda t: t.to_broadcast((P, SSD_HEADS, SSD_P))
    with stage(nc, tag + "_chunks") as (sb, ps, sem):
        pick = sb("pick", [96, SSD_HEADS, P], BF16)
        npick = sb("neg_pick", [96, SSD_HEADS, P], BF16)
        mask = sb("mask", [P, 4, P], BF16)
        st = sb("chunk", [P, 2, 4, P])
        gs = sb("cb", [P, 2, 1, P])
        bt = sb("b_tokens", [P, 2, P])
        xd = sb("x_dt", [P, 2, SSD_HEADS, SSD_P])
        xe = sb("x_dt_rest", [P, 2, SSD_HEADS, SSD_P])
        dec = sb("decay", [P, 2, HG, P])
        mt = sb("mixed", [P, 2, HG, P])
        state = sb("state", [P, SSD_HEADS, SSD_P])
        yo = sb("y_off", [P, SSD_HEADS, SSD_P])
        pg = ps("cb_turned", [P, NT])
        pl = [ps(f"decay{n}", [P, HG, P]) for n in range(2)]
        py, po, pst = ps("y_diag", [P, NT]), ps("y_off", [P, NT]), ps("state", [P, NT])
        loaded, staged, g_ready, g_taken, l_ready, l_done, m_done = (sem(n) for n in (
            "loaded", "staged", "cb", "cb_taken", "decay", "exp_done", "mixed"))
        m_last, st_chain, o_ready, s_ready, s_done, yo_done, y_done, h_used = (sem(n) for n in (
            "last_mixed", "state_scaled", "y_off", "state_in", "state", "y_off_scaled", "y", "mixed_used"))
        with nc.Block() as block:
            @block.sync
            def _(sp):
                sp.dma_start(pick[:, :, :], dram["bc_spread"][0:96]).then_inc(loaded, 16)
                sp.dma_start(npick[:, :, :], dram["neg_pick"]).then_inc(loaded, 16)
                for j in range(4):
                    sp.dma_start(mask[:, j, :], dram["mask_k"]).then_inc(loaded, 16)

            def units(eng, one):
                with eng.Fori(0, B) as b:
                    with eng.Fori(0, CPS // 2) as c2:
                        for p in range(2):
                            one(b * CPS + 2 * c2 + p, b, 2 * c2 + p, p)

            def mix(ns, eng, u, p, g):
                eng.wait_ge(l_done, NG * u + g + 3)
                eng.wait_ge(g_taken, 4 * u + 5)
                eng.wait_ge(h_used, NG * u + g + 1)
                ns.tensor_tensor(mt[:, g % 2, :, :], dec[:, g % 2, :, :], gs[:, p, :, :].to_broadcast((P, HG, P)),
                                 ALU.mult).then_inc(m_last if g == NG - 1 else m_done, 1)

            @block.gpsimd
            def _(pool):
                def one(u, b, c, p):
                    pool.wait_ge(y_done, u + 1)
                    src = xbc[:, :, ds(b, 1), ds(c * P, P)].rearrange("p m o t -> p m (o t)")
                    nc.gpsimd.tensor_copy(st[:, p, :, :], src).then_inc(staged, 1)
                    mix(nc.gpsimd, pool, u, p, NG - 1)

                units(pool, one)

            @block.tensor
            def _(pe):
                pe.wait_ge(loaded, 96)

                def one(u, b, c, p):
                    pe.wait_ge(staged, u + 1)
                    pe.wait_ge(g_taken, 4 * u + 1)
                    nc.tensor.matmul(pg[:, 0:P], st[:, p, 2, :], st[:, p, 3, :], start=True, stop=True)
                    for j in range(3):
                        mm = nc.tensor.transpose(pg[:, (j + 1) * P:(j + 2) * P], st[:, p, j, :], net.ident[:, :])
                    mm.then_inc(g_ready, 1)
                    pe.wait_ge(s_done, u + 1)
                    pe.wait_ge(yo_done, u + 1)
                    nc.tensor.matmul(po[:, 0:DI], st[:, p, 3, :], state[:, :, :].rearrange("p h e -> p (h e)"),
                                     start=True, stop=True).then_inc(o_ready, 1)

                    def decays(g):
                        pe.wait_ge(l_done, NG * u + g + 1)
                        for q in range(2):
                            h0 = g * HG + 4 * q
                            dst = pl[g % 2][:, 4 * q:4 * q + 4, :]
                            nc.tensor.matmul(dst, net.identb[:, :], mask[:, :, :], start=True, stop=False)
                            nc.tensor.matmul(dst, csp[0:96, ds(u * P, P)], npick[:, h0:h0 + 4, :], start=False, stop=False)
                            for j in range(4):
                                mm = nc.tensor.matmul(dst[:, j, :], pick[:, h0 + j, :], csp[0:96, ds(u * P, P)],
                                                      start=False, stop=(j == 3))
                        mm.then_inc(l_ready, 1)

                    def values(g):
                        if g == NG - 1:
                            pe.wait_ge(m_last, u + 1)
                        else:
                            pe.wait_ge(m_done, (NG - 1) * u + g + 1)
                        if g == 0:
                            pe.wait_ge(y_done, u + 2)
                        for h in range(HG):
                            hh = g * HG + h
                            mm = nc.tensor.matmul(py[:, hh * SSD_P:(hh + 1) * SSD_P], mt[:, g % 2, h, :],
                                                  xd[:, p, hh, :], start=True, stop=True)
                        mm.then_inc(h_used, 1)

                    for g in range(NG):
                        decays(g)
                        if g == 1:
                            pe.wait_ge(g_taken, 4 * u + 5)
                            pe.wait_ge(s_done, u + 1)
                            nc.tensor.matmul(pst[:, 0:DI], bt[:, p, :], xe[:, p, :, :].rearrange("p h e -> p (h e)"),
                                             start=True, stop=True).then_inc(s_ready, 1)
                        if g:
                            values(g - 1)
                    values(NG - 1)

                units(pe, one)

            @block.scalar
            def _(act):
                nc.scalar.preload_act_table_set("natural_log_exp_and_others")
                act.sem_inc(l_done, 2)

                def one(u, b, c, p):
                    for g in range(NG):
                        act.wait_ge(l_ready, NG * u + g + 1)
                        act.wait_ge(h_used, NG * u + g + 1)
                        nc.scalar.activation(dec[:, g % 2, :, :], pl[g % 2][:, :, :], ACT.Exp).then_inc(l_done, 1)

                units(act, one)

            @block.vector
            def _(dve):
                nc.vector.memset(state[:, :, :], 0.0).then_inc(s_done, 1)
                dve.sem_inc(y_done, 2)
                dve.sem_inc(yo_done, 1)
                dve.sem_inc(g_taken, 1)
                dve.sem_inc(h_used, 2)

                def one(u, b, c, p):
                    v = lambda t: t[:, ds(u, 1), :].rearrange("p o h -> p h o")
                    tok = pg[:, P:P + DI].rearrange("p (h e) -> p h e", e=SSD_P)
                    dve.wait_ge(g_ready, u + 1)
                    nc.vector.tensor_copy(gs[:, p, 0, :], pg[:, 0:P]).then_inc(g_taken, 1)
                    nc.vector.tensor_tensor(xd[:, p, :, :], tok, wide(v(dt)), ALU.mult).then_inc(g_taken, 1)
                    nc.vector.tensor_copy(bt[:, p, :], pg[:, P + DI:P + DI + P]).then_inc(g_taken, 1)
                    dve.wait_ge(g_taken, 4 * u + 4)
                    nc.vector.tensor_tensor(xe[:, p, :, :], xd[:, p, :, :], wide(v(e_out)), ALU.mult).then_inc(g_taken, 1)
                    dve.wait_ge(o_ready, u + 1)
                    nc.vector.tensor_tensor(yo[:, :, :], po[:, 0:DI].rearrange("p (h e) -> p h e", e=SSD_P),
                                            wide(v(e_cs)), ALU.mult).then_inc(yo_done, 1)
                    nc.vector.tensor_tensor(state[:, :, :], state[:, :, :], wide(v(e_all)), ALU.mult).then_inc(st_chain, 1)
                    mix(nc.vector, dve, u, p, 0)
                    dve.wait_ge(s_ready, u + 1)
                    dve.wait_ge(st_chain, u + 1)
                    nc.vector.tensor_tensor(state[:, :, :], pst[:, 0:DI].rearrange("p (h e) -> p h e", e=SSD_P),
                                            state[:, :, :], ALU.add).then_inc(s_done, 1)
                    for g in range(1, NG - 1):
                        mix(nc.vector, dve, u, p, g)
                    dve.wait_ge(h_used, NG * u + NG + 2)
                    dve.wait_ge(yo_done, u + 2)
                    dst = xbc[:, 0:2, ds(b, 1), ds(c * P, P)].rearrange("p m o t -> p m (o t)")
                    nc.vector.tensor_tensor(dst, py[:, 0:DI].rearrange("p (m t) -> p m t", m=2),
                                            yo[:, :, :].rearrange("p (m h) e -> p m (h e)", m=2), ALU.add
                                            ).then_inc(y_done, 1)

                units(dve, one)


def ssd_output(net, tag, xbc, zs, w_out, DI):
    nc, x = net.nc, net.x
    with stage(nc, tag + "_out") as (sb, ps, sem):
        sq = sb("squares", [P, CPS, DI])
        st = sb("stats", [P, 6, CPS, 1])
        yn = sb("gated", [P, 2, CPS, DI])
        yt = sb("turned", [P, 2, 2, NT])
        py = ps("turned", [P, 2, 2, NT])
        po = ps("proj", [P, 2, NT])
        c, normed, turned, copied, ready, done = (sem(n) for n in (
            "chain", "normed", "turned", "copied", "ready", "done"))
        with nc.Block() as block:
            @block.vector
            def _(dve):
                n = [0]

                def step(a):
                    a.then_inc(c, 1)
                    n[0] += 1
                    dve.wait_ge(c, n[0])

                wide = lambda t: t.to_broadcast((P, CPS, DI))

                def normalize(b):
                    y = xbc[:, 0:2, b, 0:S].rearrange("p m (c t) -> p c m t", t=P)
                    if b >= 2:
                        dve.wait_ge(turned, 2 * (b - 1))
                    g = yn[:, b % 2, :, :]
                    g4 = g.rearrange("p c (m t) -> p c m t", m=2)
                    step(nc.vector.tensor_reduce(st[:, 0, :, 0], y, AX.XY, ALU.add))
                    step(nc.vector.tensor_scalar(st[:, 1, :, :], st[:, 0, :, :], 1.0 / DI, None, ALU.mult))
                    step(nc.vector.tensor_tensor(g4, y, st[:, 1, :, :].unsqueeze(2).to_broadcast((P, CPS, 2, P)), ALU.subtract))
                    step(nc.vector.tensor_tensor(sq[:, :, :], g, g, ALU.mult))
                    step(nc.vector.tensor_reduce(st[:, 2, :, 0], sq[:, :, :], AX.X, ALU.add))
                    dve.wait_ge(c, n[0] + 2)
                    n[0] += 2
                    step(nc.vector.tensor_tensor(g, g, wide(st[:, 4, :, :]), ALU.mult))
                    step(nc.vector.tensor_tensor(g, g, zs[:, b * CPS:(b + 1) * CPS, :], ALU.mult))
                    dve.sem_inc(normed, 1)

                def add(t):
                    dve.wait_ge(ready, t + 1)
                    nc.vector.tensor_tensor(x[:, t * NT:(t + 1) * NT], po[:, t % 2, :], x[:, t * NT:(t + 1) * NT],
                                            ALU.add).then_inc(done, 1)

                normalize(0)
                for b in range(B):
                    if b + 1 < B:
                        normalize(b + 1)
                    add(2 * b)
                    add(2 * b + 1)

            @block.scalar
            def _(act):
                nc.scalar.preload_act_table_set("natural_log_exp_and_others")
                def root(b):
                    act.wait_ge(c, 9 * b + 5)
                    nc.scalar.activation(st[:, 3, :, :], st[:, 2, :, :], ACT.Ln, bias=net.ln_eps,
                                         scale=1.0 / DI).then_inc(c, 1)
                    act.wait_ge(c, 9 * b + 6)
                    nc.scalar.activation(st[:, 4, :, :], st[:, 3, :, :], ACT.Exp, scale=-0.5).then_inc(c, 1)

                def copy(t):
                    act.wait_ge(turned, t + 1)
                    if t >= 2:
                        act.wait_ge(ready, t - 1)
                    nc.scalar.activation(yt[:, t % 2, :, :], py[:, t % 2, :, :], ACT.Copy).then_inc(copied, 1)

                root(0)
                for b in range(B):
                    if b + 1 < B:
                        root(b + 1)
                    copy(2 * b)
                    copy(2 * b + 1)

            @block.tensor
            def _(pe):
                for t in range(TILES):
                    b = t // 2
                    pe.wait_ge(normed, b + 1)
                    if t >= 2:
                        pe.wait_ge(copied, t - 1)
                    for m in range(2):
                        for k in range(4):
                            mm = nc.tensor.transpose(py[:, t % 2, m, k * P:(k + 1) * P],
                                                     yn[:, b % 2, 4 * (t % 2) + k, m * P:(m + 1) * P], net.ident[:, :])
                    mm.then_inc(turned, 1)
                    pe.wait_ge(copied, t + 1)
                    if t >= 2:
                        pe.wait_ge(done, t - 1)
                    for m in range(2):
                        mm = nc.tensor.matmul(po[:, t % 2, :], w_out[:, m, :], yt[:, t % 2, m, :],
                                              start=(m == 0), stop=(m == 1))
                    mm.then_inc(ready, 1)


def build(nc, dram, out):
    with ExitStack() as ctx:
        net = Net(nc, ctx, dram)
        load_consts(net)
        for l in LAYERS:
            if l in (1, 3):
                ternary_ffn(net, f"l{l}", "f0_up", "f0_dn", True, 0.0)
            if l in (9, 11):
                ternary_ffn(net, f"l{l}", "f2_up", "f2_dn", False, 1e-8, "f2_b1", "f2_b2")
            if l == 2:
                attention(net, "l2", dict(wq="a0_wq", wk="a0_wk", wv="a0_wv", wo="a0_wo"), 8, 8 ** -0.5, decay=True)
            if l in (4, 6):
                n = "a1" if l == 4 else "b1"
                attention(net, f"l{l}", {m: f"{n}_{m}" for m in ("wq", "wk", "wq_sw", "wk_sw", "wv", "wo", "bq", "bk",
                                                                 "bq_sw", "bk_sw", "bv", "bo")},
                          8, 8 ** -0.5, rope=True, bias=True, out_bias=True)
            if l == 8:
                attention(net, "l8", {m: f"a2_{m}" for m in ("wq", "wk", "wv", "wo", "bq", "bk", "bv", "bo")},
                          8, 8 ** -0.5, bias=True, out_bias=True)
            if l in (5, 7):
                experts_ffn(net, f"l{l}", dict(router="m1_router", fc="m1_fc", proj="m1_proj"))
            if l in (13, 15):
                gated_ffn(net, f"l{l}")
            if l == 10:
                ssd(net, "l10")
            if l == 0:
                selective_ssm(net, "l0", "s0_", 2, 4, 3, True, True, True, True)
            if l == 12:
                selective_ssm(net, "l12", "s3_", 1, 3, 1, False, False, False, False)
            if l == 14:
                attention(net, "l14", {m: f"b3_{m}" for m in ("wq", "wk", "wv", "wo", "bo")}, 4, 0.5,
                          alibi=True, out_bias=True)
        store_out(net, out)


def thirds(a):
    bf = mybir.dt.np(BF16)
    hi = a.astype(bf)
    mid = (a - hi.astype(np.float32)).astype(bf)
    low = (a - hi.astype(np.float32) - mid.astype(np.float32)).astype(bf)
    return np.stack([hi, mid, low])


def shape_constants():
    bf = mybir.dt.np(BF16)
    f = np.float32
    pos = np.arange(S, dtype=f)
    d = np.arange(P) % 8
    freq = (1.0 / 10000.0 ** ((d // 2 * 2).astype(f) / 8)).astype(f)
    theta = pos[None] * freq[:, None]
    sign = np.where(d % 2 == 0, -1.0, 1.0).astype(f)[:, None]
    rope = np.stack([np.cos(theta), np.sin(theta) * sign], 1).astype(f)
    i = np.arange(P)
    mask_q = np.where(i[:, None] < i[None], NEG, 0.0).astype(bf)
    nums = np.linspace(0.0, 1.0, 241).astype(f)
    vals = np.concatenate([np.ones(15, f), 1.0 - nums ** f(1.0 / np.e)]).astype(f)
    dist = np.clip(np.arange(DECAY_SPAN)[None] - i[:, None], 0, 255)
    slopes = (2.0 ** (-8.0 * np.arange(1, HEADS + 1) / HEADS)).astype(f)
    sl = np.broadcast_to(thirds(slopes)[:, :, None], (3, HEADS, S))
    nq = thirds(-(slopes[:, None] * pos[None]))
    aq = np.concatenate([sl, sl, nq]).reshape(9, 4, 4, S).transpose(1, 0, 2, 3)
    hi, lo = np.floor(pos / 8) * 8, pos % 8
    ak = np.broadcast_to(np.stack([hi] * 3 + [lo] * 3 + [np.ones(S, f)] * 3)[:, None], (9, 4, S)).astype(bf)
    sel = np.broadcast_to(np.eye(P, EXPERTS, dtype=f)[:, :, None], (P, EXPERTS, P)).astype(bf)
    spread = np.zeros((P, 32, P), bf)
    for part in range(3):
        for n in range(32):
            spread[32 * part + n, n] = 1.0
    ones9 = np.zeros((P, 9), f)
    ones9[:, 8] = 1.0
    return {
        "ident": np.eye(P, dtype=f), "rope": rope, "mask_q": mask_q, "mask_k": mask_q.T,
        "decay": vals[dist], "ones9": ones9, "ones_rows": np.ones((3, 4, S), bf),
        "alibi_q": np.tile(aq, (4, 1, 1, 1)).reshape(GROUPS * 9, 4, S), "alibi_k": ak, "expert_select": sel, "bc_spread": spread, "neg_pick": -spread[0:96],
        "triangle": (i[:, None] <= i[None]).astype(f), "last_row": np.broadcast_to((i == P - 1)[:, None], (P, P)).astype(f),
    }


def attention_layouts(i):
    row, one = (lambda v: v.reshape(1, -1)), (lambda v: v.reshape(-1, 1))
    swap = np.arange(P) ^ 1
    out = {}
    w = i["L0_attn_b_W_attn"]
    out.update(a0_wq=w[:, :P], a0_wk=w[:, P:2 * P], a0_wv=w[:, 2 * P:], a0_wo=i["L0_attn_b_W_proj"])
    for n, wn, f in (("a1", "L1_attn_a_w", lambda m: m.T), ("b1", "L1_attn_b_W", lambda m: m)):
        q, k, bq, bk = f(i[wn + "q"]), f(i[wn + "k"]), i[wn[:-1] + "bq"], i[wn[:-1] + "bk"]
        out.update({f"{n}_wq": q, f"{n}_wk": k, f"{n}_wv": f(i[wn + "v"]), f"{n}_wo": f(i[wn + "o"]),
                    f"{n}_wq_sw": q[:, swap], f"{n}_wk_sw": k[:, swap], f"{n}_bq": one(bq), f"{n}_bk": one(bk),
                    f"{n}_bq_sw": one(bq[swap]), f"{n}_bk_sw": one(bk[swap]),
                    f"{n}_bv": row(i[wn[:-1] + "bv"]), f"{n}_bo": one(i[wn[:-1] + "bo"])})
    w = i["L2_attn_a_attn_W"].reshape(D, HEADS, 3, 8)
    b = i["L2_attn_a_attn_b"].reshape(HEADS, 3, 8)
    for j, n in enumerate("qkv"):
        out[f"a2_w{n}"] = w[:, :, j].reshape(D, P)
        out[f"a2_b{n}"] = (row if n == "v" else one)(b[:, j].reshape(P))
    out.update(a2_wo=i["L2_attn_a_out_W"], a2_bo=one(i["L2_attn_a_out_b"]))
    out.update(b3_wq=np.tile(i["L3_attn_b_Wq"], (1, 2)), b3_wk=np.tile(i["L3_attn_b_Wk"], (1, 8)),
               b3_wv=np.tile(i["L3_attn_b_Wv"], (1, 4)), b3_wo=i["L3_attn_b_Wp"], b3_bo=one(i["L3_attn_b_bp"]))
    return out


def ffn_layouts(i):
    col = lambda v: v.reshape(-1, P).T
    kcn = lambda w: w.reshape(HC, P, -1).transpose(1, 0, 2)
    g = lambda n: i["L3_ffn_" + n]
    return {
        "m1_router": i["L1_ffn_router_w"].T,
        "m1_fc": i["L1_ffn_expert_fc"].transpose(1, 0, 2),
        "m1_proj": i["L1_ffn_expert_proj"].transpose(2, 0, 1).reshape(HC, P, EXPERTS, P).transpose(1, 2, 0, 3),
        "g3_w1": g("w1_w").T, "g3_w2": g("w2_w").T, "g3_h1": kcn(g("h1_w").T), "g3_h2": kcn(g("h2_w").T),
        "g3_w3": kcn(g("w3_w").T),
        "g3_scales": np.concatenate([col(g(n)) for n in ("w1_s", "w2_s", "h1_s", "h2_s", "w3_s")], 1),
    }


def ssm_layouts(i):
    f = np.float32
    hcol = lambda v: v.reshape(-1, P).T

    def cols(H, taps, **c):
        out = np.zeros((P, 64), f)
        for at, n in ((0, "bin"), (4, "cvb"), (6, "dtb"), (8, "dbb"), (9, "rms"), (10, "bout")):
            if n in c:
                v = np.zeros(-(-c[n].size // P) * P, f)
                v[:c[n].size] = c[n]
                v = hcol(v)
                out[:, at:at + v.shape[1]] = v
        out[:, 16:16 + H * taps] = c["cvw"].reshape(H, P, taps).transpose(1, 0, 2).reshape(P, H * taps)
        return out

    def chunks(m, H):
        return m.reshape(H, P, -1).transpose(1, 0, 2)

    def triple(bc, extra=None):
        z = np.zeros(bc.shape[:-1] + (32,), f)
        if extra is not None:
            z[..., :extra.shape[-1]] = extra
        return np.concatenate([bc, bc, bc, z], -1)

    g = lambda n: i["L0_attn_a_" + n]
    W, b = g("dbc_W"), g("dbc_b")
    dup = np.zeros((P, 2, P), f)
    dup[96:112] = g("dup_W").reshape(16, 2, P)
    out = {
        "s0_win": g("in_W"), "s0_a": g("A_log").reshape(2, P, NS).transpose(1, 0, 2),
        "s0_cols": cols(2, 4, bin=g("in_b"), cvb=g("conv_b"), dtb=g("dup_b"), dbb=triple(b[16:], b[:16]),
                        rms=g("rms_w"), bout=g("out_b"), cvw=g("conv_w")),
        "s0_dbc": chunks(triple(W[:, 16:], W[:, :16]), 2), "s0_dt": dup, "s0_out": chunks(g("out_W"), 2),
    }
    g = lambda n: i["L3_attn_a_" + n]
    out.update({
        "s3_win": np.concatenate([g("Win"), g("Wg")], 1), "s3_a": g("A")[:, None],
        "s3_cols": cols(1, 3, bin=np.concatenate([g("b_in"), g("bg")]), cvb=g("convb"), dtb=g("bdt"),
                        dbb=triple(np.concatenate([g("bb"), g("bc")])), bout=g("bout"), cvw=g("convw")),
        "s3_dbc": triple(np.concatenate([g("Wb"), g("Wc")], 1))[:, None], "s3_dt": g("Wdt")[:, None],
        "s3_out": g("Wout")[:, None],
    })
    return out


def ssd_layouts(i):
    g = lambda n: i["L2_attn_b_" + n]
    w = g("in_proj_w").T
    conv = np.concatenate([g("conv_w"), g("conv_b")[:, None]], 1).reshape(4, P, 5).transpose(1, 0, 2)
    return {
        "d2_w": w[:, 256:768], "d2_wz": np.concatenate([w[:, :256], w[:, 768:]], 1), "d2_conv": conv,
        "d2_out": g("out_proj_w").T.reshape(2, P, D).transpose(1, 0, 2), "d2_dtb": g("dt_bias").reshape(1, -1),
        "d2_lnw": g("ln_w").reshape(1, -1), "d2_alog": g("A_log").reshape(1, -1),
    }


def layouts(i):
    col = lambda v: np.ascontiguousarray(v.reshape(-1, P).T)
    return {
        "x": i["L0_attn_a_x"].reshape(T, D).T,
        **shape_constants(), **attention_layouts(i), **ffn_layouts(i), **ssm_layouts(i), **ssd_layouts(i),
        "f0_up": i["L0_ffn_w_up"].T,
        "f0_dn": i["L0_ffn_w_down"].T,
        "f2_up": i["L2_ffn_W1"].T,
        "f2_dn": i["L2_ffn_W2"].T,
        "f2_b1": col(i["L2_ffn_b1"]),
        "f2_b2": col(i["L2_ffn_b2"]),
    }


def kernel(**inputs):
    import concourse.bacc as bacc
    from concourse.bass_utils import run_bass_kernel_spmd

    nc = bacc.Bacc("TRN2", target_bir_lowering=False, num_devices=1)
    arrays = {n: np.ascontiguousarray(a) for n, a in layouts({k: np.asarray(v) for k, v in inputs.items()}).items()}
    dram = {n: nc.dram_tensor(n + "_dram", a.shape, mybir.dt.from_np(a.dtype), kind="ExternalInput").ap()
            for n, a in arrays.items()}
    out = nc.dram_tensor("out_dram", (P, T), F32, kind="ExternalOutput").ap()
    build(nc, dram, out)
    r = run_bass_kernel_spmd(nc, [{n + "_dram": a for n, a in arrays.items()}], core_ids=[0])
    return np.ascontiguousarray(r.results[0]["out_dram"].T).reshape(B, S, D)
```

```python
from contextlib import ExitStack, contextmanager

import numpy as np
import concourse.bass as bass
from concourse import mybir

ALU = mybir.AluOpType
ACT = mybir.ActivationFunctionType
AX = mybir.AxisListType
F32 = mybir.dt.float32
BF16 = mybir.dt.bfloat16
ds = bass.ds

LAYERS = list(range(16))
P = 128
B, S, D = 4, 1024, 128
T = B * S
NT = 512
TILES = T // NT
LN_EPS = 1e-5
RMS_EPS = 1e-6
RMS_FLOOR = 1e-8
NEG = -1e30


@contextmanager
def stage(nc, tag):
    with ExitStack() as ctx:
        sems = []

        def sb(name, shape, dt=F32):
            return ctx.enter_context(nc.sbuf_tensor(f"{tag}_{name}", shape, dt))

        def ps(name, shape):
            return ctx.enter_context(nc.psum_tensor(f"{tag}_ps_{name}", shape, F32))

        def sem(name):
            s = nc.alloc_semaphore(f"{tag}_{name}")
            sems.append(s)
            return s

        yield sb, ps, sem
        nc.clear_and_free_semaphores(sems)
        nc.all_engine_barrier()


class Net:

    def __init__(self, nc, ctx, dram):
        self.nc, self.dram = nc, dram
        sb = lambda n, s, d=F32: ctx.enter_context(nc.sbuf_tensor(n, s, d))
        self.x = sb("x_res", [P, T])
        self.xn = sb("x_norm", [P, T])
        self.ident = sb("ident", [P, P])
        self.center = sb("center", [P, P])
        self.ones = sb("ones_over_1", [P, P])
        self.mean = sb("ones_over_d", [P, P])
        self.identb = sb("ident_bf16", [P, P], BF16)
        self.cols = sb("const_cols", [P, 8])
        self.ln_eps = self.cols[:, 0:1]
        self.rms_eps = self.cols[:, 1:2]
        self.one = self.cols[:, 2:3]
        self.zero = self.cols[:, 3:4]
        self.rms_floor = self.cols[:, 4:5]


def load_consts(net):
    nc = net.nc
    with stage(nc, "init") as (sb, ps, sem):
        loaded, made = sem("loaded"), sem("made")
        with nc.Block() as block:
            @block.sync
            def _(sp):
                sp.dma_start(net.x[:, :], net.dram["x"]).then_inc(loaded, 16)
                sp.dma_start(net.ident[:, :], net.dram["ident"]).then_inc(loaded, 16)
                sp.wait_ge(loaded, 32)

            @block.vector
            def _(dve):
                for j, v in enumerate((LN_EPS, RMS_EPS, 1.0, 0.0, RMS_FLOOR)):
                    nc.vector.memset(net.cols[:, j:j + 1], v)
                nc.vector.memset(net.ones[:, :], 1.0)
                nc.vector.memset(net.mean[:, :], 1.0 / D)
                dve.wait_ge(loaded, 32)
                nc.vector.tensor_scalar(net.center[:, :], net.ident[:, :], -1.0 / D, None, ALU.add)
                nc.vector.tensor_copy(net.identb[:, :], net.ident[:, :])


def store_out(net, out):
    nc = net.nc
    with stage(nc, "fin") as (sb, ps, sem):
        stored = sem("stored")
        with nc.Block() as block:
            @block.sync
            def _(sp):
                sp.dma_start(out, net.x[:, :]).then_inc(stored, 16)
                sp.wait_ge(stored, 16)


def layer_norm(net, tag, rms=None):
    nc = net.nc
    x, xn = net.x, net.xn
    with stage(nc, tag) as (sb, ps, sem):
        cen = ps("centered", [P, 2, NT])
        var = ps("var", [P, 2, NT])
        sq = sb("squares", [P, 2, NT])
        lnv = sb("log_var", [P, 2, NT])
        rstd = sb("rstd", [P, 2, NT])
        ms = sb("mean_square", [P, 2, NT]) if rms else None
        lms = sb("log_ms", [P, 2, NT]) if rms else None
        root = sb("root", [P, 2, NT]) if rms else None
        cen_free = sem("centered_free")
        cen_ready, sq_ready, var_ready = sem("centered"), sem("squares"), sem("var")
        ln_ready, rstd_ready = sem("log_var"), sem("rstd")
        ms_ready, lms_ready, rt_ready, f_ready = sem("ms"), sem("lms"), sem("root"), sem("factor")
        f2_ready = sem("log_root")
        with nc.Block() as block:
            @block.tensor
            def _(pe):
                with pe.Fori(0, TILES // 2) as i:
                    for p in range(2):
                        pe.wait_ge(cen_free, 2 * i + p + 1)
                        nc.tensor.matmul(cen[:, p, :], net.center[:, :], x[:, ds((2 * i + p) * NT, NT)],
                                         start=True, stop=True).then_inc(cen_ready, 1)
                    for p in range(2):
                        pe.wait_ge(sq_ready, 2 * i + p + 1)
                        nc.tensor.matmul(var[:, p, :], net.mean[:, :], sq[:, p, :],
                                         start=True, stop=True).then_inc(var_ready, 1)

            @block.scalar
            def _(act):
                nc.scalar.preload_act_table_set("natural_log_exp_and_others")
                with act.Fori(0, TILES // 2) as i:
                    for p in range(2):
                        act.wait_ge(cen_ready, 2 * i + p + 1)
                        nc.scalar.activation(sq[:, p, :], cen[:, p, :], ACT.Square).then_inc(sq_ready, 1)
                    for p in range(2):
                        act.wait_ge(var_ready, 2 * i + p + 1)
                        nc.scalar.activation(lnv[:, p, :], var[:, p, :], ACT.Ln,
                                             bias=net.ln_eps).then_inc(ln_ready, 1)
                        act.wait_ge(ln_ready, 2 * i + p + 1)
                        nc.scalar.activation(rstd[:, p, :], lnv[:, p, :], ACT.Exp,
                                             scale=-0.5).then_inc(rstd_ready, 1)
                        if rms:
                            act.wait_ge(ms_ready, 2 * i + p + 1)
                            nc.scalar.activation(lms[:, p, :], ms[:, p, :], ACT.Ln).then_inc(lms_ready, 1)
                            act.wait_ge(lms_ready, 2 * i + p + 1)
                            fac = rms[2][:, ds((2 * i + p) * NT, NT)]
                            if rms[0] == "div":
                                nc.scalar.activation(root[:, p, :], lms[:, p, :], ACT.Exp, scale=0.5).then_inc(rt_ready, 1)
                                act.wait_ge(rt_ready, 2 * i + p + 1)
                                nc.scalar.activation(root[:, p, :], root[:, p, :], ACT.Ln,
                                                     bias=net.rms_floor).then_inc(f2_ready, 1)
                                act.wait_ge(f2_ready, 2 * i + p + 1)
                                nc.scalar.activation(fac, root[:, p, :], ACT.Exp, scale=-1.0)
                            else:
                                nc.scalar.activation(fac, lms[:, p, :], ACT.Exp, scale=-0.5)

            @block.vector
            def _(dve):
                dve.sem_inc(cen_free, 2)
                with dve.Fori(0, TILES // 2) as i:
                    for p in range(2):
                        tok = ds((2 * i + p) * NT, NT)
                        dve.wait_ge(rstd_ready, 2 * i + p + 1)
                        last = nc.vector.tensor_tensor(xn[:, tok], cen[:, p, :], rstd[:, p, :], ALU.mult)
                        if rms:
                            last.then_inc(f_ready, 1)
                            nc.vector.tensor_tensor(ms[:, p, :], var[:, p, :], rstd[:, p, :],
                                                    ALU.mult).then_inc(f_ready, 1)
                            dve.wait_ge(f_ready, 4 * i + 2 * p + 2)
                            nc.vector.tensor_tensor(ms[:, p, :], ms[:, p, :], rstd[:, p, :],
                                                    ALU.mult).then_inc(cen_free, 1)
                            dve.wait_ge(cen_free, 2 * i + p + 3)
                            nc.vector.tensor_scalar(ms[:, p, :], ms[:, p, :],
                                                    1e-19 if rms[0] == "div" else rms[1], None,
                                                    ALU.max if rms[0] == "div" else ALU.add
                                                    ).then_inc(ms_ready, 1)
                        else:
                            last.then_inc(cen_free, 1)


def ternary_ffn(net, tag, wup, wdn, rms_in, floor, b1=None, b2=None):
    nc, x, xn = net.nc, net.x, net.xn
    FC = 4
    NW = P * FC * P
    with stage(nc, tag) as (sb, ps, sem):
        if rms_in:
            fac = sb("rms_factor", [P, T])
            layer_norm(net, tag + "_ln", ("div", RMS_FLOOR, fac))
        else:
            layer_norm(net, tag + "_ln")
        w = [sb("w_up", [P, FC * P]), sb("w_down", [P, FC * P])]
        wt = [sb("q_up", [P, FC * P]), sb("q_down", [P, FC * P])]
        neg = sb("below", [P, FC * P])
        absum = sb("abs_sum", [P, 2])
        thr = sb("threshold", [P, 4])
        bias = sb("biases", [P, 8])
        g = sb("hidden", [P, 2, FC, NT])
        gsq = sb("hidden_sq", [P, FC, NT])
        ssum = sb("sum_sq", [P, NT])
        y = sb("down", [P, T])
        msq = sb("mean_sq", [P, T]) if rms_in else None
        pw = ps("weight_sum", [P, NT])
        ph = ps("up", [P, 2, 2, NT])
        py = ps("down_acc", [P, 2, NT])
        pm = ps("ms_acc", [P, NT])
        w_in, abs_ready, wsum_ready, w_ready, chain = (sem(n) for n in (
            "weights_in", "abs_ready", "wsum_ready", "w_ready", "chain"))
        x_ready, up_ready, gelu_done, g_free = (sem(n) for n in (
            "x_ready", "up_ready", "gelu_done", "g_free"))
        ss_ready, dn_ready, dn_free, tail_a, tail_b = (sem(n) for n in (
            "ss_ready", "dn_ready", "dn_free", "tail_act", "tail_dve"))
        with nc.Block() as block:
            @block.sync
            def _(sp):
                sp.dma_start(w[0][:, :], net.dram[wup]).then_inc(w_in, 16)
                sp.dma_start(w[1][:, :].rearrange("p (k d) -> p k d", k=FC),
                             net.dram[wdn].rearrange("(k p) d -> p k d", p=P)).then_inc(w_in, 16)
                if b1:
                    sp.dma_start(bias[:, 0:4], net.dram[b1]).then_inc(w_in, 16)
                    sp.dma_start(bias[:, 4:5], net.dram[b2]).then_inc(w_in, 16)

            def down(pe, i, p):
                pe.wait_ge(gelu_done, 4 * i + 2 * p + 4)
                pe.wait_ge(dn_free, 2 * i + p + 1)
                for k in range(FC):
                    mm = nc.tensor.matmul(py[:, p, :], wt[1][:, k * P:(k + 1) * P], g[:, p, k, :],
                                          start=(k == 0), stop=(k == FC - 1))
                mm.then_inc(dn_ready, 1)
                if rms_in:
                    pe.wait_ge(ss_ready, 2 * i + p + 1)
                    nc.tensor.matmul(pm[:, :], net.ones[:, :], ssum[:, :], start=True, stop=True).then_inc(dn_ready, 1)

            @block.tensor
            def _(pe):
                pe.wait_ge(abs_ready, 1)
                nc.tensor.matmul(pw[:, 0:2], net.ones[:, :], absum[:, :], start=True, stop=True).then_inc(wsum_ready, 1)
                pe.wait_ge(w_ready, 1)
                with pe.Fori(0, TILES // 2) as i:
                    for p in range(2):
                        if rms_in:
                            pe.wait_ge(x_ready, 2 * i + p + 1)
                        for half in range(2):
                            pe.wait_ge(gelu_done, 4 * i + 2 * p + half + 1)
                            for c in range(2):
                                k = 2 * half + c
                                mm = nc.tensor.matmul(ph[:, half, c, :], wt[0][:, k * P:(k + 1) * P],
                                                      xn[:, ds((2 * i + p) * NT, NT)], start=True, stop=True)
                            mm.then_inc(up_ready, 1)
                        if p == 1:
                            down(pe, i, 0)
                    down(pe, i, 1)

            @block.scalar
            def _(act):
                act.sem_inc(gelu_done, 2)
                with act.Fori(0, TILES // 2) as i:
                    for p in range(2):
                        act.wait_ge(g_free, 2 * i + p + 1)
                        for half in range(2):
                            act.wait_ge(up_ready, 4 * i + 2 * p + half + 1)
                            if b1:
                                for c in range(2):
                                    k = 2 * half + c
                                    a = nc.scalar.activation(g[:, p, k, :], ph[:, half, c, :],
                                                             ACT.Gelu, bias=bias[:, k:k + 1])
                            else:
                                a = nc.scalar.activation(g[:, p, 2 * half:2 * half + 2, :], ph[:, half, :, :], ACT.Gelu)
                            a.then_inc(gelu_done, 1)
                if rms_in:
                    nc.scalar.preload_act_table_set("natural_log_exp_and_others")
                    steps = ((ACT.Ln, {}), (ACT.Exp, dict(scale=0.5)), (ACT.Ln, dict(bias=net.rms_floor)),
                             (ACT.Exp, dict(scale=-1.0)))
                    for k, (func, more) in enumerate(steps):
                        for q in range(4):
                            if k == 0:
                                act.wait_ge(x_ready, TILES + 4 * (q + 1))
                            else:
                                act.wait_ge(tail_a, 4 * (k - 1) + q + 1)
                            part = msq[:, q * 2 * NT:(q + 1) * 2 * NT]
                            nc.scalar.activation(part, part, func, **more).then_inc(tail_a, 1)

            @block.vector
            def _(dve):
                dve.wait_ge(w_in, 64 if b1 else 32)
                for m in range(2):
                    last = nc.vector.tensor_reduce(absum[:, m:m + 1], w[m][:, :], AX.X, ALU.add,
                                                   apply_absolute_value=True)
                last.then_inc(abs_ready, 1)
                dve.wait_ge(wsum_ready, 1)
                nc.vector.tensor_scalar(thr[:, 0:2], pw[:, 0:2], 1.0 / NW, floor, ALU.mult, ALU.max).then_inc(chain, 1)
                dve.wait_ge(chain, 1)
                nc.vector.tensor_scalar(thr[:, 2:4], thr[:, 0:2], -0.5, None, ALU.mult).then_inc(chain, 1)
                dve.wait_ge(chain, 2)
                nc.vector.tensor_scalar(thr[:, 0:2], thr[:, 0:2], 0.5, None, ALU.mult).then_inc(chain, 1)
                dve.wait_ge(chain, 3)
                n = 3
                for m in range(2):
                    nc.vector.tensor_scalar(neg[:, :], w[m][:, :], thr[:, 2 + m:3 + m], None, ALU.is_lt).then_inc(chain, 1)
                    n += 1
                    dve.wait_ge(chain, n)
                    nc.vector.scalar_tensor_tensor(wt[m][:, :], w[m][:, :], thr[:, m:m + 1], neg[:, :],
                                                   ALU.is_gt, ALU.subtract).then_inc(chain, 1)
                    n += 1
                    dve.wait_ge(chain, n)
                    nc.vector.tensor_tensor(wt[m][:, :], wt[m][:, :], w[m][:, :], ALU.subtract).then_inc(chain, 1)
                    n += 1
                    dve.wait_ge(chain, n)
                    nc.vector.tensor_tensor(wt[m][:, :], w[m][:, :], wt[m][:, :], ALU.add).then_inc(chain, 1)
                    n += 1
                    dve.wait_ge(chain, n)
                dve.sem_inc(w_ready, 1)
                dve.sem_inc(g_free, 2)
                dve.sem_inc(dn_free, 2)
                if rms_in:
                    with dve.Fori(0, TILES) as i:
                        tok = ds(i * NT, NT)
                        nc.vector.tensor_tensor(xn[:, tok], xn[:, tok], fac[:, tok], ALU.mult).then_inc(x_ready, 1)
                with dve.Fori(0, TILES // 2) as i:
                    for p in range(2):
                        tok = ds((2 * i + p) * NT, NT)
                        if rms_in:
                            dve.wait_ge(gelu_done, 4 * i + 2 * p + 4)
                            c0 = n + (2 * i + p) * 3
                            nc.vector.tensor_tensor(gsq[:, :, :], g[:, p, :, :], g[:, p, :, :], ALU.mult).then_inc(chain, 1)
                            dve.wait_ge(chain, c0 + 1)
                            nc.vector.tensor_tensor(gsq[:, 0:2, :], gsq[:, 0:2, :], gsq[:, 2:4, :], ALU.add).then_inc(chain, 1)
                            dve.wait_ge(chain, c0 + 2)
                            nc.vector.tensor_tensor(ssum[:, :], gsq[:, 0, :], gsq[:, 1, :], ALU.add).then_inc(chain, 1)
                            dve.wait_ge(chain, c0 + 3)
                            dve.sem_inc(ss_ready, 1)
                            dve.wait_ge(dn_ready, 2 * (2 * i + p) + 2)
                            nc.vector.tensor_copy(y[:, tok], py[:, p, :]).then_inc(x_ready, 1)
                            nc.vector.tensor_scalar(msq[:, tok], pm[:, :], 1.0 / (FC * P), 1e-19,
                                                    ALU.mult, ALU.max).then_inc(x_ready, 1)
                            dve.wait_ge(x_ready, TILES + (2 * i + p) * 2 + 2)
                        else:
                            dve.wait_ge(dn_ready, 2 * i + p + 1)
                            nc.vector.scalar_tensor_tensor(x[:, tok], py[:, p, :], bias[:, 4:5], x[:, tok],
                                                           ALU.add, ALU.add).then_inc(x_ready, 1)
                            dve.wait_ge(x_ready, 2 * i + p + 1)
                        dve.sem_inc(g_free, 1)
                        dve.sem_inc(dn_free, 1)
                if rms_in:
                    for q in range(4):
                        part = slice(q * 2 * NT, (q + 1) * 2 * NT)
                        dve.wait_ge(tail_a, 12 + q + 1)
                        nc.vector.tensor_tensor(y[:, part], y[:, part], msq[:, part], ALU.mult).then_inc(tail_b, 1)
                    for q in range(4):
                        part = slice(q * 2 * NT, (q + 1) * 2 * NT)
                        dve.wait_ge(tail_b, q + 1)
                        nc.vector.tensor_tensor(x[:, part], x[:, part], y[:, part], ALU.add)


HEADS = 16
GROUPS = B * HEADS // 4
KT = S // P
PAIRS = ((0, 0), (0, 1), (0, 2), (1, 0), (1, 1), (2, 0))
AHEAD = 24
TURN_COST = 1200
DECAY_SPAN = 384


def attention(net, tag, w, dq, scale, rope=False, alibi=False, decay=False, bias=False, out_bias=False):
    nc, x, xn, dram = net.nc, net.x, net.xn, net.dram
    R = HEADS * dq
    GR = 4 * dq
    r0 = 6 * dq + (9 if alibi else 0)
    layer_norm(net, tag + "_ln")
    parts = {n: nc.dram_tensor(f"{tag}_{n}_rows", (B * HEADS * 6 * dq, S), BF16, kind="Internal").ap() for n in "qk"}
    heads_out = nc.dram_tensor(f"{tag}_heads_out", (B * P, S), F32, kind="Internal").ap()
    sums = nc.dram_tensor(f"{tag}_sums", (4 * GROUPS, S), F32, kind="Internal").ap()
    rsums = nc.dram_tensor(f"{tag}_rsums", (4 * GROUPS, S), F32, kind="Internal").ap()
    with ExitStack() as ctx:
        v = ctx.enter_context(nc.sbuf_tensor(f"{tag}_v", [P, GROUPS, KT, 4, 9], F32))
        attn_project(net, tag, w, dq, rope, bias, decay, parts, v)
        attn_core(net, tag, w, dq, r0, scale, alibi, decay, parts, v, heads_out, sums)
    attn_output(net, tag, w, out_bias, heads_out, sums, rsums)


def attn_project(net, tag, w, dq, rope, bias, decay, parts, v):
    nc, xn, dram = net.nc, net.xn, net.dram
    R = HEADS * dq
    with stage(nc, tag + "_proj") as (sb, ps, sem):
        ws = [sb(f"w{n}", [P, P]) for n in range(4 if rope else 2)]
        wv = sb("wv", [P, P])
        bcol = sb("bias_cols", [P, 4])
        bv = sb("bias_v", [P, P])
        tab = sb("cos_sin", [P, 2, S]) if rope else None
        t1, t2 = sb("t1", [P, 2, NT]), sb("t2", [P, 2, NT])
        part = sb("parts", [P, 2, 3, T], BF16)
        pq = ps("qk", [P, 4, NT])
        pv = ps("v", [P, 2, NT])
        w_in, mm_ready, mm_free, v_ready, v_free = (sem(n) for n in ("w_in", "mm", "mm_free", "v_mm", "v_free"))
        val, hi, rest, mid, low, made, stored, t_free = (sem(n) for n in (
            "value", "hi", "rest", "mid", "low", "made", "stored", "t_free"))
        n_in = [0]
        NW = len(ws)
        with nc.Block() as block:
            @block.sync
            def _(sp):
                for j, n in enumerate(("wq", "wk", "wq_sw", "wk_sw")[:NW]):
                    sp.dma_start(ws[j][:, :], dram[w[n]]).then_inc(w_in, 16)
                    n_in[0] += 16
                    if bias:
                        sp.dma_start(bcol[0:R, j:j + 1], dram[w["b" + n[1:]]]).then_inc(w_in, 16)
                        n_in[0] += 16
                sp.dma_start(wv[:, :], dram[w["wv"]]).then_inc(w_in, 16)
                n_in[0] += 16
                if bias:
                    sp.dma_start(bv[:, :], dram[w["bv"]].to_broadcast((P, P))).then_inc(w_in, 16)
                    n_in[0] += 16
                if rope:
                    sp.dma_start(tab[:, :, :], dram["rope"]).then_inc(w_in, 16)
                    n_in[0] += 16
                for b in range(B):
                    sp.wait_ge(hi, 4 * (b + 1))
                    sp.wait_ge(mid, 4 * (b + 1))
                    sp.wait_ge(low, 4 * (b + 1))
                    for j, n in enumerate("qk"):
                        for slot in range(6):
                            sp.dma_start(parts[n].rearrange("(b h s d) t -> b s h d t", b=B, s=6, d=dq)[b, slot],
                                         part[0:R, j, PAIRS[slot][j], b * S:(b + 1) * S]).then_inc(stored, 16)
                sp.wait_ge(stored, 16 * 12 * B)

            @block.tensor
            def _(pe):
                pe.wait_ge(w_in, n_in[0])
                with pe.Fori(0, TILES) as i:
                    for j in range(2):
                        pe.wait_ge(mm_free, 2 * i + j + 1)
                        for m in range(j, NW, 2):
                            mm = nc.tensor.matmul(pq[:, m, :], ws[m][:, :], xn[:, ds(i * NT, NT)],
                                                  start=True, stop=True)
                        mm.then_inc(mm_ready, 1)
                for m in range(T // P):
                    if m % 4 == 0 and m >= 8:
                        pe.wait_ge(v_free, m // 4 - 1)
                    mm = nc.tensor.matmul(pv[:, m // 4 % 2, m % 4 * P:(m % 4 + 1) * P],
                                          xn[:, m * P:(m + 1) * P], wv[:, :], start=True, stop=True)
                    if m % 4 == 3:
                        mm.then_inc(v_ready, 1)

            @block.vector
            def _(dve):
                nc.vector.memset(v[:, :, :, :, 8:9], 0.0 if decay else 1.0)
                dve.wait_ge(w_in, n_in[0])
                dve.sem_inc(mm_free, 2)
                with dve.Fori(0, B) as b:
                    for h in range(2):
                        for j in range(2):
                            n = 4 * b + 2 * h + j
                            dve.wait_ge(mm_ready, n + 1)
                            dve.wait_ge(t_free, n + 1)
                            if rope:
                                nc.vector.scalar_tensor_tensor(t1[0:R, j, :], pq[0:R, j, :], bcol[0:R, j:j + 1],
                                                               tab[0:R, 0, h * NT:(h + 1) * NT], ALU.add, ALU.mult)
                                nc.vector.scalar_tensor_tensor(t2[0:R, j, :], pq[0:R, 2 + j, :], bcol[0:R, 2 + j:3 + j],
                                                               tab[0:R, 1, h * NT:(h + 1) * NT], ALU.add, ALU.mult
                                                               ).then_inc(made, 1)
                                dve.wait_ge(made, n + 1)
                                nc.vector.tensor_tensor(t1[0:R, j, :], t1[0:R, j, :], t2[0:R, j, :],
                                                        ALU.add).then_inc(val, 1)
                            elif bias:
                                nc.vector.tensor_scalar(t1[0:R, j, :], pq[0:R, j, :], bcol[0:R, j:j + 1], None,
                                                        ALU.add).then_inc(val, 1)
                            else:
                                nc.vector.tensor_copy(t1[0:R, j, :], pq[0:R, j, :]).then_inc(val, 1)
                            dve.wait_ge(val, n + 1)
                            dve.sem_inc(mm_free, 1)
                for m in range(T // P // 4):
                    dve.wait_ge(v_ready, m + 1)
                    for c in range(4):
                        tile = 4 * m + c
                        dst = v[:, 4 * (tile // KT):4 * (tile // KT) + 4, tile % KT, :, 0:8]
                        src = pv[:, m % 2, c * P:(c + 1) * P].rearrange("p (g h e) -> p g h e", g=4, e=8)
                        if bias:
                            a = nc.vector.tensor_tensor(dst, src, bv[:, :].rearrange("p (g h e) -> p g h e", g=4, e=8),
                                                        ALU.add)
                        else:
                            a = nc.vector.tensor_copy(dst, src)
                    a.then_inc(v_free, 1)

            @block.scalar
            def _(act):
                with act.Fori(0, TILES) as i:
                    for j in range(2):
                        n = 2 * i + j
                        tok = ds(i * NT, NT)
                        act.wait_ge(val, n + 1)
                        nc.scalar.activation(part[0:R, j, 0, tok], t1[0:R, j, :], ACT.Copy).then_inc(hi, 1)
                        act.wait_ge(rest, n + 1)
                        nc.scalar.activation(part[0:R, j, 1, tok], t1[0:R, j, :], ACT.Copy).then_inc(mid, 1)

            @block.gpsimd
            def _(pool):
                pool.sem_inc(t_free, 2)
                with pool.Fori(0, TILES) as i:
                    for j in range(2):
                        n = 2 * i + j
                        tok = ds(i * NT, NT)
                        pool.wait_ge(hi, n + 1)
                        nc.gpsimd.tensor_tensor(t1[0:R, j, :], t1[0:R, j, :], part[0:R, j, 0, tok],
                                                ALU.subtract).then_inc(rest, 1)
                        pool.wait_ge(mid, n + 1)
                        nc.gpsimd.tensor_tensor(part[0:R, j, 2, tok], t1[0:R, j, :], part[0:R, j, 1, tok],
                                                ALU.subtract).then_inc(low, 1)
                        pool.wait_ge(low, n + 1)
                        pool.sem_inc(t_free, 1)


def attn_core(net, tag, w, dq, r0, scale, alibi, decay, parts, v, heads_out, sums):
    nc, dram = net.nc, net.dram
    GR = 4 * dq
    first = [(qt, 0, min(qt + 1, 4) * P) for qt in range(KT)]
    P1 = 4 * 12
    with stage(nc, tag + "_core") as (sb, ps, sem):
        qs = [sb(f"q_rows{u}", [P, 4, S], BF16) for u in range(3)]
        ks = [sb(f"k_rows{u}", [P, 4, S], BF16) for u in range(3)]
        vs = [sb(f"v_group{u}", [P, KT, 4, 9]) for u in range(3)]
        pt = sb("probs", [P, 2, 4, S])
        pw = sb("probs_decayed", [P, 2, 4, DECAY_SPAN]) if decay else None
        dtab = sb("decay", [P, DECAY_SPAN]) if decay else None
        ones9 = sb("ones9", [P, 9]) if decay else None
        maskq = sb("mask_q_rows", [P, P], BF16)
        maskk = sb("mask_k_rows", [P, P], BF16)
        mx = sb("chunk_max", [P, 4, 12])
        nm = sb("neg_max", [P, 4, 8])
        mrest = sb("max_rest", [32, P])
        mpart = sb("max_parts", [32, 3, P], BF16)
        oev = sb("out_sums", [P, S])
        pa = [ps(f"scores_a{n}", [P, NT]) for n in range(2)]
        pb = [ps(f"scores_b{n}", [P, S]) for n in range(2)]
        acc = ps("acc", [P, S])
        c_in, stack_in = sem("consts_in"), [sem(f"stack_in{u}") for u in range(3)]
        a_ready, a_free = sem("scores_a"), sem("scores_a_free")
        b_ready, b_free = sem("scores_b"), sem("exp_done")
        m_chain, nm_ready, mp_ready, m_in = (sem(n) for n in ("max_chain", "neg_max", "max_parts", "max_rows_in"))
        q_cleared, k_cleared = sem("q_cleared"), sem("k_cleared")
        vs_ready, acc_free, pv_done = (sem(n) for n in ("v_group", "acc_free", "pv_done"))
        o_stored, dec_ready, z_ready = sem("out_stored"), sem("decayed"), sem("acc_zeroed")

        def load_stack(sp, n, u):
            for n_, dst in (("q", qs[u]), ("k", ks[u])):
                src = parts[n_][ds(n * 24 * dq, 24 * dq), :].rearrange("(j r) t -> r j t", j=4)
                sp.dma_start(dst[0:6 * dq, :, :], src).then_inc(stack_in[u], 16)
            sp.dma_start(qs[u][r0:r0 + 3, :, :], dram["zero_rows"]).then_inc(stack_in[u], 16)
            if alibi:
                sp.dma_start(qs[u][6 * dq:r0, :, :], dram["alibi_q"][ds(n * 9, 9)]).then_inc(stack_in[u], 16)

        NST = 16 * (3 + (1 if alibi else 0))
        CIN = 16 * (5 + (3 if alibi else 0) + (2 if decay else 0))
        PV0 = 2 * KT + 1

        with nc.Block() as block:
            order = [(qt, j, c) for qt in range(KT) for j in range(4) for c in range(1 if qt < 4 else 2)]
            P1_COST = [min(NT, (qt + 1) * P - c * NT) + 60 for qt, j, c in order] + [TURN_COST]
            P1_ALL = sum(P1_COST)
            P2_COST = lambda kt: S - kt * P + 180
            P2_ALL = 4 * sum(P2_COST(kt) for kt in range(KT))

            @block.sync
            def _(sp):
                sp.dma_start(maskq[:, :], dram["mask_q"]).then_inc(c_in, 16)
                sp.dma_start(maskk[:, :], dram["mask_k"]).then_inc(c_in, 16)
                if decay:
                    sp.dma_start(dtab[:, :], dram["decay"]).then_inc(c_in, 16)
                    sp.dma_start(ones9[:, :], dram["ones9"]).then_inc(c_in, 16)
                for u in range(3):
                    sp.wait_ge(q_cleared, u + 1)
                    sp.wait_ge(k_cleared, u + 1)
                    sp.dma_start(ks[u][r0:r0 + 3, :, :], dram["ones_rows"]).then_inc(c_in, 16)
                    if alibi:
                        sp.dma_start(ks[u][6 * dq:r0, :, :], dram["alibi_k"]).then_inc(c_in, 16)
                for u in range(3):
                    sp.wait_ge(q_cleared, u + 1)
                    sp.wait_ge(k_cleared, u + 1)
                    load_stack(sp, u, u)

                def max_rows(n, u):
                    sp.wait_ge(mp_ready, n + 1)
                    for s in range(3):
                        sp.dma_start(qs[u][r0 + s:r0 + s + 1, :, :].rearrange("o j (k q) -> o (j k) q", q=P),
                                     mpart[:, s, :]).then_inc(m_in, 16)

                def output(n):
                    sp.wait_ge(acc_free, n + 2)
                    for j in range(4):
                        sp.dma_start(heads_out[ds(n * 32 + 8 * j, 8), :],
                                     oev[32 * j:32 * j + 8, :]).then_inc(o_stored, 16)
                        sp.dma_start(sums[ds(n * 4 + j, 1), :],
                                     oev[32 * j + 8:32 * j + 9, :]).then_inc(o_stored, 16)

                def one(n, u, load=True, nxt=True):
                    if nxt:
                        max_rows(n + 1, (u + 1) % 3)
                    sp.wait_ge(pv_done, KT * (n + 1) + PV0)
                    if load:
                        load_stack(sp, n + 3, u)
                    output(n)

                max_rows(0, 0)
                with sp.Fori(0, GROUPS // 3 - 1) as i:
                    for u in range(3):
                        one(3 * i + u, u)
                for n in range(GROUPS - GROUPS % 3 - 3, GROUPS):
                    one(n, n % 3, load=n + 3 < GROUPS, nxt=n + 1 < GROUPS)
                sp.wait_ge(o_stored, 8 * 16 * (GROUPS + 1))

            def p1_chunk(pe, n, u, k):
                qt, j, c = order[k]
                a0, a1 = c * NT, min((c + 1) * NT, (qt + 1) * P)
                slot = k % 2
                pe.wait_ge(a_free, n * (P1 + 1) + k + (3 if k == 0 else 2))
                diag = a1 == (qt + 1) * P
                mm = nc.tensor.matmul(pa[slot][:, 0:a1 - a0], qs[u][:, j, qt * P:(qt + 1) * P],
                                      ks[u][:, j, a0:a1], start=True, stop=not diag)
                if diag:
                    mm = nc.tensor.matmul(pa[slot][:, a1 - a0 - P:a1 - a0], net.identb[:, :], maskq[:, :],
                                          start=False, stop=True)
                mm.then_inc(a_ready, 1)

            def p1_turn(pe, n):
                pe.wait_ge(nm_ready, n + 1)
                pe.wait_ge(a_free, n * (P1 + 1) + P1 + 2)
                nc.tensor.transpose(pa[0][0:32, 0:P], nm[:, :, :].rearrange("p j k -> p (j k)"),
                                    net.ident[:, :]).then_inc(a_ready, 1)

            def p2_scores(pe, n, u, kt, j):
                pe.wait_ge(b_free, 32 * n + 4 * kt + j + 1)
                for c in range(2):
                    a0, a1 = max(c * NT, kt * P), (c + 1) * NT
                    if a0 >= a1:
                        continue
                    diag = a0 == kt * P
                    mm = nc.tensor.matmul(pb[j % 2][:, a0:a1], ks[u][:, j, kt * P:(kt + 1) * P],
                                          qs[u][:, j, a0:a1], start=True, stop=not diag)
                    if diag:
                        mm = nc.tensor.matmul(pb[j % 2][:, a0:a0 + P], net.identb[:, :], maskk[:, :],
                                              start=False, stop=True)
                mm.then_inc(b_ready, 1)

            def p2_values(pe, n, u, kt, c):
                a0, a1 = max(c * NT, kt * P), (c + 1) * NT
                if a0 >= a1:
                    return False
                if a0 == kt * P:
                    pe.wait_ge(b_free, 32 * n + 4 * kt + 4 + 2)
                    if decay:
                        pe.wait_ge(dec_ready, KT * n + kt + 1)
                    if kt == 0:
                        pe.wait_ge(vs_ready, n + 1)
                        pe.wait_ge(acc_free, n + 1)
                last_kt = kt == 4 * c + 3
                for j in range(4):
                    o = acc[32 * j:32 * j + 9, :]
                    mm = nc.tensor.matmul(o[:, a0:a1], ones9[:, :] if decay else vs[u][:, kt, j, :],
                                          pt[:, kt % 2, j, a0:a1], start=(kt == 0), stop=last_kt and not decay,
                                          tile_position=(0, 32 * j))
                if decay:
                    d1 = min(a1, kt * P + DECAY_SPAN)
                    if a0 < d1:
                        for j in range(4):
                            mm = nc.tensor.matmul(acc[32 * j:32 * j + 9, a0:d1], vs[u][:, kt, j, :],
                                                  pw[:, kt % 2, j, a0 - kt * P:d1 - kt * P], start=False,
                                                  stop=last_kt, tile_position=(0, 32 * j))
                if c == 1:
                    mm.then_inc(pv_done, 1)
                return True

            @block.tensor
            def _(pe):
                pe.wait_ge(c_in, CIN)
                pe.wait_ge(z_ready, 1)
                pe.wait_ge(stack_in[0], NST)
                for k in range(P1):
                    p1_chunk(pe, 0, 0, k)
                p1_turn(pe, 0)
                pe.wait_ge(stack_in[1], NST)
                for k in range(AHEAD):
                    p1_chunk(pe, 1, 1, k)

                def one(n, u, i, left=2):
                    steps = iter([(1, k) for k in range(AHEAD, P1)] + [(1, P1)] + [(2, k) for k in range(AHEAD)])
                    at, spent, passed = next(steps), 0, 0
                    pe.wait_ge(m_in, 48 * n + 96)
                    for kt in range(KT):
                        for j in range(4):
                            p2_scores(pe, n, u, kt, j)
                            passed += P2_COST(kt)
                            while at and spent <= passed * P1_ALL / P2_ALL:
                                g, k = at
                                if g <= left and k == P1:
                                    p1_turn(pe, n + 1)
                                elif g <= left:
                                    if g == 2 and k == 0:
                                        pe.wait_ge(stack_in[(u + 2) % 3], NST * (i + (u + 2) // 3 + 1))
                                    p1_chunk(pe, n + g, (u + g) % 3, k)
                                spent += P1_COST[k]
                                at = next(steps, None)
                            if kt and j % 2:
                                p2_values(pe, n, u, kt - 1, j // 2)
                    assert at is None
                    p2_values(pe, n, u, KT - 1, 1)

                with pe.Fori(0, GROUPS // 3 - 1) as i:
                    for u in range(3):
                        one(3 * i + u, u, i)
                for n in range(GROUPS - GROUPS % 3 - 3, GROUPS):
                    one(n, n % 3, n // 3, left=GROUPS - 1 - n)

            @block.scalar
            def _(act):
                nc.scalar.preload_act_table_set("natural_log_exp_and_others")
                act.sem_inc(b_free, 2)

                def one(n):
                    for kt in range(KT):
                        for j in range(4):
                            act.wait_ge(b_ready, 32 * n + 4 * kt + j + 1)
                            if j == 0:
                                act.wait_ge(pv_done, KT * n + kt - 1 + PV0)
                            nc.scalar.activation(pt[:, kt % 2, j, kt * P:S], pb[j % 2][:, kt * P:S], ACT.Exp,
                                                 scale=scale).then_inc(b_free, 1)

                with act.Fori(0, GROUPS) as n:
                    one(n)

            @block.gpsimd
            def _(pool):
                for u in range(3):
                    nc.gpsimd.memset(ks[u][:, :, :], 0.0).then_inc(k_cleared, 1)
                if decay:
                    pool.wait_ge(c_in, CIN)

                def one(n, u):
                    pool.wait_ge(pv_done, KT * n - 2 * KT + PV0)
                    nc.gpsimd.tensor_copy(vs[u][:, :, :, :], v[:, ds(n, 1), :, :, :].rearrange(
                        "p o k j e -> p (o k) j e")).then_inc(vs_ready, 1)
                    if decay:
                        for kt in range(KT):
                            wd = min(DECAY_SPAN, S - kt * P)
                            pool.wait_ge(b_free, 32 * n + 4 * kt + 6)
                            nc.gpsimd.tensor_tensor(
                                pw[:, kt % 2, :, 0:wd], pt[:, kt % 2, :, kt * P:kt * P + wd],
                                dtab[:, 0:wd].unsqueeze(1).to_broadcast((P, 4, wd)), ALU.mult
                            ).then_inc(dec_ready, 1)

                with pool.Fori(0, GROUPS // 3) as i:
                    for u in range(3):
                        one(3 * i + u, u)
                one(GROUPS - 1, 0)

            @block.vector
            def _(dve):
                for u in range(3):
                    nc.vector.memset(qs[u][:, :, :], 0.0).then_inc(q_cleared, 1)
                nc.vector.memset(acc[:, :], 0.0).then_inc(z_ready, 1)
                dve.sem_inc(a_free, 3)
                dve.sem_inc(pv_done, PV0)
                dve.sem_inc(acc_free, 1)

                def p1_max(n, chunks):
                    for k in chunks:
                        qt, j, c = order[k]
                        a0, a1 = c * NT, min((c + 1) * NT, (qt + 1) * P)
                        dve.wait_ge(a_ready, n * (P1 + 1) + k + 1)
                        nc.vector.tensor_reduce(mx[:, j, qt + 4 * c:qt + 4 * c + 1], pa[k % 2][:, 0:a1 - a0],
                                                AX.X, ALU.max).then_inc(a_free, 1)

                def p1_rows(n):
                    dve.wait_ge(a_free, n * (P1 + 1) + P1 + 3)
                    nc.vector.tensor_scalar(nm[:, :, 0:4], mx[:, :, 0:4], -1.0, None, ALU.mult)
                    nc.vector.tensor_tensor(nm[:, :, 4:8], mx[:, :, 4:8], mx[:, :, 8:12],
                                            ALU.max).then_inc(m_chain, 1)
                    dve.wait_ge(m_chain, 4 * n + 1)
                    nc.vector.tensor_scalar(nm[:, :, 4:8], nm[:, :, 4:8], -1.0, None, ALU.mult).then_inc(nm_ready, 1)
                    t = pa[0]
                    dve.wait_ge(a_ready, n * (P1 + 1) + P1 + 1)
                    dve.wait_ge(m_in, 48 * n + 48)
                    nc.vector.tensor_copy(mpart[:, 0, :], t[0:32, 0:P]).then_inc(m_chain, 1)
                    dve.wait_ge(m_chain, 4 * n + 2)
                    nc.vector.tensor_tensor(mrest[:, :], t[0:32, 0:P], mpart[:, 0, :], ALU.subtract).then_inc(m_chain, 1)
                    dve.wait_ge(m_chain, 4 * n + 3)
                    nc.vector.tensor_copy(mpart[:, 1, :], mrest[:, :]).then_inc(m_chain, 1)
                    dve.wait_ge(m_chain, 4 * n + 4)
                    nc.vector.tensor_tensor(mpart[:, 2, :], mrest[:, :], mpart[:, 1, :],
                                            ALU.subtract).then_inc(mp_ready, 1)
                    dve.sem_inc(a_free, 1)

                def evac(n):
                    dve.wait_ge(o_stored, 128 * n + 128)
                    dve.wait_ge(pv_done, KT * (n + 1) + PV0)
                    nc.vector.tensor_copy(oev[:, :], acc[:, :]).then_inc(acc_free, 1)

                dve.sem_inc(m_in, 48)
                dve.sem_inc(o_stored, 128)
                p1_max(0, range(P1))
                p1_rows(0)
                p1_max(1, range(AHEAD))
                with dve.Fori(0, GROUPS - 2) as n:
                    p1_max(n + 1, range(AHEAD, P1))
                    p1_rows(n + 1)
                    p1_max(n + 2, range(AHEAD))
                    evac(n)
                p1_max(GROUPS - 1, range(AHEAD, P1))
                p1_rows(GROUPS - 1)
                evac(GROUPS - 2)
                evac(GROUPS - 1)


def attn_output(net, tag, w, out_bias, heads_out, sums, rsums):
    nc, x, dram = net.nc, net.x, net.dram
    with stage(nc, tag + "_out") as (sb, ps, sem):
        wo = sb("wo", [P, P])
        bo = sb("bo", [P, 1])
        o = sb("heads", [P, T])
        r = sb("inverse", [P, T])
        s = sb("sums", [P, 4 * GROUPS * S // P])
        py = ps("proj", [P, 2, NT])
        s_in, r_made, r_out, r_in, o_ready, y_ready, y_free = (sem(n) for n in (
            "s_in", "r_made", "r_out", "r_in", "o_ready", "y_ready", "y_free"))
        with nc.Block() as block:
            @block.sync
            def _(sp):
                half = S // 2
                lay = lambda t: t.rearrange("r (a c) -> (r a) c", a=2)
                sp.dma_start(s[:, :], lay(sums)).then_inc(s_in, 16)
                sp.dma_start(wo[:, :], dram[w["wo"]]).then_inc(r_in, 16)
                if out_bias:
                    sp.dma_start(bo[:, :], dram[w["bo"]]).then_inc(r_in, 16)
                sp.dma_start(o[:, :].rearrange("p (b t) -> p b t", b=B),
                             heads_out.rearrange("(b p) t -> p b t", b=B)).then_inc(r_in, 16)
                sp.wait_ge(r_made, 1)
                sp.dma_start(lay(rsums), s[:, :]).then_inc(r_out, 16)
                sp.wait_ge(r_out, 16)
                for h in range(HEADS):
                    src = rsums.rearrange("(b h) t -> h b t", h=HEADS)[h:h + 1].to_broadcast((8, B, S))
                    sp.dma_start(r[8 * h:8 * h + 8, :].rearrange("p (b t) -> p b t", b=B), src).then_inc(r_in, 16)

            @block.vector
            def _(dve):
                dve.wait_ge(s_in, 16)
                nc.vector.reciprocal(s[:, :], s[:, :]).then_inc(r_made, 1)
                dve.wait_ge(r_in, 16 * (2 + HEADS + (1 if out_bias else 0)))
                dve.sem_inc(y_free, 2)
                with dve.Fori(0, TILES) as i:
                    tok = ds(i * NT, NT)
                    nc.vector.tensor_tensor(o[:, tok], o[:, tok], r[:, tok], ALU.mult).then_inc(o_ready, 1)
                with dve.Fori(0, TILES // 2) as i:
                    for p in range(2):
                        tok = ds((2 * i + p) * NT, NT)
                        dve.wait_ge(y_ready, 2 * i + p + 1)
                        if out_bias:
                            nc.vector.scalar_tensor_tensor(x[:, tok], py[:, p, :], bo[:, 0:1], x[:, tok],
                                                           ALU.add, ALU.add).then_inc(y_free, 1)
                        else:
                            nc.vector.tensor_tensor(x[:, tok], py[:, p, :], x[:, tok], ALU.add).then_inc(y_free, 1)

            @block.tensor
            def _(pe):
                with pe.Fori(0, TILES // 2) as i:
                    for p in range(2):
                        pe.wait_ge(o_ready, 2 * i + p + 1)
                        pe.wait_ge(y_free, 2 * i + p + 1)
                        nc.tensor.matmul(py[:, p, :], wo[:, :], o[:, ds((2 * i + p) * NT, NT)],
                                         start=True, stop=True).then_inc(y_ready, 1)


EXPERTS = 8
HC = 4


def experts_ffn(net, tag, w):
    nc, x, xn, dram = net.nc, net.x, net.xn, net.dram
    NTOK = T // P
    layer_norm(net, tag + "_ln")
    with stage(nc, tag) as (sb, ps, sem):
        fc = sb("expert_fc", [P, EXPERTS, HC * P])
        pj = sb("expert_proj", [P, EXPERTS, HC, P])
        rw = sb("router", [P, EXPERTS])
        sel = sb("expert_select", [P, EXPERTS, P], BF16)
        mask_t = sb("mask_rows", [P, T], BF16)
        loaded, routed = sem("loaded"), sem("routed")
        with stage(nc, tag + "_route") as (sb2, ps2, sem2):
            rank = sb2("rank", [P, NTOK, EXPERTS])
            top = sb2("top", [P, 2, NTOK, 1])
            eq = sb2("is_top", [P, 2, NTOK, EXPERTS])
            pl = ps2("logits", [P, NTOK, EXPERTS])
            pt = ps2("mask_rows", [EXPERTS, 2, NT])
            lg, chain, turned, copied = (sem2(n) for n in ("logits", "chain", "turned", "copied"))
            with nc.Block() as block:
                @block.sync
                def _(sp):
                    sp.dma_start(rw[:, :], dram[w["router"]]).then_inc(routed, 16)
                    sp.dma_start(sel[:, :, :], dram["expert_select"]).then_inc(loaded, 16)
                    sp.dma_start(fc[:, :, :], dram[w["fc"]]).then_inc(loaded, 16)
                    sp.dma_start(pj[:, :, :, :], dram[w["proj"]]).then_inc(loaded, 16)

                @block.tensor
                def _(pe):
                    pe.wait_ge(routed, 16)
                    for m in range(NTOK):
                        mm = nc.tensor.matmul(pl[:, m, :], xn[:, m * P:(m + 1) * P], rw[:, :], start=True, stop=True)
                    mm.then_inc(lg, 1)
                    pe.wait_ge(chain, 5)
                    for m in range(NTOK):
                        if m % 4 == 0 and m >= 8:
                            pe.wait_ge(copied, m // 4 - 1)
                        mm = nc.tensor.transpose(pt[:, m // 4 % 2, m % 4 * P:(m % 4 + 1) * P], eq[:, 1, m, :],
                                                 net.ident[:, :])
                        if m % 4 == 3:
                            mm.then_inc(turned, 1)

                @block.vector
                def _(dve):
                    nc.vector.memset(mask_t[:, :], 0.0)
                    for e in range(EXPERTS):
                        nc.vector.memset(rank[:, :, e:e + 1], float(EXPERTS - e))
                    wide = lambda t: t.to_broadcast((P, NTOK, EXPERTS))
                    dve.wait_ge(lg, 1)
                    nc.vector.tensor_reduce(top[:, 0, :, 0], pl[:, :, :], AX.X, ALU.max).then_inc(chain, 1)
                    dve.wait_ge(chain, 1)
                    nc.vector.tensor_tensor(eq[:, 0, :, :], pl[:, :, :], wide(top[:, 0, :, :]), ALU.is_equal).then_inc(chain, 1)
                    dve.wait_ge(chain, 2)
                    nc.vector.tensor_tensor(eq[:, 0, :, :], eq[:, 0, :, :], rank[:, :, :], ALU.mult).then_inc(chain, 1)
                    dve.wait_ge(chain, 3)
                    nc.vector.tensor_reduce(top[:, 1, :, 0], eq[:, 0, :, :], AX.X, ALU.max).then_inc(chain, 1)
                    dve.wait_ge(chain, 4)
                    nc.vector.tensor_tensor(eq[:, 1, :, :], eq[:, 0, :, :], wide(top[:, 1, :, :]), ALU.is_equal).then_inc(chain, 1)
                    for m in range(TILES):
                        dve.wait_ge(turned, m + 1)
                        nc.vector.tensor_copy(mask_t[0:EXPERTS, m * NT:(m + 1) * NT], pt[:, m % 2, :]).then_inc(copied, 1)

        xm = sb("masked", [P, 2, NT])
        r = sb("relu", [P, 2, 2, NT])
        h = sb("hidden", [P, 2, HC, NT])
        pb = ps("mask", [P, 2, NT])
        pu = ps("up", [P, 2, 2, NT])
        py = ps("down", [P, NT])
        bc_ready, xm_ready, up_ready, relu_done, sq_done, dn_done, y_free = (sem(n) for n in (
            "mask", "masked", "up", "relu", "square", "down", "y_free"))
        E = EXPERTS
        with nc.Block() as block:
            @block.tensor
            def _(pe):
                pe.wait_ge(loaded, 48)

                def spread(i, e):
                    n = E * i + e
                    pe.wait_ge(xm_ready, n + 1)
                    nc.tensor.matmul(pb[:, e % 2, :], sel[:, e, :], mask_t[:, ds(i * NT, NT)],
                                     start=True, stop=True).then_inc(bc_ready, 1)

                def up(i, e):
                    n = E * i + e
                    pe.wait_ge(xm_ready, n + 3)
                    for half in range(2):
                        pe.wait_ge(relu_done, 2 * n + half + 1)
                        for c in range(2):
                            k = 2 * half + c
                            mm = nc.tensor.matmul(pu[:, half, c, :], fc[:, e, k * P:(k + 1) * P], xm[:, e % 2, :],
                                                  start=True, stop=True)
                        mm.then_inc(up_ready, 1)

                def down(i, e):
                    n = E * i + e
                    pe.wait_ge(sq_done, 2 * n + 4)
                    if e == 0:
                        pe.wait_ge(y_free, i + 1)
                    for k in range(HC):
                        mm = nc.tensor.matmul(py[:, :], pj[:, e, k, :], h[:, e % 2, k, :],
                                              start=(e == 0 and k == 0), stop=(e == E - 1 and k == HC - 1))
                    mm.then_inc(dn_done, 1)

                with pe.Fori(0, TILES) as i:
                    spread(i, 0)
                    spread(i, 1)
                    for e in range(E):
                        up(i, e)
                        if e:
                            down(i, e - 1)
                        if 1 <= e < E - 1:
                            spread(i, e + 1)
                    down(i, E - 1)

            @block.scalar
            def _(act):
                act.sem_inc(relu_done, 2)
                with act.Fori(0, TILES) as i:
                    for e in range(E):
                        for half in range(2):
                            n = 2 * (E * i + e) + half
                            act.wait_ge(up_ready, n + 1)
                            act.wait_ge(sq_done, n + 1)
                            nc.scalar.activation(r[:, half, :, :], pu[:, half, :, :], ACT.Relu).then_inc(relu_done, 1)

            @block.vector
            def _(dve):
                dve.sem_inc(xm_ready, 2)
                dve.sem_inc(sq_done, 2)
                dve.sem_inc(dn_done, 2)
                dve.sem_inc(y_free, 1)

                def masked(i, e):
                    n = E * i + e
                    dve.wait_ge(bc_ready, n + 1)
                    nc.vector.tensor_tensor(xm[:, e % 2, :], pb[:, e % 2, :], xn[:, ds(i * NT, NT)],
                                            ALU.mult).then_inc(xm_ready, 1)

                with dve.Fori(0, TILES) as i:
                    masked(i, 0)
                    masked(i, 1)
                    for e in range(E):
                        n = E * i + e
                        dve.wait_ge(dn_done, n + 1)
                        for half in range(2):
                            dve.wait_ge(relu_done, 2 * n + half + 3)
                            nc.vector.tensor_tensor(h[:, e % 2, 2 * half:2 * half + 2, :], r[:, half, :, :],
                                                    r[:, half, :, :], ALU.mult).then_inc(sq_done, 1)
                        if 1 <= e < E - 1:
                            masked(i, e + 1)
                    dve.wait_ge(dn_done, E * i + E + 2)
                    tok = ds(i * NT, NT)
                    nc.vector.tensor_tensor(x[:, tok], py[:, :], x[:, tok], ALU.add).then_inc(y_free, 1)


def gated_ffn(net, tag):
    nc, x, xn, dram = net.nc, net.x, net.xn, net.dram
    layer_norm(net, tag + "_ln")
    with stage(nc, tag) as (sb, ps, sem):
        w12 = [sb("w1", [P, HC * P]), sb("w2", [P, HC * P])]
        wh = [sb("h1", [P, HC, HC * P]), sb("h2", [P, HC, HC * P])]
        w3 = sb("w3", [P, HC, P])
        sc = sb("scales", [P, 17])
        h0 = sb("gated", [P, HC, T])
        loaded = sem("loaded")
        with stage(nc, tag + "_gate") as (sb2, ps2, sem2):
            sg = sb2("silu", [P, 2, NT])
            pg = ps2("gate_up", [P, 2, 2, NT])
            ready, silu, done = sem2("ready"), sem2("silu"), sem2("done")
            with nc.Block() as block:
                @block.sync
                def _(sp):
                    for t, n in ((w12[0], "w1"), (w12[1], "w2"), (sc, "scales")):
                        sp.dma_start(t[:, :], dram["g3_" + n]).then_inc(loaded, 16)
                    sp.dma_start(wh[0][:, :, :], dram["g3_h1"]).then_inc(loaded, 16)
                    sp.dma_start(wh[1][:, :, :], dram["g3_h2"]).then_inc(loaded, 16)
                    sp.dma_start(w3[:, :, :], dram["g3_w3"]).then_inc(loaded, 16)

                @block.tensor
                def _(pe):
                    pe.wait_ge(loaded, 96)
                    with pe.Fori(0, TILES) as i:
                        for k in range(HC):
                            pe.wait_ge(done, HC * i + k + 1)
                            for m in range(2):
                                mm = nc.tensor.matmul(pg[:, k % 2, m, :], w12[m][:, k * P:(k + 1) * P],
                                                      xn[:, ds(i * NT, NT)], start=True, stop=True)
                            mm.then_inc(ready, 1)

                @block.scalar
                def _(act):
                    act.wait_ge(loaded, 96)
                    nc.scalar.preload_act_table_set("silu_and_others")
                    with act.Fori(0, TILES) as i:
                        for k in range(HC):
                            act.wait_ge(ready, HC * i + k + 1)
                            act.wait_ge(done, HC * i + k + 1)
                            nc.scalar.activation(sg[:, k % 2, :], pg[:, k % 2, 0, :], ACT.Silu,
                                                 scale=sc[:, k:k + 1]).then_inc(silu, 1)

                @block.vector
                def _(dve):
                    dve.sem_inc(done, 2)
                    with dve.Fori(0, TILES) as i:
                        for k in range(HC):
                            dve.wait_ge(silu, HC * i + k + 1)
                            nc.vector.scalar_tensor_tensor(h0[:, k, ds(i * NT, NT)], pg[:, k % 2, 1, :],
                                                           sc[:, 4 + k:5 + k], sg[:, k % 2, :], ALU.mult,
                                                           ALU.mult).then_inc(done, 1)

        g = [sb("gelu1", [P, 2, HC, NT]), sb("gelu2", [P, 2, HC, NT])]
        ph = ps("hidden", [P, 4, NT])
        py = ps("out", [P, 2, NT])
        h_ready, h_done, y_ready, y_free = (sem(n) for n in ("hidden", "gelu", "y", "y_free"))
        with nc.Block() as block:
            @block.tensor
            def _(pe):
                def layer(i, p, m):
                    for k in range(HC):
                        n = 16 * i + 8 * m + 4 * p + k
                        pe.wait_ge(h_done, n + 1)
                        if m and k == 0:
                            pe.wait_ge(h_done, 4 + 16 * i + 4 * p + 4)
                        for c in range(HC):
                            src = g[0][:, p, c, :] if m else h0[:, c, ds((2 * i + p) * NT, NT)]
                            mm = nc.tensor.matmul(ph[:, k, :], wh[m][:, c, k * P:(k + 1) * P], src,
                                                  start=(c == 0), stop=(c == HC - 1))
                        mm.then_inc(h_ready, 1)

                with pe.Fori(0, TILES // 2) as i:
                    for m in range(2):
                        for p in range(2):
                            layer(i, p, m)
                    for p in range(2):
                        pe.wait_ge(h_done, 4 + 16 * i + 8 + 4 * p + 4)
                        pe.wait_ge(y_free, 2 * i + p + 1)
                        for c in range(HC):
                            mm = nc.tensor.matmul(py[:, p, :], w3[:, c, :], g[1][:, p, c, :],
                                                  start=(c == 0), stop=(c == HC - 1))
                        mm.then_inc(y_ready, 1)

            @block.scalar
            def _(act):
                act.sem_inc(h_done, 4)
                with act.Fori(0, TILES // 2) as i:
                    for m in range(2):
                        for p in range(2):
                            for k in range(HC):
                                n = 16 * i + 8 * m + 4 * p + k
                                act.wait_ge(h_ready, n + 1)
                                if m and k == 0:
                                    act.wait_ge(y_ready, 2 * i + p + 1)
                                nc.scalar.activation(g[m][:, p, k, :], ph[:, k, :], ACT.Gelu,
                                                     scale=sc[:, 8 + 4 * m + k:9 + 4 * m + k]).then_inc(h_done, 1)

            @block.vector
            def _(dve):
                dve.sem_inc(y_free, 2)
                dve.sem_inc(y_ready, 2)
                with dve.Fori(0, TILES // 2) as i:
                    for p in range(2):
                        tok = ds((2 * i + p) * NT, NT)
                        dve.wait_ge(y_ready, 2 * i + p + 3)
                        nc.vector.scalar_tensor_tensor(x[:, tok], py[:, p, :], sc[:, 16:17], x[:, tok],
                                                       ALU.mult, ALU.add).then_inc(y_free, 1)


NS = 16


def selective_ssm(net, tag, w, H, taps, left, rms, low_rank, a_is_log, residual):
    nc, x, xn, dram = net.nc, net.x, net.xn, net.dram
    PADDED = S + taps - 1
    with stage(nc, tag) as (sb, ps, sem):
        gate = sb("gate", [P, H, T])
        xs = sb("xs", [P, H, T])
        cols = sb("cols", [P, 64])
        bin_, cvb, dtb, dbb, rmsw, bout = (cols[:, a:b] for a, b in ((0, 4), (4, 6), (6, 8), (8, 9), (9, 10), (10, 11)))
        cvw = cols[:, 16:16 + H * taps].rearrange("p (h k) -> p h k", h=H)
        acol = sb("a_cols", [P, H, NS])
        w_dbc = sb("w_dbc", [P, H, P])
        w_dt = sb("w_dt", [P, H, P])
        w_out = sb("w_out", [P, H, P])
        spread = sb("spread", [P, 32, P], BF16)
        loaded = sem("loaded")
        with ExitStack() as fctx:
            fac = fctx.enter_context(nc.sbuf_tensor(f"{tag}_rms_factor", [P, T], F32)) if rms else None
            layer_norm(net, tag + "_ln", ("rsqrt", RMS_EPS, fac) if rms else None)
            ssm_input(net, tag, w, H, taps, left, rms, fac, gate, xs, cols, bin_, cvb, rmsw, cvw, acol, w_dbc, w_dt,
                      w_out, spread, loaded, PADDED)
        delta = sb("delta", [P, H, T])
        bcp = sb("bc_parts", [P, T], BF16)
        ssm_delta(net, tag, H, low_rank, a_is_log, xs, delta, bcp, dtb, dbb, acol, w_dbc, w_dt)
        ssm_scan(net, tag, H, xs, delta, bcp, acol, spread)
        ssm_output(net, tag, H, xs, gate, w_out, bout, residual)


def ssm_input(net, tag, w, H, taps, left, rms, fac, gate, xs, cols, bin_, cvb, rmsw, cvw, acol, w_dbc, w_dt, w_out,
              spread, loaded, PADDED):
    nc, x, xn, dram = net.nc, net.x, net.xn, net.dram
    with stage(nc, tag + "_in") as (sb, ps, sem):
        win = sb("w_in", [P, 2 * H * P])
        xp = sb("padded", [P, H, B, PADDED])
        hh = sb("rms_normed", [P, 2, NT])
        cv = sb("conv", [P, 2, 2, S])
        pp = ps("proj", [P, 4, NT])
        h_ready, p_ready, p_free, padded, conv, xs_done, chain, pads = (sem(n) for n in (
            "h", "proj", "proj_free", "padded", "conv", "xs", "chain", "pads"))
        M = 2 * H
        with nc.Block() as block:
            @block.sync
            def _(sp):
                for t, n in ((win, "win"), (cols, "cols")):
                    sp.dma_start(t[:, :], dram[w + n]).then_inc(loaded, 16)
                for t, n in ((acol, "a"), (w_dbc, "dbc"), (w_dt, "dt"), (w_out, "out")):
                    sp.dma_start(t[:, :, :], dram[w + n]).then_inc(loaded, 16)
                sp.dma_start(spread[:, :, :], dram["bc_spread"]).then_inc(loaded, 16)

            @block.tensor
            def _(pe):
                pe.wait_ge(loaded, 112)
                with pe.Fori(0, TILES // 2) as i:
                    for p in range(2):
                        tok = ds((2 * i + p) * NT, NT)
                        if rms:
                            pe.wait_ge(h_ready, 2 * i + p + 1)
                        for m in range(M):
                            n = (2 * i + p) * M + m
                            pe.wait_ge(p_free, n + 1)
                            nc.tensor.matmul(pp[:, (p * M + m) % 4, :], win[:, m * P:(m + 1) * P],
                                             hh[:, p, :] if rms else xn[:, tok], start=True, stop=True
                                             ).then_inc(p_ready, 1)

            @block.scalar
            def _(act):
                act.wait_ge(loaded, 112)
                act.wait_ge(chain, 1)
                act.sem_inc(p_free, 4)
                nc.scalar.preload_act_table_set("silu_and_others")
                with act.Fori(0, B) as b:
                    for p in range(2):
                        tok = ds((2 * b + p) * NT, NT)
                        for m in range(M):
                            act.wait_ge(p_ready, (2 * b + p) * M + m + 1)
                            src = pp[:, (p * M + m) % 4, :]
                            if m < H:
                                dst = xp[:, m, ds(b, 1), left + p * NT:left + (p + 1) * NT].rearrange("p o t -> p (o t)")
                                nc.scalar.activation(dst, src, ACT.Identity, bias=bin_[:, m:m + 1]).then_inc(p_free, 1)
                            else:
                                nc.scalar.activation(gate[:, m - H, tok], src, ACT.Silu,
                                                     bias=bin_[:, m:m + 1]).then_inc(p_free, 1)
                with act.Fori(0, B) as b:
                    for h in range(H):
                        act.wait_ge(conv, H * b + h + 1)
                        nc.scalar.activation(xs[:, h, ds(b * S, S)], cv[:, 1, h, :], ACT.Silu).then_inc(xs_done, 1)

            @block.vector
            def _(dve):
                nc.vector.memset(xp[:, :, :, 0:left], 0.0).then_inc(pads, 1)
                if taps - 1 - left:
                    nc.vector.memset(xp[:, :, :, left + S:PADDED], 0.0).then_inc(pads, 1)
                dve.wait_ge(pads, 2 if taps - 1 - left else 1)
                dve.sem_inc(xs_done, H)
                dve.wait_ge(loaded, 112)
                dve.sem_inc(chain, 1)
                if rms:
                    with dve.Fori(0, TILES // 2) as i:
                        for p in range(2):
                            tok = ds((2 * i + p) * NT, NT)
                            dve.wait_ge(p_free, (2 * i + p) * M + 1)
                            nc.vector.scalar_tensor_tensor(hh[:, p, :], xn[:, tok], rmsw[:, 0:1], fac[:, tok],
                                                           ALU.mult, ALU.mult).then_inc(h_ready, 1)
                with dve.Fori(0, B) as b:
                    for h in range(H):
                        dve.wait_ge(p_free, 4 + (2 * b + 2) * M)
                        dve.wait_ge(xs_done, H * b + h + 1)
                        for k in range(taps):
                            src = xp[:, h, ds(b, 1), k:k + S].rearrange("p o t -> p (o t)")
                            last = k == taps - 1
                            dst = cv[:, 1 if last else 0, h, :]
                            if k == 0:
                                a = nc.vector.tensor_scalar(dst, src, cvw[:, h, 0:1], cvb[:, h:h + 1], ALU.mult, ALU.add)
                            else:
                                dve.wait_ge(chain, (H * b + h) * (taps - 1) + k + 1)
                                a = nc.vector.scalar_tensor_tensor(dst, src, cvw[:, h, k:k + 1], cv[:, 0, h, :],
                                                                   ALU.mult, ALU.add)
                            a.then_inc(conv if last else chain, 1)


def ssm_delta(net, tag, H, low_rank, a_is_log, xs, delta, bcp, dtb, dbb, acol, w_dbc, w_dt):
    nc = net.nc
    with stage(nc, tag + "_dt") as (sb, ps, sem):
        z = sb("dbc", [P, 2, NT])
        hi = sb("hi", [P, 2, NT], BF16)
        mid = sb("mid", [P, 2, NT], BF16)
        rest = sb("rest", [P, 2, NT])
        ab = sb("softplus", [P, 2, H, 3, NT])
        mx = sb("before_softplus", [P, 2, H, NT])
        pz = ps("dbc", [P, 2, NT])
        pd = ps("delta", [P, 2, H, NT])
        z_ready, z_done, d_ready, l_done, u_done, parts, a_chain, d_chain = (sem(n) for n in (
            "dbc", "dbc_done", "delta", "log_done", "u_done", "parts", "act_chain", "dve_chain"))
        with nc.Block() as block:
            @block.gpsimd
            def _(pool):
                nc.gpsimd.memset(bcp[96:P, :], 0.0)

            @block.tensor
            def _(pe):
                with pe.Fori(0, TILES // 2) as i:
                    for p in range(2):
                        pe.wait_ge(z_done, 2 * i + p + 1)
                        for h in range(H):
                            mm = nc.tensor.matmul(pz[:, p, :], w_dbc[:, h, :], xs[:, h, ds((2 * i + p) * NT, NT)],
                                                  start=(h == 0), stop=(h == H - 1))
                        mm.then_inc(z_ready, 1)
                    for p in range(2):
                        if low_rank:
                            pe.wait_ge(z_done, 2 * i + p + 3)
                        pe.wait_ge(u_done, 2 * i + p + 1)
                        for h in range(H):
                            src = z[:, p, :] if low_rank else xs[:, h, ds((2 * i + p) * NT, NT)]
                            mm = nc.tensor.matmul(pd[:, p, h, :], w_dt[:, h, :], src, start=True, stop=True)
                        mm.then_inc(d_ready, 1)

            @block.scalar
            def _(act):
                nc.scalar.preload_act_table_set("natural_log_exp_and_others")
                C = [0]
                if a_is_log:
                    nc.scalar.activation(acol[:, :, :], acol[:, :, :], ACT.Exp).then_inc(a_chain, 1)
                    C[0] = 1
                with act.Fori(0, TILES // 2) as i:
                    for p in range(2):
                        act.wait_ge(d_chain, 2 * (2 * i + p) + 1)
                        for h in range(H):
                            q = (2 * i + p) * H + h
                            nc.scalar.activation(ab[:, p, h, 0, :], mx[:, p, h, :], ACT.Abs).then_inc(a_chain, 1)
                            act.wait_ge(a_chain, 2 * q + C[0] + 1)
                            nc.scalar.activation(ab[:, p, h, 1, :], ab[:, p, h, 0, :], ACT.Exp,
                                                 scale=-1.0).then_inc(a_chain, 1)
                            act.wait_ge(a_chain, 2 * q + C[0] + 2)
                            a = nc.scalar.activation(ab[:, p, h, 2, :], ab[:, p, h, 1, :], ACT.Ln, bias=net.one)
                        a.then_inc(l_done, 1)

            @block.vector
            def _(dve):
                dve.sem_inc(z_done, 2)
                dve.sem_inc(u_done, 2)
                if a_is_log:
                    dve.wait_ge(a_chain, 1)
                    nc.vector.tensor_scalar(acol[:, :, :], acol[:, :, :], -1.0, None, ALU.mult)
                with dve.Fori(0, TILES // 2) as i:
                    for p in range(2):
                        t = 2 * i + p
                        tok = ds(t * NT, NT)
                        dve.wait_ge(z_ready, t + 1)
                        nc.vector.tensor_scalar(z[:, p, :], pz[:, p, :], dbb[:, 0:1], None, ALU.add).then_inc(z_done, 1)
                        dve.wait_ge(z_done, t + 3)
                        nc.vector.tensor_copy(hi[0:96, p, :], z[0:96, p, :]).then_inc(parts, 1)
                        dve.wait_ge(parts, 3 * t + 1)
                        nc.vector.tensor_tensor(rest[0:96, p, :], z[0:96, p, :], hi[0:96, p, :], ALU.subtract
                                                ).then_inc(parts, 1)
                        nc.vector.tensor_copy(bcp[0:32, tok], hi[0:32, p, :])
                        dve.wait_ge(parts, 3 * t + 2)
                        nc.vector.tensor_copy(mid[0:96, p, :], rest[0:96, p, :]).then_inc(parts, 1)
                        dve.wait_ge(parts, 3 * t + 3)
                        nc.vector.tensor_copy(bcp[32:64, tok], mid[32:64, p, :])
                        nc.vector.tensor_tensor(bcp[64:96, tok], rest[64:96, p, :], mid[64:96, p, :], ALU.subtract)
                    for p in range(2):
                        t = 2 * i + p
                        tok = ds(t * NT, NT)
                        dve.wait_ge(d_ready, t + 1)
                        for h in range(H):
                            a = nc.vector.tensor_scalar(mx[:, p, h, :], pd[:, p, h, :], dtb[:, h:h + 1], None,
                                                        ALU.add)
                        a.then_inc(d_chain, 1)
                        dve.wait_ge(l_done, t + 1)
                        nc.vector.scalar_tensor_tensor(delta[:, :, tok], mx[:, p, :, :], 0.0, ab[:, p, :, 2, :],
                                                       ALU.max, ALU.add).then_inc(d_chain, 1)
                        dve.wait_ge(d_chain, 2 * t + 2)
                        nc.vector.tensor_tensor(xs[:, :, tok], xs[:, :, tok], delta[:, :, tok],
                                                ALU.mult).then_inc(u_done, 1)


def ssm_scan(net, tag, H, xs, delta, bcp, acol, spread):
    nc = net.nc
    R, RS = 2, 4
    NC = 3 - H
    with stage(nc, tag + "_scan") as (sb, ps, sem):
        decay = sb("decay", [P, R, S])
        bs = sb("b_rows", [P, RS, S])
        bx = sb("bx", [P, R, S])
        hs = sb("states", [P, RS, S])
        hc = sb("states_c", [P, R, S])
        pb, pc = ps("b_rows", [P, S]), ps("c_rows", [P, NC, S])
        acc = ps("y", [P, H, S])
        b_ready, bs_done, c_ready, hc_done, y_done, y_out, a_done, bx_done, scanned, paced = (
            sem(n) for n in ("b_rows", "b_copied", "c_rows", "states_c", "summed", "y_out", "decay", "bx", "scanned",
                             "paced"))
        with nc.Block() as block:
            @block.tensor
            def _(pe):
                def b_rows(b, n):
                    s = NS * b + n
                    pe.wait_ge(bs_done, s + 1)
                    for c in range(2):
                        mm = nc.tensor.matmul(pb[:, c * NT:(c + 1) * NT], spread[:, n, :],
                                              bcp[:, ds(b * S + c * NT, NT)], start=True, stop=True)
                    mm.then_inc(b_ready, 1)

                def c_rows(b, n):
                    pe.wait_ge(hc_done, H * (NS * b + n) + H + RS - H * NC)
                    for c in range(2):
                        mm = nc.tensor.matmul(pc[:, n % NC, c * NT:(c + 1) * NT], spread[:, NS + n, :],
                                              bcp[:, ds(b * S + c * NT, NT)], start=True, stop=True)
                    mm.then_inc(c_ready, 1)

                def add_up(b, n, halves=range(H)):
                    for h in halves:
                        q = (NS * b + n) * H + h
                        pe.wait_ge(hc_done, q + 1 + RS)
                        if n == 0:
                            pe.wait_ge(y_out, b + 1)
                        for c in range(2):
                            mm = nc.tensor.matmul(acc[:, h, c * NT:(c + 1) * NT], net.ident[:, :],
                                                  hc[:, (n * H + h) % R, c * NT:(c + 1) * NT],
                                                  start=(n == 0), stop=(n == NS - 1))
                        mm.then_inc(y_done, 1)

                with pe.Fori(0, B) as b:
                    b_rows(b, 0)
                    b_rows(b, 1)
                    for n in range(NS):
                        if n + 2 < NS:
                            b_rows(b, n + 2)
                        if n:
                            add_up(b, n - 1, range(H - 1))
                        c_rows(b, n)
                        if n:
                            add_up(b, n - 1, range(H - 1, H))
                    add_up(b, NS - 1)

            @block.scalar
            def _(act):
                nc.scalar.preload_act_table_set("natural_log_exp_and_others")
                act.sem_inc(bs_done, 1)

                def copy_b(b, n):
                    s = NS * b + n
                    act.wait_ge(b_ready, s + 1)
                    act.wait_ge(bx_done, H * s + H)
                    nc.scalar.activation(bs[:, n % RS, :], pb[:, :], ACT.Copy).then_inc(bs_done, 1)

                with act.Fori(0, B) as b:
                    copy_b(b, 0)
                    for n in range(NS):
                        s = NS * b + n
                        if n + 1 < NS:
                            copy_b(b, n + 1)
                        for h in range(H):
                            q = H * s + h
                            act.wait_ge(scanned, q + 1)
                            act.sem_inc(paced, 1)
                            nc.scalar.activation(decay[:, (n * H + h) % R, :], delta[:, h, ds(b * S, S)], ACT.Exp,
                                                 scale=acol[:, h, n:n + 1]).then_inc(a_done, 1)

            @block.gpsimd
            def _(pool):
                pool.sem_inc(bx_done, RS * H)
                with pool.Fori(0, B) as b:
                    for n in range(NS):
                        s = NS * b + n
                        pool.wait_ge(bs_done, s + 2)
                        for h in range(H):
                            q = H * s + h
                            pool.wait_ge(scanned, q + 1)
                            pool.sem_inc(paced, 1)
                            nc.gpsimd.tensor_tensor(bx[:, (n * H + h) % R, :], xs[:, h, ds(b * S, S)], bs[:, n % RS, :],
                                                    ALU.mult).then_inc(bx_done, 1)

            @block.vector
            def _(dve):
                dve.sem_inc(scanned, R)
                dve.sem_inc(hc_done, RS)
                dve.sem_inc(y_done, R)
                dve.sem_inc(y_out, 1)

                def scan(q, m):
                    dve.wait_ge(a_done, q + 1)
                    dve.wait_ge(bx_done, q + RS * H + 1)
                    dve.wait_ge(hc_done, q + 1)
                    nc.vector.tensor_tensor_scan(hs[:, m % RS, :], decay[:, m % R, :], bx[:, m % R, :], 0.0, ALU.mult,
                                                 ALU.add).then_inc(scanned, 1)

                def times_c(b, m):
                    q, n = NS * H * b + m, m // H
                    if m % H == 0:
                        dve.wait_ge(c_ready, NS * b + n + 1)
                    dve.wait_ge(y_done, q + 1)
                    dve.wait_ge(scanned, q + 1 + R)
                    nc.vector.tensor_tensor(hc[:, m % R, :], hs[:, m % RS, :], pc[:, n % NC, :], ALU.mult).then_inc(hc_done, 1)

                with dve.Fori(0, B) as b:
                    for m in range(NS * H):
                        scan(NS * H * b + m, m)
                        if m:
                            times_c(b, m - 1)
                    times_c(b, NS * H - 1)
                    dve.wait_ge(y_done, H * NS * (b + 1) + R)
                    nc.vector.tensor_copy(xs[:, :, ds(b * S, S)], acc[:, :, :]).then_inc(y_out, 1)


def ssm_output(net, tag, H, y, gate, w_out, bout, residual):
    nc, x, xn = net.nc, net.x, net.xn
    with stage(nc, tag + "_out") as (sb, ps, sem):
        py = ps("proj", [P, 2, NT])
        gated, ready, free, added = sem("gated"), sem("ready"), sem("free"), sem("added")
        with nc.Block() as block:
            @block.gpsimd
            def _(pool):
                with pool.Fori(0, TILES) as i:
                    tok = ds(i * NT, NT)
                    nc.gpsimd.tensor_tensor(y[:, :, tok], y[:, :, tok], gate[:, :, tok], ALU.mult).then_inc(gated, 1)

            @block.tensor
            def _(pe):
                with pe.Fori(0, TILES // 2) as i:
                    for p in range(2):
                        pe.wait_ge(gated, 2 * i + p + 1)
                        pe.wait_ge(free, 2 * i + p + 1)
                        for h in range(H):
                            mm = nc.tensor.matmul(py[:, p, :], w_out[:, h, :], y[:, h, ds((2 * i + p) * NT, NT)],
                                                  start=(h == 0), stop=(h == H - 1))
                        mm.then_inc(ready, 1)

            @block.vector
            def _(dve):
                if residual:
                    nc.vector.tensor_tensor(x[:, :], x[:, :], xn[:, :], ALU.add).then_inc(added, 1)
                    dve.wait_ge(added, 1)
                dve.sem_inc(free, 2)
                with dve.Fori(0, TILES // 2) as i:
                    for p in range(2):
                        tok = ds((2 * i + p) * NT, NT)
                        dve.wait_ge(ready, 2 * i + p + 1)
                        nc.vector.scalar_tensor_tensor(x[:, tok], py[:, p, :], bout[:, 0:1], x[:, tok],
                                                       ALU.add, ALU.add).then_inc(free, 1)


SSD_HEADS, SSD_P = 32, 8
UNITS = T // P
CPS = S // P


def ssd(net, tag):
    nc, x, xn, dram = net.nc, net.x, net.xn, net.dram
    taps, DI = 4, 2 * P
    PADDED = S + taps - 1
    layer_norm(net, tag + "_ln")
    with stage(nc, tag) as (sb, ps, sem):
        xbc = sb("xbc", [P, 4, B, PADDED])
        zs = sb("gate", [P, UNITS, DI])
        dt = sb("dt", [P, UNITS, SSD_HEADS])
        e_cs = sb("exp_cs", [P, UNITS, SSD_HEADS])
        e_out = sb("exp_rest", [P, UNITS, SSD_HEADS])
        e_all = sb("exp_chunk", [P, UNITS, SSD_HEADS])
        csp = sb("cs_parts", [P, T], BF16)
        w_out = sb("w_out", [P, 2, P])
        ssd_input(net, tag, xbc, zs, dt, w_out, PADDED, taps, DI)
        ssd_steps(net, tag, dt, e_cs, e_out, e_all, csp)
        ssd_chunks(net, tag, xbc, dt, e_cs, e_out, e_all, csp, DI)
        ssd_output(net, tag, xbc, zs, w_out, DI)


def ssd_input(net, tag, xbc, zs, dt, w_out, PADDED, taps, DI):
    nc, xn, dram = net.nc, net.xn, net.dram
    with stage(nc, tag + "_in") as (sb, ps, sem):
        w = sb("w_xbc", [P, 4 * P])
        wz = sb("w_z_dt", [P, DI + SSD_HEADS])
        cvw = sb("conv_w", [P, 4, taps + 1])
        dtb = sb("dt_bias", [P, SSD_HEADS])
        lnw = sb("ln_w", [P, DI])
        cv = sb("conv", [P, 2, 2, S])
        pp = ps("proj", [P, 4, NT])
        pz = ps("z", [P, 2, NT])
        loaded, p_ready, p_free, z_ready, z_silu, z_free, conv, xs_done, chain, pads = (sem(n) for n in (
            "loaded", "proj", "proj_free", "z", "z_silu", "z_free", "conv", "xs", "chain", "pads"))
        with nc.Block() as block:
            @block.sync
            def _(sp):
                for t, n in ((w, "w"), (wz, "wz")):
                    sp.dma_start(t[:, :], dram["d2_" + n]).then_inc(loaded, 16)
                sp.dma_start(cvw[:, :, :], dram["d2_conv"]).then_inc(loaded, 16)
                sp.dma_start(w_out[:, :, :], dram["d2_out"]).then_inc(loaded, 16)
                sp.dma_start(dtb[:, :], dram["d2_dtb"].to_broadcast((P, SSD_HEADS))).then_inc(loaded, 16)
                sp.dma_start(lnw[:, :], dram["d2_lnw"].to_broadcast((P, DI))).then_inc(loaded, 16)

            @block.tensor
            def _(pe):
                pe.wait_ge(loaded, 96)
                with pe.Fori(0, TILES) as i:
                    for m in range(4):
                        pe.wait_ge(p_free, 4 * i + m + 1)
                        nc.tensor.matmul(pp[:, m, :], w[:, m * P:(m + 1) * P], xn[:, ds(i * NT, NT)],
                                         start=True, stop=True).then_inc(p_ready, 1)
                for u in range(UNITS):
                    if u >= 2:
                        pe.wait_ge(z_free, u - 1)
                    nc.tensor.matmul(pz[:, u % 2, 0:DI + SSD_HEADS], xn[:, u * P:(u + 1) * P], wz[:, :],
                                     start=True, stop=True).then_inc(z_ready, 1)

            @block.scalar
            def _(act):
                nc.scalar.preload_act_table_set("silu_and_others")
                act.sem_inc(p_free, 4)
                with act.Fori(0, B) as b:
                    for p in range(2):
                        for m in range(4):
                            act.wait_ge(p_ready, 8 * b + 4 * p + m + 1)
                            dst = xbc[:, m, ds(b, 1), 3 + p * NT:3 + (p + 1) * NT].rearrange("p o t -> p (o t)")
                            nc.scalar.activation(dst, pp[:, m, :], ACT.Copy).then_inc(p_free, 1)
                for u in range(UNITS):
                    act.wait_ge(z_ready, u + 1)
                    nc.scalar.activation(zs[:, u, :], pz[:, u % 2, 0:DI], ACT.Silu).then_inc(z_silu, 1)
                with act.Fori(0, B) as b:
                    for m in range(4):
                        act.wait_ge(conv, 4 * b + m + 1)
                        dst = xbc[:, m, ds(b, 1), 0:S].rearrange("p o t -> p (o t)")
                        nc.scalar.activation(dst, cv[:, 1, m % 2, :], ACT.Silu).then_inc(xs_done, 1)

            @block.vector
            def _(dve):
                nc.vector.memset(xbc[:, :, :, 0:taps - 1], 0.0).then_inc(pads, 1)
                dve.wait_ge(pads, 1)
                dve.sem_inc(xs_done, 2)
                dve.wait_ge(loaded, 96)
                for u in range(UNITS):
                    dve.wait_ge(z_silu, u + 1)
                    nc.vector.tensor_tensor(dt[:, u, :], pz[:, u % 2, DI:DI + SSD_HEADS], dtb[:, :],
                                            ALU.add).then_inc(z_free, 1)
                with dve.Fori(0, B) as b:
                    for m in range(4):
                        dve.wait_ge(p_free, 4 + 8 * b + 8)
                        dve.wait_ge(xs_done, 4 * b + m + 1)
                        for k in range(taps):
                            src = xbc[:, m, ds(b, 1), k:k + S].rearrange("p o t -> p (o t)")
                            last = k == taps - 1
                            dst = cv[:, 1 if last else 0, m % 2, :]
                            if k == 0:
                                a = nc.vector.tensor_scalar(dst, src, cvw[:, m, 0:1], cvw[:, m, taps:taps + 1],
                                                            ALU.mult, ALU.add)
                            else:
                                dve.wait_ge(chain, (4 * b + m) * (taps - 1) + k)
                                a = nc.vector.scalar_tensor_tensor(dst, src, cvw[:, m, k:k + 1], cv[:, 0, m % 2, :],
                                                                   ALU.mult, ALU.add)
                            a.then_inc(conv if last else chain, 1)

            @block.gpsimd
            def _(pool):
                pool.wait_ge(loaded, 96)
                for u in range(UNITS):
                    pool.wait_ge(z_silu, u + 1)
                    nc.gpsimd.tensor_tensor(zs[:, u, :], zs[:, u, :], lnw[:, :], ALU.mult)


def ssd_steps(net, tag, dt, e_cs, e_out, e_all, csp):
    nc, dram = net.nc, net.dram
    W = UNITS * SSD_HEADS
    flat = lambda t: t[:, :, :].rearrange("p u h -> p (u h)")
    with stage(nc, tag + "_dt") as (sb, ps, sem):
        tri = sb("triangle", [P, P])
        last = sb("last_row", [P, P])
        arow = sb("a_row", [P, 1, SSD_HEADS])
        t1, t2, t3 = sb("t1", [P, W]), sb("t2", [P, W]), sb("t3", [P, W])
        cs = sb("cs", [P, UNITS, SSD_HEADS])
        rest = sb("rest", [SSD_HEADS, 2, NT])
        pc = ps("cs", [P, W])
        pl = ps("cs_end", [P, W])
        pt = ps("turned", [SSD_HEADS, 2, NT])
        loaded, c, pe_done, turned, taken = (sem(n) for n in ("loaded", "chain", "products", "turned", "taken"))
        part = sem("parts")
        with nc.Block() as block:
            @block.sync
            def _(sp):
                sp.dma_start(tri[:, :], dram["triangle"]).then_inc(loaded, 16)
                sp.dma_start(last[:, :], dram["last_row"]).then_inc(loaded, 16)
                sp.dma_start(arow[:, 0, :], dram["d2_alog"].to_broadcast((P, SSD_HEADS))).then_inc(loaded, 16)

            @block.scalar
            def _(act):
                nc.scalar.preload_act_table_set("natural_log_exp_and_others")
                act.wait_ge(loaded, 48)
                nc.scalar.activation(t1[:, :], flat(dt), ACT.Abs).then_inc(c, 1)
                act.wait_ge(c, 1)
                nc.scalar.activation(t2[:, :], t1[:, :], ACT.Exp, scale=-1.0).then_inc(c, 1)
                act.wait_ge(c, 2)
                nc.scalar.activation(t3[:, :], t2[:, :], ACT.Ln, bias=net.one).then_inc(c, 1)
                nc.scalar.activation(arow[:, :, :], arow[:, :, :], ACT.Exp).then_inc(c, 1)
                act.wait_ge(c, 8)
                nc.scalar.activation(flat(e_cs), flat(cs), ACT.Exp).then_inc(c, 1)
                nc.scalar.activation(flat(e_all), t2[:, :], ACT.Exp).then_inc(c, 1)
                nc.scalar.activation(flat(e_out), t3[:, :], ACT.Exp).then_inc(c, 1)

            @block.vector
            def _(dve):
                nc.vector.memset(csp[96:P, :], 0.0)
                dve.wait_ge(c, 4)
                nc.vector.scalar_tensor_tensor(flat(dt), flat(dt), 0.0, t3[:, :], ALU.max, ALU.add).then_inc(c, 1)
                dve.wait_ge(c, 5)
                nc.vector.scalar_tensor_tensor(t1[:, :].rearrange("p (u h) -> p u h", u=UNITS), dt[:, :, :], -1.0,
                                               arow[:, :, :].to_broadcast((P, UNITS, SSD_HEADS)), ALU.mult,
                                               ALU.mult).then_inc(c, 1)
                dve.wait_ge(pe_done, 1)
                nc.vector.tensor_copy(flat(cs), pc[:, :]).then_inc(taken, 1)
                dve.wait_ge(pe_done, 2)
                nc.vector.tensor_copy(t2[:, :], pl[:, :]).then_inc(c, 1)
                dve.wait_ge(c, 7)
                dve.wait_ge(taken, 1)
                nc.vector.tensor_tensor(t3[:, :], t2[:, :], flat(cs), ALU.subtract).then_inc(c, 1)
                for m in range(TILES):
                    tok = slice(m * NT, (m + 1) * NT)
                    dve.wait_ge(turned, m + 1)
                    nc.vector.tensor_copy(csp[0:32, tok], pt[:, m % 2, :]).then_inc(part, 1)
                    dve.wait_ge(part, 4 * m + 1)
                    nc.vector.tensor_tensor(rest[:, m % 2, :], pt[:, m % 2, :], csp[0:32, tok],
                                            ALU.subtract).then_inc(part, 1)
                    dve.wait_ge(part, 4 * m + 2)
                    nc.vector.tensor_copy(csp[32:64, tok], rest[:, m % 2, :]).then_inc(part, 1)
                    dve.wait_ge(part, 4 * m + 3)
                    nc.vector.tensor_copy(t1[0:32, 0:NT], csp[32:64, tok]).then_inc(part, 1)
                    dve.wait_ge(part, 4 * m + 4)
                    nc.vector.tensor_tensor(csp[64:96, tok], rest[:, m % 2, :], t1[0:32, 0:NT],
                                            ALU.subtract).then_inc(taken, 1)
                dve.wait_ge(c, 11)
                first = lambda t: t[:, :, :].rearrange("p (b c) h -> p b c h", b=B)[:, :, 0, :]
                nc.vector.memset(first(e_cs), 0.0)
                nc.vector.memset(first(e_all), 0.0)

            @block.tensor
            def _(pe):
                pe.wait_ge(c, 6)
                for k in range(W // NT):
                    mm = nc.tensor.matmul(pc[:, k * NT:(k + 1) * NT], tri[:, :], t1[:, k * NT:(k + 1) * NT],
                                          start=True, stop=True)
                mm.then_inc(pe_done, 1)
                pe.wait_ge(taken, 1)
                for k in range(W // NT):
                    mm = nc.tensor.matmul(pl[:, k * NT:(k + 1) * NT], last[:, :],
                                          cs[:, :, :].rearrange("p u h -> p (u h)")[:, k * NT:(k + 1) * NT],
                                          start=True, stop=True)
                mm.then_inc(pe_done, 1)
                for u in range(UNITS):
                    if u % 4 == 0 and u >= 8:
                        pe.wait_ge(taken, u // 4)
                    mm = nc.tensor.transpose(pt[:, u // 4 % 2, u % 4 * P:(u % 4 + 1) * P], cs[:, u, :], net.ident[:, :])
                    if u % 4 == 3:
                        mm.then_inc(turned, 1)


def ssd_chunks(net, tag, xbc, dt, e_cs, e_out, e_all, csp, DI):
    nc, dram = net.nc, net.dram
    HG = 8
    NG = SSD_HEADS // HG
    wide = lambda t: t.to_broadcast((P, SSD_HEADS, SSD_P))
    with stage(nc, tag + "_chunks") as (sb, ps, sem):
        pick = sb("pick", [P, SSD_HEADS, P], BF16)
        npick = sb("neg_pick", [P, SSD_HEADS, P], BF16)
        mask = sb("mask", [P, 4, P], BF16)
        st = sb("chunk", [P, 2, 4, P])
        gs = sb("cb", [P, 2, 1, P])
        bt = sb("b_tokens", [P, 2, P])
        xd = sb("x_dt", [P, 2, SSD_HEADS, SSD_P])
        xe = sb("x_dt_rest", [P, 2, SSD_HEADS, SSD_P])
        dec = sb("decay", [P, 2, HG, P])
        mt = sb("mixed", [P, 2, HG, P])
        state = sb("state", [P, SSD_HEADS, SSD_P])
        yo = sb("y_off", [P, SSD_HEADS, SSD_P])
        pg = ps("cb_turned", [P, NT])
        pl = [ps(f"decay{n}", [P, HG, P]) for n in range(2)]
        py, po, pst = ps("y_diag", [P, NT]), ps("y_off", [P, NT]), ps("state", [P, NT])
        loaded, staged, g_ready, g_taken, l_ready, l_done, m_done = (sem(n) for n in (
            "loaded", "staged", "cb", "cb_taken", "decay", "exp_done", "mixed"))
        st_chain, o_ready, s_ready, s_done, yo_done, y_done, h_used = (sem(n) for n in (
            "state_scaled", "y_off", "state_in", "state", "y_off_scaled", "y", "mixed_used"))
        with nc.Block() as block:
            @block.sync
            def _(sp):
                sp.dma_start(pick[:, :, :], dram["bc_spread"]).then_inc(loaded, 16)
                sp.dma_start(npick[:, :, :], dram["neg_pick"]).then_inc(loaded, 16)
                for j in range(4):
                    sp.dma_start(mask[:, j, :], dram["mask_k"]).then_inc(loaded, 16)

            def units(eng, one, first=None):
                with eng.Fori(0, B) as b:
                    if first:
                        first(b * CPS, 0)
                    with eng.Fori(0, CPS // 2 - 1) as c2:
                        for p in range(2):
                            one(b * CPS + 2 * c2 + p, b, 2 * c2 + p, p, True)
                    for p in range(2):
                        one(b * CPS + CPS - 2 + p, b, CPS - 2 + p, p, p == 0)

            @block.gpsimd
            def _(pool):
                def one(u, b, c, p, more):
                    pool.wait_ge(y_done, u + 1)
                    src = xbc[:, :, ds(b, 1), ds(c * P, P)].rearrange("p m o t -> p m (o t)")
                    nc.gpsimd.tensor_copy(st[:, p, :, :], src).then_inc(staged, 1)

                units(pool, one)

            @block.tensor
            def _(pe):
                pe.wait_ge(loaded, 96)

                def prepare(u, p):
                    pe.wait_ge(staged, u + 1)
                    pe.wait_ge(g_taken, 4 * u + 1)
                    nc.tensor.matmul(pg[:, 0:P], st[:, p, 2, :], st[:, p, 3, :], start=True, stop=True)
                    for j in range(3):
                        mm = nc.tensor.transpose(pg[:, (j + 1) * P:(j + 2) * P], st[:, p, j, :], net.ident[:, :])
                    mm.then_inc(g_ready, 1)

                def decays(u, g):
                    pe.wait_ge(l_done, NG * u + g + 1)
                    for q in range(2):
                        h0 = g * HG + 4 * q
                        dst = pl[g % 2][:, 4 * q:4 * q + 4, :]
                        nc.tensor.matmul(dst, net.identb[:, :], mask[:, :, :], start=True, stop=False)
                        nc.tensor.matmul(dst, csp[:, ds(u * P, P)], npick[:, h0:h0 + 4, :], start=False, stop=False)
                        for j in range(4):
                            mm = nc.tensor.matmul(dst[:, j, :], pick[:, h0 + j, :], csp[:, ds(u * P, P)],
                                                  start=False, stop=(j == 3))
                    mm.then_inc(l_ready, 1)

                def first(u, p):
                    prepare(u, p)
                    decays(u, 0)
                    decays(u, 1)

                def one(u, b, c, p, more):
                    def values(g):
                        pe.wait_ge(m_done, NG * u + g + 3)
                        if g == 0:
                            pe.wait_ge(y_done, u + 2)
                        for h in range(HG):
                            hh = g * HG + h
                            mm = nc.tensor.matmul(py[:, hh * SSD_P:(hh + 1) * SSD_P], mt[:, g % 2, h, :],
                                                  xd[:, p, hh, :], start=True, stop=True)
                        mm.then_inc(h_used, 1)

                    pe.wait_ge(s_done, u + 1)
                    pe.wait_ge(yo_done, u + 1)
                    nc.tensor.matmul(po[:, 0:DI], st[:, p, 3, :], state[:, :, :].rearrange("p h e -> p (h e)"),
                                     start=True, stop=True).then_inc(o_ready, 1)
                    pe.wait_ge(g_taken, 4 * u + 5)
                    nc.tensor.matmul(pst[:, 0:DI], bt[:, p, :], xe[:, p, :, :].rearrange("p h e -> p (h e)"),
                                     start=True, stop=True).then_inc(s_ready, 1)
                    decays(u, 2)
                    values(0)
                    decays(u, 3)
                    values(1)
                    if more:
                        prepare(u + 1, 1 - p)
                        decays(u + 1, 0)
                    values(2)
                    if more:
                        decays(u + 1, 1)
                    values(3)

                units(pe, one, first)

            @block.scalar
            def _(act):
                nc.scalar.preload_act_table_set("natural_log_exp_and_others")
                act.sem_inc(l_done, 2)

                def one(u, b, c, p, more):
                    for g in range(NG):
                        act.wait_ge(l_ready, NG * u + g + 1)
                        act.wait_ge(m_done, NG * u + g + 1)
                        nc.scalar.activation(dec[:, g % 2, :, :], pl[g % 2][:, :, :], ACT.Exp).then_inc(l_done, 1)

                units(act, one)

            @block.vector
            def _(dve):
                nc.vector.memset(state[:, :, :], 0.0).then_inc(s_done, 1)
                dve.sem_inc(y_done, 2)
                dve.sem_inc(yo_done, 1)
                dve.sem_inc(g_taken, 1)
                dve.sem_inc(h_used, 2)
                dve.sem_inc(m_done, 2)
                v = lambda t, u: t[:, ds(u, 1), :].rearrange("p o h -> p h o")

                def take(u, p):
                    tok = pg[:, P:P + DI].rearrange("p (h e) -> p h e", e=SSD_P)
                    dve.wait_ge(g_ready, u + 1)
                    nc.vector.tensor_copy(gs[:, p, 0, :], pg[:, 0:P]).then_inc(g_taken, 1)
                    nc.vector.tensor_tensor(xd[:, p, :, :], tok, wide(v(dt, u)), ALU.mult).then_inc(g_taken, 1)
                    nc.vector.tensor_copy(bt[:, p, :], pg[:, P + DI:P + DI + P]).then_inc(g_taken, 1)
                    dve.wait_ge(g_taken, 4 * u + 4)
                    nc.vector.tensor_tensor(xe[:, p, :, :], xd[:, p, :, :], wide(v(e_out, u)), ALU.mult).then_inc(g_taken, 1)

                def one(u, b, c, p, more):
                    def mix(g):
                        dve.wait_ge(l_done, NG * u + g + 3)
                        dve.wait_ge(g_taken, 4 * u + 5)
                        dve.wait_ge(h_used, NG * u + g + 1)
                        nc.vector.tensor_tensor(mt[:, g % 2, :, :], dec[:, g % 2, :, :],
                                                gs[:, p, :, :].to_broadcast((P, HG, P)), ALU.mult).then_inc(m_done, 1)

                    mix(0)
                    dve.wait_ge(o_ready, u + 1)
                    dve.wait_ge(y_done, u + 2)
                    nc.vector.tensor_tensor(yo[:, :, :], po[:, 0:DI].rearrange("p (h e) -> p h e", e=SSD_P),
                                            wide(v(e_cs, u)), ALU.mult).then_inc(yo_done, 1)
                    nc.vector.tensor_tensor(state[:, :, :], state[:, :, :], wide(v(e_all, u)), ALU.mult).then_inc(st_chain, 1)
                    mix(1)
                    dve.wait_ge(s_ready, u + 1)
                    dve.wait_ge(st_chain, u + 1)
                    nc.vector.tensor_tensor(state[:, :, :], pst[:, 0:DI].rearrange("p (h e) -> p h e", e=SSD_P),
                                            state[:, :, :], ALU.add).then_inc(s_done, 1)
                    mix(2)
                    mix(3)
                    if more:
                        take(u + 1, 1 - p)
                    dve.wait_ge(h_used, NG * u + NG + 2)
                    dve.wait_ge(yo_done, u + 2)
                    dst = xbc[:, 0:2, ds(b, 1), ds(c * P, P)].rearrange("p m o t -> p m (o t)")
                    nc.vector.tensor_tensor(dst, py[:, 0:DI].rearrange("p (m t) -> p m t", m=2),
                                            yo[:, :, :].rearrange("p (m h) e -> p m (h e)", m=2), ALU.add
                                            ).then_inc(y_done, 1)

                units(dve, one, take)


def ssd_output(net, tag, xbc, zs, w_out, DI):
    nc, x = net.nc, net.x
    with stage(nc, tag + "_out") as (sb, ps, sem):
        sq = sb("squares", [P, CPS, DI])
        st = sb("stats", [P, 6, CPS, 1])
        yn = sb("gated", [P, 2, CPS, DI])
        yt = sb("turned", [P, 2, 2, NT])
        py = ps("turned", [P, 2, 2, NT])
        po = ps("proj", [P, 2, NT])
        c, normed, turned, copied, ready, done = (sem(n) for n in (
            "chain", "normed", "turned", "copied", "ready", "done"))
        with nc.Block() as block:
            @block.vector
            def _(dve):
                n = [0]

                def step(a):
                    a.then_inc(c, 1)
                    n[0] += 1
                    dve.wait_ge(c, n[0])

                wide = lambda t: t.to_broadcast((P, CPS, DI))

                def normalize(b):
                    y = xbc[:, 0:2, b, 0:S].rearrange("p m (c t) -> p c m t", t=P)
                    if b >= 2:
                        dve.wait_ge(turned, 2 * (b - 1))
                    g = yn[:, b % 2, :, :]
                    g4 = g.rearrange("p c (m t) -> p c m t", m=2)
                    step(nc.vector.tensor_reduce(st[:, 0, :, 0], y, AX.XY, ALU.add))
                    step(nc.vector.tensor_scalar(st[:, 1, :, :], st[:, 0, :, :], 1.0 / DI, None, ALU.mult))
                    step(nc.vector.tensor_tensor(g4, y, st[:, 1, :, :].unsqueeze(2).to_broadcast((P, CPS, 2, P)), ALU.subtract))
                    step(nc.vector.tensor_tensor(sq[:, :, :], g, g, ALU.mult))
                    step(nc.vector.tensor_reduce(st[:, 2, :, 0], sq[:, :, :], AX.X, ALU.add))
                    dve.wait_ge(c, n[0] + 2)
                    n[0] += 2
                    step(nc.vector.tensor_tensor(g, g, wide(st[:, 4, :, :]), ALU.mult))
                    step(nc.vector.tensor_tensor(g, g, zs[:, b * CPS:(b + 1) * CPS, :], ALU.mult))
                    dve.sem_inc(normed, 1)

                def add(t):
                    dve.wait_ge(ready, t + 1)
                    nc.vector.tensor_tensor(x[:, t * NT:(t + 1) * NT], po[:, t % 2, :], x[:, t * NT:(t + 1) * NT],
                                            ALU.add).then_inc(done, 1)

                normalize(0)
                for b in range(B):
                    if b + 1 < B:
                        normalize(b + 1)
                    add(2 * b)
                    add(2 * b + 1)

            @block.scalar
            def _(act):
                nc.scalar.preload_act_table_set("natural_log_exp_and_others")
                def root(b):
                    act.wait_ge(c, 9 * b + 5)
                    nc.scalar.activation(st[:, 3, :, :], st[:, 2, :, :], ACT.Ln, bias=net.ln_eps,
                                         scale=1.0 / DI).then_inc(c, 1)
                    act.wait_ge(c, 9 * b + 6)
                    nc.scalar.activation(st[:, 4, :, :], st[:, 3, :, :], ACT.Exp, scale=-0.5).then_inc(c, 1)

                def copy(t):
                    act.wait_ge(turned, t + 1)
                    if t >= 2:
                        act.wait_ge(ready, t - 1)
                    nc.scalar.activation(yt[:, t % 2, :, :], py[:, t % 2, :, :], ACT.Copy).then_inc(copied, 1)

                root(0)
                for b in range(B):
                    if b + 1 < B:
                        root(b + 1)
                    copy(2 * b)
                    copy(2 * b + 1)

            @block.tensor
            def _(pe):
                for t in range(TILES):
                    b = t // 2
                    pe.wait_ge(normed, b + 1)
                    if t >= 2:
                        pe.wait_ge(copied, t - 1)
                    for m in range(2):
                        for k in range(4):
                            mm = nc.tensor.transpose(py[:, t % 2, m, k * P:(k + 1) * P],
                                                     yn[:, b % 2, 4 * (t % 2) + k, m * P:(m + 1) * P], net.ident[:, :])
                    mm.then_inc(turned, 1)
                    pe.wait_ge(copied, t + 1)
                    if t >= 2:
                        pe.wait_ge(done, t - 1)
                    for m in range(2):
                        mm = nc.tensor.matmul(po[:, t % 2, :], w_out[:, m, :], yt[:, t % 2, m, :],
                                              start=(m == 0), stop=(m == 1))
                    mm.then_inc(ready, 1)


def build(nc, dram, out):
    with ExitStack() as ctx:
        net = Net(nc, ctx, dram)
        load_consts(net)
        for l in LAYERS:
            if l in (1, 3):
                ternary_ffn(net, f"l{l}", "f0_up", "f0_dn", True, 0.0)
            if l in (9, 11):
                ternary_ffn(net, f"l{l}", "f2_up", "f2_dn", False, 1e-8, "f2_b1", "f2_b2")
            if l == 2:
                attention(net, "l2", dict(wq="a0_wq", wk="a0_wk", wv="a0_wv", wo="a0_wo"), 8, 8 ** -0.5, decay=True)
            if l in (4, 6):
                n = "a1" if l == 4 else "b1"
                attention(net, f"l{l}", {m: f"{n}_{m}" for m in ("wq", "wk", "wq_sw", "wk_sw", "wv", "wo", "bq", "bk",
                                                                 "bq_sw", "bk_sw", "bv", "bo")},
                          8, 8 ** -0.5, rope=True, bias=True, out_bias=True)
            if l == 8:
                attention(net, "l8", {m: f"a2_{m}" for m in ("wq", "wk", "wv", "wo", "bq", "bk", "bv", "bo")},
                          8, 8 ** -0.5, bias=True, out_bias=True)
            if l in (5, 7):
                experts_ffn(net, f"l{l}", dict(router="m1_router", fc="m1_fc", proj="m1_proj"))
            if l in (13, 15):
                gated_ffn(net, f"l{l}")
            if l == 10:
                ssd(net, "l10")
            if l == 0:
                selective_ssm(net, "l0", "s0_", 2, 4, 3, True, True, True, True)
            if l == 12:
                selective_ssm(net, "l12", "s3_", 1, 3, 1, False, False, False, False)
            if l == 14:
                attention(net, "l14", {m: f"b3_{m}" for m in ("wq", "wk", "wv", "wo", "bo")}, 4, 0.5,
                          alibi=True, out_bias=True)
        store_out(net, out)


def thirds(a):
    bf = mybir.dt.np(BF16)
    hi = a.astype(bf)
    mid = (a - hi.astype(np.float32)).astype(bf)
    low = (a - hi.astype(np.float32) - mid.astype(np.float32)).astype(bf)
    return np.stack([hi, mid, low])


def shape_constants():
    bf = mybir.dt.np(BF16)
    f = np.float32
    pos = np.arange(S, dtype=f)
    d = np.arange(P) % 8
    freq = (1.0 / 10000.0 ** ((d // 2 * 2).astype(f) / 8)).astype(f)
    theta = pos[None] * freq[:, None]
    sign = np.where(d % 2 == 0, -1.0, 1.0).astype(f)[:, None]
    rope = np.stack([np.cos(theta), np.sin(theta) * sign], 1).astype(f)
    i = np.arange(P)
    mask_q = np.where(i[:, None] < i[None], NEG, 0.0).astype(bf)
    nums = np.linspace(0.0, 1.0, 241).astype(f)
    vals = np.concatenate([np.ones(15, f), 1.0 - nums ** f(1.0 / np.e)]).astype(f)
    dist = np.clip(np.arange(DECAY_SPAN)[None] - i[:, None], 0, 255)
    slopes = (2.0 ** (-8.0 * np.arange(1, HEADS + 1) / HEADS)).astype(f)
    sl = np.broadcast_to(thirds(slopes)[:, :, None], (3, HEADS, S))
    nq = thirds(-(slopes[:, None] * pos[None]))
    aq = np.concatenate([sl, sl, nq]).reshape(9, 4, 4, S).transpose(1, 0, 2, 3)
    hi, lo = np.floor(pos / 8) * 8, pos % 8
    ak = np.broadcast_to(np.stack([hi] * 3 + [lo] * 3 + [np.ones(S, f)] * 3)[:, None], (9, 4, S)).astype(bf)
    sel = np.broadcast_to(np.eye(P, EXPERTS, dtype=f)[:, :, None], (P, EXPERTS, P)).astype(bf)
    spread = np.zeros((P, 32, P), bf)
    for part in range(3):
        for n in range(32):
            spread[32 * part + n, n] = 1.0
    ones9 = np.zeros((P, 9), f)
    ones9[:, 8] = 1.0
    return {
        "ident": np.eye(P, dtype=f), "rope": rope, "mask_q": mask_q, "mask_k": mask_q.T,
        "decay": vals[dist], "ones9": ones9, "ones_rows": np.ones((3, 4, S), bf), "zero_rows": np.zeros((3, 4, S), bf),
        "alibi_q": np.tile(aq, (4, 1, 1, 1)).reshape(GROUPS * 9, 4, S), "alibi_k": ak, "expert_select": sel, "bc_spread": spread, "neg_pick": -spread,
        "triangle": (i[:, None] <= i[None]).astype(f), "last_row": np.broadcast_to((i == P - 1)[:, None], (P, P)).astype(f),
    }


def attention_layouts(i):
    row, one = (lambda v: v.reshape(1, -1)), (lambda v: v.reshape(-1, 1))
    swap = np.arange(P) ^ 1
    out = {}
    w = i["L0_attn_b_W_attn"]
    out.update(a0_wq=w[:, :P], a0_wk=w[:, P:2 * P], a0_wv=w[:, 2 * P:], a0_wo=i["L0_attn_b_W_proj"])
    for n, wn, f in (("a1", "L1_attn_a_w", lambda m: m.T), ("b1", "L1_attn_b_W", lambda m: m)):
        q, k, bq, bk = f(i[wn + "q"]), f(i[wn + "k"]), i[wn[:-1] + "bq"], i[wn[:-1] + "bk"]
        out.update({f"{n}_wq": q, f"{n}_wk": k, f"{n}_wv": f(i[wn + "v"]), f"{n}_wo": f(i[wn + "o"]),
                    f"{n}_wq_sw": q[:, swap], f"{n}_wk_sw": k[:, swap], f"{n}_bq": one(bq), f"{n}_bk": one(bk),
                    f"{n}_bq_sw": one(bq[swap]), f"{n}_bk_sw": one(bk[swap]),
                    f"{n}_bv": row(i[wn[:-1] + "bv"]), f"{n}_bo": one(i[wn[:-1] + "bo"])})
    w = i["L2_attn_a_attn_W"].reshape(D, HEADS, 3, 8)
    b = i["L2_attn_a_attn_b"].reshape(HEADS, 3, 8)
    for j, n in enumerate("qkv"):
        out[f"a2_w{n}"] = w[:, :, j].reshape(D, P)
        out[f"a2_b{n}"] = (row if n == "v" else one)(b[:, j].reshape(P))
    out.update(a2_wo=i["L2_attn_a_out_W"], a2_bo=one(i["L2_attn_a_out_b"]))
    out.update(b3_wq=np.tile(i["L3_attn_b_Wq"], (1, 2)), b3_wk=np.tile(i["L3_attn_b_Wk"], (1, 8)),
               b3_wv=np.tile(i["L3_attn_b_Wv"], (1, 4)), b3_wo=i["L3_attn_b_Wp"], b3_bo=one(i["L3_attn_b_bp"]))
    return out


def ffn_layouts(i):
    col = lambda v: v.reshape(-1, P).T
    kcn = lambda w: w.reshape(HC, P, -1).transpose(1, 0, 2)
    g = lambda n: i["L3_ffn_" + n]
    return {
        "m1_router": i["L1_ffn_router_w"].T,
        "m1_fc": i["L1_ffn_expert_fc"].transpose(1, 0, 2),
        "m1_proj": i["L1_ffn_expert_proj"].transpose(2, 0, 1).reshape(HC, P, EXPERTS, P).transpose(1, 2, 0, 3),
        "g3_w1": g("w1_w").T, "g3_w2": g("w2_w").T, "g3_h1": kcn(g("h1_w").T), "g3_h2": kcn(g("h2_w").T),
        "g3_w3": kcn(g("w3_w").T),
        "g3_scales": np.concatenate([col(g(n)) for n in ("w1_s", "w2_s", "h1_s", "h2_s", "w3_s")], 1),
    }


def ssm_layouts(i):
    f = np.float32
    hcol = lambda v: v.reshape(-1, P).T

    def cols(H, taps, **c):
        out = np.zeros((P, 64), f)
        for at, n in ((0, "bin"), (4, "cvb"), (6, "dtb"), (8, "dbb"), (9, "rms"), (10, "bout")):
            if n in c:
                v = np.zeros(-(-c[n].size // P) * P, f)
                v[:c[n].size] = c[n]
                v = hcol(v)
                out[:, at:at + v.shape[1]] = v
        out[:, 16:16 + H * taps] = c["cvw"].reshape(H, P, taps).transpose(1, 0, 2).reshape(P, H * taps)
        return out

    def chunks(m, H):
        return m.reshape(H, P, -1).transpose(1, 0, 2)

    def triple(bc, extra=None):
        z = np.zeros(bc.shape[:-1] + (32,), f)
        if extra is not None:
            z[..., :extra.shape[-1]] = extra
        return np.concatenate([bc, bc, bc, z], -1)

    g = lambda n: i["L0_attn_a_" + n]
    W, b = g("dbc_W"), g("dbc_b")
    dup = np.zeros((P, 2, P), f)
    dup[96:112] = g("dup_W").reshape(16, 2, P)
    out = {
        "s0_win": g("in_W"), "s0_a": g("A_log").reshape(2, P, NS).transpose(1, 0, 2),
        "s0_cols": cols(2, 4, bin=g("in_b"), cvb=g("conv_b"), dtb=g("dup_b"), dbb=triple(b[16:], b[:16]),
                        rms=g("rms_w"), bout=g("out_b"), cvw=g("conv_w")),
        "s0_dbc": chunks(triple(W[:, 16:], W[:, :16]), 2), "s0_dt": dup, "s0_out": chunks(g("out_W"), 2),
    }
    g = lambda n: i["L3_attn_a_" + n]
    out.update({
        "s3_win": np.concatenate([g("Win"), g("Wg")], 1), "s3_a": g("A")[:, None],
        "s3_cols": cols(1, 3, bin=np.concatenate([g("b_in"), g("bg")]), cvb=g("convb"), dtb=g("bdt"),
                        dbb=triple(np.concatenate([g("bb"), g("bc")])), bout=g("bout"), cvw=g("convw")),
        "s3_dbc": triple(np.concatenate([g("Wb"), g("Wc")], 1))[:, None], "s3_dt": g("Wdt")[:, None],
        "s3_out": g("Wout")[:, None],
    })
    return out


def ssd_layouts(i):
    g = lambda n: i["L2_attn_b_" + n]
    w = g("in_proj_w").T
    conv = np.concatenate([g("conv_w"), g("conv_b")[:, None]], 1).reshape(4, P, 5).transpose(1, 0, 2)
    return {
        "d2_w": w[:, 256:768], "d2_wz": np.concatenate([w[:, :256], w[:, 768:]], 1), "d2_conv": conv,
        "d2_out": g("out_proj_w").T.reshape(2, P, D).transpose(1, 0, 2), "d2_dtb": g("dt_bias").reshape(1, -1),
        "d2_lnw": g("ln_w").reshape(1, -1), "d2_alog": g("A_log").reshape(1, -1),
    }


def layouts(i):
    col = lambda v: np.ascontiguousarray(v.reshape(-1, P).T)
    return {
        "x": i["L0_attn_a_x"].reshape(T, D).T,
        **shape_constants(), **attention_layouts(i), **ffn_layouts(i), **ssm_layouts(i), **ssd_layouts(i),
        "f0_up": i["L0_ffn_w_up"].T,
        "f0_dn": i["L0_ffn_w_down"].T,
        "f2_up": i["L2_ffn_W1"].T,
        "f2_dn": i["L2_ffn_W2"].T,
        "f2_b1": col(i["L2_ffn_b1"]),
        "f2_b2": col(i["L2_ffn_b2"]),
    }


def kernel(**inputs):
    import concourse.bacc as bacc
    from concourse.bass_utils import run_bass_kernel_spmd

    nc = bacc.Bacc("TRN2", target_bir_lowering=False, num_devices=1)
    arrays = {n: np.ascontiguousarray(a) for n, a in layouts({k: np.asarray(v) for k, v in inputs.items()}).items()}
    dram = {n: nc.dram_tensor(n + "_dram", a.shape, mybir.dt.from_np(a.dtype), kind="ExternalInput").ap()
            for n, a in arrays.items()}
    out = nc.dram_tensor("out_dram", (P, T), F32, kind="ExternalOutput").ap()
    build(nc, dram, out)
    r = run_bass_kernel_spmd(nc, [{n + "_dram": a for n, a in arrays.items()}], core_ids=[0])
    return np.ascontiguousarray(r.results[0]["out_dram"].T).reshape(B, S, D)
```

```python
from contextlib import ExitStack, contextmanager

import numpy as np
import concourse.bass as bass
from concourse import mybir

ALU = mybir.AluOpType
ACT = mybir.ActivationFunctionType
AX = mybir.AxisListType
F32 = mybir.dt.float32
BF16 = mybir.dt.bfloat16
ds = bass.ds

LAYERS = list(range(16))
P = 128
B, S, D = 4, 1024, 128
T = B * S
NT = 512
TILES = T // NT
LN_EPS = 1e-5
RMS_EPS = 1e-6
RMS_FLOOR = 1e-8
NEG = -1e30


@contextmanager
def stage(nc, tag):
    with ExitStack() as ctx:
        sems = []

        def sb(name, shape, dt=F32):
            return ctx.enter_context(nc.sbuf_tensor(f"{tag}_{name}", shape, dt))

        def ps(name, shape):
            return ctx.enter_context(nc.psum_tensor(f"{tag}_ps_{name}", shape, F32))

        def sem(name):
            s = nc.alloc_semaphore(f"{tag}_{name}")
            sems.append(s)
            return s

        yield sb, ps, sem
        nc.clear_and_free_semaphores(sems)
        nc.all_engine_barrier()


class Net:

    def __init__(self, nc, ctx, dram):
        self.nc, self.dram = nc, dram
        sb = lambda n, s, d=F32: ctx.enter_context(nc.sbuf_tensor(n, s, d))
        self.x = sb("x_res", [P, T])
        self.xn = sb("x_norm", [P, T])
        self.ident = sb("ident", [P, P])
        self.center = sb("center", [P, P])
        self.ones = sb("ones_over_1", [P, P])
        self.mean = sb("ones_over_d", [P, P])
        self.identb = sb("ident_bf16", [P, P], BF16)
        self.cols = sb("const_cols", [P, 8])
        self.ln_eps = self.cols[:, 0:1]
        self.rms_eps = self.cols[:, 1:2]
        self.one = self.cols[:, 2:3]
        self.zero = self.cols[:, 3:4]
        self.rms_floor = self.cols[:, 4:5]


def load_consts(net):
    nc = net.nc
    with stage(nc, "init") as (sb, ps, sem):
        loaded, made = sem("loaded"), sem("made")
        with nc.Block() as block:
            @block.sync
            def _(sp):
                sp.dma_start(net.x[:, :], net.dram["x"]).then_inc(loaded, 16)
                sp.dma_start(net.ident[:, :], net.dram["ident"]).then_inc(loaded, 16)
                sp.wait_ge(loaded, 32)

            @block.vector
            def _(dve):
                for j, v in enumerate((LN_EPS, RMS_EPS, 1.0, 0.0, RMS_FLOOR)):
                    nc.vector.memset(net.cols[:, j:j + 1], v)
                nc.vector.memset(net.ones[:, :], 1.0)
                nc.vector.memset(net.mean[:, :], 1.0 / D)
                dve.wait_ge(loaded, 32)
                nc.vector.tensor_scalar(net.center[:, :], net.ident[:, :], -1.0 / D, None, ALU.add)
                nc.vector.tensor_copy(net.identb[:, :], net.ident[:, :])


def store_out(net, out):
    nc = net.nc
    with stage(nc, "fin") as (sb, ps, sem):
        stored = sem("stored")
        with nc.Block() as block:
            @block.sync
            def _(sp):
                sp.dma_start(out, net.x[:, :]).then_inc(stored, 16)
                sp.wait_ge(stored, 16)


def layer_norm(net, tag, rms=None):
    nc = net.nc
    x, xn = net.x, net.xn
    R = 4
    with stage(nc, tag) as (sb, ps, sem):
        cen = ps("centered", [P, R, NT])
        var = ps("var", [P, R, NT])
        sq = sb("squares", [P, R, NT])
        lnv = sb("log_var", [P, R, NT])
        rstd = sb("rstd", [P, R, NT])
        ms = sb("mean_square", [P, R, NT]) if rms else None
        root = sb("root", [P, R, NT]) if rms else None
        cen_free = sem("centered_free")
        cen_ready, sq_ready, var_ready = sem("centered"), sem("squares"), sem("var")
        ln_ready, rstd_ready = sem("log_var"), sem("rstd")
        xn_ready, ms_ready, log_ready, root_ready, logr_ready, fac_ready = (sem(n) for n in (
            "xn", "ms", "log_ms", "root", "log_root", "factor"))
        with nc.Block() as block:
            @block.tensor
            def _(pe):
                for t in range(TILES + 1):
                    if t < TILES:
                        if t >= R:
                            pe.wait_ge(cen_free, t - R + 1)
                        nc.tensor.matmul(cen[:, t % R, :], net.center[:, :], x[:, t * NT:(t + 1) * NT],
                                         start=True, stop=True).then_inc(cen_ready, 1)
                    if t >= 1:
                        pe.wait_ge(sq_ready, t)
                        nc.tensor.matmul(var[:, (t - 1) % R, :], net.mean[:, :], sq[:, (t - 1) % R, :],
                                         start=True, stop=True).then_inc(var_ready, 1)

            @block.scalar
            def _(act):
                nc.scalar.preload_act_table_set("natural_log_exp_and_others")

                def square(t):
                    act.wait_ge(cen_ready, t + 1)
                    nc.scalar.activation(sq[:, t % R, :], cen[:, t % R, :], ACT.Square).then_inc(sq_ready, 1)

                def log_var(t):
                    act.wait_ge(var_ready, t + 1)
                    if t >= R:
                        act.wait_ge(rstd_ready, t - R + 1)
                    nc.scalar.activation(lnv[:, t % R, :], var[:, t % R, :], ACT.Ln, bias=net.ln_eps).then_inc(ln_ready, 1)

                def inverse_root(t):
                    act.wait_ge(ln_ready, t + 1)
                    if t >= R:
                        act.wait_ge(ms_ready if rms else xn_ready, t - R + 1)
                    nc.scalar.activation(rstd[:, t % R, :], lnv[:, t % R, :], ACT.Exp, scale=-0.5).then_inc(rstd_ready, 1)

                def log_ms(t):
                    act.wait_ge(ms_ready, t + 1)
                    if t >= R:
                        act.wait_ge(fac_ready, t - R + 1)
                    nc.scalar.activation(root[:, t % R, :], ms[:, t % R, :], ACT.Ln).then_inc(log_ready, 1)

                def root_ms(t):
                    act.wait_ge(log_ready, t + 1)
                    nc.scalar.activation(root[:, t % R, :], root[:, t % R, :], ACT.Exp, scale=0.5).then_inc(root_ready, 1)

                def log_root(t):
                    act.wait_ge(root_ready, t + 1)
                    nc.scalar.activation(root[:, t % R, :], root[:, t % R, :], ACT.Ln,
                                         bias=net.rms_floor).then_inc(logr_ready, 1)

                def factor(t):
                    act.wait_ge(logr_ready if rms[0] == "div" else log_ready, t + 1)
                    nc.scalar.activation(rms[2][:, t * NT:(t + 1) * NT], root[:, t % R, :], ACT.Exp,
                                         scale=-1.0 if rms[0] == "div" else -0.5).then_inc(fac_ready, 1)

                steps = [(0, square), (1, log_var), (1, inverse_root)]
                if rms:
                    steps += [(4, log_ms), (5, root_ms), (6, log_root), (7, factor)] if rms[0] == "div" else [
                        (5, log_ms), (6, factor)]
                for t in range(TILES + steps[-1][0]):
                    for lag, step in steps:
                        if 0 <= t - lag < TILES:
                            step(t - lag)

            @block.vector
            def _(dve):
                for t in range(TILES):
                    dve.wait_ge(rstd_ready, t + 1)
                    a = nc.vector.tensor_tensor(xn[:, t * NT:(t + 1) * NT], cen[:, t % R, :], rstd[:, t % R, :], ALU.mult)
                    if not rms:
                        a.then_inc(xn_ready, 1)
                        dve.wait_ge(xn_ready, t + 1)
                        dve.sem_inc(cen_free, 1)
                        continue
                    if t >= R:
                        dve.wait_ge(log_ready, t - R + 1)
                    nc.vector.tensor_tensor(ms[:, t % R, :], var[:, t % R, :], rstd[:, t % R, :],
                                            ALU.mult).then_inc(cen_free, 1)
                    dve.wait_ge(cen_free, t + 1)
                    nc.vector.tensor_tensor(ms[:, t % R, :], ms[:, t % R, :], rstd[:, t % R, :],
                                            ALU.mult).then_inc(xn_ready, 1)
                    dve.wait_ge(xn_ready, t + 1)
                    nc.vector.tensor_scalar(ms[:, t % R, :], ms[:, t % R, :], 1e-19 if rms[0] == "div" else rms[1], None,
                                            ALU.max if rms[0] == "div" else ALU.add).then_inc(ms_ready, 1)


def ternary_ffn(net, tag, wup, wdn, rms_in, floor, b1=None, b2=None):
    nc, x, xn = net.nc, net.x, net.xn
    FC = 4
    NW = P * FC * P
    with stage(nc, tag) as (sb, ps, sem):
        if rms_in:
            fac = sb("rms_factor", [P, T])
            layer_norm(net, tag + "_ln", ("div", RMS_FLOOR, fac))
        else:
            layer_norm(net, tag + "_ln")
        w = [sb("w_up", [P, FC * P]), sb("w_down", [P, FC * P])]
        wt = [sb("q_up", [P, FC * P]), sb("q_down", [P, FC * P])]
        neg = sb("below", [P, FC * P])
        absum = sb("abs_sum", [P, 2])
        thr = sb("threshold", [P, 4])
        bias = sb("biases", [P, 8])
        g = sb("hidden", [P, 2, FC, NT])
        gsq = sb("hidden_sq", [P, FC, NT])
        ssum = sb("sum_sq", [P, NT])
        y = sb("down", [P, T])
        msq = sb("mean_sq", [P, T]) if rms_in else None
        pw = ps("weight_sum", [P, NT])
        ph = ps("up", [P, 2, 2, NT])
        py = ps("down_acc", [P, 2, NT])
        pm = ps("ms_acc", [P, NT])
        w_in, abs_ready, wsum_ready, w_ready, chain = (sem(n) for n in (
            "weights_in", "abs_ready", "wsum_ready", "w_ready", "chain"))
        x_ready, up_ready, gelu_done, g_free = (sem(n) for n in (
            "x_ready", "up_ready", "gelu_done", "g_free"))
        ss_ready, dn_ready, dn_free, tail_a, tail_b = (sem(n) for n in (
            "ss_ready", "dn_ready", "dn_free", "tail_act", "tail_dve"))
        with nc.Block() as block:
            @block.sync
            def _(sp):
                sp.dma_start(w[0][:, :], net.dram[wup]).then_inc(w_in, 16)
                sp.dma_start(w[1][:, :].rearrange("p (k d) -> p k d", k=FC),
                             net.dram[wdn].rearrange("(k p) d -> p k d", p=P)).then_inc(w_in, 16)
                if b1:
                    sp.dma_start(bias[:, 0:4], net.dram[b1]).then_inc(w_in, 16)
                    sp.dma_start(bias[:, 4:5], net.dram[b2]).then_inc(w_in, 16)

            def down(pe, i, p):
                pe.wait_ge(gelu_done, 4 * i + 2 * p + 4)
                pe.wait_ge(dn_free, 2 * i + p + 1)
                for k in range(FC):
                    mm = nc.tensor.matmul(py[:, p, :], wt[1][:, k * P:(k + 1) * P], g[:, p, k, :],
                                          start=(k == 0), stop=(k == FC - 1))
                mm.then_inc(dn_ready, 1)
                if rms_in:
                    pe.wait_ge(ss_ready, 2 * i + p + 1)
                    nc.tensor.matmul(pm[:, :], net.ones[:, :], ssum[:, :], start=True, stop=True).then_inc(dn_ready, 1)

            @block.tensor
            def _(pe):
                pe.wait_ge(abs_ready, 1)
                nc.tensor.matmul(pw[:, 0:2], net.ones[:, :], absum[:, :], start=True, stop=True).then_inc(wsum_ready, 1)
                pe.wait_ge(w_ready, 1)
                with pe.Fori(0, TILES // 2) as i:
                    for p in range(2):
                        if rms_in:
                            pe.wait_ge(x_ready, 2 * i + p + 1)
                        for half in range(2):
                            pe.wait_ge(gelu_done, 4 * i + 2 * p + half + 1)
                            for c in range(2):
                                k = 2 * half + c
                                mm = nc.tensor.matmul(ph[:, half, c, :], wt[0][:, k * P:(k + 1) * P],
                                                      xn[:, ds((2 * i + p) * NT, NT)], start=True, stop=True)
                            mm.then_inc(up_ready, 1)
                        if p == 1:
                            down(pe, i, 0)
                    down(pe, i, 1)

            @block.scalar
            def _(act):
                act.sem_inc(gelu_done, 2)
                with act.Fori(0, TILES // 2) as i:
                    for p in range(2):
                        act.wait_ge(g_free, 2 * i + p + 1)
                        for half in range(2):
                            act.wait_ge(up_ready, 4 * i + 2 * p + half + 1)
                            if b1:
                                for c in range(2):
                                    k = 2 * half + c
                                    a = nc.scalar.activation(g[:, p, k, :], ph[:, half, c, :],
                                                             ACT.Gelu, bias=bias[:, k:k + 1])
                            else:
                                a = nc.scalar.activation(g[:, p, 2 * half:2 * half + 2, :], ph[:, half, :, :], ACT.Gelu)
                            a.then_inc(gelu_done, 1)
                if rms_in:
                    nc.scalar.preload_act_table_set("natural_log_exp_and_others")
                    steps = ((ACT.Ln, {}), (ACT.Exp, dict(scale=0.5)), (ACT.Ln, dict(bias=net.rms_floor)),
                             (ACT.Exp, dict(scale=-1.0)))
                    for k, (func, more) in enumerate(steps):
                        for q in range(4):
                            if k == 0:
                                act.wait_ge(x_ready, TILES + 4 * (q + 1))
                            else:
                                act.wait_ge(tail_a, 4 * (k - 1) + q + 1)
                            part = msq[:, q * 2 * NT:(q + 1) * 2 * NT]
                            nc.scalar.activation(part, part, func, **more).then_inc(tail_a, 1)

            @block.vector
            def _(dve):
                dve.wait_ge(w_in, 64 if b1 else 32)
                for m in range(2):
                    last = nc.vector.tensor_reduce(absum[:, m:m + 1], w[m][:, :], AX.X, ALU.add,
                                                   apply_absolute_value=True)
                last.then_inc(abs_ready, 1)
                dve.wait_ge(wsum_ready, 1)
                nc.vector.tensor_scalar(thr[:, 0:2], pw[:, 0:2], 1.0 / NW, floor, ALU.mult, ALU.max).then_inc(chain, 1)
                dve.wait_ge(chain, 1)
                nc.vector.tensor_scalar(thr[:, 2:4], thr[:, 0:2], -0.5, None, ALU.mult).then_inc(chain, 1)
                dve.wait_ge(chain, 2)
                nc.vector.tensor_scalar(thr[:, 0:2], thr[:, 0:2], 0.5, None, ALU.mult).then_inc(chain, 1)
                dve.wait_ge(chain, 3)
                n = 3
                for m in range(2):
                    nc.vector.tensor_scalar(neg[:, :], w[m][:, :], thr[:, 2 + m:3 + m], None, ALU.is_lt).then_inc(chain, 1)
                    n += 1
                    dve.wait_ge(chain, n)
                    nc.vector.scalar_tensor_tensor(wt[m][:, :], w[m][:, :], thr[:, m:m + 1], neg[:, :],
                                                   ALU.is_gt, ALU.subtract).then_inc(chain, 1)
                    n += 1
                    dve.wait_ge(chain, n)
                    nc.vector.tensor_tensor(wt[m][:, :], wt[m][:, :], w[m][:, :], ALU.subtract).then_inc(chain, 1)
                    n += 1
                    dve.wait_ge(chain, n)
                    nc.vector.tensor_tensor(wt[m][:, :], w[m][:, :], wt[m][:, :], ALU.add).then_inc(chain, 1)
                    n += 1
                    dve.wait_ge(chain, n)
                dve.sem_inc(w_ready, 1)
                dve.sem_inc(g_free, 2)
                dve.sem_inc(dn_free, 2)
                if rms_in:
                    with dve.Fori(0, TILES) as i:
                        tok = ds(i * NT, NT)
                        nc.vector.tensor_tensor(xn[:, tok], xn[:, tok], fac[:, tok], ALU.mult).then_inc(x_ready, 1)
                with dve.Fori(0, TILES // 2) as i:
                    for p in range(2):
                        tok = ds((2 * i + p) * NT, NT)
                        if rms_in:
                            dve.wait_ge(gelu_done, 4 * i + 2 * p + 4)
                            c0 = n + (2 * i + p) * 3
                            nc.vector.tensor_tensor(gsq[:, :, :], g[:, p, :, :], g[:, p, :, :], ALU.mult).then_inc(chain, 1)
                            dve.wait_ge(chain, c0 + 1)
                            nc.vector.tensor_tensor(gsq[:, 0:2, :], gsq[:, 0:2, :], gsq[:, 2:4, :], ALU.add).then_inc(chain, 1)
                            dve.wait_ge(chain, c0 + 2)
                            nc.vector.tensor_tensor(ssum[:, :], gsq[:, 0, :], gsq[:, 1, :], ALU.add).then_inc(chain, 1)
                            dve.wait_ge(chain, c0 + 3)
                            dve.sem_inc(ss_ready, 1)
                            dve.wait_ge(dn_ready, 2 * (2 * i + p) + 2)
                            nc.vector.tensor_copy(y[:, tok], py[:, p, :]).then_inc(x_ready, 1)
                            nc.vector.tensor_scalar(msq[:, tok], pm[:, :], 1.0 / (FC * P), 1e-19,
                                                    ALU.mult, ALU.max).then_inc(x_ready, 1)
                            dve.wait_ge(x_ready, TILES + (2 * i + p) * 2 + 2)
                        else:
                            dve.wait_ge(dn_ready, 2 * i + p + 1)
                            nc.vector.scalar_tensor_tensor(x[:, tok], py[:, p, :], bias[:, 4:5], x[:, tok],
                                                           ALU.add, ALU.add).then_inc(x_ready, 1)
                            dve.wait_ge(x_ready, 2 * i + p + 1)
                        dve.sem_inc(g_free, 1)
                        dve.sem_inc(dn_free, 1)
                if rms_in:
                    for q in range(4):
                        part = slice(q * 2 * NT, (q + 1) * 2 * NT)
                        dve.wait_ge(tail_a, 12 + q + 1)
                        nc.vector.tensor_tensor(y[:, part], y[:, part], msq[:, part], ALU.mult).then_inc(tail_b, 1)
                    for q in range(4):
                        part = slice(q * 2 * NT, (q + 1) * 2 * NT)
                        dve.wait_ge(tail_b, q + 1)
                        nc.vector.tensor_tensor(x[:, part], x[:, part], y[:, part], ALU.add)


HEADS = 16
GROUPS = B * HEADS // 4
KT = S // P
PAIRS = ((0, 0), (0, 1), (0, 2), (1, 0), (1, 1), (2, 0))
AHEAD = 24
TURN_COST = 1200
DECAY_SPAN = 384


def attention(net, tag, w, dq, scale, rope=False, alibi=False, decay=False, bias=False, out_bias=False):
    nc, x, xn, dram = net.nc, net.x, net.xn, net.dram
    R = HEADS * dq
    GR = 4 * dq
    r0 = 6 * dq + (9 if alibi else 0)
    layer_norm(net, tag + "_ln")
    parts = {n: nc.dram_tensor(f"{tag}_{n}_rows", (B * HEADS * 6 * dq, S), BF16, kind="Internal").ap() for n in "qk"}
    heads_out = nc.dram_tensor(f"{tag}_heads_out", (B * P, S), F32, kind="Internal").ap()
    sums = nc.dram_tensor(f"{tag}_sums", (4 * GROUPS, S), F32, kind="Internal").ap()
    rsums = nc.dram_tensor(f"{tag}_rsums", (4 * GROUPS, S), F32, kind="Internal").ap()
    with ExitStack() as ctx:
        v = ctx.enter_context(nc.sbuf_tensor(f"{tag}_v", [P, GROUPS, KT, 4, 9], F32))
        qs, ks = ([ctx.enter_context(nc.sbuf_tensor(f"{tag}_{n}_rows_sb{u}", [P, 4, S], BF16)) for u in range(3)]
                  for n in "qk")
        attn_project(net, tag, w, dq, rope, bias, decay, parts, v, qs, ks)
        attn_core(net, tag, w, dq, r0, scale, alibi, decay, parts, v, qs, ks, heads_out, sums)
    attn_output(net, tag, w, out_bias, heads_out, sums, rsums)


def attn_project(net, tag, w, dq, rope, bias, decay, parts, v, qs, ks):
    nc, xn, dram = net.nc, net.xn, net.dram
    R = HEADS * dq
    with stage(nc, tag + "_proj") as (sb, ps, sem):
        ws = [sb(f"w{n}", [P, P]) for n in range(4 if rope else 2)]
        wv = sb("wv", [P, P])
        bcol = sb("bias_cols", [P, 4])
        bv = sb("bias_v", [P, P])
        tab = sb("cos_sin", [P, 2, S]) if rope else None
        t1, t2 = sb("t1", [P, 2, 2, NT]), sb("t2", [P, 2, 2, NT])
        part = sb("parts", [P, 2, 3, T], BF16)
        pq = ps("qk", [P, 4, NT])
        pv = ps("v", [P, 2, NT])
        w_in, mm_ready, mm_free, v_ready, v_free = (sem(n) for n in ("w_in", "mm", "mm_free", "v_mm", "v_free"))
        val, hi, rest, mid, low, made, stored, t_free = (sem(n) for n in (
            "value", "hi", "rest", "mid", "low", "made", "stored", "t_free"))
        n_in = [0]
        NW = len(ws)
        with nc.Block() as block:
            @block.sync
            def _(sp):
                for j, n in enumerate(("wq", "wk", "wq_sw", "wk_sw")[:NW]):
                    sp.dma_start(ws[j][:, :], dram[w[n]]).then_inc(w_in, 16)
                    n_in[0] += 16
                    if bias:
                        sp.dma_start(bcol[0:R, j:j + 1], dram[w["b" + n[1:]]]).then_inc(w_in, 16)
                        n_in[0] += 16
                sp.dma_start(wv[:, :], dram[w["wv"]]).then_inc(w_in, 16)
                n_in[0] += 16
                if bias:
                    sp.dma_start(bv[:, :], dram[w["bv"]].to_broadcast((P, P))).then_inc(w_in, 16)
                    n_in[0] += 16
                if rope:
                    sp.dma_start(tab[:, :, :], dram["rope"]).then_inc(w_in, 16)
                    n_in[0] += 16
                for b in range(B):
                    sp.wait_ge(hi, 4 * (b + 1))
                    sp.wait_ge(mid, 4 * (b + 1))
                    sp.wait_ge(low, 4 * (b + 1))
                    for j, n in enumerate("qk"):
                        for slot in range(6):
                            sp.dma_start(parts[n].rearrange("(b h s d) t -> b s h d t", b=B, s=6, d=dq)[b, slot],
                                         part[0:R, j, PAIRS[slot][j], b * S:(b + 1) * S]).then_inc(stored, 16)
                sp.wait_ge(stored, 16 * 12 * B)

            @block.tensor
            def _(pe):
                pe.wait_ge(w_in, n_in[0])
                with pe.Fori(0, TILES) as i:
                    for j in range(2):
                        pe.wait_ge(mm_free, 2 * i + j + 1)
                        for m in range(j, NW, 2):
                            mm = nc.tensor.matmul(pq[:, m, :], ws[m][:, :], xn[:, ds(i * NT, NT)],
                                                  start=True, stop=True)
                        mm.then_inc(mm_ready, 1)
                for m in range(T // P):
                    if m % 4 == 0 and m >= 8:
                        pe.wait_ge(v_free, m // 4 - 1)
                    mm = nc.tensor.matmul(pv[:, m // 4 % 2, m % 4 * P:(m % 4 + 1) * P],
                                          xn[:, m * P:(m + 1) * P], wv[:, :], start=True, stop=True)
                    if m % 4 == 3:
                        mm.then_inc(v_ready, 1)

            @block.vector
            def _(dve):
                nc.vector.memset(v[:, :, :, :, 8:9], 0.0 if decay else 1.0)
                for rows in (qs[0], ks[0], qs[1], ks[1]):
                    nc.vector.memset(rows[:, :, :], 0.0)
                dve.wait_ge(w_in, n_in[0])
                dve.sem_inc(mm_free, 2)
                with dve.Fori(0, B) as b:
                    for h in range(2):
                        for j in range(2):
                            n = 4 * b + 2 * h + j
                            dve.wait_ge(mm_ready, n + 1)
                            dve.wait_ge(t_free, n + 1)
                            if rope:
                                nc.vector.scalar_tensor_tensor(t1[0:R, j, h, :], pq[0:R, j, :], bcol[0:R, j:j + 1],
                                                               tab[0:R, 0, h * NT:(h + 1) * NT], ALU.add, ALU.mult)
                                nc.vector.scalar_tensor_tensor(t2[0:R, j, h, :], pq[0:R, 2 + j, :], bcol[0:R, 2 + j:3 + j],
                                                               tab[0:R, 1, h * NT:(h + 1) * NT], ALU.add, ALU.mult
                                                               ).then_inc(made, 1)
                                dve.wait_ge(made, n + 1)
                                nc.vector.tensor_tensor(t1[0:R, j, h, :], t1[0:R, j, h, :], t2[0:R, j, h, :],
                                                        ALU.add).then_inc(val, 1)
                            elif bias:
                                nc.vector.tensor_scalar(t1[0:R, j, h, :], pq[0:R, j, :], bcol[0:R, j:j + 1], None,
                                                        ALU.add).then_inc(val, 1)
                            else:
                                nc.vector.tensor_copy(t1[0:R, j, h, :], pq[0:R, j, :]).then_inc(val, 1)
                            dve.wait_ge(val, n + 1)
                            dve.sem_inc(mm_free, 1)
                for m in range(T // P // 4):
                    dve.wait_ge(v_ready, m + 1)
                    for c in range(4):
                        tile = 4 * m + c
                        dst = v[:, 4 * (tile // KT):4 * (tile // KT) + 4, tile % KT, :, 0:8]
                        src = pv[:, m % 2, c * P:(c + 1) * P].rearrange("p (g h e) -> p g h e", g=4, e=8)
                        if bias:
                            a = nc.vector.tensor_tensor(dst, src, bv[:, :].rearrange("p (g h e) -> p g h e", g=4, e=8),
                                                        ALU.add)
                        else:
                            a = nc.vector.tensor_copy(dst, src)
                    a.then_inc(v_free, 1)

            @block.scalar
            def _(act):
                def first(b, m):
                    h, j = m // 2, m % 2
                    act.wait_ge(val, 4 * b + m + 1)
                    nc.scalar.activation(part[0:R, j, 0, ds(b * S + h * NT, NT)], t1[0:R, j, h, :],
                                         ACT.Copy).then_inc(hi, 1)

                def second(b, m):
                    h, j = m // 2, m % 2
                    act.wait_ge(rest, 4 * b + m + 1)
                    nc.scalar.activation(part[0:R, j, 1, ds(b * S + h * NT, NT)], t1[0:R, j, h, :],
                                         ACT.Copy).then_inc(mid, 1)

                with act.Fori(0, B) as b:
                    for m in range(4):
                        first(b, m)
                        if m:
                            second(b, m - 1)
                    second(b, 3)

            @block.gpsimd
            def _(pool):
                pool.sem_inc(t_free, 4)
                for rows in (qs[2], ks[2]):
                    nc.gpsimd.memset(rows[:, :, :], 0.0)

                def remain(b, m):
                    h, j = m // 2, m % 2
                    pool.wait_ge(hi, 4 * b + m + 1)
                    nc.gpsimd.tensor_tensor(t1[0:R, j, h, :], t1[0:R, j, h, :], part[0:R, j, 0, ds(b * S + h * NT, NT)],
                                            ALU.subtract).then_inc(rest, 1)

                def third(b, m):
                    h, j = m // 2, m % 2
                    tok = ds(b * S + h * NT, NT)
                    pool.wait_ge(mid, 4 * b + m + 1)
                    nc.gpsimd.tensor_tensor(part[0:R, j, 2, tok], t1[0:R, j, h, :], part[0:R, j, 1, tok],
                                            ALU.subtract).then_inc(low, 1)

                with pool.Fori(0, B) as b:
                    for m in range(4):
                        remain(b, m)
                        if m:
                            third(b, m - 1)
                            pool.wait_ge(low, 4 * b + m)
                            pool.sem_inc(t_free, 1)
                    third(b, 3)
                    pool.wait_ge(low, 4 * b + 4)
                    pool.sem_inc(t_free, 1)


def attn_core(net, tag, w, dq, r0, scale, alibi, decay, parts, v, qs, ks, heads_out, sums):
    nc, dram = net.nc, net.dram
    GR = 4 * dq
    first = [(qt, 0, min(qt + 1, 4) * P) for qt in range(KT)]
    P1 = 4 * 12
    with stage(nc, tag + "_core") as (sb, ps, sem):
        vs = [sb(f"v_group{u}", [P, KT, 4, 9]) for u in range(3)]
        pt = sb("probs", [P, 2, 4, S])
        pw = sb("probs_decayed", [P, 2, 4, DECAY_SPAN]) if decay else None
        dtab = sb("decay", [P, DECAY_SPAN]) if decay else None
        ones9 = sb("ones9", [P, 9]) if decay else None
        maskq = sb("mask_q_rows", [P, P], BF16)
        maskk = sb("mask_k_rows", [P, P], BF16)
        mx = sb("chunk_max", [P, 4, 12])
        nm = sb("neg_max", [P, 4, 8])
        mrest = sb("max_rest", [32, P])
        mpart = sb("max_parts", [32, 3, P], BF16)
        oev = sb("out_sums", [P, S])
        pa = [ps(f"scores_a{n}", [P, NT]) for n in range(2)]
        pb = [ps(f"scores_b{n}", [P, S]) for n in range(2)]
        acc = ps("acc", [P, S])
        c_in, stack_in = sem("consts_in"), [sem(f"stack_in{u}") for u in range(3)]
        a_ready, a_free = sem("scores_a"), sem("scores_a_free")
        b_ready, b_free = sem("scores_b"), sem("exp_done")
        m_chain, nm_ready, mp_ready, m_in = (sem(n) for n in ("max_chain", "neg_max", "max_parts", "max_rows_in"))
        vs_ready, acc_free, pv_done = (sem(n) for n in ("v_group", "acc_free", "pv_done"))
        o_stored, dec_ready, z_ready = sem("out_stored"), sem("decayed"), sem("acc_zeroed")

        def load_stack(sp, n, u):
            for n_, dst in (("q", qs[u]), ("k", ks[u])):
                src = parts[n_][ds(n * 24 * dq, 24 * dq), :].rearrange("(j r) t -> r j t", j=4)
                sp.dma_start(dst[0:6 * dq, :, :], src).then_inc(stack_in[u], 16)
            sp.dma_start(qs[u][r0:r0 + 3, :, :], dram["zero_rows"]).then_inc(stack_in[u], 16)
            if alibi:
                sp.dma_start(qs[u][6 * dq:r0, :, :], dram["alibi_q"][ds(n * 9, 9)]).then_inc(stack_in[u], 16)

        NST = 16 * (3 + (1 if alibi else 0))
        CIN = 16 * (5 + (3 if alibi else 0) + (2 if decay else 0))
        PV0 = 2 * KT + 1

        with nc.Block() as block:
            order = [(qt, j, c) for qt in range(KT) for j in range(4) for c in range(1 if qt < 4 else 2)]
            P1_COST = [min(NT, (qt + 1) * P - c * NT) + 60 for qt, j, c in order] + [TURN_COST]
            P1_ALL = sum(P1_COST)
            P2_COST = lambda kt: S - kt * P + 180
            P2_ALL = 4 * sum(P2_COST(kt) for kt in range(KT))

            @block.sync
            def _(sp):
                sp.dma_start(maskq[:, :], dram["mask_q"]).then_inc(c_in, 16)
                sp.dma_start(maskk[:, :], dram["mask_k"]).then_inc(c_in, 16)
                if decay:
                    sp.dma_start(dtab[:, :], dram["decay"]).then_inc(c_in, 16)
                    sp.dma_start(ones9[:, :], dram["ones9"]).then_inc(c_in, 16)
                for u in range(3):
                    sp.dma_start(ks[u][r0:r0 + 3, :, :], dram["ones_rows"]).then_inc(c_in, 16)
                    if alibi:
                        sp.dma_start(ks[u][6 * dq:r0, :, :], dram["alibi_k"]).then_inc(c_in, 16)
                for u in range(3):
                    load_stack(sp, u, u)

                def max_rows(n, u):
                    sp.wait_ge(mp_ready, n + 1)
                    for s in range(3):
                        sp.dma_start(qs[u][r0 + s:r0 + s + 1, :, :].rearrange("o j (k q) -> o (j k) q", q=P),
                                     mpart[:, s, :]).then_inc(m_in, 16)

                def output(n):
                    sp.wait_ge(acc_free, n + 2)
                    for j in range(4):
                        sp.dma_start(heads_out[ds(n * 32 + 8 * j, 8), :],
                                     oev[32 * j:32 * j + 8, :]).then_inc(o_stored, 16)
                        sp.dma_start(sums[ds(n * 4 + j, 1), :],
                                     oev[32 * j + 8:32 * j + 9, :]).then_inc(o_stored, 16)

                def one(n, u, load=True, nxt=True):
                    if nxt:
                        max_rows(n + 1, (u + 1) % 3)
                    sp.wait_ge(pv_done, KT * (n + 1) + PV0)
                    if load:
                        load_stack(sp, n + 3, u)
                    output(n)

                max_rows(0, 0)
                with sp.Fori(0, GROUPS // 3 - 1) as i:
                    for u in range(3):
                        one(3 * i + u, u)
                for n in range(GROUPS - GROUPS % 3 - 3, GROUPS):
                    one(n, n % 3, load=n + 3 < GROUPS, nxt=n + 1 < GROUPS)
                sp.wait_ge(o_stored, 8 * 16 * (GROUPS + 1))

            def p1_chunk(pe, n, u, k):
                qt, j, c = order[k]
                a0, a1 = c * NT, min((c + 1) * NT, (qt + 1) * P)
                slot = k % 2
                pe.wait_ge(a_free, n * (P1 + 1) + k + (3 if k == 0 else 2))
                diag = a1 == (qt + 1) * P
                mm = nc.tensor.matmul(pa[slot][:, 0:a1 - a0], qs[u][:, j, qt * P:(qt + 1) * P],
                                      ks[u][:, j, a0:a1], start=True, stop=not diag)
                if diag:
                    mm = nc.tensor.matmul(pa[slot][:, a1 - a0 - P:a1 - a0], net.identb[:, :], maskq[:, :],
                                          start=False, stop=True)
                mm.then_inc(a_ready, 1)

            def p1_turn(pe, n):
                pe.wait_ge(nm_ready, n + 1)
                pe.wait_ge(a_free, n * (P1 + 1) + P1 + 2)
                nc.tensor.transpose(pa[0][0:32, 0:P], nm[:, :, :].rearrange("p j k -> p (j k)"),
                                    net.ident[:, :]).then_inc(a_ready, 1)

            def p2_scores(pe, n, u, kt, j):
                pe.wait_ge(b_free, 32 * n + 4 * kt + j + 1)
                for c in range(2):
                    a0, a1 = max(c * NT, kt * P), (c + 1) * NT
                    if a0 >= a1:
                        continue
                    diag = a0 == kt * P
                    mm = nc.tensor.matmul(pb[j % 2][:, a0:a1], ks[u][:, j, kt * P:(kt + 1) * P],
                                          qs[u][:, j, a0:a1], start=True, stop=not diag)
                    if diag:
                        mm = nc.tensor.matmul(pb[j % 2][:, a0:a0 + P], net.identb[:, :], maskk[:, :],
                                              start=False, stop=True)
                mm.then_inc(b_ready, 1)

            def p2_values(pe, n, u, kt, c):
                a0, a1 = max(c * NT, kt * P), (c + 1) * NT
                if a0 >= a1:
                    return False
                if a0 == kt * P:
                    pe.wait_ge(b_free, 32 * n + 4 * kt + 4 + 2)
                    if kt == 0:
                        pe.wait_ge(vs_ready, n + 1)
                        pe.wait_ge(acc_free, n + 1)
                last_kt = kt == 4 * c + 3
                for j in range(4):
                    o = acc[32 * j:32 * j + 9, :]
                    mm = nc.tensor.matmul(o[:, a0:a1], ones9[:, :] if decay else vs[u][:, kt, j, :],
                                          pt[:, kt % 2, j, a0:a1], start=(kt == 0), stop=last_kt and not decay,
                                          tile_position=(0, 32 * j))
                if decay:
                    d1 = min(a1, kt * P + DECAY_SPAN)
                    if a0 < d1:
                        pe.wait_ge(dec_ready, 4 * (KT * n + kt) + 4)
                        for j in range(4):
                            mm = nc.tensor.matmul(acc[32 * j:32 * j + 9, a0:d1], vs[u][:, kt, j, :],
                                                  pw[:, kt % 2, j, a0 - kt * P:d1 - kt * P], start=False,
                                                  stop=last_kt, tile_position=(0, 32 * j))
                if c == 1:
                    mm.then_inc(pv_done, 1)
                return True

            @block.tensor
            def _(pe):
                pe.wait_ge(c_in, CIN)
                pe.wait_ge(z_ready, 1)
                pe.wait_ge(stack_in[0], NST)
                for k in range(P1):
                    p1_chunk(pe, 0, 0, k)
                p1_turn(pe, 0)
                pe.wait_ge(stack_in[1], NST)
                for k in range(AHEAD):
                    p1_chunk(pe, 1, 1, k)

                def one(n, u, i, left=2):
                    steps = iter([(1, k) for k in range(AHEAD, P1)] + [(1, P1)] + [(2, k) for k in range(AHEAD)])
                    at, spent, passed = next(steps), 0, 0
                    pe.wait_ge(m_in, 48 * n + 96)
                    for kt in range(KT):
                        for j in range(4):
                            p2_scores(pe, n, u, kt, j)
                            passed += P2_COST(kt)
                            while at and spent <= passed * P1_ALL / P2_ALL:
                                g, k = at
                                if g <= left and k == P1:
                                    p1_turn(pe, n + 1)
                                elif g <= left:
                                    if g == 2 and k == 0:
                                        pe.wait_ge(stack_in[(u + 2) % 3], NST * (i + (u + 2) // 3 + 1))
                                    p1_chunk(pe, n + g, (u + g) % 3, k)
                                spent += P1_COST[k]
                                at = next(steps, None)
                            if kt and j % 2:
                                p2_values(pe, n, u, kt - 1, j // 2)
                    assert at is None
                    p2_values(pe, n, u, KT - 1, 1)

                with pe.Fori(0, GROUPS // 3 - 1) as i:
                    for u in range(3):
                        one(3 * i + u, u, i)
                for n in range(GROUPS - GROUPS % 3 - 3, GROUPS):
                    one(n, n % 3, n // 3, left=GROUPS - 1 - n)

            @block.scalar
            def _(act):
                nc.scalar.preload_act_table_set("natural_log_exp_and_others")
                act.sem_inc(b_free, 2)

                def one(n):
                    for kt in range(KT):
                        for j in range(4):
                            act.wait_ge(b_ready, 32 * n + 4 * kt + j + 1)
                            if j == 0:
                                act.wait_ge(pv_done, KT * n + kt - 1 + PV0)
                            nc.scalar.activation(pt[:, kt % 2, j, kt * P:S], pb[j % 2][:, kt * P:S], ACT.Exp,
                                                 scale=scale).then_inc(b_free, 1)

                with act.Fori(0, GROUPS) as n:
                    one(n)

            @block.gpsimd
            def _(pool):
                if decay:
                    pool.wait_ge(c_in, CIN)

                def one(n, u):
                    pool.wait_ge(pv_done, KT * n - 2 * KT + PV0)
                    nc.gpsimd.tensor_copy(vs[u][:, :, :, :], v[:, ds(n, 1), :, :, :].rearrange(
                        "p o k j e -> p (o k) j e")).then_inc(vs_ready, 1)
                    if decay:
                        for kt in range(KT):
                            wd = min(DECAY_SPAN, S - kt * P)
                            for j in range(4):
                                pool.wait_ge(b_free, 32 * n + 4 * kt + j + 3)
                                pool.wait_ge(pv_done, KT * n + kt - 1 + PV0)
                                nc.gpsimd.tensor_tensor(
                                    pw[:, kt % 2, j, 0:wd], pt[:, kt % 2, j, kt * P:kt * P + wd],
                                    dtab[:, 0:wd], ALU.mult).then_inc(dec_ready, 1)

                with pool.Fori(0, GROUPS // 3) as i:
                    for u in range(3):
                        one(3 * i + u, u)
                one(GROUPS - 1, 0)

            @block.vector
            def _(dve):
                nc.vector.memset(acc[:, :], 0.0).then_inc(z_ready, 1)
                dve.sem_inc(a_free, 3)
                dve.sem_inc(pv_done, PV0)
                dve.sem_inc(acc_free, 1)

                def p1_max(n, chunks):
                    for k in chunks:
                        qt, j, c = order[k]
                        a0, a1 = c * NT, min((c + 1) * NT, (qt + 1) * P)
                        dve.wait_ge(a_ready, n * (P1 + 1) + k + 1)
                        nc.vector.tensor_reduce(mx[:, j, qt + 4 * c:qt + 4 * c + 1], pa[k % 2][:, 0:a1 - a0],
                                                AX.X, ALU.max).then_inc(a_free, 1)

                def p1_rows(n):
                    dve.wait_ge(a_free, n * (P1 + 1) + P1 + 3)
                    nc.vector.tensor_scalar(nm[:, :, 0:4], mx[:, :, 0:4], -1.0, None, ALU.mult)
                    nc.vector.tensor_tensor(nm[:, :, 4:8], mx[:, :, 4:8], mx[:, :, 8:12],
                                            ALU.max).then_inc(m_chain, 1)
                    dve.wait_ge(m_chain, 4 * n + 1)
                    nc.vector.tensor_scalar(nm[:, :, 4:8], nm[:, :, 4:8], -1.0, None, ALU.mult).then_inc(nm_ready, 1)
                    t = pa[0]
                    dve.wait_ge(a_ready, n * (P1 + 1) + P1 + 1)
                    dve.wait_ge(m_in, 48 * n + 48)
                    nc.vector.tensor_copy(mpart[:, 0, :], t[0:32, 0:P]).then_inc(m_chain, 1)
                    dve.wait_ge(m_chain, 4 * n + 2)
                    nc.vector.tensor_tensor(mrest[:, :], t[0:32, 0:P], mpart[:, 0, :], ALU.subtract).then_inc(m_chain, 1)
                    dve.wait_ge(m_chain, 4 * n + 3)
                    nc.vector.tensor_copy(mpart[:, 1, :], mrest[:, :]).then_inc(m_chain, 1)
                    dve.wait_ge(m_chain, 4 * n + 4)
                    nc.vector.tensor_tensor(mpart[:, 2, :], mrest[:, :], mpart[:, 1, :],
                                            ALU.subtract).then_inc(mp_ready, 1)
                    dve.sem_inc(a_free, 1)

                def evac(n):
                    dve.wait_ge(o_stored, 128 * n + 128)
                    dve.wait_ge(pv_done, KT * (n + 1) + PV0)
                    nc.vector.tensor_copy(oev[:, :], acc[:, :]).then_inc(acc_free, 1)

                dve.sem_inc(m_in, 48)
                dve.sem_inc(o_stored, 128)
                p1_max(0, range(P1))
                p1_rows(0)
                p1_max(1, range(AHEAD))
                with dve.Fori(0, GROUPS - 2) as n:
                    p1_max(n + 1, range(AHEAD, P1))
                    p1_rows(n + 1)
                    p1_max(n + 2, range(AHEAD))
                    evac(n)
                p1_max(GROUPS - 1, range(AHEAD, P1))
                p1_rows(GROUPS - 1)
                evac(GROUPS - 2)
                evac(GROUPS - 1)


def attn_output(net, tag, w, out_bias, heads_out, sums, rsums):
    nc, x, dram = net.nc, net.x, net.dram
    with stage(nc, tag + "_out") as (sb, ps, sem):
        wo = sb("wo", [P, P])
        bo = sb("bo", [P, 1])
        o = sb("heads", [P, B, S])
        r = sb("inverse_rows", [P, B, S])
        py = ps("proj", [P, 2, NT])
        packed = sb("inverse", [P, B, HEADS * S // P])
        w_in, o_ready, y_ready, y_free, inverted = (sem(n) for n in ("w_in", "o_ready", "y_ready", "y_free", "inverted"))
        s_in, r_out, r_in = ([sem(f"{n}{b}") for b in range(B)] for n in ("sums_in", "inverse_out", "sequence_in"))
        with nc.Block() as block:
            @block.sync
            def _(sp):
                pack = lambda t, b: t[b * HEADS:(b + 1) * HEADS, :].rearrange("h (a c) -> (h a) c", a=P // HEADS)
                for b in range(B):
                    sp.dma_start(packed[:, b, :], pack(sums, b)).then_inc(s_in[b], 16)
                sp.dma_start(wo[:, :], dram[w["wo"]]).then_inc(w_in, 16)
                if out_bias:
                    sp.dma_start(bo[:, :], dram[w["bo"]]).then_inc(w_in, 16)
                for b in range(B):
                    sp.wait_ge(inverted, b + 1)
                    sp.dma_start(pack(rsums, b), packed[:, b, :]).then_inc(r_out[b], 16)
                    sp.dma_start(o[:, b, :], heads_out[b * P:(b + 1) * P, :]).then_inc(r_in[b], 16)
                for b in range(B):
                    sp.wait_ge(r_out[b], 16)
                    src = rsums[b * HEADS:(b + 1) * HEADS, :].rearrange("(h o) t -> h o t", o=1)
                    sp.dma_start(r[:, b, :], src.to_broadcast((HEADS, P // HEADS, S))).then_inc(r_in[b], 16)

            @block.vector
            def _(dve):
                dve.sem_inc(y_free, 2)
                for b in range(B):
                    dve.wait_ge(s_in[b], 16)
                    nc.vector.reciprocal(packed[:, b, :], packed[:, b, :]).then_inc(inverted, 1)

                def add(t):
                    tok = slice(t * NT, (t + 1) * NT)
                    dve.wait_ge(y_ready, t + 1)
                    if out_bias:
                        nc.vector.scalar_tensor_tensor(x[:, tok], py[:, t % 2, :], bo[:, 0:1], x[:, tok],
                                                       ALU.add, ALU.add).then_inc(y_free, 1)
                    else:
                        nc.vector.tensor_tensor(x[:, tok], py[:, t % 2, :], x[:, tok], ALU.add).then_inc(y_free, 1)

                for t in range(TILES):
                    b, c = t // 2, t % 2 * NT
                    if c == 0:
                        dve.wait_ge(r_in[b], 32)
                    nc.vector.tensor_tensor(o[:, b, c:c + NT], o[:, b, c:c + NT], r[:, b, c:c + NT],
                                            ALU.mult).then_inc(o_ready, 1)
                    if t:
                        if t == 1:
                            dve.wait_ge(w_in, 32 if out_bias else 16)
                        add(t - 1)
                add(TILES - 1)

            @block.tensor
            def _(pe):
                pe.wait_ge(w_in, 32 if out_bias else 16)
                for t in range(TILES):
                    b, c = t // 2, t % 2 * NT
                    pe.wait_ge(o_ready, t + 1)
                    pe.wait_ge(y_free, t + 1)
                    nc.tensor.matmul(py[:, t % 2, :], wo[:, :], o[:, b, c:c + NT], start=True,
                                     stop=True).then_inc(y_ready, 1)


EXPERTS = 8
HC = 4


def experts_ffn(net, tag, w):
    nc, x, xn, dram = net.nc, net.x, net.xn, net.dram
    NTOK = T // P
    layer_norm(net, tag + "_ln")
    with stage(nc, tag) as (sb, ps, sem):
        fc = sb("expert_fc", [P, EXPERTS, HC * P])
        pj = sb("expert_proj", [P, EXPERTS, HC, P])
        rw = sb("router", [P, EXPERTS])
        sel = sb("expert_select", [P, EXPERTS, P], BF16)
        mask_t = sb("mask_rows", [P, T], BF16)
        loaded, routed = sem("loaded"), sem("routed")
        with stage(nc, tag + "_route") as (sb2, ps2, sem2):
            rank = sb2("rank", [P, NTOK, EXPERTS])
            top = sb2("top", [P, 2, NTOK, 1])
            eq = sb2("is_top", [P, 2, NTOK, EXPERTS])
            pl = ps2("logits", [P, NTOK, EXPERTS])
            pt = ps2("mask_rows", [EXPERTS, 2, NT])
            lg, chain, turned, copied = (sem2(n) for n in ("logits", "chain", "turned", "copied"))
            with nc.Block() as block:
                @block.sync
                def _(sp):
                    sp.dma_start(rw[:, :], dram[w["router"]]).then_inc(routed, 16)
                    sp.dma_start(sel[:, :, :], dram["expert_select"]).then_inc(loaded, 16)
                    sp.dma_start(fc[:, :, :], dram[w["fc"]]).then_inc(loaded, 16)
                    sp.dma_start(pj[:, :, :, :], dram[w["proj"]]).then_inc(loaded, 16)

                @block.tensor
                def _(pe):
                    pe.wait_ge(routed, 16)
                    for m in range(NTOK):
                        mm = nc.tensor.matmul(pl[:, m, :], xn[:, m * P:(m + 1) * P], rw[:, :], start=True, stop=True)
                    mm.then_inc(lg, 1)
                    pe.wait_ge(chain, 5)
                    for m in range(NTOK):
                        if m % 4 == 0 and m >= 8:
                            pe.wait_ge(copied, m // 4 - 1)
                        mm = nc.tensor.transpose(pt[:, m // 4 % 2, m % 4 * P:(m % 4 + 1) * P], eq[:, 1, m, :],
                                                 net.ident[:, :])
                        if m % 4 == 3:
                            mm.then_inc(turned, 1)

                @block.vector
                def _(dve):
                    nc.vector.memset(mask_t[:, :], 0.0)
                    for e in range(EXPERTS):
                        nc.vector.memset(rank[:, :, e:e + 1], float(EXPERTS - e))
                    wide = lambda t: t.to_broadcast((P, NTOK, EXPERTS))
                    dve.wait_ge(lg, 1)
                    nc.vector.tensor_reduce(top[:, 0, :, 0], pl[:, :, :], AX.X, ALU.max).then_inc(chain, 1)
                    dve.wait_ge(chain, 1)
                    nc.vector.tensor_tensor(eq[:, 0, :, :], pl[:, :, :], wide(top[:, 0, :, :]), ALU.is_equal).then_inc(chain, 1)
                    dve.wait_ge(chain, 2)
                    nc.vector.tensor_tensor(eq[:, 0, :, :], eq[:, 0, :, :], rank[:, :, :], ALU.mult).then_inc(chain, 1)
                    dve.wait_ge(chain, 3)
                    nc.vector.tensor_reduce(top[:, 1, :, 0], eq[:, 0, :, :], AX.X, ALU.max).then_inc(chain, 1)
                    dve.wait_ge(chain, 4)
                    nc.vector.tensor_tensor(eq[:, 1, :, :], eq[:, 0, :, :], wide(top[:, 1, :, :]), ALU.is_equal).then_inc(chain, 1)
                    for m in range(TILES):
                        dve.wait_ge(turned, m + 1)
                        nc.vector.tensor_copy(mask_t[0:EXPERTS, m * NT:(m + 1) * NT], pt[:, m % 2, :]).then_inc(copied, 1)

        xm = sb("masked", [P, 2, NT])
        r = sb("relu", [P, 2, 2, NT])
        h = sb("hidden", [P, 2, HC, NT])
        pb = ps("mask", [P, 2, NT])
        pu = ps("up", [P, 2, 2, NT])
        py = ps("down", [P, NT])
        bc_ready, xm_ready, up_ready, relu_done, sq_done, dn_done, y_free = (sem(n) for n in (
            "mask", "masked", "up", "relu", "square", "down", "y_free"))
        E = EXPERTS
        with nc.Block() as block:
            @block.tensor
            def _(pe):
                pe.wait_ge(loaded, 48)

                def spread(i, e):
                    n = E * i + e
                    pe.wait_ge(xm_ready, n + 1)
                    nc.tensor.matmul(pb[:, e % 2, :], sel[:, e, :], mask_t[:, ds(i * NT, NT)],
                                     start=True, stop=True).then_inc(bc_ready, 1)

                def up(i, e):
                    n = E * i + e
                    pe.wait_ge(xm_ready, n + 3)
                    for half in range(2):
                        pe.wait_ge(relu_done, 2 * n + half + 1)
                        for c in range(2):
                            k = 2 * half + c
                            mm = nc.tensor.matmul(pu[:, half, c, :], fc[:, e, k * P:(k + 1) * P], xm[:, e % 2, :],
                                                  start=True, stop=True)
                        mm.then_inc(up_ready, 1)

                def down(i, e):
                    n = E * i + e
                    pe.wait_ge(sq_done, 2 * n + 4)
                    if e == 0:
                        pe.wait_ge(y_free, i + 1)
                    for k in range(HC):
                        mm = nc.tensor.matmul(py[:, :], pj[:, e, k, :], h[:, e % 2, k, :],
                                              start=(e == 0 and k == 0), stop=(e == E - 1 and k == HC - 1))
                    mm.then_inc(dn_done, 1)

                with pe.Fori(0, TILES) as i:
                    spread(i, 0)
                    spread(i, 1)
                    for e in range(E):
                        up(i, e)
                        if 1 <= e < E - 1:
                            spread(i, e + 1)
                        if e:
                            down(i, e - 1)
                    down(i, E - 1)

            @block.scalar
            def _(act):
                act.sem_inc(relu_done, 2)
                with act.Fori(0, TILES) as i:
                    for e in range(E):
                        for half in range(2):
                            n = 2 * (E * i + e) + half
                            act.wait_ge(up_ready, n + 1)
                            act.wait_ge(sq_done, n + 1)
                            nc.scalar.activation(r[:, half, :, :], pu[:, half, :, :], ACT.Relu).then_inc(relu_done, 1)

            @block.vector
            def _(dve):
                dve.sem_inc(xm_ready, 2)
                dve.sem_inc(sq_done, 2)
                dve.sem_inc(dn_done, 2)
                dve.sem_inc(y_free, 1)

                def masked(i, e):
                    n = E * i + e
                    dve.wait_ge(bc_ready, n + 1)
                    nc.vector.tensor_tensor(xm[:, e % 2, :], pb[:, e % 2, :], xn[:, ds(i * NT, NT)],
                                            ALU.mult).then_inc(xm_ready, 1)

                with dve.Fori(0, TILES) as i:
                    masked(i, 0)
                    masked(i, 1)
                    for e in range(E):
                        n = E * i + e
                        dve.wait_ge(dn_done, n + 1)
                        for half in range(2):
                            dve.wait_ge(relu_done, 2 * n + half + 3)
                            nc.vector.tensor_tensor(h[:, e % 2, 2 * half:2 * half + 2, :], r[:, half, :, :],
                                                    r[:, half, :, :], ALU.mult).then_inc(sq_done, 1)
                        if 1 <= e < E - 1:
                            masked(i, e + 1)
                    dve.wait_ge(dn_done, E * i + E + 2)
                    tok = ds(i * NT, NT)
                    nc.vector.tensor_tensor(x[:, tok], py[:, :], x[:, tok], ALU.add).then_inc(y_free, 1)


def gated_ffn(net, tag):
    nc, x, xn, dram = net.nc, net.x, net.xn, net.dram
    layer_norm(net, tag + "_ln")
    with stage(nc, tag) as (sb, ps, sem):
        w12 = [sb("w1", [P, HC * P]), sb("w2", [P, HC * P])]
        wh = [sb("h1", [P, HC, HC * P]), sb("h2", [P, HC, HC * P])]
        w3 = sb("w3", [P, HC, P])
        sc = sb("scales", [P, 17])
        h0 = sb("gated", [P, HC, T])
        loaded = sem("loaded")
        with stage(nc, tag + "_gate") as (sb2, ps2, sem2):
            sg = sb2("silu", [P, 2, NT])
            pg = ps2("gate_up", [P, 2, 2, NT])
            ready, silu, done = sem2("ready"), sem2("silu"), sem2("done")
            with nc.Block() as block:
                @block.sync
                def _(sp):
                    for t, n in ((w12[0], "w1"), (w12[1], "w2"), (sc, "scales")):
                        sp.dma_start(t[:, :], dram["g3_" + n]).then_inc(loaded, 16)
                    sp.dma_start(wh[0][:, :, :], dram["g3_h1"]).then_inc(loaded, 16)
                    sp.dma_start(wh[1][:, :, :], dram["g3_h2"]).then_inc(loaded, 16)
                    sp.dma_start(w3[:, :, :], dram["g3_w3"]).then_inc(loaded, 16)

                @block.tensor
                def _(pe):
                    pe.wait_ge(loaded, 96)
                    with pe.Fori(0, TILES) as i:
                        for k in range(HC):
                            pe.wait_ge(done, HC * i + k + 1)
                            for m in range(2):
                                mm = nc.tensor.matmul(pg[:, k % 2, m, :], w12[m][:, k * P:(k + 1) * P],
                                                      xn[:, ds(i * NT, NT)], start=True, stop=True)
                            mm.then_inc(ready, 1)

                @block.scalar
                def _(act):
                    act.wait_ge(loaded, 96)
                    nc.scalar.preload_act_table_set("silu_and_others")
                    with act.Fori(0, TILES) as i:
                        for k in range(HC):
                            act.wait_ge(ready, HC * i + k + 1)
                            act.wait_ge(done, HC * i + k + 1)
                            nc.scalar.activation(sg[:, k % 2, :], pg[:, k % 2, 0, :], ACT.Silu,
                                                 scale=sc[:, k:k + 1]).then_inc(silu, 1)

                @block.vector
                def _(dve):
                    dve.sem_inc(done, 2)
                    with dve.Fori(0, TILES) as i:
                        for k in range(HC):
                            dve.wait_ge(silu, HC * i + k + 1)
                            nc.vector.scalar_tensor_tensor(h0[:, k, ds(i * NT, NT)], pg[:, k % 2, 1, :],
                                                           sc[:, 4 + k:5 + k], sg[:, k % 2, :], ALU.mult,
                                                           ALU.mult).then_inc(done, 1)

        g = [sb("gelu1", [P, 2, HC, NT]), sb("gelu2", [P, 2, HC, NT])]
        ph = ps("hidden", [P, 4, NT])
        py = ps("out", [P, 2, NT])
        h_ready, h_done, y_ready, y_free = (sem(n) for n in ("hidden", "gelu", "y", "y_free"))
        with nc.Block() as block:
            @block.tensor
            def _(pe):
                def layer(i, p, m):
                    for k in range(HC):
                        n = 16 * i + 8 * m + 4 * p + k
                        pe.wait_ge(h_done, n + 1)
                        if m and k == 0:
                            pe.wait_ge(h_done, 4 + 16 * i + 4 * p + 4)
                        for c in range(HC):
                            src = g[0][:, p, c, :] if m else h0[:, c, ds((2 * i + p) * NT, NT)]
                            mm = nc.tensor.matmul(ph[:, k, :], wh[m][:, c, k * P:(k + 1) * P], src,
                                                  start=(c == 0), stop=(c == HC - 1))
                        mm.then_inc(h_ready, 1)

                with pe.Fori(0, TILES // 2) as i:
                    for m in range(2):
                        for p in range(2):
                            layer(i, p, m)
                    for p in range(2):
                        pe.wait_ge(h_done, 4 + 16 * i + 8 + 4 * p + 4)
                        pe.wait_ge(y_free, 2 * i + p + 1)
                        for c in range(HC):
                            mm = nc.tensor.matmul(py[:, p, :], w3[:, c, :], g[1][:, p, c, :],
                                                  start=(c == 0), stop=(c == HC - 1))
                        mm.then_inc(y_ready, 1)

            @block.scalar
            def _(act):
                act.sem_inc(h_done, 4)
                with act.Fori(0, TILES // 2) as i:
                    for m in range(2):
                        for p in range(2):
                            for k in range(HC):
                                n = 16 * i + 8 * m + 4 * p + k
                                act.wait_ge(h_ready, n + 1)
                                if m and k == 0:
                                    act.wait_ge(y_ready, 2 * i + p + 1)
                                nc.scalar.activation(g[m][:, p, k, :], ph[:, k, :], ACT.Gelu,
                                                     scale=sc[:, 8 + 4 * m + k:9 + 4 * m + k]).then_inc(h_done, 1)

            @block.vector
            def _(dve):
                dve.sem_inc(y_free, 2)
                dve.sem_inc(y_ready, 2)
                with dve.Fori(0, TILES // 2) as i:
                    for p in range(2):
                        tok = ds((2 * i + p) * NT, NT)
                        dve.wait_ge(y_ready, 2 * i + p + 3)
                        nc.vector.scalar_tensor_tensor(x[:, tok], py[:, p, :], sc[:, 16:17], x[:, tok],
                                                       ALU.mult, ALU.add).then_inc(y_free, 1)


NS = 16


def selective_ssm(net, tag, w, H, taps, left, rms, low_rank, a_is_log, residual):
    nc, x, xn, dram = net.nc, net.x, net.xn, net.dram
    PADDED = S + taps - 1
    with stage(nc, tag) as (sb, ps, sem):
        gate = sb("gate", [P, H, T])
        xs = sb("xs", [P, H, T])
        cols = sb("cols", [P, 64])
        bin_, cvb, dtb, dbb, rmsw, bout = (cols[:, a:b] for a, b in ((0, 4), (4, 6), (6, 8), (8, 9), (9, 10), (10, 11)))
        cvw = cols[:, 16:16 + H * taps].rearrange("p (h k) -> p h k", h=H)
        acol = sb("a_cols", [P, H, NS])
        w_dbc = sb("w_dbc", [P, H, P])
        w_dt = sb("w_dt", [P, H, P])
        w_out = sb("w_out", [P, H, P])
        spread = sb("spread", [P, 32, P], BF16)
        loaded = sem("loaded")
        with ExitStack() as fctx:
            fac = fctx.enter_context(nc.sbuf_tensor(f"{tag}_rms_factor", [P, T], F32)) if rms else None
            layer_norm(net, tag + "_ln", ("rsqrt", RMS_EPS, fac) if rms else None)
            ssm_input(net, tag, w, H, taps, left, rms, fac, gate, xs, cols, bin_, cvb, rmsw, cvw, acol, w_dbc, w_dt,
                      w_out, spread, loaded, PADDED)
        delta = sb("delta", [P, H, T])
        bcp = sb("bc_parts", [P, T], BF16)
        ssm_delta(net, tag, H, low_rank, a_is_log, xs, delta, bcp, dtb, dbb, acol, w_dbc, w_dt)
        ssm_scan(net, tag, H, xs, delta, bcp, acol, spread)
        ssm_output(net, tag, H, xs, gate, w_out, bout, residual)


def ssm_input(net, tag, w, H, taps, left, rms, fac, gate, xs, cols, bin_, cvb, rmsw, cvw, acol, w_dbc, w_dt, w_out,
              spread, loaded, PADDED):
    nc, x, xn, dram = net.nc, net.x, net.xn, net.dram
    with stage(nc, tag + "_in") as (sb, ps, sem):
        win = sb("w_in", [P, 2 * H * P])
        xp = sb("padded", [P, H, B, PADDED])
        hh = sb("rms_normed", [P, 2, NT])
        cv = sb("conv", [P, 2, 2, S])
        pp = ps("proj", [P, 4, NT])
        h_ready, p_ready, p_free, padded, conv, xs_done, chain, pads = (sem(n) for n in (
            "h", "proj", "proj_free", "padded", "conv", "xs", "chain", "pads"))
        M = 2 * H
        with nc.Block() as block:
            @block.sync
            def _(sp):
                for t, n in ((win, "win"), (cols, "cols")):
                    sp.dma_start(t[:, :], dram[w + n]).then_inc(loaded, 16)
                for t, n in ((acol, "a"), (w_dbc, "dbc"), (w_dt, "dt"), (w_out, "out")):
                    sp.dma_start(t[:, :, :], dram[w + n]).then_inc(loaded, 16)
                sp.dma_start(spread[:, :, :], dram["bc_spread"]).then_inc(loaded, 16)

            @block.tensor
            def _(pe):
                pe.wait_ge(loaded, 112)
                with pe.Fori(0, TILES // 2) as i:
                    for p in range(2):
                        tok = ds((2 * i + p) * NT, NT)
                        if rms:
                            pe.wait_ge(h_ready, 2 * i + p + 1)
                        for m in range(M):
                            n = (2 * i + p) * M + m
                            pe.wait_ge(p_free, n + 1)
                            nc.tensor.matmul(pp[:, (p * M + m) % 4, :], win[:, m * P:(m + 1) * P],
                                             hh[:, p, :] if rms else xn[:, tok], start=True, stop=True
                                             ).then_inc(p_ready, 1)

            @block.scalar
            def _(act):
                act.wait_ge(loaded, 112)
                act.wait_ge(chain, 1)
                act.sem_inc(p_free, 4)
                nc.scalar.preload_act_table_set("silu_and_others")
                with act.Fori(0, B) as b:
                    for p in range(2):
                        tok = ds((2 * b + p) * NT, NT)
                        for m in range(M):
                            act.wait_ge(p_ready, (2 * b + p) * M + m + 1)
                            src = pp[:, (p * M + m) % 4, :]
                            if m < H:
                                dst = xp[:, m, ds(b, 1), left + p * NT:left + (p + 1) * NT].rearrange("p o t -> p (o t)")
                                nc.scalar.activation(dst, src, ACT.Identity, bias=bin_[:, m:m + 1]).then_inc(p_free, 1)
                            else:
                                nc.scalar.activation(gate[:, m - H, tok], src, ACT.Silu,
                                                     bias=bin_[:, m:m + 1]).then_inc(p_free, 1)
                with act.Fori(0, B) as b:
                    for h in range(H):
                        act.wait_ge(conv, H * b + h + 1)
                        nc.scalar.activation(xs[:, h, ds(b * S, S)], cv[:, 1, h, :], ACT.Silu).then_inc(xs_done, 1)

            @block.vector
            def _(dve):
                nc.vector.memset(xp[:, :, :, 0:left], 0.0).then_inc(pads, 1)
                if taps - 1 - left:
                    nc.vector.memset(xp[:, :, :, left + S:PADDED], 0.0).then_inc(pads, 1)
                dve.wait_ge(pads, 2 if taps - 1 - left else 1)
                dve.sem_inc(xs_done, H)
                dve.wait_ge(loaded, 112)
                dve.sem_inc(chain, 1)
                if rms:
                    with dve.Fori(0, TILES // 2) as i:
                        for p in range(2):
                            tok = ds((2 * i + p) * NT, NT)
                            dve.wait_ge(p_free, (2 * i + p) * M + 1)
                            nc.vector.scalar_tensor_tensor(hh[:, p, :], xn[:, tok], rmsw[:, 0:1], fac[:, tok],
                                                           ALU.mult, ALU.mult).then_inc(h_ready, 1)
                with dve.Fori(0, B) as b:
                    for h in range(H):
                        dve.wait_ge(p_free, 4 + (2 * b + 2) * M)
                        dve.wait_ge(xs_done, H * b + h + 1)
                        for k in range(taps):
                            src = xp[:, h, ds(b, 1), k:k + S].rearrange("p o t -> p (o t)")
                            last = k == taps - 1
                            dst = cv[:, 1 if last else 0, h, :]
                            if k == 0:
                                a = nc.vector.tensor_scalar(dst, src, cvw[:, h, 0:1], cvb[:, h:h + 1], ALU.mult, ALU.add)
                            else:
                                dve.wait_ge(chain, (H * b + h) * (taps - 1) + k + 1)
                                a = nc.vector.scalar_tensor_tensor(dst, src, cvw[:, h, k:k + 1], cv[:, 0, h, :],
                                                                   ALU.mult, ALU.add)
                            a.then_inc(conv if last else chain, 1)


def ssm_delta(net, tag, H, low_rank, a_is_log, xs, delta, bcp, dtb, dbb, acol, w_dbc, w_dt):
    nc = net.nc
    with stage(nc, tag + "_dt") as (sb, ps, sem):
        z = sb("dbc", [P, 2, NT])
        hi = sb("hi", [P, 2, NT], BF16)
        mid = sb("mid", [P, 2, NT], BF16)
        rest = sb("rest", [P, 2, NT])
        ab = sb("softplus", [P, 2, H, 3, NT])
        mx = sb("before_softplus", [P, 2, H, NT])
        pz = ps("dbc", [P, 2, NT])
        pd = ps("delta", [P, 2, H, NT])
        z_ready, z_done, hi_done, rest_done, mid_done, low_done = (sem(n) for n in (
            "dbc", "dbc_biased", "hi", "rest", "mid", "low_stored"))
        stored, paced = sem("parts_stored"), sem("paced")
        d_ready, mx_done, abs_done, exp_done, log_done, delta_done, a_ready = (sem(n) for n in (
            "delta_product", "delta_biased", "abs", "exp", "log", "delta", "a_exp"))
        with nc.Block() as block:
            @block.tensor
            def _(pe):
                with pe.Fori(0, TILES // 2) as i:
                    for p in range(2):
                        pe.wait_ge(z_done, 2 * i + p + 1)
                        for h in range(H):
                            mm = nc.tensor.matmul(pz[:, p, :], w_dbc[:, h, :], xs[:, h, ds((2 * i + p) * NT, NT)],
                                                  start=(h == 0), stop=(h == H - 1))
                        mm.then_inc(z_ready, 1)
                    for p in range(2):
                        if low_rank:
                            pe.wait_ge(z_done, 2 * i + p + 3)
                        pe.wait_ge(mx_done, 2 * i + p + 1)
                        for h in range(H):
                            src = z[:, p, :] if low_rank else xs[:, h, ds((2 * i + p) * NT, NT)]
                            mm = nc.tensor.matmul(pd[:, p, h, :], w_dt[:, h, :], src, start=True, stop=True)
                        mm.then_inc(d_ready, 1)

            @block.scalar
            def _(act):
                nc.scalar.preload_act_table_set("natural_log_exp_and_others")
                act.sem_inc(low_done, 2)
                act.sem_inc(stored, 2)
                act.sem_inc(delta_done, 2)
                if a_is_log:
                    nc.scalar.activation(acol[:, :, :], acol[:, :, :], ACT.Exp).then_inc(a_ready, 1)
                with act.Fori(0, TILES // 2) as i:
                    for p in range(2):
                        t = 2 * i + p
                        act.wait_ge(z_done, t + 3)
                        act.wait_ge(low_done, t + 1)
                        act.wait_ge(stored, t + 1)
                        nc.scalar.activation(hi[0:96, p, :], z[0:96, p, :], ACT.Copy).then_inc(hi_done, 1)
                    for p in range(2):
                        t = 2 * i + p
                        act.wait_ge(rest_done, t + 1)
                        nc.scalar.activation(mid[0:96, p, :], rest[0:96, p, :], ACT.Copy).then_inc(mid_done, 1)
                        act.wait_ge(hi_done, t + 1)
                        nc.scalar.activation(bcp[0:32, ds(t * NT, NT)], hi[0:32, p, :], ACT.Copy)
                        act.wait_ge(mid_done, t + 1)
                        act.sem_inc(paced, 1)
                        nc.scalar.activation(bcp[32:64, ds(t * NT, NT)], mid[32:64, p, :], ACT.Copy).then_inc(stored, 1)
                    for p in range(2):
                        t = 2 * i + p
                        act.wait_ge(mx_done, t + 3)
                        act.wait_ge(delta_done, t + 1)
                        nc.scalar.activation(ab[:, p, :, 0, :], mx[:, p, :, :], ACT.Abs).then_inc(abs_done, 1)
                        act.wait_ge(abs_done, t + 1)
                        nc.scalar.activation(ab[:, p, :, 1, :], ab[:, p, :, 0, :], ACT.Exp, scale=-1.0).then_inc(exp_done, 1)
                        act.wait_ge(exp_done, t + 1)
                        nc.scalar.activation(ab[:, p, :, 2, :], ab[:, p, :, 1, :], ACT.Ln, bias=net.one).then_inc(log_done, 1)

            @block.vector
            def _(dve):
                nc.vector.memset(bcp[96:P, :], 0.0)
                dve.sem_inc(z_done, 2)
                dve.sem_inc(mx_done, 2)
                if a_is_log:
                    dve.wait_ge(a_ready, 1)
                    nc.vector.tensor_scalar(acol[:, :, :], acol[:, :, :], -1.0, None, ALU.mult)
                with dve.Fori(0, TILES // 2) as i:
                    for p in range(2):
                        t = 2 * i + p
                        dve.wait_ge(z_ready, t + 1)
                        nc.vector.tensor_scalar(z[:, p, :], pz[:, p, :], dbb[:, 0:1], None, ALU.add).then_inc(z_done, 1)
                    for p in range(2):
                        t = 2 * i + p
                        dve.wait_ge(hi_done, t + 1)
                        nc.vector.tensor_tensor(rest[0:96, p, :], z[0:96, p, :], hi[0:96, p, :], ALU.subtract
                                                ).then_inc(rest_done, 1)
                    for p in range(2):
                        t = 2 * i + p
                        dve.wait_ge(d_ready, t + 1)
                        for h in range(H):
                            a = nc.vector.tensor_scalar(mx[:, p, h, :], pd[:, p, h, :], dtb[:, h:h + 1], None,
                                                        ALU.add)
                        a.then_inc(mx_done, 1)
                    for p in range(2):
                        t = 2 * i + p
                        dve.wait_ge(mid_done, t + 1)
                        nc.vector.tensor_tensor(bcp[64:96, ds(t * NT, NT)], rest[64:96, p, :], mid[64:96, p, :],
                                                ALU.subtract).then_inc(low_done, 1)
                    for p in range(2):
                        t = 2 * i + p
                        dve.wait_ge(log_done, t + 1)
                        nc.vector.scalar_tensor_tensor(delta[:, :, ds(t * NT, NT)], mx[:, p, :, :], 0.0, ab[:, p, :, 2, :],
                                                       ALU.max, ALU.add).then_inc(delta_done, 1)

            @block.gpsimd
            def _(pool):
                with pool.Fori(0, TILES // 2) as i:
                    for p in range(2):
                        t = 2 * i + p
                        tok = ds(t * NT, NT)
                        pool.wait_ge(delta_done, t + 3)
                        nc.gpsimd.tensor_tensor(xs[:, :, tok], xs[:, :, tok], delta[:, :, tok], ALU.mult)


def ssm_scan(net, tag, H, xs, delta, bcp, acol, spread):
    nc = net.nc
    R, RS = 2, 4
    NC = 3 - H
    with stage(nc, tag + "_scan") as (sb, ps, sem):
        decay = sb("decay", [P, R, S])
        bs = sb("b_rows", [P, RS, S])
        bx = sb("bx", [P, R, S])
        hs = sb("states", [P, RS, S])
        hc = sb("states_c", [P, R, S])
        pb, pc = ps("b_rows", [P, S]), ps("c_rows", [P, NC, S])
        acc = ps("y", [P, H, S])
        b_ready, bs_done, c_ready, hc_done, y_done, y_out, a_done, bx_done, scanned, paced = (
            sem(n) for n in ("b_rows", "b_copied", "c_rows", "states_c", "summed", "y_out", "decay", "bx", "scanned",
                             "paced"))
        with nc.Block() as block:
            @block.tensor
            def _(pe):
                def b_rows(b, n):
                    s = NS * b + n
                    pe.wait_ge(bs_done, s + 1)
                    for c in range(2):
                        mm = nc.tensor.matmul(pb[:, c * NT:(c + 1) * NT], spread[:, n, :],
                                              bcp[:, ds(b * S + c * NT, NT)], start=True, stop=True)
                    mm.then_inc(b_ready, 1)

                def c_rows(b, n):
                    pe.wait_ge(hc_done, H * (NS * b + n) + H + RS - H * NC)
                    for c in range(2):
                        mm = nc.tensor.matmul(pc[:, n % NC, c * NT:(c + 1) * NT], spread[:, NS + n, :],
                                              bcp[:, ds(b * S + c * NT, NT)], start=True, stop=True)
                    mm.then_inc(c_ready, 1)

                def add_up(b, n, halves=range(H)):
                    for h in halves:
                        q = (NS * b + n) * H + h
                        pe.wait_ge(hc_done, q + 1 + RS)
                        if n == 0:
                            pe.wait_ge(y_out, b + 1)
                        for c in range(2):
                            mm = nc.tensor.matmul(acc[:, h, c * NT:(c + 1) * NT], net.ident[:, :],
                                                  hc[:, (n * H + h) % R, c * NT:(c + 1) * NT],
                                                  start=(n == 0), stop=(n == NS - 1))
                        mm.then_inc(y_done, 1)

                with pe.Fori(0, B) as b:
                    b_rows(b, 0)
                    b_rows(b, 1)
                    for n in range(NS):
                        if n + 2 < NS:
                            b_rows(b, n + 2)
                        if n:
                            add_up(b, n - 1, range(H - 1))
                        c_rows(b, n)
                        if n:
                            add_up(b, n - 1, range(H - 1, H))
                    add_up(b, NS - 1)

            @block.scalar
            def _(act):
                nc.scalar.preload_act_table_set("natural_log_exp_and_others")
                act.sem_inc(bs_done, 1)

                def copy_b(b, n):
                    s = NS * b + n
                    act.wait_ge(b_ready, s + 1)
                    act.wait_ge(bx_done, H * s + H)
                    nc.scalar.activation(bs[:, n % RS, :], pb[:, :], ACT.Copy).then_inc(bs_done, 1)

                with act.Fori(0, B) as b:
                    copy_b(b, 0)
                    for n in range(NS):
                        s = NS * b + n
                        if n + 1 < NS:
                            copy_b(b, n + 1)
                        for h in range(H):
                            q = H * s + h
                            act.wait_ge(scanned, q + 1)
                            act.sem_inc(paced, 1)
                            nc.scalar.activation(decay[:, (n * H + h) % R, :], delta[:, h, ds(b * S, S)], ACT.Exp,
                                                 scale=acol[:, h, n:n + 1]).then_inc(a_done, 1)

            @block.gpsimd
            def _(pool):
                pool.sem_inc(bx_done, RS * H)
                with pool.Fori(0, B) as b:
                    for n in range(NS):
                        s = NS * b + n
                        pool.wait_ge(bs_done, s + 2)
                        for h in range(H):
                            q = H * s + h
                            pool.wait_ge(scanned, q + 1)
                            pool.sem_inc(paced, 1)
                            nc.gpsimd.tensor_tensor(bx[:, (n * H + h) % R, :], xs[:, h, ds(b * S, S)], bs[:, n % RS, :],
                                                    ALU.mult).then_inc(bx_done, 1)

            @block.vector
            def _(dve):
                dve.sem_inc(scanned, R)
                dve.sem_inc(hc_done, RS)
                dve.sem_inc(y_done, R)
                dve.sem_inc(y_out, 1)

                def scan(q, m):
                    dve.wait_ge(a_done, q + 1)
                    dve.wait_ge(bx_done, q + RS * H + 1)
                    dve.wait_ge(hc_done, q + 1)
                    nc.vector.tensor_tensor_scan(hs[:, m % RS, :], decay[:, m % R, :], bx[:, m % R, :], 0.0, ALU.mult,
                                                 ALU.add).then_inc(scanned, 1)

                def times_c(b, m):
                    q, n = NS * H * b + m, m // H
                    if m % H == 0:
                        dve.wait_ge(c_ready, NS * b + n + 1)
                    dve.wait_ge(y_done, q + 1)
                    dve.wait_ge(scanned, q + 1 + R)
                    nc.vector.tensor_tensor(hc[:, m % R, :], hs[:, m % RS, :], pc[:, n % NC, :], ALU.mult).then_inc(hc_done, 1)

                with dve.Fori(0, B) as b:
                    for m in range(NS * H):
                        scan(NS * H * b + m, m)
                        if m:
                            times_c(b, m - 1)
                    times_c(b, NS * H - 1)
                    dve.wait_ge(y_done, H * NS * (b + 1) + R)
                    nc.vector.tensor_copy(xs[:, :, ds(b * S, S)], acc[:, :, :]).then_inc(y_out, 1)


def ssm_output(net, tag, H, y, gate, w_out, bout, residual):
    nc, x, xn = net.nc, net.x, net.xn
    with stage(nc, tag + "_out") as (sb, ps, sem):
        py = ps("proj", [P, 2, NT])
        gated, ready, free, added = sem("gated"), sem("ready"), sem("free"), sem("added")
        with nc.Block() as block:
            @block.gpsimd
            def _(pool):
                with pool.Fori(0, TILES) as i:
                    tok = ds(i * NT, NT)
                    nc.gpsimd.tensor_tensor(y[:, :, tok], y[:, :, tok], gate[:, :, tok], ALU.mult).then_inc(gated, 1)

            @block.tensor
            def _(pe):
                with pe.Fori(0, TILES // 2) as i:
                    for p in range(2):
                        pe.wait_ge(gated, 2 * i + p + 1)
                        pe.wait_ge(free, 2 * i + p + 1)
                        for h in range(H):
                            mm = nc.tensor.matmul(py[:, p, :], w_out[:, h, :], y[:, h, ds((2 * i + p) * NT, NT)],
                                                  start=(h == 0), stop=(h == H - 1))
                        mm.then_inc(ready, 1)

            @block.vector
            def _(dve):
                if residual:
                    nc.vector.tensor_tensor(x[:, :], x[:, :], xn[:, :], ALU.add).then_inc(added, 1)
                    dve.wait_ge(added, 1)
                dve.sem_inc(free, 2)
                with dve.Fori(0, TILES // 2) as i:
                    for p in range(2):
                        tok = ds((2 * i + p) * NT, NT)
                        dve.wait_ge(ready, 2 * i + p + 1)
                        nc.vector.scalar_tensor_tensor(x[:, tok], py[:, p, :], bout[:, 0:1], x[:, tok],
                                                       ALU.add, ALU.add).then_inc(free, 1)


SSD_HEADS, SSD_P = 32, 8
UNITS = T // P
CPS = S // P


def ssd(net, tag):
    nc, x, xn, dram = net.nc, net.x, net.xn, net.dram
    taps, DI = 4, 2 * P
    PADDED = S + taps - 1
    layer_norm(net, tag + "_ln")
    with stage(nc, tag) as (sb, ps, sem):
        xbc = sb("xbc", [P, 4, B, PADDED])
        zs = sb("gate", [P, UNITS, DI])
        dt = sb("dt", [P, UNITS, SSD_HEADS])
        e_cs = sb("exp_cs", [P, UNITS, SSD_HEADS])
        e_out = sb("exp_rest", [P, UNITS, SSD_HEADS])
        e_all = sb("exp_chunk", [P, UNITS, SSD_HEADS])
        csp = sb("cs_parts", [P, T], BF16)
        w_out = sb("w_out", [P, 2, P])
        ssd_input(net, tag, xbc, zs, dt, w_out, PADDED, taps, DI)
        ssd_steps(net, tag, dt, e_cs, e_out, e_all, csp)
        ssd_chunks(net, tag, xbc, dt, e_cs, e_out, e_all, csp, DI)
        ssd_output(net, tag, xbc, zs, w_out, DI)


def ssd_input(net, tag, xbc, zs, dt, w_out, PADDED, taps, DI):
    nc, xn, dram = net.nc, net.xn, net.dram
    with stage(nc, tag + "_in") as (sb, ps, sem):
        w = sb("w_xbc", [P, 4 * P])
        wz = sb("w_z_dt", [P, DI + SSD_HEADS])
        cvw = sb("conv_w", [P, 4, taps + 1])
        dtb = sb("dt_bias", [P, SSD_HEADS])
        lnw = sb("ln_w", [P, DI])
        cv = sb("conv", [P, 2, 2, S])
        pp = ps("proj", [P, 4, NT])
        pz = ps("z", [P, 2, NT])
        loaded, p_ready, p_free, z_ready, z_free, conv, xs_done, chain, pads = (sem(n) for n in (
            "loaded", "proj", "proj_free", "z", "z_free", "conv", "xs", "chain", "pads"))
        with nc.Block() as block:
            @block.sync
            def _(sp):
                for t, n in ((w, "w"), (wz, "wz")):
                    sp.dma_start(t[:, :], dram["d2_" + n]).then_inc(loaded, 16)
                sp.dma_start(cvw[:, :, :], dram["d2_conv"]).then_inc(loaded, 16)
                sp.dma_start(w_out[:, :, :], dram["d2_out"]).then_inc(loaded, 16)
                sp.dma_start(dtb[:, :], dram["d2_dtb"].to_broadcast((P, SSD_HEADS))).then_inc(loaded, 16)
                sp.dma_start(lnw[:, :], dram["d2_lnw"].to_broadcast((P, DI))).then_inc(loaded, 16)

            @block.tensor
            def _(pe):
                pe.wait_ge(loaded, 96)
                for b in range(B):
                    for p in range(2):
                        for m in range(4):
                            if b or p:
                                pe.wait_ge(p_free, 4 * (2 * b + p - 1) + m + 1)
                            nc.tensor.matmul(pp[:, m, :], w[:, m * P:(m + 1) * P],
                                             xn[:, b * S + p * NT:b * S + (p + 1) * NT],
                                             start=True, stop=True).then_inc(p_ready, 1)
                    for u in range(b * CPS, (b + 1) * CPS):
                        if u >= 2:
                            pe.wait_ge(z_free, u - 1)
                        nc.tensor.matmul(pz[:, u % 2, 0:DI + SSD_HEADS], xn[:, u * P:(u + 1) * P], wz[:, :],
                                         start=True, stop=True).then_inc(z_ready, 1)

            @block.scalar
            def _(act):
                nc.scalar.preload_act_table_set("silu_and_others")
                act.wait_ge(loaded, 96)
                for b in range(B + 1):
                    if b < B:
                        act.wait_ge(pads, 1)
                        for p in range(2):
                            for m in range(4):
                                act.wait_ge(p_ready, 8 * b + 4 * p + m + 1)
                                nc.scalar.activation(xbc[:, m, b, 3 + p * NT:3 + (p + 1) * NT], pp[:, m, :],
                                                     ACT.Copy).then_inc(p_free, 1)
                        for u in range(b * CPS, (b + 1) * CPS):
                            act.wait_ge(z_ready, u + 1)
                            nc.scalar.activation(zs[:, u, :], pz[:, u % 2, 0:DI], ACT.Silu)
                            nc.scalar.activation(dt[:, u, :], pz[:, u % 2, DI:DI + SSD_HEADS], ACT.Copy).then_inc(z_free, 1)
                    if b:
                        for m in range(4):
                            act.wait_ge(conv, 4 * (b - 1) + m + 1)
                            nc.scalar.activation(xbc[:, m, b - 1, 0:S], cv[:, 1, m % 2, :], ACT.Silu).then_inc(xs_done, 1)

            @block.vector
            def _(dve):
                nc.vector.memset(xbc[:, :, :, 0:taps - 1], 0.0).then_inc(pads, 1)
                dve.sem_inc(xs_done, 2)
                dve.wait_ge(loaded, 96)
                with dve.Fori(0, B) as b:
                    for m in range(4):
                        dve.wait_ge(p_free, 8 * b + 8)
                        dve.wait_ge(xs_done, 4 * b + m + 1)
                        for k in range(taps):
                            src = xbc[:, m, ds(b, 1), k:k + S].rearrange("p o t -> p (o t)")
                            last = k == taps - 1
                            dst = cv[:, 1 if last else 0, m % 2, :]
                            if k == 0:
                                a = nc.vector.tensor_scalar(dst, src, cvw[:, m, 0:1], cvw[:, m, taps:taps + 1],
                                                            ALU.mult, ALU.add)
                            else:
                                dve.wait_ge(chain, (4 * b + m) * (taps - 1) + k)
                                a = nc.vector.scalar_tensor_tensor(dst, src, cvw[:, m, k:k + 1], cv[:, 0, m % 2, :],
                                                                   ALU.mult, ALU.add)
                            a.then_inc(conv if last else chain, 1)

            @block.gpsimd
            def _(pool):
                pool.wait_ge(loaded, 96)
                for u in range(UNITS):
                    pool.wait_ge(z_free, u + 1)
                    nc.gpsimd.tensor_tensor(zs[:, u, :], zs[:, u, :], lnw[:, :], ALU.mult)
                    nc.gpsimd.tensor_tensor(dt[:, u, :], dt[:, u, :], dtb[:, :], ALU.add)


def ssd_steps(net, tag, dt, e_cs, e_out, e_all, csp):
    nc, dram = net.nc, net.dram
    W = UNITS * SSD_HEADS
    flat = lambda t: t[:, :, :].rearrange("p u h -> p (u h)")
    with stage(nc, tag + "_dt") as (sb, ps, sem):
        tri = sb("triangle", [P, P])
        last = sb("last_row", [P, P])
        arow = sb("a_row", [P, 1, SSD_HEADS])
        t1, t2, t3 = sb("t1", [P, W]), sb("t2", [P, W]), sb("t3", [P, W])
        cs = sb("cs", [P, UNITS, SSD_HEADS])
        rest = sb("rest", [SSD_HEADS, 2, NT])
        pc = ps("cs", [P, W])
        pl = ps("cs_end", [P, W])
        pt = ps("turned", [SSD_HEADS, 2, NT])
        loaded, c, pe_done, turned, taken = (sem(n) for n in ("loaded", "chain", "products", "turned", "taken"))
        part = sem("parts")
        with nc.Block() as block:
            @block.sync
            def _(sp):
                sp.dma_start(tri[:, :], dram["triangle"]).then_inc(loaded, 16)
                sp.dma_start(last[:, :], dram["last_row"]).then_inc(loaded, 16)
                sp.dma_start(arow[:, 0, :], dram["d2_alog"].to_broadcast((P, SSD_HEADS))).then_inc(loaded, 16)

            @block.scalar
            def _(act):
                nc.scalar.preload_act_table_set("natural_log_exp_and_others")
                act.wait_ge(loaded, 48)
                nc.scalar.activation(t1[:, :], flat(dt), ACT.Abs).then_inc(c, 1)
                act.wait_ge(c, 1)
                nc.scalar.activation(t2[:, :], t1[:, :], ACT.Exp, scale=-1.0).then_inc(c, 1)
                act.wait_ge(c, 2)
                nc.scalar.activation(t3[:, :], t2[:, :], ACT.Ln, bias=net.one).then_inc(c, 1)
                nc.scalar.activation(arow[:, :, :], arow[:, :, :], ACT.Exp).then_inc(c, 1)
                act.wait_ge(c, 8)
                nc.scalar.activation(flat(e_cs), flat(cs), ACT.Exp).then_inc(c, 1)
                nc.scalar.activation(flat(e_all), t2[:, :], ACT.Exp).then_inc(c, 1)
                nc.scalar.activation(flat(e_out), t3[:, :], ACT.Exp).then_inc(c, 1)

            @block.vector
            def _(dve):
                nc.vector.memset(csp[96:P, :], 0.0)
                dve.wait_ge(c, 4)
                nc.vector.scalar_tensor_tensor(flat(dt), flat(dt), 0.0, t3[:, :], ALU.max, ALU.add).then_inc(c, 1)
                dve.wait_ge(c, 5)
                nc.vector.scalar_tensor_tensor(t1[:, :].rearrange("p (u h) -> p u h", u=UNITS), dt[:, :, :], -1.0,
                                               arow[:, :, :].to_broadcast((P, UNITS, SSD_HEADS)), ALU.mult,
                                               ALU.mult).then_inc(c, 1)
                dve.wait_ge(pe_done, 1)
                nc.vector.tensor_copy(flat(cs), pc[:, :]).then_inc(taken, 1)
                dve.wait_ge(pe_done, 2)
                nc.vector.tensor_copy(t2[:, :], pl[:, :]).then_inc(c, 1)
                dve.wait_ge(c, 7)
                dve.wait_ge(taken, 1)
                nc.vector.tensor_tensor(t3[:, :], t2[:, :], flat(cs), ALU.subtract).then_inc(c, 1)
                for m in range(TILES):
                    tok = slice(m * NT, (m + 1) * NT)
                    dve.wait_ge(turned, m + 1)
                    nc.vector.tensor_copy(csp[0:32, tok], pt[:, m % 2, :]).then_inc(part, 1)
                    dve.wait_ge(part, 4 * m + 1)
                    nc.vector.tensor_tensor(rest[:, m % 2, :], pt[:, m % 2, :], csp[0:32, tok],
                                            ALU.subtract).then_inc(part, 1)
                    dve.wait_ge(part, 4 * m + 2)
                    nc.vector.tensor_copy(csp[32:64, tok], rest[:, m % 2, :]).then_inc(part, 1)
                    dve.wait_ge(part, 4 * m + 3)
                    nc.vector.tensor_copy(t1[0:32, 0:NT], csp[32:64, tok]).then_inc(part, 1)
                    dve.wait_ge(part, 4 * m + 4)
                    nc.vector.tensor_tensor(csp[64:96, tok], rest[:, m % 2, :], t1[0:32, 0:NT],
                                            ALU.subtract).then_inc(taken, 1)
                dve.wait_ge(c, 11)
                first = lambda t: t[:, :, :].rearrange("p (b c) h -> p b c h", b=B)[:, :, 0, :]
                nc.vector.memset(first(e_cs), 0.0)
                nc.vector.memset(first(e_all), 0.0)

            @block.tensor
            def _(pe):
                pe.wait_ge(c, 6)
                for k in range(W // NT):
                    mm = nc.tensor.matmul(pc[:, k * NT:(k + 1) * NT], tri[:, :], t1[:, k * NT:(k + 1) * NT],
                                          start=True, stop=True)
                mm.then_inc(pe_done, 1)
                pe.wait_ge(taken, 1)
                for k in range(W // NT):
                    mm = nc.tensor.matmul(pl[:, k * NT:(k + 1) * NT], last[:, :],
                                          cs[:, :, :].rearrange("p u h -> p (u h)")[:, k * NT:(k + 1) * NT],
                                          start=True, stop=True)
                mm.then_inc(pe_done, 1)
                for u in range(UNITS):
                    if u % 4 == 0 and u >= 8:
                        pe.wait_ge(taken, u // 4)
                    mm = nc.tensor.transpose(pt[:, u // 4 % 2, u % 4 * P:(u % 4 + 1) * P], cs[:, u, :], net.ident[:, :])
                    if u % 4 == 3:
                        mm.then_inc(turned, 1)


def ssd_chunks(net, tag, xbc, dt, e_cs, e_out, e_all, csp, DI):
    nc, dram = net.nc, net.dram
    HG = 8
    NG = SSD_HEADS // HG
    wide = lambda t: t.to_broadcast((P, SSD_HEADS, SSD_P))
    with stage(nc, tag + "_chunks") as (sb, ps, sem):
        pick = sb("pick", [P, SSD_HEADS, P], BF16)
        npick = sb("neg_pick", [P, SSD_HEADS, P], BF16)
        mask = sb("mask", [P, 4, P], BF16)
        st = sb("chunk", [P, 2, 4, P])
        gs = sb("cb", [P, 2, 1, P])
        bt = sb("b_tokens", [P, 2, P])
        xd = sb("x_dt", [P, 2, SSD_HEADS, SSD_P])
        xe = sb("x_dt_rest", [P, 2, SSD_HEADS, SSD_P])
        dec = sb("decay", [P, 2, HG, P])
        mt = sb("mixed", [P, 2, HG, P])
        state = sb("state", [P, SSD_HEADS, SSD_P])
        yo = sb("y_off", [P, SSD_HEADS, SSD_P])
        pg = ps("cb_turned", [P, NT])
        pl = [ps(f"decay{n}", [P, HG, P]) for n in range(2)]
        py, po, pst = ps("y_diag", [P, NT]), ps("y_off", [P, NT]), ps("state", [P, NT])
        loaded, staged, g_ready, g_taken, l_ready, l_done, m_done = (sem(n) for n in (
            "loaded", "staged", "cb", "cb_taken", "decay", "exp_done", "mixed"))
        st_chain, o_ready, s_ready, s_done, yo_done, y_done, h_used = (sem(n) for n in (
            "state_scaled", "y_off", "state_in", "state", "y_off_scaled", "y", "mixed_used"))
        with nc.Block() as block:
            @block.sync
            def _(sp):
                sp.dma_start(pick[:, :, :], dram["bc_spread"]).then_inc(loaded, 16)
                sp.dma_start(npick[:, :, :], dram["neg_pick"]).then_inc(loaded, 16)
                for j in range(4):
                    sp.dma_start(mask[:, j, :], dram["mask_k"]).then_inc(loaded, 16)

            def units(eng, one, first=None):
                with eng.Fori(0, B) as b:
                    if first:
                        first(b * CPS, 0)
                    with eng.Fori(0, CPS // 2 - 1) as c2:
                        for p in range(2):
                            one(b * CPS + 2 * c2 + p, b, 2 * c2 + p, p, True)
                    for p in range(2):
                        one(b * CPS + CPS - 2 + p, b, CPS - 2 + p, p, p == 0)

            @block.gpsimd
            def _(pool):
                def one(u, b, c, p, more):
                    pool.wait_ge(y_done, u + 1)
                    src = xbc[:, :, ds(b, 1), ds(c * P, P)].rearrange("p m o t -> p m (o t)")
                    nc.gpsimd.tensor_copy(st[:, p, :, :], src).then_inc(staged, 1)

                units(pool, one)

            @block.tensor
            def _(pe):
                pe.wait_ge(loaded, 96)

                def prepare(u, p):
                    pe.wait_ge(staged, u + 1)
                    pe.wait_ge(g_taken, 4 * u + 1)
                    nc.tensor.matmul(pg[:, 0:P], st[:, p, 2, :], st[:, p, 3, :], start=True, stop=True)
                    for j in range(3):
                        mm = nc.tensor.transpose(pg[:, (j + 1) * P:(j + 2) * P], st[:, p, j, :], net.ident[:, :])
                    mm.then_inc(g_ready, 1)

                def decays(u, g):
                    pe.wait_ge(l_done, NG * u + g + 1)
                    for q in range(2):
                        h0 = g * HG + 4 * q
                        dst = pl[g % 2][:, 4 * q:4 * q + 4, :]
                        nc.tensor.matmul(dst, net.identb[:, :], mask[:, :, :], start=True, stop=False)
                        nc.tensor.matmul(dst, csp[:, ds(u * P, P)], npick[:, h0:h0 + 4, :], start=False, stop=False)
                        for j in range(4):
                            mm = nc.tensor.matmul(dst[:, j, :], pick[:, h0 + j, :], csp[:, ds(u * P, P)],
                                                  start=False, stop=(j == 3))
                    mm.then_inc(l_ready, 1)

                def first(u, p):
                    prepare(u, p)
                    decays(u, 0)
                    decays(u, 1)

                def one(u, b, c, p, more):
                    def values(g):
                        pe.wait_ge(m_done, NG * u + g + 3)
                        if g == 0:
                            pe.wait_ge(y_done, u + 2)
                        for h in range(HG):
                            hh = g * HG + h
                            mm = nc.tensor.matmul(py[:, hh * SSD_P:(hh + 1) * SSD_P], mt[:, g % 2, h, :],
                                                  xd[:, p, hh, :], start=True, stop=True)
                        mm.then_inc(h_used, 1)

                    pe.wait_ge(s_done, u + 1)
                    pe.wait_ge(yo_done, u + 1)
                    nc.tensor.matmul(po[:, 0:DI], st[:, p, 3, :], state[:, :, :].rearrange("p h e -> p (h e)"),
                                     start=True, stop=True).then_inc(o_ready, 1)
                    pe.wait_ge(g_taken, 4 * u + 5)
                    nc.tensor.matmul(pst[:, 0:DI], bt[:, p, :], xe[:, p, :, :].rearrange("p h e -> p (h e)"),
                                     start=True, stop=True).then_inc(s_ready, 1)
                    decays(u, 2)
                    values(0)
                    decays(u, 3)
                    values(1)
                    if more:
                        prepare(u + 1, 1 - p)
                        decays(u + 1, 0)
                    values(2)
                    if more:
                        decays(u + 1, 1)
                    values(3)

                units(pe, one, first)

            @block.scalar
            def _(act):
                nc.scalar.preload_act_table_set("natural_log_exp_and_others")
                act.sem_inc(l_done, 2)

                def one(u, b, c, p, more):
                    for g in range(NG):
                        act.wait_ge(l_ready, NG * u + g + 1)
                        act.wait_ge(m_done, NG * u + g + 1)
                        nc.scalar.activation(dec[:, g % 2, :, :], pl[g % 2][:, :, :], ACT.Exp).then_inc(l_done, 1)

                units(act, one)

            @block.vector
            def _(dve):
                nc.vector.memset(state[:, :, :], 0.0).then_inc(s_done, 1)
                dve.sem_inc(y_done, 2)
                dve.sem_inc(yo_done, 1)
                dve.sem_inc(g_taken, 1)
                dve.sem_inc(h_used, 2)
                dve.sem_inc(m_done, 2)
                v = lambda t, u: t[:, ds(u, 1), :].rearrange("p o h -> p h o")

                def take(u, p):
                    tok = pg[:, P:P + DI].rearrange("p (h e) -> p h e", e=SSD_P)
                    dve.wait_ge(g_ready, u + 1)
                    nc.vector.tensor_copy(gs[:, p, 0, :], pg[:, 0:P]).then_inc(g_taken, 1)
                    nc.vector.tensor_tensor(xd[:, p, :, :], tok, wide(v(dt, u)), ALU.mult).then_inc(g_taken, 1)
                    nc.vector.tensor_copy(bt[:, p, :], pg[:, P + DI:P + DI + P]).then_inc(g_taken, 1)
                    dve.wait_ge(g_taken, 4 * u + 4)
                    nc.vector.tensor_tensor(xe[:, p, :, :], xd[:, p, :, :], wide(v(e_out, u)), ALU.mult).then_inc(g_taken, 1)

                def one(u, b, c, p, more):
                    def mix(g):
                        dve.wait_ge(l_done, NG * u + g + 3)
                        dve.wait_ge(g_taken, 4 * u + 5)
                        dve.wait_ge(h_used, NG * u + g + 1)
                        nc.vector.tensor_tensor(mt[:, g % 2, :, :], dec[:, g % 2, :, :],
                                                gs[:, p, :, :].to_broadcast((P, HG, P)), ALU.mult).then_inc(m_done, 1)

                    mix(0)
                    dve.wait_ge(o_ready, u + 1)
                    dve.wait_ge(y_done, u + 2)
                    nc.vector.tensor_tensor(yo[:, :, :], po[:, 0:DI].rearrange("p (h e) -> p h e", e=SSD_P),
                                            wide(v(e_cs, u)), ALU.mult).then_inc(yo_done, 1)
                    nc.vector.tensor_tensor(state[:, :, :], state[:, :, :], wide(v(e_all, u)), ALU.mult).then_inc(st_chain, 1)
                    mix(1)
                    dve.wait_ge(s_ready, u + 1)
                    dve.wait_ge(st_chain, u + 1)
                    nc.vector.tensor_tensor(state[:, :, :], pst[:, 0:DI].rearrange("p (h e) -> p h e", e=SSD_P),
                                            state[:, :, :], ALU.add).then_inc(s_done, 1)
                    mix(2)
                    mix(3)
                    if more:
                        take(u + 1, 1 - p)
                    dve.wait_ge(h_used, NG * u + NG + 2)
                    dve.wait_ge(yo_done, u + 2)
                    dst = xbc[:, 0:2, ds(b, 1), ds(c * P, P)].rearrange("p m o t -> p m (o t)")
                    nc.vector.tensor_tensor(dst, py[:, 0:DI].rearrange("p (m t) -> p m t", m=2),
                                            yo[:, :, :].rearrange("p (m h) e -> p m (h e)", m=2), ALU.add
                                            ).then_inc(y_done, 1)

                units(dve, one, take)


def ssd_output(net, tag, xbc, zs, w_out, DI):
    nc, x = net.nc, net.x
    with stage(nc, tag + "_out") as (sb, ps, sem):
        sq = sb("squares", [P, CPS, DI])
        st = sb("stats", [P, 6, CPS, 1])
        yn = sb("gated", [P, 2, CPS, DI])
        yt = sb("turned", [P, 2, 2, NT])
        py = ps("turned", [P, 2, 2, NT])
        po = ps("proj", [P, 2, NT])
        c, normed, turned, copied, ready, done = (sem(n) for n in (
            "chain", "normed", "turned", "copied", "ready", "done"))
        with nc.Block() as block:
            @block.vector
            def _(dve):
                n = [0]

                def step(a):
                    a.then_inc(c, 1)
                    n[0] += 1
                    dve.wait_ge(c, n[0])

                wide = lambda t: t.to_broadcast((P, CPS, DI))

                def normalize(b):
                    y = xbc[:, 0:2, b, 0:S].rearrange("p m (c t) -> p c m t", t=P)
                    if b >= 2:
                        dve.wait_ge(turned, 2 * (b - 1))
                    g = yn[:, b % 2, :, :]
                    g4 = g.rearrange("p c (m t) -> p c m t", m=2)
                    step(nc.vector.tensor_reduce(st[:, 0, :, 0], y, AX.XY, ALU.add))
                    step(nc.vector.tensor_scalar(st[:, 1, :, :], st[:, 0, :, :], 1.0 / DI, None, ALU.mult))
                    step(nc.vector.tensor_tensor(g4, y, st[:, 1, :, :].unsqueeze(2).to_broadcast((P, CPS, 2, P)), ALU.subtract))
                    step(nc.vector.tensor_tensor(sq[:, :, :], g, g, ALU.mult))
                    step(nc.vector.tensor_reduce(st[:, 2, :, 0], sq[:, :, :], AX.X, ALU.add))
                    dve.wait_ge(c, n[0] + 2)
                    n[0] += 2
                    step(nc.vector.tensor_tensor(g, g, wide(st[:, 4, :, :]), ALU.mult))
                    step(nc.vector.tensor_tensor(g, g, zs[:, b * CPS:(b + 1) * CPS, :], ALU.mult))
                    dve.sem_inc(normed, 1)

                def add(t):
                    dve.wait_ge(ready, t + 1)
                    nc.vector.tensor_tensor(x[:, t * NT:(t + 1) * NT], po[:, t % 2, :], x[:, t * NT:(t + 1) * NT],
                                            ALU.add).then_inc(done, 1)

                normalize(0)
                for b in range(B):
                    if b + 1 < B:
                        normalize(b + 1)
                    add(2 * b)
                    add(2 * b + 1)

            @block.scalar
            def _(act):
                nc.scalar.preload_act_table_set("natural_log_exp_and_others")
                def root(b):
                    act.wait_ge(c, 9 * b + 5)
                    nc.scalar.activation(st[:, 3, :, :], st[:, 2, :, :], ACT.Ln, bias=net.ln_eps,
                                         scale=1.0 / DI).then_inc(c, 1)
                    act.wait_ge(c, 9 * b + 6)
                    nc.scalar.activation(st[:, 4, :, :], st[:, 3, :, :], ACT.Exp, scale=-0.5).then_inc(c, 1)

                def copy(t):
                    act.wait_ge(turned, t + 1)
                    if t >= 2:
                        act.wait_ge(ready, t - 1)
                    nc.scalar.activation(yt[:, t % 2, :, :], py[:, t % 2, :, :], ACT.Copy).then_inc(copied, 1)

                root(0)
                for b in range(B):
                    if b + 1 < B:
                        root(b + 1)
                    copy(2 * b)
                    copy(2 * b + 1)

            @block.tensor
            def _(pe):
                for t in range(TILES):
                    b = t // 2
                    pe.wait_ge(normed, b + 1)
                    if t >= 2:
                        pe.wait_ge(copied, t - 1)
                    for m in range(2):
                        for k in range(4):
                            mm = nc.tensor.transpose(py[:, t % 2, m, k * P:(k + 1) * P],
                                                     yn[:, b % 2, 4 * (t % 2) + k, m * P:(m + 1) * P], net.ident[:, :])
                    mm.then_inc(turned, 1)
                    pe.wait_ge(copied, t + 1)
                    if t >= 2:
                        pe.wait_ge(done, t - 1)
                    for m in range(2):
                        mm = nc.tensor.matmul(po[:, t % 2, :], w_out[:, m, :], yt[:, t % 2, m, :],
                                              start=(m == 0), stop=(m == 1))
                    mm.then_inc(ready, 1)


def build(nc, dram, out):
    with ExitStack() as ctx:
        net = Net(nc, ctx, dram)
        load_consts(net)
        for l in LAYERS:
            if l in (1, 3):
                ternary_ffn(net, f"l{l}", "f0_up", "f0_dn", True, 0.0)
            if l in (9, 11):
                ternary_ffn(net, f"l{l}", "f2_up", "f2_dn", False, 1e-8, "f2_b1", "f2_b2")
            if l == 2:
                attention(net, "l2", dict(wq="a0_wq", wk="a0_wk", wv="a0_wv", wo="a0_wo"), 8, 8 ** -0.5, decay=True)
            if l in (4, 6):
                n = "a1" if l == 4 else "b1"
                attention(net, f"l{l}", {m: f"{n}_{m}" for m in ("wq", "wk", "wq_sw", "wk_sw", "wv", "wo", "bq", "bk",
                                                                 "bq_sw", "bk_sw", "bv", "bo")},
                          8, 8 ** -0.5, rope=True, bias=True, out_bias=True)
            if l == 8:
                attention(net, "l8", {m: f"a2_{m}" for m in ("wq", "wk", "wv", "wo", "bq", "bk", "bv", "bo")},
                          8, 8 ** -0.5, bias=True, out_bias=True)
            if l in (5, 7):
                experts_ffn(net, f"l{l}", dict(router="m1_router", fc="m1_fc", proj="m1_proj"))
            if l in (13, 15):
                gated_ffn(net, f"l{l}")
            if l == 10:
                ssd(net, "l10")
            if l == 0:
                selective_ssm(net, "l0", "s0_", 2, 4, 3, True, True, True, True)
            if l == 12:
                selective_ssm(net, "l12", "s3_", 1, 3, 1, False, False, False, False)
            if l == 14:
                attention(net, "l14", {m: f"b3_{m}" for m in ("wq", "wk", "wv", "wo", "bo")}, 4, 0.5,
                          alibi=True, out_bias=True)
        store_out(net, out)


def thirds(a):
    bf = mybir.dt.np(BF16)
    hi = a.astype(bf)
    mid = (a - hi.astype(np.float32)).astype(bf)
    low = (a - hi.astype(np.float32) - mid.astype(np.float32)).astype(bf)
    return np.stack([hi, mid, low])


def shape_constants():
    bf = mybir.dt.np(BF16)
    f = np.float32
    pos = np.arange(S, dtype=f)
    d = np.arange(P) % 8
    freq = (1.0 / 10000.0 ** ((d // 2 * 2).astype(f) / 8)).astype(f)
    theta = pos[None] * freq[:, None]
    sign = np.where(d % 2 == 0, -1.0, 1.0).astype(f)[:, None]
    rope = np.stack([np.cos(theta), np.sin(theta) * sign], 1).astype(f)
    i = np.arange(P)
    mask_q = np.where(i[:, None] < i[None], NEG, 0.0).astype(bf)
    nums = np.linspace(0.0, 1.0, 241).astype(f)
    vals = np.concatenate([np.ones(15, f), 1.0 - nums ** f(1.0 / np.e)]).astype(f)
    dist = np.clip(np.arange(DECAY_SPAN)[None] - i[:, None], 0, 255)
    slopes = (2.0 ** (-8.0 * np.arange(1, HEADS + 1) / HEADS)).astype(f)
    sl = np.broadcast_to(thirds(slopes)[:, :, None], (3, HEADS, S))
    nq = thirds(-(slopes[:, None] * pos[None]))
    aq = np.concatenate([sl, sl, nq]).reshape(9, 4, 4, S).transpose(1, 0, 2, 3)
    hi, lo = np.floor(pos / 8) * 8, pos % 8
    ak = np.broadcast_to(np.stack([hi] * 3 + [lo] * 3 + [np.ones(S, f)] * 3)[:, None], (9, 4, S)).astype(bf)
    sel = np.broadcast_to(np.eye(P, EXPERTS, dtype=f)[:, :, None], (P, EXPERTS, P)).astype(bf)
    spread = np.zeros((P, 32, P), bf)
    for part in range(3):
        for n in range(32):
            spread[32 * part + n, n] = 1.0
    ones9 = np.zeros((P, 9), f)
    ones9[:, 8] = 1.0
    return {
        "ident": np.eye(P, dtype=f), "rope": rope, "mask_q": mask_q, "mask_k": mask_q.T,
        "decay": vals[dist], "ones9": ones9, "ones_rows": np.ones((3, 4, S), bf), "zero_rows": np.zeros((3, 4, S), bf),
        "alibi_q": np.tile(aq, (4, 1, 1, 1)).reshape(GROUPS * 9, 4, S), "alibi_k": ak, "expert_select": sel, "bc_spread": spread, "neg_pick": -spread,
        "triangle": (i[:, None] <= i[None]).astype(f), "last_row": np.broadcast_to((i == P - 1)[:, None], (P, P)).astype(f),
    }


def attention_layouts(i):
    row, one = (lambda v: v.reshape(1, -1)), (lambda v: v.reshape(-1, 1))
    swap = np.arange(P) ^ 1
    out = {}
    w = i["L0_attn_b_W_attn"]
    out.update(a0_wq=w[:, :P], a0_wk=w[:, P:2 * P], a0_wv=w[:, 2 * P:], a0_wo=i["L0_attn_b_W_proj"])
    for n, wn, f in (("a1", "L1_attn_a_w", lambda m: m.T), ("b1", "L1_attn_b_W", lambda m: m)):
        q, k, bq, bk = f(i[wn + "q"]), f(i[wn + "k"]), i[wn[:-1] + "bq"], i[wn[:-1] + "bk"]
        out.update({f"{n}_wq": q, f"{n}_wk": k, f"{n}_wv": f(i[wn + "v"]), f"{n}_wo": f(i[wn + "o"]),
                    f"{n}_wq_sw": q[:, swap], f"{n}_wk_sw": k[:, swap], f"{n}_bq": one(bq), f"{n}_bk": one(bk),
                    f"{n}_bq_sw": one(bq[swap]), f"{n}_bk_sw": one(bk[swap]),
                    f"{n}_bv": row(i[wn[:-1] + "bv"]), f"{n}_bo": one(i[wn[:-1] + "bo"])})
    w = i["L2_attn_a_attn_W"].reshape(D, HEADS, 3, 8)
    b = i["L2_attn_a_attn_b"].reshape(HEADS, 3, 8)
    for j, n in enumerate("qkv"):
        out[f"a2_w{n}"] = w[:, :, j].reshape(D, P)
        out[f"a2_b{n}"] = (row if n == "v" else one)(b[:, j].reshape(P))
    out.update(a2_wo=i["L2_attn_a_out_W"], a2_bo=one(i["L2_attn_a_out_b"]))
    out.update(b3_wq=np.tile(i["L3_attn_b_Wq"], (1, 2)), b3_wk=np.tile(i["L3_attn_b_Wk"], (1, 8)),
               b3_wv=np.tile(i["L3_attn_b_Wv"], (1, 4)), b3_wo=i["L3_attn_b_Wp"], b3_bo=one(i["L3_attn_b_bp"]))
    return out


def ffn_layouts(i):
    col = lambda v: v.reshape(-1, P).T
    kcn = lambda w: w.reshape(HC, P, -1).transpose(1, 0, 2)
    g = lambda n: i["L3_ffn_" + n]
    return {
        "m1_router": i["L1_ffn_router_w"].T,
        "m1_fc": i["L1_ffn_expert_fc"].transpose(1, 0, 2),
        "m1_proj": i["L1_ffn_expert_proj"].transpose(2, 0, 1).reshape(HC, P, EXPERTS, P).transpose(1, 2, 0, 3),
        "g3_w1": g("w1_w").T, "g3_w2": g("w2_w").T, "g3_h1": kcn(g("h1_w").T), "g3_h2": kcn(g("h2_w").T),
        "g3_w3": kcn(g("w3_w").T),
        "g3_scales": np.concatenate([col(g(n)) for n in ("w1_s", "w2_s", "h1_s", "h2_s", "w3_s")], 1),
    }


def ssm_layouts(i):
    f = np.float32
    hcol = lambda v: v.reshape(-1, P).T

    def cols(H, taps, **c):
        out = np.zeros((P, 64), f)
        for at, n in ((0, "bin"), (4, "cvb"), (6, "dtb"), (8, "dbb"), (9, "rms"), (10, "bout")):
            if n in c:
                v = np.zeros(-(-c[n].size // P) * P, f)
                v[:c[n].size] = c[n]
                v = hcol(v)
                out[:, at:at + v.shape[1]] = v
        out[:, 16:16 + H * taps] = c["cvw"].reshape(H, P, taps).transpose(1, 0, 2).reshape(P, H * taps)
        return out

    def chunks(m, H):
        return m.reshape(H, P, -1).transpose(1, 0, 2)

    def triple(bc, extra=None):
        z = np.zeros(bc.shape[:-1] + (32,), f)
        if extra is not None:
            z[..., :extra.shape[-1]] = extra
        return np.concatenate([bc, bc, bc, z], -1)

    g = lambda n: i["L0_attn_a_" + n]
    W, b = g("dbc_W"), g("dbc_b")
    dup = np.zeros((P, 2, P), f)
    dup[96:112] = g("dup_W").reshape(16, 2, P)
    out = {
        "s0_win": g("in_W"), "s0_a": g("A_log").reshape(2, P, NS).transpose(1, 0, 2),
        "s0_cols": cols(2, 4, bin=g("in_b"), cvb=g("conv_b"), dtb=g("dup_b"), dbb=triple(b[16:], b[:16]),
                        rms=g("rms_w"), bout=g("out_b"), cvw=g("conv_w")),
        "s0_dbc": chunks(triple(W[:, 16:], W[:, :16]), 2), "s0_dt": dup, "s0_out": chunks(g("out_W"), 2),
    }
    g = lambda n: i["L3_attn_a_" + n]
    out.update({
        "s3_win": np.concatenate([g("Win"), g("Wg")], 1), "s3_a": g("A")[:, None],
        "s3_cols": cols(1, 3, bin=np.concatenate([g("b_in"), g("bg")]), cvb=g("convb"), dtb=g("bdt"),
                        dbb=triple(np.concatenate([g("bb"), g("bc")])), bout=g("bout"), cvw=g("convw")),
        "s3_dbc": triple(np.concatenate([g("Wb"), g("Wc")], 1))[:, None], "s3_dt": g("Wdt")[:, None],
        "s3_out": g("Wout")[:, None],
    })
    return out


def ssd_layouts(i):
    g = lambda n: i["L2_attn_b_" + n]
    w = g("in_proj_w").T
    conv = np.concatenate([g("conv_w"), g("conv_b")[:, None]], 1).reshape(4, P, 5).transpose(1, 0, 2)
    return {
        "d2_w": w[:, 256:768], "d2_wz": np.concatenate([w[:, :256], w[:, 768:]], 1), "d2_conv": conv,
        "d2_out": g("out_proj_w").T.reshape(2, P, D).transpose(1, 0, 2), "d2_dtb": g("dt_bias").reshape(1, -1),
        "d2_lnw": g("ln_w").reshape(1, -1), "d2_alog": g("A_log").reshape(1, -1),
    }


def layouts(i):
    col = lambda v: np.ascontiguousarray(v.reshape(-1, P).T)
    return {
        "x": i["L0_attn_a_x"].reshape(T, D).T,
        **shape_constants(), **attention_layouts(i), **ffn_layouts(i), **ssm_layouts(i), **ssd_layouts(i),
        "f0_up": i["L0_ffn_w_up"].T,
        "f0_dn": i["L0_ffn_w_down"].T,
        "f2_up": i["L2_ffn_W1"].T,
        "f2_dn": i["L2_ffn_W2"].T,
        "f2_b1": col(i["L2_ffn_b1"]),
        "f2_b2": col(i["L2_ffn_b2"]),
    }


def kernel(**inputs):
    import concourse.bacc as bacc
    from concourse.bass_utils import run_bass_kernel_spmd

    nc = bacc.Bacc("TRN2", target_bir_lowering=False, num_devices=1)
    arrays = {n: np.ascontiguousarray(a) for n, a in layouts({k: np.asarray(v) for k, v in inputs.items()}).items()}
    dram = {n: nc.dram_tensor(n + "_dram", a.shape, mybir.dt.from_np(a.dtype), kind="ExternalInput").ap()
            for n, a in arrays.items()}
    out = nc.dram_tensor("out_dram", (P, T), F32, kind="ExternalOutput").ap()
    build(nc, dram, out)
    r = run_bass_kernel_spmd(nc, [{n + "_dram": a for n, a in arrays.items()}], core_ids=[0])
    return np.ascontiguousarray(r.results[0]["out_dram"].T).reshape(B, S, D)
```
